# Optimizing a Trainium2 kernel written in Bass

```python
import numpy as np
import jax
import jax.numpy as jnp

def _softmax(x, axis=-1):
    return jax.nn.softmax(x, axis=axis)

def _gelu(x):
    return jax.nn.gelu(x, approximate=True)

def _silu(x):
    return jax.nn.silu(x)

def _sigmoid(x):
    return jax.nn.sigmoid(x)

def _layernorm(x, axis=-1, eps=1e-05):
    m = jnp.mean(x, axis=axis, keepdims=True)
    v = jnp.var(x, axis=axis, keepdims=True)
    return (x - m) / jnp.sqrt(v + eps)

def _scatter_add(tgt, idx, src, axis=0):
    return tgt.at[idx].add(src)

def _segment_sum(src, seg, n):
    return jax.ops.segment_sum(src, seg, n)
kernel_name = 'mk_xattn_ffn_d4_seqx_r8_311dc0'

def setup_inputs(seed: int=0):
    np.random.seed(seed)
    _w = jnp.asarray

    def _rec_inputs():
        import jax
        import jax.numpy as jnp
        _rk = jax.random.key(seed)
        x = -0.0002928 + 1 * jax.random.normal(jax.random.fold_in(_rk, 1), (64, 128, 128), jnp.float32)
        _lenS = 128 - jax.random.randint(jax.random.fold_in(_rk, 7), (64,), 0, max(1, 128 // 4) + 1, jnp.int32)
        _lenS2 = 77 - jax.random.randint(jax.random.fold_in(_rk, 8), (64,), 0, max(1, 77 // 4) + 1, jnp.int32)
        _ctx_1024P = jax.random.normal(jax.random.fold_in(_rk, 11), (64, 16, 128), jnp.float32)
        _ctx_1024c = jax.random.dirichlet(jax.random.fold_in(_rk, 511), 0.3 * jnp.ones((16,), jnp.float32), (64, 77))
        _ctx_1024t = jnp.einsum('bsk,bkd->bsd', _ctx_1024c, _ctx_1024P)
        _ctx_1024t = _ctx_1024t * jax.lax.rsqrt(jnp.mean(jnp.square(_ctx_1024t)) + 1e-12) * 0.953939
        ctx_1024 = -1.39393e-06 + 0.999914 * (_ctx_1024t + 0.3 * jax.random.normal(jax.random.fold_in(_rk, 611), (64, 77, 128), jnp.float32))
        _validS = jnp.arange(128)[None, :] < _lenS[:, None]
        _validS2 = jnp.arange(77)[None, :] < _lenS2[:, None]
        _causal = jnp.tril(jnp.ones((128, 128), dtype=bool))
        mask_Bx1x1xS2_bk0 = jnp.logical_not(jnp.broadcast_to(_validS2[:, None, None, :], (64, 1, 1, 77)))
        mask_BxS_ff1 = jnp.where(jnp.ones((64, 128), dtype=bool), 1.0, 0.0).astype(jnp.float32)
        mask_BxS2_ik0 = jnp.where(jnp.broadcast_to(_validS2[:, :], (64, 77)), 0, 1).astype(jnp.int32)
        return (x, ctx_1024, mask_Bx1x1xS2_bk0, mask_BxS_ff1, mask_BxS2_ik0)
    x, ctx_1024, mask_Bx1x1xS2_bk0, mask_BxS_ff1, mask_BxS2_ik0 = _rec_inputs()

    def _L0_xattn_setup():
        import jax, jax.numpy as jnp
        import numpy as np
        import math
        D_MODEL = 128
        N_HEADS = 16
        D_HEAD = D_MODEL // N_HEADS
        NUM_BUCKETS = 32
        MAX_DISTANCE = 128
        B, LQ, LK = (2, 256, 256)

        def _rel_pos_bucket(rel):
            n = jnp.clip(-rel, 0, None)
            max_exact = NUM_BUCKETS // 2
            is_small = n < max_exact
            val_if_large = max_exact + (jnp.log(n.astype(jnp.float32) / max_exact + 1e-09) / math.log(MAX_DISTANCE / max_exact) * (NUM_BUCKETS - max_exact)).astype(jnp.int32)
            val_if_large = jnp.minimum(val_if_large, NUM_BUCKETS - 1)
            return jnp.where(is_small, n, val_if_large)
        key = jax.random.key(seed)
        ks = jax.random.split(key, 9)
        scale = 1.0 / math.sqrt(D_MODEL)
        q = jax.random.normal(ks[0], (B, LQ, D_MODEL), dtype=jnp.float32)
        k = jax.random.normal(ks[1], (B, LK, D_MODEL), dtype=jnp.float32)
        v = jax.random.normal(ks[2], (B, LK, D_MODEL), dtype=jnp.float32)
        key_padding_mask = jax.random.randint(ks[3], (B, 1, 1, LK), 0, 2).astype(bool)
        Wq = jax.random.normal(ks[4], (D_MODEL, D_MODEL), dtype=jnp.float32) * scale
        Wk = jax.random.normal(ks[5], (D_MODEL, D_MODEL), dtype=jnp.float32) * scale
        Wv = jax.random.normal(ks[6], (D_MODEL, D_MODEL), dtype=jnp.float32) * scale
        Wo = jax.random.normal(ks[7], (D_MODEL, D_MODEL), dtype=jnp.float32) * scale
        rel_emb = jax.random.normal(ks[8], (NUM_BUCKETS, N_HEADS), dtype=jnp.float32) * 0.02
        return {'q': q, 'k': k, 'v': v, 'key_padding_mask': key_padding_mask, 'Wq': Wq, 'Wk': Wk, 'Wv': Wv, 'Wo': Wo, 'rel_emb': rel_emb}
    _L0_xattn_all = _L0_xattn_setup()
    _L0_xattn_in = {k: v for k, v in _L0_xattn_all.items() if k in ('Wq', 'Wk', 'Wv', 'Wo', 'rel_emb')}
    del _L0_xattn_all

    def _L0_ffn_setup():
        import jax, jax.numpy as jnp
        import numpy as np
        EPS = 1e-05

        def _layernorm(x, w, b):
            mu = jnp.mean(x, axis=-1, keepdims=True)
            var = jnp.mean((x - mu) ** 2, axis=-1, keepdims=True)
            return (x - mu) * jax.lax.rsqrt(var + EPS) * w + b

        def _rope_tables(T, D, base=10000.0):
            inv_freq = 1.0 / base ** (jnp.arange(0, D, 2, dtype=jnp.float32) / D)
            t = jnp.arange(T, dtype=jnp.float32)
            freqs = jnp.einsum('i,j->ij', t, inv_freq)
            emb = jnp.concatenate([freqs, freqs], axis=-1)
            return (jnp.cos(emb), jnp.sin(emb))

        def _rotate_half(x):
            x1, x2 = (x[..., :x.shape[-1] // 2], x[..., x.shape[-1] // 2:])
            return jnp.concatenate([-x2, x1], axis=-1)

        def _attn(x, ln_w, ln_b, conv_w, attn_w, proj_w, n_head):
            B, T, C = x.shape
            D = C // n_head
            h = _layernorm(x, ln_w, ln_b)
            hc = jnp.transpose(h, (0, 2, 1))
            hc = jnp.pad(hc, ((0, 0), (0, 0), (2, 0)))
            hc = jax.lax.conv_general_dilated(hc, conv_w, window_strides=(1,), padding='VALID', dimension_numbers=('NCH', 'OIH', 'NCH'), feature_group_count=C)
            h = jnp.transpose(hc, (0, 2, 1))
            qkv = h @ attn_w
            q, k, v = jnp.split(qkv, 3, axis=-1)
            q = q.reshape(B, T, n_head, D)
            k = k.reshape(B, T, n_head, D)
            v = v.reshape(B, T, n_head, D)
            cos, sin = _rope_tables(T, D)
            cos = cos[None, :, None, :]
            sin = sin[None, :, None, :]
            q = q * cos + _rotate_half(q) * sin
            k = k * cos + _rotate_half(k) * sin
            scores = jnp.einsum('bqhd,bkhd->bhqk', q, k) / jnp.sqrt(jnp.float32(D))
            causal = jnp.tril(jnp.ones((T, T), dtype=bool))
            scores = jnp.where(causal, scores, jnp.float32(-1e+30))
            p = jax.nn.softmax(scores, axis=-1)
            y = jnp.einsum('bhqk,bkhd->bqhd', p, v).reshape(B, T, C)
            return y @ proj_w

        def _moe(x, ln_w, ln_b, router_w, expert_wv, expert_proj):
            h = _layernorm(x, ln_w, ln_b)
            logits = h @ router_w
            expert_idx = jnp.argmax(logits, axis=-1)
            E = router_w.shape[-1]
            out = jnp.zeros_like(x)
            for e in range(E):
                gv = h @ expert_wv[e]
                gate_raw, value = jnp.split(gv, 2, axis=-1)
                y = gate_raw * jax.nn.sigmoid(gate_raw) * value @ expert_proj[e]
                out = out + jnp.where((expert_idx == e)[..., None], y, 0.0)
            return out
        C, H, E, B, T = (128, 16, 4, 4, 128)
        Dff = 4 * C
        key = jax.random.key(seed)
        ks = jax.random.split(key, 8)
        s = 0.02
        return {'x': jax.random.normal(ks[0], (B, T, C), dtype=jnp.float32), 'ln1_w': jnp.ones((C,), jnp.float32), 'ln1_b': jnp.zeros((C,), jnp.float32), 'ln2_w': jnp.ones((C,), jnp.float32), 'ln2_b': jnp.zeros((C,), jnp.float32), 'conv_w': jax.random.normal(ks[1], (C, 1, 3), dtype=jnp.float32) * 0.1, 'attn_w': jax.random.normal(ks[2], (C, 3 * C), dtype=jnp.float32) * s, 'proj_w': jax.random.normal(ks[3], (C, C), dtype=jnp.float32) * s, 'router_w': jax.random.normal(ks[4], (C, E), dtype=jnp.float32) * s, 'expert_wv': jax.random.normal(ks[5], (E, C, 2 * Dff), dtype=jnp.float32) * s, 'expert_proj': jax.random.normal(ks[6], (E, Dff, C), dtype=jnp.float32) * s}
    _L0_ffn_all = _L0_ffn_setup()
    _L0_ffn_in = {k: v for k, v in _L0_ffn_all.items() if k in ('ln1_w', 'ln1_b', 'ln2_w', 'ln2_b', 'conv_w', 'attn_w', 'proj_w', 'router_w', 'expert_wv', 'expert_proj')}
    del _L0_ffn_all

    def _L1_xattn_setup():
        import jax, jax.numpy as jnp
        import numpy as np
        B, SQ, SK, D = (4, 256, 256, 128)
        key = jax.random.key(seed)
        ks = jax.random.split(key, 8)
        s = 1.0 / np.sqrt(D)
        return {'input_seq': jax.random.normal(ks[0], (B, SQ, D), jnp.float32), 'condition_seq': jax.random.normal(ks[1], (B, SK, D), jnp.float32), 'Wq': jax.random.normal(ks[2], (D, D), jnp.float32) * s, 'bq': jnp.zeros((D,), jnp.float32), 'Wk': jax.random.normal(ks[3], (D, D), jnp.float32) * s, 'bk': jnp.zeros((D,), jnp.float32), 'Wv': jax.random.normal(ks[4], (D, D), jnp.float32) * s, 'bv': jnp.zeros((D,), jnp.float32)}
    _L1_xattn_all = _L1_xattn_setup()
    _L1_xattn_in = {k: v for k, v in _L1_xattn_all.items() if k in ('Wq', 'bq', 'Wk', 'bk', 'Wv', 'bv')}
    del _L1_xattn_all

    def _L1_ffn_setup():
        import jax, jax.numpy as jnp
        import numpy as np
        B, S, D_MODEL, D_HIDDEN = (4, 256, 128, 512)

        def act_quant(x):
            scale = 127.0 / jnp.clip(jnp.max(jnp.abs(x), axis=-1, keepdims=True), 1e-05)
            return jnp.clip(jnp.round(x * scale), -128, 127) / scale

        def weight_quant(w):
            scale = 1.0 / jnp.clip(jnp.mean(jnp.abs(w)), 1e-05)
            return jnp.clip(jnp.round(w * scale), -1, 1) / scale

        def bit_linear(x, w):
            xq = x + jax.lax.stop_gradient(act_quant(x) - x)
            wq = w + jax.lax.stop_gradient(weight_quant(w) - w)
            return jnp.einsum('bsd,hd->bsh', xq, wq)

        def depthwise_conv1d(x_bcl, w, b):
            y = jax.lax.conv_general_dilated(x_bcl, w, window_strides=(1,), padding=[(1, 1)], dimension_numbers=('NCH', 'OIH', 'NCH'), feature_group_count=x_bcl.shape[1])
            return y + b[None, :, None]
        key = jax.random.key(seed)
        ks = jax.random.split(key, 5)
        lim1 = 1.0 / np.sqrt(D_MODEL)
        lim2 = 1.0 / np.sqrt(D_HIDDEN)
        limc = 1.0 / np.sqrt(3.0)
        return {'x': jax.random.normal(ks[0], (B, S, D_MODEL), dtype=jnp.float32), 'w1': jax.random.uniform(ks[1], (D_HIDDEN, D_MODEL), jnp.float32, -lim1, lim1), 'conv_w': jax.random.uniform(ks[2], (D_HIDDEN, 1, 3), jnp.float32, -limc, limc), 'conv_b': jax.random.uniform(ks[3], (D_HIDDEN,), jnp.float32, -limc, limc), 'w2': jax.random.uniform(ks[4], (D_MODEL, D_HIDDEN), jnp.float32, -lim2, lim2)}
    _L1_ffn_all = _L1_ffn_setup()
    _L1_ffn_in = {k: v for k, v in _L1_ffn_all.items() if k in ('w1', 'conv_w', 'conv_b', 'w2')}
    del _L1_ffn_all

    def _L2_xattn_setup():
        import jax, jax.numpy as jnp
        import numpy as np
        B, L_ENC, L_DEC, D = (16, 64, 128, 128)
        key = jax.random.key(seed)
        k1, k2, k3, k4, k5, k6 = jax.random.split(key, 6)
        encoder_hc = jax.random.normal(k1, (B, L_ENC, D), dtype=jnp.float32)
        decoder_hq = jax.random.normal(k2, (B, L_DEC, D), dtype=jnp.float32)
        w_sim = jax.random.normal(k3, (3 * D,), dtype=jnp.float32) * 0.02
        b_sim = jax.random.normal(k4, (1,), dtype=jnp.float32) * 0.02
        W_qv = jax.random.normal(k5, (4 * D, D), dtype=jnp.float32) * 0.02
        b_qv = jax.random.normal(k6, (D,), dtype=jnp.float32) * 0.02
        return {'encoder_hc': encoder_hc, 'decoder_hq': decoder_hq, 'w_sim': w_sim, 'b_sim': b_sim, 'W_qv': W_qv, 'b_qv': b_qv}
    _L2_xattn_all = _L2_xattn_setup()
    _L2_xattn_in = {k: v for k, v in _L2_xattn_all.items() if k in ('w_sim', 'b_sim', 'W_qv', 'b_qv')}
    del _L2_xattn_all

    def _L2_ffn_setup():
        import jax, jax.numpy as jnp
        import numpy as np
        BLOCK = 32
        W_BITS = 4
        ACT_BITS = 16

        def act_qdq(x):
            qmax = 2.0 ** (ACT_BITS - 1) - 1.0
            scale = jnp.maximum(jnp.max(jnp.abs(x)) / qmax, 1e-12)
            return jnp.clip(jnp.round(x / scale), -qmax - 1.0, qmax) * scale

        def fixed_qdq_u16(x):
            scale = 1.0 / 65536.0
            return jnp.clip(jnp.round(x / scale), 0.0, 65535.0) * scale

        def lpbq_dequant(w):
            O, I = w.shape
            qmax = 2.0 ** (W_BITS - 1) - 1.0
            wb = w.reshape(O, I // BLOCK, BLOCK)
            s = jnp.maximum(jnp.max(jnp.abs(wb), axis=-1, keepdims=True) / qmax, 1e-12)
            wq = jnp.clip(jnp.round(wb / s), -qmax - 1.0, qmax) * s
            return wq.reshape(O, I)
        key = jax.random.key(seed)
        k1, k2, k3, k4 = jax.random.split(key, 4)
        B, S, H, I = (2, 512, 128, 384)
        x = jax.random.normal(k1, (B, S, H), jnp.float32)
        w_gate = jax.random.normal(k2, (I, H), jnp.float32) * 0.02
        w_up = jax.random.normal(k3, (I, H), jnp.float32) * 0.02
        w_down = jax.random.normal(k4, (H, I), jnp.float32) * 0.02
        return {'x': x, 'w_gate': w_gate, 'w_up': w_up, 'w_down': w_down}
    _L2_ffn_all = _L2_ffn_setup()
    _L2_ffn_in = {k: v for k, v in _L2_ffn_all.items() if k in ('w_gate', 'w_up', 'w_down')}
    del _L2_ffn_all

    def _L3_xattn_setup():
        import jax, jax.numpy as jnp
        import numpy as np
        B, F, T, D = (8, 32, 32, 128)
        NEG = -1e+30
        key = jax.random.key(seed)
        ks = jax.random.split(key, 10)
        s = 1.0 / np.sqrt(D)
        return {'features': jax.random.normal(ks[0], (B, F, D), jnp.float32), 'masks': jnp.ones((B, F), jnp.float32), 'textual_features': jax.random.normal(ks[1], (B, T, D), jnp.float32), 'q_masks': jax.random.randint(ks[2], (B, T), 0, 2, jnp.int32), 'Ws': jax.random.normal(ks[3], (D, D), jnp.float32) * s, 'W': jax.random.normal(ks[4], (D, D), jnp.float32) * s, 'w': jax.random.normal(ks[5], (D, 1), jnp.float32) * s, 'b': jax.random.normal(ks[6], (1, D), jnp.float32) * s, 'Wcw': jax.random.normal(ks[7], (1, D), jnp.float32) * s, 'bcw': jnp.zeros((1,), jnp.float32), 'Wcb': jax.random.normal(ks[8], (1, D), jnp.float32) * s, 'bcb': jnp.zeros((1,), jnp.float32)}
    _L3_xattn_all = _L3_xattn_setup()
    _L3_xattn_in = {k: v for k, v in _L3_xattn_all.items() if k in ('Ws', 'W', 'w', 'b', 'Wcw', 'bcw', 'Wcb', 'bcb')}
    del _L3_xattn_all

    def _L3_ffn_setup():
        import jax, jax.numpy as jnp
        import numpy as np
        H = 128
        E = 8
        B, S = (4, 256)
        key = jax.random.key(seed)
        k1, k2, k3, k4 = jax.random.split(key, 4)
        x = jax.random.normal(k1, (B, S, H), dtype=jnp.float32)
        wg = jax.random.normal(k2, (H, E), dtype=jnp.float32) * 0.02
        W = jax.random.normal(k3, (E, H, H), dtype=jnp.float32) * 0.02
        b = jax.random.normal(k4, (E, H), dtype=jnp.float32) * 0.02
        return {'x': x, 'wg': wg, 'W': W, 'b': b}
    _L3_ffn_all = _L3_ffn_setup()
    _L3_ffn_in = {k: v for k, v in _L3_ffn_all.items() if k in ('wg', 'W', 'b')}
    del _L3_ffn_all
    return {'x': x, 'ctx_1024': ctx_1024, 'mask_Bx1x1xS2_bk0': mask_Bx1x1xS2_bk0, 'mask_BxS_ff1': mask_BxS_ff1, 'mask_BxS2_ik0': mask_BxS2_ik0, 'L0_xattn_Wq': _L0_xattn_in['Wq'], 'L0_xattn_Wk': _L0_xattn_in['Wk'], 'L0_xattn_Wv': _L0_xattn_in['Wv'], 'L0_xattn_Wo': _L0_xattn_in['Wo'], 'L0_xattn_rel_emb': _L0_xattn_in['rel_emb'], 'L0_ffn_ln1_w': _L0_ffn_in['ln1_w'], 'L0_ffn_ln1_b': _L0_ffn_in['ln1_b'], 'L0_ffn_ln2_w': _L0_ffn_in['ln2_w'], 'L0_ffn_ln2_b': _L0_ffn_in['ln2_b'], 'L0_ffn_conv_w': _L0_ffn_in['conv_w'], 'L0_ffn_attn_w': _L0_ffn_in['attn_w'], 'L0_ffn_proj_w': _L0_ffn_in['proj_w'], 'L0_ffn_router_w': _L0_ffn_in['router_w'], 'L0_ffn_expert_wv': _L0_ffn_in['expert_wv'], 'L0_ffn_expert_proj': _L0_ffn_in['expert_proj'], 'L1_xattn_Wq': _L1_xattn_in['Wq'], 'L1_xattn_bq': _L1_xattn_in['bq'], 'L1_xattn_Wk': _L1_xattn_in['Wk'], 'L1_xattn_bk': _L1_xattn_in['bk'], 'L1_xattn_Wv': _L1_xattn_in['Wv'], 'L1_xattn_bv': _L1_xattn_in['bv'], 'L1_ffn_w1': _L1_ffn_in['w1'], 'L1_ffn_conv_w': _L1_ffn_in['conv_w'], 'L1_ffn_conv_b': _L1_ffn_in['conv_b'], 'L1_ffn_w2': _L1_ffn_in['w2'], 'L2_xattn_w_sim': _L2_xattn_in['w_sim'], 'L2_xattn_b_sim': _L2_xattn_in['b_sim'], 'L2_xattn_W_qv': _L2_xattn_in['W_qv'], 'L2_xattn_b_qv': _L2_xattn_in['b_qv'], 'L2_ffn_w_gate': _L2_ffn_in['w_gate'], 'L2_ffn_w_up': _L2_ffn_in['w_up'], 'L2_ffn_w_down': _L2_ffn_in['w_down'], 'L3_xattn_Ws': _L3_xattn_in['Ws'], 'L3_xattn_W': _L3_xattn_in['W'], 'L3_xattn_w': _L3_xattn_in['w'], 'L3_xattn_b': _L3_xattn_in['b'], 'L3_xattn_Wcw': _L3_xattn_in['Wcw'], 'L3_xattn_bcw': _L3_xattn_in['bcw'], 'L3_xattn_Wcb': _L3_xattn_in['Wcb'], 'L3_xattn_bcb': _L3_xattn_in['bcb'], 'L3_ffn_wg': _L3_ffn_in['wg'], 'L3_ffn_W': _L3_ffn_in['W'], 'L3_ffn_b': _L3_ffn_in['b']}

def reference(x, ctx_1024, mask_Bx1x1xS2_bk0, mask_BxS_ff1, mask_BxS2_ik0, L0_xattn_Wq, L0_xattn_Wk, L0_xattn_Wv, L0_xattn_Wo, L0_xattn_rel_emb, L0_ffn_ln1_w, L0_ffn_ln1_b, L0_ffn_ln2_w, L0_ffn_ln2_b, L0_ffn_conv_w, L0_ffn_attn_w, L0_ffn_proj_w, L0_ffn_router_w, L0_ffn_expert_wv, L0_ffn_expert_proj, L1_xattn_Wq, L1_xattn_bq, L1_xattn_Wk, L1_xattn_bk, L1_xattn_Wv, L1_xattn_bv, L1_ffn_w1, L1_ffn_conv_w, L1_ffn_conv_b, L1_ffn_w2, L2_xattn_w_sim, L2_xattn_b_sim, L2_xattn_W_qv, L2_xattn_b_qv, L2_ffn_w_gate, L2_ffn_w_up, L2_ffn_w_down, L3_xattn_Ws, L3_xattn_W, L3_xattn_w, L3_xattn_b, L3_xattn_Wcw, L3_xattn_bcw, L3_xattn_Wcb, L3_xattn_bcb, L3_ffn_wg, L3_ffn_W, L3_ffn_b):
    import jax
    import jax.numpy as jnp

    def _L0_xattn_ref(q, k, v, key_padding_mask, Wq, Wk, Wv, Wo, rel_emb):
        import jax, jax.numpy as jnp
        import numpy as np
        import math
        D_MODEL = 128
        N_HEADS = 16
        D_HEAD = D_MODEL // N_HEADS
        NUM_BUCKETS = 32
        MAX_DISTANCE = 128
        B, LQ, LK = (2, 256, 256)

        def _rel_pos_bucket(rel):
            n = jnp.clip(-rel, 0, None)
            max_exact = NUM_BUCKETS // 2
            is_small = n < max_exact
            val_if_large = max_exact + (jnp.log(n.astype(jnp.float32) / max_exact + 1e-09) / math.log(MAX_DISTANCE / max_exact) * (NUM_BUCKETS - max_exact)).astype(jnp.int32)
            val_if_large = jnp.minimum(val_if_large, NUM_BUCKETS - 1)
            return jnp.where(is_small, n, val_if_large)
        Bq, Lq, _ = q.shape
        Lk = k.shape[1]
        qh = (q @ Wq.T).reshape(Bq, Lq, N_HEADS, D_HEAD).transpose(0, 2, 1, 3)
        kh = (k @ Wk.T).reshape(Bq, Lk, N_HEADS, D_HEAD).transpose(0, 2, 1, 3)
        vh = (v @ Wv.T).reshape(Bq, Lk, N_HEADS, D_HEAD).transpose(0, 2, 1, 3)
        scores = jnp.einsum('bhqd,bhkd->bhqk', qh, kh) / math.sqrt(D_HEAD)
        rel = jnp.arange(Lk, dtype=jnp.int32)[None, :] - jnp.arange(Lq, dtype=jnp.int32)[:, None]
        buckets = _rel_pos_bucket(rel)
        bias = rel_emb[buckets]
        scores = scores + bias.transpose(2, 0, 1)[None]
        scores = jnp.where(key_padding_mask, scores, -1000000000.0)
        attn = jax.nn.softmax(scores, axis=-1)
        out = jnp.einsum('bhqk,bhkd->bhqd', attn, vh)
        out = out.transpose(0, 2, 1, 3).reshape(Bq, Lq, D_MODEL)
        return out @ Wo.T

    def _L0_ffn_ref(x, ln1_w, ln1_b, ln2_w, ln2_b, conv_w, attn_w, proj_w, router_w, expert_wv, expert_proj):
        import jax, jax.numpy as jnp
        import numpy as np
        EPS = 1e-05

        def _layernorm(x, w, b):
            mu = jnp.mean(x, axis=-1, keepdims=True)
            var = jnp.mean((x - mu) ** 2, axis=-1, keepdims=True)
            return (x - mu) * jax.lax.rsqrt(var + EPS) * w + b

        def _rope_tables(T, D, base=10000.0):
            inv_freq = 1.0 / base ** (jnp.arange(0, D, 2, dtype=jnp.float32) / D)
            t = jnp.arange(T, dtype=jnp.float32)
            freqs = jnp.einsum('i,j->ij', t, inv_freq)
            emb = jnp.concatenate([freqs, freqs], axis=-1)
            return (jnp.cos(emb), jnp.sin(emb))

        def _rotate_half(x):
            x1, x2 = (x[..., :x.shape[-1] // 2], x[..., x.shape[-1] // 2:])
            return jnp.concatenate([-x2, x1], axis=-1)

        def _attn(x, ln_w, ln_b, conv_w, attn_w, proj_w, n_head):
            B, T, C = x.shape
            D = C // n_head
            h = _layernorm(x, ln_w, ln_b)
            hc = jnp.transpose(h, (0, 2, 1))
            hc = jnp.pad(hc, ((0, 0), (0, 0), (2, 0)))
            hc = jax.lax.conv_general_dilated(hc, conv_w, window_strides=(1,), padding='VALID', dimension_numbers=('NCH', 'OIH', 'NCH'), feature_group_count=C)
            h = jnp.transpose(hc, (0, 2, 1))
            qkv = h @ attn_w
            q, k, v = jnp.split(qkv, 3, axis=-1)
            q = q.reshape(B, T, n_head, D)
            k = k.reshape(B, T, n_head, D)
            v = v.reshape(B, T, n_head, D)
            cos, sin = _rope_tables(T, D)
            cos = cos[None, :, None, :]
            sin = sin[None, :, None, :]
            q = q * cos + _rotate_half(q) * sin
            k = k * cos + _rotate_half(k) * sin
            scores = jnp.einsum('bqhd,bkhd->bhqk', q, k) / jnp.sqrt(jnp.float32(D))
            causal = jnp.tril(jnp.ones((T, T), dtype=bool))
            scores = jnp.where(causal, scores, jnp.float32(-1e+30))
            p = jax.nn.softmax(scores, axis=-1)
            y = jnp.einsum('bhqk,bkhd->bqhd', p, v).reshape(B, T, C)
            return y @ proj_w

        def _moe(x, ln_w, ln_b, router_w, expert_wv, expert_proj):
            h = _layernorm(x, ln_w, ln_b)
            logits = h @ router_w
            expert_idx = jnp.argmax(logits, axis=-1)
            E = router_w.shape[-1]
            out = jnp.zeros_like(x)
            for e in range(E):
                gv = h @ expert_wv[e]
                gate_raw, value = jnp.split(gv, 2, axis=-1)
                y = gate_raw * jax.nn.sigmoid(gate_raw) * value @ expert_proj[e]
                out = out + jnp.where((expert_idx == e)[..., None], y, 0.0)
            return out
        n_head = 16
        x = x + _attn(x, ln1_w, ln1_b, conv_w, attn_w, proj_w, n_head)
        x = x + _moe(x, ln2_w, ln2_b, router_w, expert_wv, expert_proj)
        return x

    def _L1_xattn_ref(input_seq, condition_seq, Wq, bq, Wk, bk, Wv, bv):
        import jax, jax.numpy as jnp
        import numpy as np
        B, SQ, SK, D = (4, 256, 256, 128)
        q = jnp.einsum('bsd,ed->bse', input_seq, Wq) + bq
        k = jnp.einsum('btd,ed->bte', condition_seq, Wk) + bk
        v = jnp.einsum('btd,ed->bte', condition_seq, Wv) + bv
        scores = jnp.einsum('bse,bte->bst', q, k)
        attn = jax.nn.softmax(scores, axis=-1)
        attended = jnp.einsum('bst,bte->bse', attn, v)
        return attended

    def _L1_ffn_ref(x, w1, conv_w, conv_b, w2):
        import jax, jax.numpy as jnp
        import numpy as np
        B, S, D_MODEL, D_HIDDEN = (4, 256, 128, 512)

        def act_quant(x):
            scale = 127.0 / jnp.clip(jnp.max(jnp.abs(x), axis=-1, keepdims=True), 1e-05)
            return jnp.clip(jnp.round(x * scale), -128, 127) / scale

        def weight_quant(w):
            scale = 1.0 / jnp.clip(jnp.mean(jnp.abs(w)), 1e-05)
            return jnp.clip(jnp.round(w * scale), -1, 1) / scale

        def bit_linear(x, w):
            xq = x + jax.lax.stop_gradient(act_quant(x) - x)
            wq = w + jax.lax.stop_gradient(weight_quant(w) - w)
            return jnp.einsum('bsd,hd->bsh', xq, wq)

        def depthwise_conv1d(x_bcl, w, b):
            y = jax.lax.conv_general_dilated(x_bcl, w, window_strides=(1,), padding=[(1, 1)], dimension_numbers=('NCH', 'OIH', 'NCH'), feature_group_count=x_bcl.shape[1])
            return y + b[None, :, None]
        h = bit_linear(x, w1)
        h = depthwise_conv1d(h.transpose(0, 2, 1), conv_w, conv_b)
        h = h.transpose(0, 2, 1)
        h = jax.nn.silu(h)
        return bit_linear(h, w2)

    def _L2_xattn_ref(encoder_hc, decoder_hq, w_sim, b_sim, W_qv, b_qv):
        import jax, jax.numpy as jnp
        import numpy as np
        B, L_ENC, L_DEC, D = (16, 64, 128, 128)
        d = encoder_hc.shape[-1]
        w1, w2, w3 = (w_sim[:d], w_sim[d:2 * d], w_sim[2 * d:])
        Sim = (encoder_hc @ w1)[:, :, None] + (decoder_hq @ w2)[:, None, :] + jnp.einsum('bid,bjd->bij', encoder_hc * w3, decoder_hq) + b_sim[0]
        A = jax.nn.softmax(Sim, axis=2)
        hq_hat = jnp.einsum('bij,bjd->bid', A, decoder_hq)
        Batt = jax.nn.softmax(jnp.max(Sim, axis=2), axis=1)
        hc_bar = jnp.einsum('bi,bid->bd', Batt, encoder_hc)[:, None, :]
        hc_hat = jnp.broadcast_to(hc_bar, encoder_hc.shape)
        feats = jnp.concatenate([encoder_hc, hq_hat, encoder_hc * hq_hat, encoder_hc * hc_hat], axis=-1)
        hcq = feats @ W_qv + b_qv
        return hcq

    def _L2_ffn_ref(x, w_gate, w_up, w_down):
        import jax, jax.numpy as jnp
        import numpy as np
        BLOCK = 32
        W_BITS = 4
        ACT_BITS = 16

        def act_qdq(x):
            qmax = 2.0 ** (ACT_BITS - 1) - 1.0
            scale = jnp.maximum(jnp.max(jnp.abs(x)) / qmax, 1e-12)
            return jnp.clip(jnp.round(x / scale), -qmax - 1.0, qmax) * scale

        def fixed_qdq_u16(x):
            scale = 1.0 / 65536.0
            return jnp.clip(jnp.round(x / scale), 0.0, 65535.0) * scale

        def lpbq_dequant(w):
            O, I = w.shape
            qmax = 2.0 ** (W_BITS - 1) - 1.0
            wb = w.reshape(O, I // BLOCK, BLOCK)
            s = jnp.maximum(jnp.max(jnp.abs(wb), axis=-1, keepdims=True) / qmax, 1e-12)
            wq = jnp.clip(jnp.round(wb / s), -qmax - 1.0, qmax) * s
            return wq.reshape(O, I)
        x = act_qdq(x)
        up = act_qdq(x @ lpbq_dequant(w_up).T)
        gate = act_qdq(x @ lpbq_dequant(w_gate).T)
        sig = fixed_qdq_u16(jax.nn.sigmoid(gate))
        gate = act_qdq(gate * sig)
        o = act_qdq(gate * up)
        return o @ lpbq_dequant(w_down).T

    def _L3_xattn_ref(features, masks, textual_features, q_masks, Ws, W, w, b, Wcw, bcw, Wcb, bcb):
        import jax, jax.numpy as jnp
        import numpy as np
        B, F, T, D = (8, 32, 32, 128)
        NEG = -1e+30
        txt_proj = jnp.einsum('btd,de->bte', textual_features, Ws)
        feat_proj = jnp.einsum('bfd,de->bfe', features, W)
        h = jnp.tanh(txt_proj[:, None, :, :] + feat_proj[:, :, None, :] + b[None, None, :, :][..., 0, :])
        rho = jnp.einsum('bftd,d->bft', h, w[:, 0])
        qm = q_masks.astype(jnp.float32)
        rho = rho + (1.0 - qm)[:, None, :] * NEG
        att = jax.nn.softmax(rho, axis=-1)
        txt_h = jnp.einsum('bft,btd->bfd', att, textual_features)
        w_s = jnp.tanh(jnp.einsum('bfd,od->bfo', txt_h, Wcw) + bcw)
        b_s = jnp.tanh(jnp.einsum('bfd,od->bfo', txt_h, Wcb) + bcb)
        return w_s * features + b_s

    def _L3_ffn_ref(x, wg, W, b):
        import jax, jax.numpy as jnp
        import numpy as np
        H = 128
        E = 8
        B, S = (4, 256)
        Bb, Ss, Hh = x.shape
        Ee = wg.shape[1]
        T = Bb * Ss
        C = T // Ee
        xt = x.reshape(T, Hh)
        logits = xt @ wg
        probs = jax.nn.softmax(logits, axis=-1)
        idx = jnp.argmax(probs, axis=-1)
        mask = jax.nn.one_hot(idx, Ee, dtype=xt.dtype)
        locations = jnp.cumsum(mask, axis=0) - mask
        mask = mask * (locations < C).astype(xt.dtype)
        gate = jnp.sum(probs * mask, axis=-1)
        loc_s = jnp.sum(locations * mask, axis=-1).astype(jnp.int32)
        loc_oh = jax.nn.one_hot(loc_s, C, dtype=xt.dtype)
        dispatch = mask[:, :, None] * loc_oh[:, None, :]
        combine = gate[:, None, None] * dispatch
        exp_in = jnp.einsum('tec,th->ech', dispatch, xt)
        exp_out = jnp.einsum('ech,efh->ecf', exp_in, W) + b[:, None, :]
        out = jnp.einsum('tec,ecf->tf', combine, exp_out)
        return out.reshape(Bb, Ss, Hh)
    x = x + _L0_xattn_ref(_layernorm(x, axis=-1), ctx_1024, ctx_1024, mask_Bx1x1xS2_bk0, L0_xattn_Wq, L0_xattn_Wk, L0_xattn_Wv, L0_xattn_Wo, L0_xattn_rel_emb)
    x = x + _L0_ffn_ref(_layernorm(x, axis=-1), L0_ffn_ln1_w, L0_ffn_ln1_b, L0_ffn_ln2_w, L0_ffn_ln2_b, L0_ffn_conv_w, L0_ffn_attn_w, L0_ffn_proj_w, L0_ffn_router_w, L0_ffn_expert_wv, L0_ffn_expert_proj)
    x = x + _L1_xattn_ref(_layernorm(x, axis=-1), ctx_1024, L1_xattn_Wq, L1_xattn_bq, L1_xattn_Wk, L1_xattn_bk, L1_xattn_Wv, L1_xattn_bv)
    x = x + _L1_ffn_ref(_layernorm(x, axis=-1), L1_ffn_w1, L1_ffn_conv_w, L1_ffn_conv_b, L1_ffn_w2)
    x = x + _L2_xattn_ref(_layernorm(x, axis=-1), ctx_1024, L2_xattn_w_sim, L2_xattn_b_sim, L2_xattn_W_qv, L2_xattn_b_qv)
    x = x + _L2_ffn_ref(_layernorm(x, axis=-1), L2_ffn_w_gate, L2_ffn_w_up, L2_ffn_w_down)
    x = x + _L3_xattn_ref(_layernorm(x, axis=-1), mask_BxS_ff1, ctx_1024, mask_BxS2_ik0, L3_xattn_Ws, L3_xattn_W, L3_xattn_w, L3_xattn_b, L3_xattn_Wcw, L3_xattn_bcw, L3_xattn_Wcb, L3_xattn_bcb)
    x = x + _L3_ffn_ref(_layernorm(x, axis=-1), L3_ffn_wg, L3_ffn_W, L3_ffn_b)
    return x

_drawn_inputs = setup_inputs


def setup_inputs(seed=0):
    import zlib

    import numpy as np

    out = dict(_drawn_inputs(seed))
    spreads = {'L0_ffn_ln1_w': (1.0, 0.6),
     'L0_ffn_ln1_b': (0.0, 0.8),
     'L0_ffn_ln2_w': (1.0, 0.6),
     'L0_ffn_ln2_b': (0.0, 0.8),
     'L1_xattn_bq': (0.0, 0.578),
     'L1_xattn_bk': (0.0, 2.0),
     'L1_xattn_bv': (0.0, 0.8)}
    factors = {'L0_xattn_rel_emb': 8.0,
     'L0_ffn_conv_w': 8.0,
     'L0_ffn_attn_w': 8.0,
     'L0_ffn_proj_w': 8.0,
     'L0_ffn_router_w': 8.0,
     'L0_ffn_expert_wv': 7.044,
     'L0_ffn_expert_proj': 7.045,
     'L2_xattn_w_sim': 200.0,
     'L2_xattn_b_qv': 40.573,
     'L2_ffn_w_gate': 8.0,
     'L2_ffn_w_up': 8.0,
     'L2_ffn_w_down': 8.0,
     'L3_xattn_b': 200.0,
     'L3_ffn_wg': 17.798,
     'L3_ffn_W': 17.848,
     'L3_ffn_b': 200.0,
     'L1_ffn_w1': 8.0,
     'L1_ffn_conv_w': 8.0,
     'L1_ffn_conv_b': 8.0,
     'L1_ffn_w2': 8.0,
     'L3_xattn_Ws': 25.8,
     'L3_xattn_W': 42.122,
     'L3_xattn_w': 23.597,
     'L2_xattn_W_qv': 4.955,
     'L3_xattn_Wcw': 4.187,
     'L3_xattn_Wcb': 4.838}
    for name, (base, spread) in spreads.items():
        noise = np.random.default_rng([zlib.crc32(name.encode()), seed]).standard_normal(out[name].shape)
        drawn = base * np.exp(spread * noise) if base else spread * noise
        out[name] = jnp.asarray(drawn.astype(out[name].dtype))
    for name, factor in factors.items():
        out[name] = (out[name] * factor).astype(out[name].dtype)
    return out
```

```python
from contextlib import ExitStack

import numpy as np

import concourse.bass as bass
from concourse import mybir

ALU = mybir.AluOpType
ACT = mybir.ActivationFunctionType
F32 = mybir.dt.float32
BF16 = mybir.dt.bfloat16
I32 = mybir.dt.int32
U8 = mybir.dt.uint8
X_AXIS = mybir.AxisListType.X

BATCH, TOK, DIM = 64, 128, 128
KEYS = 77
HEADS, HDIM = 16, 8
VPAD = 32
GROUP = 4
HALF = HEADS // 2
BUCKETS, MAX_DISTANCE = 32, 128
MOE0, FF0 = 4, 512
CHUNKS0 = FF0 // 128
FF1 = 512
FF2 = 384
MOE3 = 8
CAPACITY = BATCH * TOK // MOE3
CH = 128
STREAMS = 4
ROUNDS = BATCH // STREAMS
BANK = 512
LN_EPS = 1e-5
ROUND = float(1.5 * 2 ** 23)
TTILE = 512
TILES = BATCH * TOK // TTILE
KT = 16


class Steps:

    def __init__(self, names, streams=STREAMS, primed=False):
        self.index = {name: n for n, name in enumerate(names.split())}
        assert len(self.index) == len(names.split())
        self.streams = streams
        self.per_round = len(self.index) * streams
        self.ahead = self.per_round if primed else 0
        self.next = 0

    def did(self, name, s):
        assert self.next % self.per_round == self.index[name] * self.streams + s, (name, s, self.next)
        self.next += 1
        return 1

    def value(self, name, s, rnd):
        return rnd * self.per_round + (self.index[name] * self.streams + s + 1 + self.ahead)


PE_1 = Steps("""
    x0.T x0.qkv x0.S0 x0.PT0 x0.PV0 x0.S1 x0.PT1 x0.PV1 x0.ygT x0.yT x0.o f0b.T f0.qkv f0.S0 f0.PT0 f0.PV0 f0.S1
    f0.PT1 f0.PV1 f0.ygT f0.yT f0.o f0c.T moe.route moe.gv0 moe.gv1 moe.down0 moe.gv2 moe.down1 moe.gv3 moe.down2
    moe.down3 x1.T x1.qkv x1.S x1.PT x1.y f1.T f1.up f1.uT f1.uqT f1.down x2.T x2.S x2.PT x2.M x2.hq x2.out f2.T
""")
ACT_1 = Steps("""
    x0.xT x0.qv x0.exp0 x0.PT0 x0.yg0 x0.exp1 x0.PT1 x0.yg1 x0.yT f0b.xT f0.v f0.exp0 f0.PT0 f0.yg0 f0.exp1 f0.PT1
    f0.yg1 f0.yT f0c.xT moe.tanh0 moe.tanh1 moe.tanh2 moe.tanh3 x1.xT x1.qkv x1.exp x1.PT f1.xT f1.mid f1.tanh
    f1.uqT x2.xT x2.exp x2.PT x2.p x2.feat f2.xT
""")
DVE_1 = Steps("""
    x0.stats x0.aggr x0.eps x0.norm x0.kT x0.kblk x0.add0 x0.max0 x0.sub0 x0.add1 x0.max1 x0.sub1 x0.rden x0.y x0.x
    f0a.stats f0a.aggr f0a.eps f0a.norm f0b.stats f0b.aggr f0b.eps f0b.norm f0.conv2 f0.conv1 f0.conv0 f0.rope f0.qk
    f0.kblk f0.max0 f0.sub0 f0.max1 f0.sub1 f0.rden f0.y f0.x f0c.stats f0c.aggr f0c.eps f0c.norm moe.max moe.eq
    moe.first moe.pick moe.add0 moe.add1 moe.add2 moe.add3 moe.x x1.stats x1.aggr x1.eps x1.norm x1.nmax x1.rden
    x1.x x1.bv f1.stats f1.aggr f1.eps f1.norm f1.amax f1.inv f1.scale f1.round f1.xq f1.tap0 f1.taps f1.silu
    f1.uamax f1.uclip f1.urec f1.uscale f1.uround f1.uq f1.x x2.stats x2.aggr x2.eps x2.norm x2.nmax x2.smax
    x2.score x2.rden x2.P x2.M x2.negM x2.rsum x2.hc x2.ehq x2.add f2.x f2.stats f2.aggr f2.eps f2.norm
""")
POOL_1 = Steps("""
    x0.rstd x0.qblk f0a.rstd f0b.rstd f0.qblk f0c.rstd x1.rstd f1.rstd x2.rstd f2.rstd
""")
PE_3 = Steps("""
    x3.T x3.proj x3.rho0 x3.rho_last x3.rho1 x3.rho2 x3.rho3 x3.rhoT x3.PT x3.h x3.gate f3.T f3.route f3.place f3.y
""")
ACT_3 = Steps("""
    x3.xT x3.proj x3.tanh0 x3.tanh_last x3.tanh1 x3.tanh2 x3.tanh3 x3.rho x3.exp x3.PT x3.h x3.gate f3.xT f3.exp
""")
DVE_3 = Steps("""
    x3.stats x3.aggr x3.eps x3.norm x3.sum0 x3.sum1 x3.sum2 x3.sum3 x3.mask x3.nmax x3.rden x3.P x3.gb x3.y x3.x
    f3.stats f3.aggr f3.eps f3.norm f3.nmax f3.rden f3.probs f3.pmax f3.eq f3.first f3.pick f3.taken f3.keep f3.w
    f3.add0 f3.add1 f3.add2 f3.add3 f3.add4 f3.add5 f3.add6 f3.add7
""")
POOL_3 = Steps("""
    x3.rstd f3.rstd
""")
MOE_DVE = Steps("""
    silu0 act0 silu1 act1 silu2 act2 silu3 act3 silu4 act4 silu5 act5 silu6 act6 silu7 act7 silu8 act8 silu9 act9
    silu10 act10 silu11 act11 silu12 act12 silu13 act13 silu14 act14 silu15 act15
""", 1)
PE_2A = Steps("""
    up gate
""", 2)
DVE_2A = Steps("""
    up gate
""", 2, primed=True)
PE_2B = Steps("""
    gate
""", 2)
ACT_2B = Steps("""
    round tanh
""", 2, primed=True)
DVE_2B = Steps("""
    gate sigmoid clip gated max
""", 2, primed=True)
PE_2C = Steps("""
    up
""", 2)
ACT_2C = Steps("""
    round
""", 2, primed=True)
DVE_2C = Steps("""
    round up product max
""", 2, primed=True)
PE_2D = Steps("""
    down
""", 2, primed=True)
DVE_2D = Steps("""
    round quant add
""", 2, primed=True)



def shape_constants():
    c = {}
    p = np.arange(128)
    c["ident"] = np.eye(128, dtype=np.float32)
    c["causal"] = np.where(p[None, :] > p[:, None], np.float32(-1e30), np.float32(0)).astype(np.float32)
    c["before"] = (p[:, None] < p[None, :]).astype(np.float32)
    c["ingroup"] = ((p[:, None] // HDIM) % GROUP == np.arange(GROUP)[None, :]).astype(np.float32)
    c["ofgroup"] = (p[:, None] // (HDIM * GROUP) == np.arange(GROUP)[None, :]).astype(np.float32)
    c["first"] = np.tile(np.arange(MOE3, 0, -1, dtype=np.float32), (128, 1))
    n = np.clip(np.arange(-(KEYS - 1), TOK), 0, None)
    exact = BUCKETS // 2
    large = exact + (np.log(np.maximum(n, exact).astype(np.float32) / np.float32(exact) + np.float32(1e-9))
                     / np.float32(np.log(MAX_DISTANCE / exact)) * np.float32(BUCKETS - exact)).astype(np.int32)
    bucket = np.where(n < exact, n, np.minimum(large, BUCKETS - 1))
    c["bucket"] = (np.arange(BUCKETS)[:, None] == bucket[None, :]).astype(np.float32)
    inv = (np.float32(1.0) / np.float32(10000.0) ** (np.arange(0, HDIM, 2, dtype=np.float32) / np.float32(HDIM))).astype(np.float32)
    ang = np.outer(np.arange(TOK, dtype=np.float32), inv).astype(np.float32)
    i = p % HDIM
    cos = np.cos(ang)[:, i % (HDIM // 2)].T
    sin = np.sin(ang)[:, i % (HDIM // 2)].T * np.where(i < HDIM // 2, -1.0, 1.0)[:, None]
    r = 1.0 / np.sqrt(HDIM)
    c["rope"] = np.stack([cos * r, cos, sin * r, sin], axis=1).astype(np.float32)
    return c


def swap_halves(w):
    k = w.shape[0]
    return np.ascontiguousarray(w.reshape(k, HEADS, 2, HDIM // 2)[:, :, ::-1, :]).reshape(k, DIM)


def build(nc, d):
    x_mid = nc.dram_tensor("x_mid", (BATCH, TOK, DIM), F32, kind="Internal").ap()
    x_mid2 = nc.dram_tensor("x_mid2", (BATCH, TOK, DIM), F32, kind="Internal").ap()
    with ExitStack() as ctx:
        shared = dict(x_mid=x_mid, x_mid2=x_mid2)
        for name, shape in (("xnT_all", [128, BATCH * TOK]), ("ident", [128, 128]), ("ones", [128, 128]),
                            ("first", [128, MOE3]), ("minus_half", [128, 1])):
            shared[name] = ctx.enter_context(nc.sbuf_tensor(name, shape, F32))
        part_1(nc, d, shared)
        part_2(nc, d, shared)
        part_3(nc, d, shared)


def part_1(nc, d, shared):
    xnT_all, ident, ones, first, minus_half, x_mid = (shared[k] for k in ("xnT_all", "ident", "ones", "first", "minus_half", "x_mid"))
    S = range(STREAMS)
    with ExitStack() as ctx:
        def sb(name, shape, dt=F32):
            return ctx.enter_context(nc.sbuf_tensor(name, shape, dt))

        def per_stream(name, shape, dt=F32):
            return [sb(f"{name}{s}", shape, dt) for s in S]

        def sem(name):
            return ctx.enter_context(nc.semaphore(name))

        ident_bf = sb("ident_bf", [128, 128], BF16)
        causal_bf = sb("causal_bf", [128, 128], BF16)
        ingroup = sb("ingroup", [128, GROUP])
        ofgroup = sb("ofgroup", [128, GROUP])
        rope = sb("rope", [128, 4, TOK])
        mask_words = sb("mask_words", [128, (BATCH + STREAMS) * KEYS // 4], I32)
        mask = mask_words[:].bitcast(U8)
        bias0 = sb("bias0", [128, HEADS, KEYS])
        w_xa0 = sb("w_xa0", [128, 4, DIM])
        ln_col = sb("ln_col", [128, 4])
        conv0_col = sb("conv0_col", [128, 3])
        w_at0 = sb("w_at0", [128, 5, DIM])
        w_pr0 = sb("w_pr0", [128, DIM])
        w_ro0 = sb("w_ro0", [128, MOE0])
        w_gv0 = sb("w_gv0", [128, MOE0, 2 * FF0])
        w_dn0 = sb("w_dn0", [128, MOE0, FF0 // CH, DIM])
        w_xa1 = sb("w_xa1", [128, 3, DIM])
        b_xa1 = sb("b_xa1", [128, 2])
        bv1 = sb("bv1", [128, DIM])
        w_up1 = sb("w_up1", [128, FF1])
        conv1_col = sb("conv1_col", [128, FF1 // CH, 4])
        w_dn1 = sb("w_dn1", [128, FF1 // CH, DIM])
        w_dn1_q = sb("w_dn1_q", [128, FF1 // CH, DIM], BF16)
        sim_col = sb("sim_col", [128, 3])
        b_sim = sb("b_sim", [128, 1])
        w_qv2 = sb("w_qv2", [128, 4, DIM])
        b_qv2 = sb("b_qv2", [128, DIM])
        prep = sb("prep", [128, 16])

        x_in = per_stream("x_in", [128, DIM])
        ctx_in = per_stream("ctx_in", [KEYS, DIM])
        ctxT_in = per_stream("ctxT_in", [128, KEYS])
        x = per_stream("x", [128, DIM])
        cx = per_stream("cx", [KEYS, DIM])
        cxT = per_stream("cxT", [128, KEYS])
        xn = per_stream("xn", [128, DIM])
        xnT_4 = sb("xnT_4", [128, STREAMS, TOK])
        xnT = [xnT_4[:, s, :] for s in S]
        h0 = per_stream("h0", [128, DIM])
        attended = per_stream("attended", [128, KEYS])
        thr = per_stream("thr", [128, KEYS])
        bias_m = per_stream("bias_m", [128, HEADS, KEYS])
        qT = per_stream("qT", [128, TOK])
        kT = per_stream("kT", [128, TOK])
        kblk = per_stream("kblk", [128, GROUP, TOK])
        qblk = per_stream("qblk", [128, GROUP, TOK])
        vaug = per_stream("vaug", [128, HEADS, VPAD])
        yg = per_stream("yg", [128, GROUP, TOK])
        prob = per_stream("prob", [128, 2 * BANK])
        probT = per_stream("probT", [128, 2 * BANK])
        y = per_stream("y", [128, DIM])
        yT = per_stream("yT", [128, TOK])
        col = per_stream("col", [128, 48])
        ps = [ctx.enter_context(nc.psum_tensor(f"ps{s}", [128, 2, BANK], F32)) for s in S]

        weights_in, consts_done, setup_pe, setup_act, setup_dve = (sem(n) for n in (
            "weights_in", "consts_done", "setup_pe", "setup_act", "setup_dve"))
        loads_in = [sem(f"loads_in{s}") for s in S]
        stores_out = [sem(f"stores_out{s}") for s in S]
        inputs_ready = sem("inputs_ready")
        mask_tail, mask_made, mask_ready, bias_kept, bias_ready = (sem(n) for n in ("mask_tail", "mask_made", "mask_ready", "bias_kept", "bias_ready"))
        moe_dve_done = sem("moe_dve_done")
        passed = sem("passed")
        pe_done, act_done, dve_done, pool_done = (sem(n) for n in ("pe_done", "act_done", "dve_done", "pool_done"))

        weight_loads = [
            (ident[:], d["ident"]), (first[:], d["first"]), (ingroup[:], d["ingroup"]), (ofgroup[:], d["ofgroup"]), (rope[:], d["rope"]),
            (prob[0][:, 0:128], d["causal"]), (prob[0][0:BUCKETS, 128:128 + TOK + KEYS - 1], d["bucket"]),
            (prob[0][0:BUCKETS, 384:384 + HEADS], d["L0_xattn_rel_emb"]),
            (mask_words[:, 0:BATCH * KEYS // 4], d["mask_Bx1x1xS2_bk0"].to_broadcast([128, BATCH * KEYS // 4])),
            (w_xa0[:, 0, :], d["L0_xattn_Wq"]), (w_xa0[:, 1, :], d["L0_xattn_Wk"]),
            (w_xa0[:, 2, :], d["L0_xattn_Wv"]), (w_xa0[:, 3, :], d["L0_xattn_Wo"]),
            (ln_col[:, 0:1], d["L0_ffn_ln1_w"]), (ln_col[:, 1:2], d["L0_ffn_ln1_b"]),
            (ln_col[:, 2:3], d["L0_ffn_ln2_w"]), (ln_col[:, 3:4], d["L0_ffn_ln2_b"]),
            (conv0_col[:], d["L0_ffn_conv_w"]), (w_at0[:], d["attn_w5"]), (w_pr0[:], d["L0_ffn_proj_w"]),
            (w_ro0[:], d["L0_ffn_router_w"]), (w_gv0[:], d["L0_ffn_expert_wv"].rearrange("e c n -> c e n")),
            (w_dn0[:], d["L0_ffn_expert_proj"].rearrange("e (k c) n -> c e k n", c=CH)),
            (w_xa1[:, 0, :], d["L1_xattn_Wq"]), (w_xa1[:, 1, :], d["L1_xattn_Wk"]), (w_xa1[:, 2, :], d["L1_xattn_Wv"]),
            (b_xa1[:, 0:1], d["L1_xattn_bq"]), (b_xa1[:, 1:2], d["L1_xattn_bk"]),
            (bv1[:], d["L1_xattn_bv"].to_broadcast([128, DIM])),
            (w_up1[:], d["L1_ffn_w1"]), (w_dn1[:], d["L1_ffn_w2"].rearrange("(k c) n -> c k n", c=CH)),
            (conv1_col[:], d["L1_ffn_conv"]), (sim_col[:], d["L2_xattn_w_sim"]), (b_sim[:], d["L2_xattn_b_sim"].to_broadcast([128, 1])),
            (w_qv2[:], d["L2_xattn_W_qv"].rearrange("(k c) n -> c k n", c=DIM)),
            (b_qv2[:], d["L2_xattn_b_qv"].to_broadcast([128, DIM])),
        ]

        def unit_banks(e, c):
            return (e * CHUNKS0 + c) % 3

        def hidden(e, c):
            return prob[c][:, (e % 2) * BANK:(e % 2 + 1) * BANK]

        SETUP_BIAS, SETUP_SUMS, SETUP_DVE = 1, 4, 13

        block = ctx.enter_context(nc.Block())

        @block.sync
        def _(sp):
            def load(s, b):
                sp.dma_start(x_in[s][:], d["x"][bass.ds(b, 1), :, :].rearrange("o t c -> t (o c)")).then_inc(loads_in[s], 16)
                sp.dma_start(ctx_in[s][:], d["ctx"][bass.ds(b, 1), :, :].rearrange("o t c -> t (o c)")).then_inc(loads_in[s], 16)
                sp.dma_start(ctxT_in[s][:], d["ctxT"][bass.ds(b, 1), :, :].rearrange("o t c -> t (o c)")).then_inc(loads_in[s], 16)

            for dst, src in weight_loads:
                sp.dma_start(dst, src).then_inc(weights_in, 16)
            for s in S:
                load(s, s)
            with sp.Fori(0, ROUNDS - 1) as r:
                for s in S:
                    sp.wait_ge(inputs_ready, r * STREAMS + s + 1)
                    load(s, r * STREAMS + (STREAMS + s))

        @block.gpsimd
        def _(pool):
            def take_inputs(s, value):
                pool.wait_ge(loads_in[s], value)
                pool.sem_inc(passed, 1)
                nc.gpsimd.tensor_copy(x[s][:], x_in[s][:])
                nc.gpsimd.tensor_copy(cx[s][:], ctx_in[s][:])
                nc.gpsimd.tensor_copy(cxT[s][:], ctxT_in[s][:]).then_inc(inputs_ready, 1)

            def mask_bias(s, masks, kept):
                pool.wait_ge(mask_ready, masks)
                nc.gpsimd.tensor_tensor(bias_m[s][:], bias0[:], attended[s][:].unsqueeze(1).to_broadcast([128, HEADS, KEYS]), ALU.mult).then_inc(bias_kept, 1)
                pool.wait_ge(bias_kept, kept)
                nc.gpsimd.tensor_tensor(bias_m[s][:], bias_m[s][:], thr[s][:].unsqueeze(1).to_broadcast([128, HEADS, KEYS]), ALU.add).then_inc(bias_ready, 1)

            def steps(r):
                def at(steps_, name, s):
                    return steps_.value(name, s, r)

                def qblocks(p, ready):
                    for s in S:
                        ready(s)
                        nc.gpsimd.tensor_tensor(qblk[s][:], qT[s][:].unsqueeze(1).to_broadcast([128, GROUP, TOK]),
                                                ofgroup[:].unsqueeze(2).to_broadcast([128, GROUP, TOK]), ALU.mult).then_inc(pool_done, POOL_1.did(f"{p}.qblk", s))

                def rstd(p):
                    for s in S:
                        pool.wait_ge(dve_done, at(DVE_1, f"{p}.eps", s))
                        nc.gpsimd.tensor_tensor(col[s][:, 9:10], col[s][:, 8:9], minus_half[:], ALU.pow).then_inc(pool_done, POOL_1.did(f"{p}.rstd", s))

                rstd("x0")
                qblocks("x0", lambda s: pool.wait_ge(act_done, at(ACT_1, "x0.qv", s)))
                rstd("f0a")
                rstd("f0b")
                qblocks("f0", lambda s: pool.wait_ge(dve_done, at(DVE_1, "f0.qk", s)))
                for s in S:
                    pool.wait_ge(dve_done, at(DVE_1, "x0.add1", s))
                    mask_bias(s, (r + 1) * STREAMS + s + 1, r * STREAMS + (STREAMS + s + 1))
                for p in ("f0c", "x1", "f1", "x2", "f2"):
                    rstd(p)

            nc.gpsimd.memset(minus_half[:], -0.5).then_inc(consts_done, 1)
            nc.gpsimd.memset(ones[:], 1.0).then_inc(consts_done, 1)
            for s in S:
                nc.gpsimd.memset(vaug[s][:], 1.0).then_inc(consts_done, 1)
            pool.wait_ge(consts_done, 2 + STREAMS)
            pool.wait_ge(setup_act, 3)
            for s in S:
                take_inputs(s, 48)
            for s in S:
                mask_bias(s, s + 1, s + 1)
            with pool.Fori(0, ROUNDS - 1) as r:
                steps(r)
                for s in S:
                    pool.wait_ge(act_done, ACT_1.value("f2.xT", s, r))
                    pool.wait_ge(stores_out[s], r * 16 + 16)
                    take_inputs(s, r * 48 + 96)
            steps(ROUNDS - 1)

        @block.scalar
        def _(act):
            act.wait_ge(setup_pe, SETUP_BIAS)
            act.wait_ge(consts_done, 2 + STREAMS)
            for n in range(3):
                k0, k1 = n * 32, min(KEYS, n * 32 + 32)
                bank = ps[n // 2][:, n % 2, 0:(k1 - k0) * HEADS]
                nc.scalar.copy(bias0[:, :, k0:k1], bank.rearrange("p (k h) -> p h k", h=HEADS)).then_inc(setup_act, 1)
            with act.Fori(0, ROUNDS) as r:
                def at(steps_, name, s):
                    return steps_.value(name, s, r)

                def xT(p, w=None):
                    for s in S:
                        act.wait_ge(pe_done, at(PE_1, f"{p}.T", s))
                        if w is None:
                            nc.scalar.copy(xnT[s][:], ps[s][:, 0, 0:TOK]).then_inc(act_done, ACT_1.did(f"{p}.xT", s))
                        else:
                            nc.scalar.activation(xnT[s][:], ps[s][:, 0, 0:TOK], ACT.Identity, scale=ln_col[:, w:w + 1], bias=ln_col[:, w + 1:w + 2]).then_inc(act_done, ACT_1.did(f"{p}.xT", s))

                def heads(p, nk):
                    for hf in range(2):
                        for s in S:
                            act.wait_ge(dve_done, at(DVE_1, f"{p}.sub{hf}", s))
                            nc.scalar.activation(prob[s][:, 0:HALF * nk], prob[s][:, 0:HALF * nk], ACT.Exp).then_inc(act_done, ACT_1.did(f"{p}.exp{hf}", s))
                        for s in S:
                            act.wait_ge(pe_done, at(PE_1, f"{p}.PT{hf}", s))
                            nc.scalar.copy(probT[s][0:nk, :], ps[s][0:nk, :, :].rearrange("p b n -> p (b n)")).then_inc(act_done, ACT_1.did(f"{p}.PT{hf}", s))
                        for s in S:
                            act.wait_ge(pe_done, at(PE_1, f"{p}.PV{hf}", s))
                            nc.scalar.copy(yg[s][:, 2 * hf:2 * hf + 2, :], ps[s][:, 0, 0:2 * TOK].rearrange("p (g t) -> p g t", g=2)).then_inc(act_done, ACT_1.did(f"{p}.yg{hf}", s))
                    for s in S:
                        act.wait_ge(pe_done, at(PE_1, f"{p}.yT", s))
                        nc.scalar.copy(yT[s][:], ps[s][:, 1, 0:TOK]).then_inc(act_done, ACT_1.did(f"{p}.yT", s))

                xT("x0")
                for s in S:
                    act.wait_ge(pe_done, at(PE_1, "x0.qkv", s))
                    nc.scalar.activation(qT[s][:], ps[s][:, 0, 0:TOK], ACT.Copy, scale=float(HDIM) ** -0.5)
                    nc.scalar.copy(vaug[s][0:KEYS, :, 0:HDIM], ps[s][0:KEYS, 0, 256:256 + DIM].rearrange("p (h e) -> p h e", h=HEADS)).then_inc(act_done, ACT_1.did("x0.qv", s))
                heads("x0", KEYS)
                xT("f0b", 0)
                for s in S:
                    act.wait_ge(pe_done, at(PE_1, "f0.qkv", s))
                    nc.scalar.copy(vaug[s][:, :, 0:HDIM], ps[s][:, 1, 0:DIM].rearrange("p (h e) -> p h e", h=HEADS)).then_inc(act_done, ACT_1.did("f0.v", s))
                heads("f0", TOK)
                xT("f0c", 2)
                for e in range(MOE0):
                    for c in range(CHUNKS0):
                        if e >= 2:
                            act.wait_ge(pe_done, at(PE_1, f"moe.down{e - 2}", STREAMS - 1))
                        act.wait_ge(pe_done, at(PE_1, f"moe.gv{e}", c))
                        nc.scalar.activation(hidden(e, c), ps[unit_banks(e, c)][:, 0, :], ACT.Tanh, scale=0.5).then_inc(act_done, ACT_1.did(f"moe.tanh{e}", c))
                xT("x1")
                for s in S:
                    act.wait_ge(pe_done, at(PE_1, "x1.qkv", s))
                    nc.scalar.activation(qT[s][:], ps[s][:, 0, 0:TOK], ACT.Identity, bias=b_xa1[:, 0:1])
                    nc.scalar.activation(kT[s][:, 0:KEYS], ps[s][:, 0, 128:128 + KEYS], ACT.Identity, bias=b_xa1[:, 1:2])
                    nc.scalar.copy(y[s][0:KEYS, :], ps[s][0:KEYS, 0, 256:256 + DIM]).then_inc(act_done, ACT_1.did("x1.qkv", s))
                for s in S:
                    act.wait_ge(dve_done, at(DVE_1, "x1.nmax", s))
                    nc.scalar.activation(prob[s][:, 0:KEYS], ps[s][:, 1, 0:KEYS], ACT.Exp, bias=col[s][:, 16:17], accum_out=col[s][:, 17:18]).then_inc(act_done, ACT_1.did("x1.exp", s))
                for s in S:
                    act.wait_ge(pe_done, at(PE_1, "x1.PT", s))
                    nc.scalar.copy(probT[s][0:KEYS, 0:TOK], ps[s][0:KEYS, 0, 0:TOK]).then_inc(act_done, ACT_1.did("x1.PT", s))
                xT("f1")
                for s in S:
                    act.wait_ge(pe_done, at(PE_1, "f1.up", s))
                    for c in range(FF1 // CH):
                        last = nc.scalar.activation(prob[s][:, c * TOK:(c + 1) * TOK], ps[s][:, 0, c * TOK:(c + 1) * TOK], ACT.Identity, scale=conv1_col[:, c, 1:2], bias=conv1_col[:, c, 3:4])
                    last.then_inc(act_done, ACT_1.did("f1.mid", s))
                for s in S:
                    act.wait_ge(dve_done, at(DVE_1, "f1.taps", s))
                    nc.scalar.activation(prob[s][:, BANK:2 * BANK], prob[s][:, 0:BANK], ACT.Tanh, scale=0.5).then_inc(act_done, ACT_1.did("f1.tanh", s))
                for s in S:
                    act.wait_ge(pe_done, at(PE_1, "f1.uqT", s))
                    nc.scalar.copy(probT[s][:, 256:512].bitcast(BF16), ps[s][:, 1, 0:256].bitcast(BF16)).then_inc(act_done, ACT_1.did("f1.uqT", s))
                for s in S:
                    act.wait_ge(pe_done, at(PE_1, "x2.T", s))
                    nc.scalar.activation(qT[s][:], ps[s][:, 0, 0:TOK], ACT.Identity, scale=sim_col[:, 2:3], bias=sim_col[:, 1:2])
                    nc.scalar.copy(xnT[s][:], ps[s][:, 0, 0:TOK]).then_inc(act_done, ACT_1.did("x2.xT", s))
                for s in S:
                    act.wait_ge(dve_done, at(DVE_1, "x2.score", s))
                    nc.scalar.activation(prob[s][:, 0:KEYS], ps[s][:, 1, 0:KEYS], ACT.Exp, bias=col[s][:, 16:17], accum_out=col[s][:, 17:18]).then_inc(act_done, ACT_1.did("x2.exp", s))
                for s in S:
                    act.wait_ge(pe_done, at(PE_1, "x2.PT", s))
                    nc.scalar.copy(probT[s][0:KEYS, 0:TOK], ps[s][0:KEYS, 0, 0:TOK]).then_inc(act_done, ACT_1.did("x2.PT", s))
                for s in S:
                    act.wait_ge(dve_done, at(DVE_1, "x2.negM", s))
                    nc.scalar.activation(col[s][:, 22:23], col[s][:, 19:20], ACT.Exp, bias=col[s][:, 21:22]).then_inc(act_done, ACT_1.did("x2.p", s))
                for s in S:
                    act.wait_ge(pe_done, at(PE_1, "x2.hq", s))
                    nc.scalar.copy(kT[s][:], ps[s][:, 0, 0:TOK])
                    act.wait_ge(dve_done, at(DVE_1, "x2.hc", s))
                    nc.scalar.activation(yT[s][:], xnT[s][:], ACT.Copy, scale=col[s][:, 24:25]).then_inc(act_done, ACT_1.did("x2.feat", s))
                for s in S:
                    act.wait_ge(dve_done, at(DVE_1, "f2.x", s))
                    act.dma_start(x_mid[bass.ds(r * STREAMS + s, 1), :, :].rearrange("o t c -> t (o c)"), x[s][:]).then_inc(stores_out[s], 16)
                for s in S:
                    act.wait_ge(pe_done, at(PE_1, "f2.T", s))
                    act.sem_inc(passed, 1)
                    nc.scalar.copy(xnT_all[:, bass.ds((r * STREAMS + s) * TOK, TOK)], ps[s][:, 0, 0:TOK]).then_inc(act_done, ACT_1.did("f2.xT", s))
            for s in S:
                act.wait_ge(stores_out[s], 16 * ROUNDS)

        @block.tensor
        def _(pe):
            pe.wait_ge(weights_in, 16 * len(weight_loads))
            pe.wait_ge(consts_done, 2 + STREAMS)
            for k in range(KEYS):
                n, j = k // 32, k % 32
                last = nc.tensor.matmul(ps[n // 2][:, n % 2, j * HEADS:(j + 1) * HEADS], prob[0][0:BUCKETS, 128 + KEYS - 1 - k:128 + KEYS - 1 - k + TOK],
                                        prob[0][0:BUCKETS, 384:384 + HEADS], start=True, stop=True)
            last.then_inc(setup_pe, 1)
            pe.wait_ge(setup_dve, SETUP_SUMS)
            nc.tensor.matmul(ps[3][:, 0, 0:2], ones[:], prep[:, 0:2], start=True, stop=True).then_inc(setup_pe, 1)
            pe.wait_ge(setup_dve, SETUP_DVE)
            pe.wait_ge(setup_act, 3)
            with pe.Fori(0, ROUNDS) as r:
                def at(steps_, name, s):
                    return steps_.value(name, s, r)

                def transpose_xn(p):
                    for s in S:
                        pe.wait_ge(dve_done, at(DVE_1, f"{p}.norm", s))
                        nc.tensor.transpose(ps[s][:, 0, 0:TOK], xn[s][:], ident[:]).then_inc(pe_done, PE_1.did(f"{p}.T", s))

                def heads(p, nk, w_out):
                    for hf in range(2):
                        for s in S:
                            if hf == 0:
                                pe.wait_ge(dve_done, at(DVE_1, f"{p}.kblk", s))
                                pe.wait_ge(pool_done, at(POOL_1, f"{p}.qblk", s))
                                pe.wait_ge(act_done, at(ACT_1, "x0.qv" if p == "x0" else "f0.v", s))
                            else:
                                pe.wait_ge(act_done, at(ACT_1, f"{p}.yg0", s))
                            for b in range(2):
                                last = nc.tensor.matmul(ps[s][:, b, 0:GROUP * nk], qblk[s][:, 2 * hf + b, :], kblk[s][:, :, 0:nk], start=True, stop=(p == "x0"))
                            if p == "f0":
                                for b in range(2):
                                    last = nc.tensor.matmul(ps[s][:, b, :], ident_bf[:], causal_bf[:].unsqueeze(1).to_broadcast([128, GROUP, TOK]), start=False, stop=True)
                            last.then_inc(pe_done, PE_1.did(f"{p}.S{hf}", s))
                        for s in S:
                            pe.wait_ge(act_done, at(ACT_1, f"{p}.exp{hf}", s))
                            for h in range(HALF):
                                last = nc.tensor.transpose(ps[s][0:nk, h // GROUP, (h % GROUP) * TOK:(h % GROUP + 1) * TOK], prob[s][:, h * nk:(h + 1) * nk], ident[:])
                            last.then_inc(pe_done, PE_1.did(f"{p}.PT{hf}", s))
                        for s in S:
                            pe.wait_ge(act_done, at(ACT_1, f"{p}.PT{hf}", s))
                            for h in range(HALF):
                                g, j = h // GROUP, h % GROUP
                                last = nc.tensor.matmul(ps[s][VPAD * j:VPAD * (j + 1), 0, g * TOK:(g + 1) * TOK], vaug[s][0:nk, HALF * hf + h, :], probT[s][0:nk, h * TOK:(h + 1) * TOK],
                                                        start=True, stop=True, tile_position=(0, VPAD * j))
                            last.then_inc(pe_done, PE_1.did(f"{p}.PV{hf}", s))
                    for s in S:
                        pe.wait_ge(act_done, at(ACT_1, f"{p}.yg1", s))
                        for g in range(GROUP):
                            last = nc.tensor.transpose(ps[s][:, 1, g * TOK:(g + 1) * TOK], yg[s][:, g, :], ident[:])
                        last.then_inc(pe_done, PE_1.did(f"{p}.ygT", s))
                    for s in S:
                        pe.wait_ge(dve_done, at(DVE_1, f"{p}.y", s))
                        nc.tensor.transpose(ps[s][:, 1, 0:TOK], y[s][:], ident[:]).then_inc(pe_done, PE_1.did(f"{p}.yT", s))
                    for s in S:
                        pe.wait_ge(act_done, at(ACT_1, f"{p}.yT", s))
                        nc.tensor.matmul(ps[s][:, 0, 0:DIM], yT[s][:], w_out, start=True, stop=True).then_inc(pe_done, PE_1.did(f"{p}.o", s))

                transpose_xn("x0")
                for s in S:
                    pe.wait_ge(act_done, at(ACT_1, "x0.xT", s))
                    nc.tensor.matmul(ps[s][:, 0, 0:TOK], w_xa0[:, 0, :], xnT[s][:], start=True, stop=True)
                    nc.tensor.matmul(ps[s][:, 0, 128:128 + KEYS], w_xa0[:, 1, :], cxT[s][:], start=True, stop=True)
                    nc.tensor.matmul(ps[s][0:KEYS, 0, 256:256 + DIM], cxT[s][:], w_xa0[:, 2, :], start=True, stop=True).then_inc(pe_done, PE_1.did("x0.qkv", s))
                heads("x0", KEYS, w_xa0[:, 3, :])
                transpose_xn("f0b")
                for s in S:
                    pe.wait_ge(dve_done, at(DVE_1, "f0.conv0", s))
                    for n in range(4):
                        nc.tensor.matmul(ps[s][:, 0, n * TOK:(n + 1) * TOK], w_at0[:, n, :], yT[s][:], start=True, stop=True)
                    nc.tensor.matmul(ps[s][:, 1, 0:DIM], yT[s][:], w_at0[:, 4, :], start=True, stop=True).then_inc(pe_done, PE_1.did("f0.qkv", s))
                heads("f0", TOK, w_pr0[:])
                transpose_xn("f0c")
                for s in S:
                    pe.wait_ge(act_done, at(ACT_1, "f0c.xT", s))
                    nc.tensor.matmul(ps[s][:, 1, 0:MOE0], xnT[s][:], w_ro0[:], start=True, stop=True).then_inc(pe_done, PE_1.did("moe.route", s))
                def gate_and_value(e):
                    for c in range(CHUNKS0):
                        u = e * CHUNKS0 + c
                        if u < 3:
                            pe.wait_ge(dve_done, at(DVE_1, "moe.pick", u))
                            if u == 0:
                                pe.wait_ge(act_done, at(ACT_1, "f0c.xT", STREAMS - 1))
                        else:
                            pe.wait_ge(moe_dve_done, at(MOE_DVE, f"act{u - 3}", 0))
                        for v in range(2):
                            last = nc.tensor.matmul(ps[unit_banks(e, c)][:, v, :], w_gv0[:, e, v * FF0 + c * CH:v * FF0 + (c + 1) * CH], xnT_4[:].rearrange("p s t -> p (s t)"), start=True, stop=True)
                        last.then_inc(pe_done, PE_1.did(f"moe.gv{e}", c))

                def down(e):
                    pe.wait_ge(moe_dve_done, at(MOE_DVE, f"act{e * CHUNKS0 + CHUNKS0 - 1}", 0))
                    for s in S:
                        if s == 0:
                            pe.wait_ge(dve_done, at(DVE_1, "moe.pick" if e < 2 else f"moe.add{e - 2}", STREAMS - 1))
                        for c in range(CHUNKS0):
                            last = nc.tensor.matmul(ps[STREAMS - 1][:, e % 2, s * DIM:(s + 1) * DIM], hidden(e, c)[:, s * TOK:(s + 1) * TOK], w_dn0[:, e, c, :], start=(c == 0), stop=(c == CHUNKS0 - 1))
                        last.then_inc(pe_done, PE_1.did(f"moe.down{e}", s))

                gate_and_value(0)
                for e in range(MOE0):
                    if e + 1 < MOE0:
                        gate_and_value(e + 1)
                    down(e)
                transpose_xn("x1")
                for s in S:
                    pe.wait_ge(act_done, at(ACT_1, "x1.xT", s))
                    nc.tensor.matmul(ps[s][:, 0, 0:TOK], w_xa1[:, 0, :], xnT[s][:], start=True, stop=True)
                    nc.tensor.matmul(ps[s][:, 0, 128:128 + KEYS], w_xa1[:, 1, :], cxT[s][:], start=True, stop=True)
                    nc.tensor.matmul(ps[s][0:KEYS, 0, 256:256 + DIM], cxT[s][:], w_xa1[:, 2, :], start=True, stop=True).then_inc(pe_done, PE_1.did("x1.qkv", s))
                for s in S:
                    pe.wait_ge(act_done, at(ACT_1, "x1.qkv", s))
                    nc.tensor.matmul(ps[s][:, 1, 0:KEYS], qT[s][:], kT[s][:, 0:KEYS], start=True, stop=True).then_inc(pe_done, PE_1.did("x1.S", s))
                for s in S:
                    pe.wait_ge(act_done, at(ACT_1, "x1.exp", s))
                    nc.tensor.transpose(ps[s][0:KEYS, 0, 0:TOK], prob[s][:, 0:KEYS], ident[:]).then_inc(pe_done, PE_1.did("x1.PT", s))
                for s in S:
                    pe.wait_ge(act_done, at(ACT_1, "x1.PT", s))
                    nc.tensor.matmul(ps[s][:, 1, 0:DIM], probT[s][0:KEYS, 0:TOK], y[s][0:KEYS, :], start=True, stop=True).then_inc(pe_done, PE_1.did("x1.y", s))
                for s in S:
                    pe.wait_ge(dve_done, at(DVE_1, "f1.xq", s))
                    nc.tensor.transpose(ps[s][:, 0, 0:TOK], xn[s][:], ident[:]).then_inc(pe_done, PE_1.did("f1.T", s))
                for s in S:
                    pe.wait_ge(act_done, at(ACT_1, "f1.xT", s))
                    for c in range(FF1 // CH):
                        last = nc.tensor.matmul(ps[s][:, 0, c * TOK:(c + 1) * TOK], w_up1[:, c * CH:(c + 1) * CH], xnT[s][:], start=True, stop=True)
                    last.then_inc(pe_done, PE_1.did("f1.up", s))
                for s in S:
                    pe.wait_ge(dve_done, at(DVE_1, "f1.silu", s))
                    for c in range(FF1 // CH):
                        last = nc.tensor.transpose(ps[s][:, 0, c * CH:(c + 1) * CH], prob[s][:, c * TOK:(c + 1) * TOK], ident[:])
                    last.then_inc(pe_done, PE_1.did("f1.uT", s))
                for s in S:
                    pe.wait_ge(dve_done, at(DVE_1, "f1.uq", s))
                    for c in range(FF1 // CH):
                        last = nc.tensor.transpose(ps[s][:, 1, 0:256].bitcast(BF16)[:, c * TOK:(c + 1) * TOK], probT[s][:, 0:256].bitcast(BF16)[:, c * CH:(c + 1) * CH], ident_bf[:])
                    last.then_inc(pe_done, PE_1.did("f1.uqT", s))
                for s in S:
                    pe.wait_ge(act_done, at(ACT_1, "f1.uqT", s))
                    for c in range(FF1 // CH):
                        last = nc.tensor.matmul(ps[s][:, 0, 0:DIM], probT[s][:, 256:512].bitcast(BF16)[:, c * TOK:(c + 1) * TOK], w_dn1_q[:, c, :], start=(c == 0), stop=(c == FF1 // CH - 1))
                    last.then_inc(pe_done, PE_1.did("f1.down", s))
                transpose_xn("x2")
                for s in S:
                    pe.wait_ge(act_done, at(ACT_1, "x2.xT", s))
                    nc.tensor.matmul(ps[s][:, 1, 0:KEYS], qT[s][:], cxT[s][:], start=True, stop=True)
                    nc.tensor.matmul(ps[s][:, 1, 80:81], xnT[s][:], sim_col[:, 0:1], start=True, stop=True).then_inc(pe_done, PE_1.did("x2.S", s))
                for s in S:
                    pe.wait_ge(dve_done, at(DVE_1, "x2.P", s))
                    nc.tensor.transpose(ps[s][0:KEYS, 0, 0:TOK], prob[s][:, 0:KEYS], ident[:])
                    nc.tensor.transpose(ps[s][0:1, 0, 128:128 + TOK], col[s][:, 19:20], ident[:]).then_inc(pe_done, PE_1.did("x2.PT", s))
                for s in S:
                    pe.wait_ge(dve_done, at(DVE_1, "x2.M", s))
                    nc.tensor.matmul(ps[s][:, 0, 256:257], ones[0:1, :], col[s][0:1, 20:21], start=True, stop=True).then_inc(pe_done, PE_1.did("x2.M", s))
                for s in S:
                    pe.wait_ge(act_done, at(ACT_1, "x2.p", s))
                    nc.tensor.matmul(ps[s][:, 1, 0:1], xn[s][:], col[s][:, 22:23], start=True, stop=True)
                    nc.tensor.matmul(ps[s][:, 1, 2:3], ones[:], col[s][:, 22:23], start=True, stop=True)
                    nc.tensor.matmul(ps[s][:, 0, 0:TOK], cx[s][:], probT[s][0:KEYS, 0:TOK], start=True, stop=True).then_inc(pe_done, PE_1.did("x2.hq", s))
                for s in S:
                    pe.wait_ge(act_done, at(ACT_1, "x2.feat", s))
                    pe.wait_ge(dve_done, at(DVE_1, "x2.ehq", s))
                    for n, f in enumerate((xnT, kT, qT, yT)):
                        last = nc.tensor.matmul(ps[s][:, 1, 0:DIM], f[s][:], w_qv2[:, n, :], start=(n == 0), stop=(n == 3))
                    last.then_inc(pe_done, PE_1.did("x2.out", s))
                transpose_xn("f2")

        @block.vector
        def _(dve):
            dve.wait_ge(weights_in, 16 * len(weight_loads))
            nc.vector.tensor_copy(causal_bf[:], prob[0][:, 0:128]).then_inc(setup_dve, 1)
            nc.vector.tensor_copy(ident_bf[:], ident[:]).then_inc(setup_dve, 1)
            flat = w_dn1[:].rearrange("p k n -> p (k n)")
            nc.vector.tensor_reduce(prep[:, 0:1], w_up1[:], X_AXIS, ALU.add, apply_absolute_value=True).then_inc(setup_dve, 1)
            nc.vector.tensor_reduce(prep[:, 1:2], flat, X_AXIS, ALU.add, apply_absolute_value=True).then_inc(setup_dve, 1)
            dve.wait_ge(setup_pe, 2)
            nc.vector.tensor_scalar(prep[:, 2:4], ps[3][:, 0, 0:2], 1.0 / (FF1 * DIM), 1e-5, ALU.mult, ALU.max).then_inc(setup_dve, 1)
            dve.wait_ge(setup_dve, 5)
            nc.vector.reciprocal(prep[:, 4:6], prep[:, 2:4]).then_inc(setup_dve, 1)
            dve.wait_ge(setup_dve, 6)
            for n, (w, out) in enumerate(((w_up1[:], w_up1[:]), (flat, w_dn1_q[:].rearrange("p k n -> p (k n)")))):
                nc.vector.tensor_scalar(w, w, prep[:, 4 + n:5 + n], ROUND, ALU.mult, ALU.add).then_inc(setup_dve, 1)
                dve.wait_ge(setup_dve, 7 + 3 * n)
                nc.vector.tensor_scalar(w, w, ROUND, 1.0, ALU.subtract, ALU.min).then_inc(setup_dve, 1)
                dve.wait_ge(setup_dve, 8 + 3 * n)
                if n == 0:
                    nc.vector.tensor_scalar(out, w, -1.0, prep[:, 2:3], ALU.max, ALU.mult).then_inc(setup_dve, 1)
                else:
                    nc.vector.tensor_scalar(out, w, -1.0, None, ALU.max).then_inc(setup_dve, 1)
                dve.wait_ge(setup_dve, 9 + 3 * n)
            nc.vector.tensor_scalar(prep[:, 6:7], prep[:, 3:4], 1.0 / 127.0, None, ALU.mult).then_inc(setup_dve, 1)

            def next_mask(s, b, made):
                nc.vector.tensor_copy(attended[s][:], mask[:, bass.ds(b * KEYS, KEYS)]).then_inc(mask_made, 1)
                dve.wait_ge(mask_made, made)
                nc.vector.tensor_scalar(thr[s][:], attended[s][:], 1e9, -1e9, ALU.mult, ALU.add).then_inc(mask_ready, 1)

            nc.vector.memset(mask_words[:, BATCH * KEYS // 4:], 0).then_inc(mask_tail, 1)
            dve.wait_ge(mask_tail, 1)
            for s in S:
                next_mask(s, s, s + 1)
            with dve.Fori(0, ROUNDS) as r:
                def at(steps_, name, s):
                    return steps_.value(name, s, r)

                def after(name, s):
                    dve.wait_ge(dve_done, at(DVE_1, name, s))

                def norm(p, src, dst, prev=None, ready=None):
                    for s in S:
                        if ready is not None:
                            ready(s)
                        else:
                            after(prev, s)
                        nc.vector.bn_stats(col[s][:, 0:6], src[s][:]).then_inc(dve_done, DVE_1.did(f"{p}.stats", s))
                    for s in S:
                        after(f"{p}.stats", s)
                        dve.sem_inc(passed, 1)
                        nc.vector.bn_aggr(col[s][:, 6:8], col[s][:, 0:6]).then_inc(dve_done, DVE_1.did(f"{p}.aggr", s))
                    for s in S:
                        after(f"{p}.aggr", s)
                        nc.vector.tensor_scalar(col[s][:, 8:9], col[s][:, 7:8], LN_EPS, None, ALU.add).then_inc(dve_done, DVE_1.did(f"{p}.eps", s))
                    for s in S:
                        dve.wait_ge(pool_done, at(POOL_1, f"{p}.rstd", s))
                        nc.vector.tensor_scalar(dst[s][:], src[s][:], col[s][:, 6:7], col[s][:, 9:10], ALU.subtract, ALU.mult).then_inc(dve_done, DVE_1.did(f"{p}.norm", s))

                def heads(p, nk):
                    for hf in range(2):
                        if p == "x0":
                            for s in S:
                                dve.wait_ge(pe_done, at(PE_1, f"{p}.S{hf}", s))
                                dve.wait_ge(bias_ready, r * STREAMS + s + 1)
                                nc.vector.tensor_tensor(prob[s][:, 0:HALF * nk].rearrange("p (b n) -> p b n", b=2), ps[s][:, :, 0:GROUP * nk],
                                                        bias_m[s][:, HALF * hf:HALF * (hf + 1), :].rearrange("p (b h) k -> p b (h k)", b=2), ALU.add).then_inc(dve_done, DVE_1.did(f"{p}.add{hf}", s))
                        for s in S:
                            if p == "x0":
                                after(f"{p}.add{hf}", s)
                                scores = prob[s][:, 0:HALF * nk].rearrange("p (h k) -> p h k", h=HALF)
                            else:
                                dve.wait_ge(pe_done, at(PE_1, f"{p}.S{hf}", s))
                                scores = ps[s][:].rearrange("p b (h k) -> p (b h) k", h=GROUP)
                            nc.vector.tensor_reduce(col[s][:, 16:16 + HALF], scores, X_AXIS, ALU.max).then_inc(dve_done, DVE_1.did(f"{p}.max{hf}", s))
                        for s in S:
                            after(f"{p}.max{hf}", s)
                            out = prob[s][:, 0:HALF * nk].rearrange("p (h k) -> p h k", h=HALF)
                            scores = out if p == "x0" else ps[s][:].rearrange("p b (h k) -> p (b h) k", h=GROUP)
                            nc.vector.tensor_tensor(out, scores, col[s][:, 16:16 + HALF].unsqueeze(2).to_broadcast([128, HALF, nk]), ALU.subtract).then_inc(dve_done, DVE_1.did(f"{p}.sub{hf}", s))
                        if p == "x0" and hf == 1:
                            for s in S:
                                next_mask(s, (r + 1) * STREAMS + s, r * STREAMS + (STREAMS + s + 1))
                    for s in S:
                        dve.wait_ge(pe_done, at(PE_1, f"{p}.ygT", s))
                        out = ps[s][:, 1, :].rearrange("p (h e) -> p h e", h=HEADS)
                        nc.vector.reciprocal(col[s][:, 24:24 + HEADS].unsqueeze(2), out[:, :, HDIM:HDIM + 1]).then_inc(dve_done, DVE_1.did(f"{p}.rden", s))
                    for s in S:
                        after(f"{p}.rden", s)
                        out = ps[s][:, 1, :].rearrange("p (h e) -> p h e", h=HEADS)
                        nc.vector.tensor_tensor(y[s][:].rearrange("p (h e) -> p h e", h=HEADS), out[:, :, 0:HDIM],
                                                col[s][:, 24:24 + HEADS].unsqueeze(2).to_broadcast([128, HEADS, HDIM]), ALU.mult).then_inc(dve_done, DVE_1.did(f"{p}.y", s))

                norm("x0", x, xn, ready=lambda s: dve.wait_ge(inputs_ready, r * STREAMS + s + 1))
                for s in S:
                    dve.wait_ge(act_done, at(ACT_1, "x0.qv", s))
                    nc.vector.tensor_tensor(kT[s][:, 0:KEYS], ps[s][:, 0, 128:128 + KEYS], attended[s][:], ALU.mult).then_inc(dve_done, DVE_1.did("x0.kT", s))
                for s in S:
                    after("x0.kT", s)
                    nc.vector.tensor_tensor(kblk[s][:, :, 0:KEYS], kT[s][:, 0:KEYS].unsqueeze(1).to_broadcast([128, GROUP, KEYS]),
                                            ingroup[:].unsqueeze(2).to_broadcast([128, GROUP, KEYS]), ALU.mult).then_inc(dve_done, DVE_1.did("x0.kblk", s))
                heads("x0", KEYS)
                for s in S:
                    dve.wait_ge(pe_done, at(PE_1, "x0.o", s))
                    nc.vector.tensor_tensor(x[s][:], ps[s][:, 0, 0:DIM], x[s][:], ALU.add).then_inc(dve_done, DVE_1.did("x0.x", s))
                norm("f0a", x, h0, "x0.x")
                norm("f0b", h0, xn, "f0a.norm")
                for n, (name, tap) in enumerate((("f0.conv2", 2), ("f0.conv1", 1), ("f0.conv0", 0))):
                    for s in S:
                        if tap == 2:
                            dve.wait_ge(act_done, at(ACT_1, "f0b.xT", s))
                            nc.vector.tensor_scalar(yT[s][:], xnT[s][:], conv0_col[:, 2:3], None, ALU.mult).then_inc(dve_done, DVE_1.did(name, s))
                        else:
                            after(f"f0.conv{tap + 1}", s)
                            sh = 2 - tap
                            nc.vector.scalar_tensor_tensor(yT[s][:, sh:], xnT[s][:, 0:TOK - sh], conv0_col[:, tap:tap + 1], yT[s][:, sh:], ALU.mult, ALU.add).then_inc(dve_done, DVE_1.did(name, s))
                for s in S:
                    dve.wait_ge(pe_done, at(PE_1, "f0.qkv", s))
                    nc.vector.tensor_tensor(prob[s][:, 0:BANK].rearrange("p (n t) -> p n t", n=4), ps[s][:, 0, :].rearrange("p (n t) -> p n t", n=4), rope[:], ALU.mult).then_inc(dve_done, DVE_1.did("f0.rope", s))
                for s in S:
                    after("f0.rope", s)
                    nc.vector.tensor_tensor(qT[s][:], prob[s][:, 0:128], prob[s][:, 256:384], ALU.add)
                    nc.vector.tensor_tensor(kT[s][:], prob[s][:, 128:256], prob[s][:, 384:512], ALU.add).then_inc(dve_done, DVE_1.did("f0.qk", s))
                for s in S:
                    after("f0.qk", s)
                    nc.vector.tensor_tensor(kblk[s][:], kT[s][:].unsqueeze(1).to_broadcast([128, GROUP, TOK]),
                                            ingroup[:].unsqueeze(2).to_broadcast([128, GROUP, TOK]), ALU.mult).then_inc(dve_done, DVE_1.did("f0.kblk", s))
                heads("f0", TOK)
                for s in S:
                    dve.wait_ge(pe_done, at(PE_1, "f0.o", s))
                    nc.vector.tensor_tensor(h0[s][:], ps[s][:, 0, 0:DIM], h0[s][:], ALU.add).then_inc(dve_done, DVE_1.did("f0.x", s))
                norm("f0c", h0, xn, "f0.x")
                for s in S:
                    dve.wait_ge(pe_done, at(PE_1, "moe.route", s))
                    nc.vector.tensor_reduce(col[s][:, 16:17], ps[s][:, 1, 0:MOE0], X_AXIS, ALU.max).then_inc(dve_done, DVE_1.did("moe.max", s))
                for s in S:
                    after("moe.max", s)
                    nc.vector.scalar_tensor_tensor(col[s][:, 20:24], ps[s][:, 1, 0:MOE0], col[s][:, 16:17], first[:, 0:MOE0], ALU.is_equal, ALU.mult).then_inc(dve_done, DVE_1.did("moe.eq", s))
                for s in S:
                    after("moe.eq", s)
                    nc.vector.tensor_reduce(col[s][:, 17:18], col[s][:, 20:24], X_AXIS, ALU.max).then_inc(dve_done, DVE_1.did("moe.first", s))
                for s in S:
                    after("moe.first", s)
                    nc.vector.tensor_scalar(col[s][:, 24:28], col[s][:, 20:24], col[s][:, 17:18], None, ALU.is_equal).then_inc(dve_done, DVE_1.did("moe.pick", s))
                def add_expert(e):
                    for s in S:
                        if s == 0:
                            dve.wait_ge(pe_done, at(PE_1, f"moe.down{e}", STREAMS - 1))
                        if e == MOE0 - 1:
                            after(f"moe.add{e - 1}", s)
                        nc.vector.scalar_tensor_tensor(h0[s][:], ps[STREAMS - 1][:, e % 2, s * DIM:(s + 1) * DIM], col[s][:, 24 + e:25 + e], h0[s][:], ALU.mult, ALU.add).then_inc(dve_done, DVE_1.did(f"moe.add{e}", s))

                for e in range(MOE0):
                    for c in range(CHUNKS0):
                        u = e * CHUNKS0 + c
                        banks = ps[unit_banks(e, c)]
                        dve.wait_ge(act_done, at(ACT_1, f"moe.tanh{e}", c))
                        nc.vector.scalar_tensor_tensor(hidden(e, c), hidden(e, c), 1.0, banks[:, 0, :], ALU.add, ALU.mult).then_inc(moe_dve_done, MOE_DVE.did(f"silu{u}", 0))
                        dve.wait_ge(moe_dve_done, at(MOE_DVE, f"silu{u}", 0))
                        nc.vector.scalar_tensor_tensor(hidden(e, c), hidden(e, c), 0.5, banks[:, 1, :], ALU.mult, ALU.mult).then_inc(moe_dve_done, MOE_DVE.did(f"act{u}", 0))
                    if e >= 1:
                        add_expert(e - 1)
                add_expert(MOE0 - 1)
                for s in S:
                    after(f"moe.add{MOE0 - 1}", s)
                    nc.vector.tensor_tensor(x[s][:], x[s][:], h0[s][:], ALU.add).then_inc(dve_done, DVE_1.did("moe.x", s))
                norm("x1", x, xn, "moe.x")
                for s in S:
                    dve.wait_ge(pe_done, at(PE_1, "x1.S", s))
                    nc.vector.tensor_reduce(col[s][:, 16:17], ps[s][:, 1, 0:KEYS], X_AXIS, ALU.max, negate=True).then_inc(dve_done, DVE_1.did("x1.nmax", s))
                for s in S:
                    dve.wait_ge(act_done, at(ACT_1, "x1.exp", s))
                    nc.vector.reciprocal(col[s][:, 18:19], col[s][:, 17:18]).then_inc(dve_done, DVE_1.did("x1.rden", s))
                for s in S:
                    dve.wait_ge(pe_done, at(PE_1, "x1.y", s))
                    after("x1.rden", s)
                    nc.vector.scalar_tensor_tensor(x[s][:], ps[s][:, 1, 0:DIM], col[s][:, 18:19], x[s][:], ALU.mult, ALU.add).then_inc(dve_done, DVE_1.did("x1.x", s))
                for s in S:
                    after("x1.x", s)
                    nc.vector.tensor_tensor(x[s][:], x[s][:], bv1[:], ALU.add).then_inc(dve_done, DVE_1.did("x1.bv", s))
                norm("f1", x, xn, "x1.bv")
                for s in S:
                    after("f1.norm", s)
                    nc.vector.tensor_reduce(col[s][:, 16:17], xn[s][:], X_AXIS, ALU.max, apply_absolute_value=True).then_inc(dve_done, DVE_1.did("f1.amax", s))
                for s in S:
                    after("f1.amax", s)
                    nc.vector.tensor_scalar(col[s][:, 17:18], col[s][:, 16:17], 1e-5, 1.0 / 127.0, ALU.max, ALU.mult).then_inc(dve_done, DVE_1.did("f1.inv", s))
                for s in S:
                    after("f1.inv", s)
                    nc.vector.reciprocal(col[s][:, 18:19], col[s][:, 17:18]).then_inc(dve_done, DVE_1.did("f1.scale", s))
                for s in S:
                    after("f1.scale", s)
                    nc.vector.tensor_scalar(xn[s][:], xn[s][:], col[s][:, 18:19], ROUND, ALU.mult, ALU.add).then_inc(dve_done, DVE_1.did("f1.round", s))
                for s in S:
                    after("f1.round", s)
                    nc.vector.tensor_scalar(xn[s][:], xn[s][:], ROUND, col[s][:, 17:18], ALU.subtract, ALU.mult).then_inc(dve_done, DVE_1.did("f1.xq", s))
                for s in S:
                    dve.wait_ge(act_done, at(ACT_1, "f1.mid", s))
                    for c in range(FF1 // CH):
                        a = c * TOK
                        last = nc.vector.scalar_tensor_tensor(prob[s][:, a + 1:a + TOK], ps[s][:, 0, a:a + TOK - 1], conv1_col[:, c, 0:1], prob[s][:, a + 1:a + TOK], ALU.mult, ALU.add)
                    last.then_inc(dve_done, DVE_1.did("f1.tap0", s))
                for s in S:
                    after("f1.tap0", s)
                    for c in range(FF1 // CH):
                        a = c * TOK
                        last = nc.vector.scalar_tensor_tensor(prob[s][:, a:a + TOK - 1], ps[s][:, 0, a + 1:a + TOK], conv1_col[:, c, 2:3], prob[s][:, a:a + TOK - 1], ALU.mult, ALU.add)
                    last.then_inc(dve_done, DVE_1.did("f1.taps", s))
                for s in S:
                    dve.wait_ge(act_done, at(ACT_1, "f1.tanh", s))
                    nc.vector.scalar_tensor_tensor(prob[s][:, 0:BANK], prob[s][:, BANK:2 * BANK], 1.0, prob[s][:, 0:BANK], ALU.add, ALU.mult).then_inc(dve_done, DVE_1.did("f1.silu", s))
                for s in S:
                    dve.wait_ge(pe_done, at(PE_1, "f1.uT", s))
                    nc.vector.tensor_reduce(col[s][:, 16:17], ps[s][:, 0, :], X_AXIS, ALU.max, apply_absolute_value=True).then_inc(dve_done, DVE_1.did("f1.uamax", s))
                for s in S:
                    after("f1.uamax", s)
                    nc.vector.tensor_scalar(col[s][:, 17:18], col[s][:, 16:17], 0.5, 1e-5, ALU.mult, ALU.max).then_inc(dve_done, DVE_1.did("f1.uclip", s))
                for s in S:
                    after("f1.uclip", s)
                    nc.vector.reciprocal(col[s][:, 18:19], col[s][:, 17:18]).then_inc(dve_done, DVE_1.did("f1.urec", s))
                for s in S:
                    after("f1.urec", s)
                    nc.vector.tensor_scalar(col[s][:, 19:20], col[s][:, 18:19], 127.0 / 2, None, ALU.mult)
                    nc.vector.tensor_scalar(col[s][:, 20:21], col[s][:, 17:18], prep[:, 6:7], None, ALU.mult).then_inc(dve_done, DVE_1.did("f1.uscale", s))
                for s in S:
                    after("f1.uscale", s)
                    nc.vector.tensor_scalar(prob[s][:, 0:BANK], ps[s][:, 0, :], col[s][:, 19:20], ROUND, ALU.mult, ALU.add).then_inc(dve_done, DVE_1.did("f1.uround", s))
                for s in S:
                    after("f1.uround", s)
                    nc.vector.tensor_scalar(probT[s][:, 0:256].bitcast(BF16), prob[s][:, 0:BANK], ROUND, None, ALU.subtract).then_inc(dve_done, DVE_1.did("f1.uq", s))
                for s in S:
                    dve.wait_ge(pe_done, at(PE_1, "f1.down", s))
                    nc.vector.scalar_tensor_tensor(x[s][:], ps[s][:, 0, 0:DIM], col[s][:, 20:21], x[s][:], ALU.mult, ALU.add).then_inc(dve_done, DVE_1.did("f1.x", s))
                norm("x2", x, xn, "f1.x")
                for s in S:
                    dve.wait_ge(pe_done, at(PE_1, "x2.S", s))
                    nc.vector.tensor_reduce(col[s][:, 16:17], ps[s][:, 1, 0:KEYS], X_AXIS, ALU.max, negate=True).then_inc(dve_done, DVE_1.did("x2.nmax", s))
                for s in S:
                    after("x2.nmax", s)
                    nc.vector.scalar_tensor_tensor(col[s][:, 18:19], col[s][:, 16:17], -1.0, ps[s][:, 1, 80:81], ALU.mult, ALU.add).then_inc(dve_done, DVE_1.did("x2.smax", s))
                for s in S:
                    after("x2.smax", s)
                    nc.vector.tensor_scalar(col[s][:, 19:20], col[s][:, 18:19], b_sim[:], None, ALU.add).then_inc(dve_done, DVE_1.did("x2.score", s))
                for s in S:
                    dve.wait_ge(act_done, at(ACT_1, "x2.exp", s))
                    nc.vector.reciprocal(col[s][:, 18:19], col[s][:, 17:18]).then_inc(dve_done, DVE_1.did("x2.rden", s))
                for s in S:
                    after("x2.rden", s)
                    nc.vector.tensor_scalar(prob[s][:, 0:KEYS], prob[s][:, 0:KEYS], col[s][:, 18:19], None, ALU.mult).then_inc(dve_done, DVE_1.did("x2.P", s))
                for s in S:
                    dve.wait_ge(act_done, at(ACT_1, "x2.PT", s))
                    nc.vector.tensor_reduce(col[s][0:1, 20:21], ps[s][0:1, 0, 128:128 + TOK], X_AXIS, ALU.max).then_inc(dve_done, DVE_1.did("x2.M", s))
                for s in S:
                    dve.wait_ge(pe_done, at(PE_1, "x2.M", s))
                    nc.vector.tensor_scalar(col[s][:, 21:22], ps[s][:, 0, 256:257], -1.0, None, ALU.mult).then_inc(dve_done, DVE_1.did("x2.negM", s))
                for s in S:
                    dve.wait_ge(pe_done, at(PE_1, "x2.hq", s))
                    nc.vector.reciprocal(col[s][:, 23:24], ps[s][:, 1, 2:3]).then_inc(dve_done, DVE_1.did("x2.rsum", s))
                for s in S:
                    after("x2.rsum", s)
                    nc.vector.tensor_scalar(col[s][:, 24:25], ps[s][:, 1, 0:1], col[s][:, 23:24], None, ALU.mult).then_inc(dve_done, DVE_1.did("x2.hc", s))
                for s in S:
                    dve.wait_ge(act_done, at(ACT_1, "x2.feat", s))
                    nc.vector.tensor_tensor(qT[s][:], ps[s][:, 0, 0:TOK], xnT[s][:], ALU.mult).then_inc(dve_done, DVE_1.did("x2.ehq", s))
                for s in S:
                    dve.wait_ge(pe_done, at(PE_1, "x2.out", s))
                    nc.vector.tensor_tensor(x[s][:], ps[s][:, 1, 0:DIM], x[s][:], ALU.add).then_inc(dve_done, DVE_1.did("x2.add", s))
                for s in S:
                    after("x2.add", s)
                    nc.vector.tensor_tensor(x[s][:], x[s][:], b_qv2[:], ALU.add).then_inc(dve_done, DVE_1.did("f2.x", s))
                norm("f2", x, xn, "f2.x")


def part_2(nc, d, shared):
    xnT_all, ident, ones, x_mid, x_mid2 = (shared[k] for k in ("xnT_all", "ident", "ones", "x_mid", "x_mid2"))
    NCH = FF2 // CH
    WIDE = NCH * TTILE
    QMAX = 32767.0
    BLOCK = 32
    NBLK = 3 * FF2 // BLOCK
    PAIR = (0, 1)
    X, UP, GATE, GATED, OUT = range(5)
    SB = TTILE // TOK
    with ExitStack() as ctx:
        def sb(name, shape, dt=F32):
            return ctx.enter_context(nc.sbuf_tensor(name, shape, dt))

        def sem(name):
            return ctx.enter_context(nc.semaphore(name))

        w_rows = sb("w_rows", [128, 3, FF2])
        w_s = sb("w_s", [128, NBLK])
        w_inv = sb("w_inv", [128, NBLK])
        wT = sb("wT", [128, 3, FF2])
        hid = sb("hid", [128, TILES, WIDE])
        stage = [sb(f"stage{n}", [128, WIDE]) for n in PAIR]
        other = [sb(f"other{n}", [128, WIDE]) for n in PAIR]
        xt = [sb(f"xt{n}", [128, SB, DIM]) for n in PAIR]
        tmax = sb("tmax", [128, 2, TILES])
        col2 = sb("stats2", [128, 8])
        scale = sb("scale", [128, 5])
        inv = sb("inv", [128, 5])
        up_gated = sb("up_gated", [128, 1])
        round_col = sb("round_col", [128, 1])
        acc = [ctx.enter_context(nc.psum_tensor(f"acc{n}", [128, NCH, BANK], F32)) for n in PAIR]
        aux = ctx.enter_context(nc.psum_tensor("aux", [128, BANK], F32))

        w_loaded, w_quantised, w_turned, scales_dve, scales_pe, x_quantised = (sem(n) for n in (
            "w_loaded", "w_quantised", "w_turned", "scales_dve", "scales_pe", "x_quantised"))
        pe_2, act_2, dve_2 = ([sem(f"{e}_2{l}") for l in "abcd"] for e in ("pe", "act", "dve"))
        passed = sem("passed2")
        x_loaded = [sem(f"x_loaded{n}") for n in PAIR]
        x_stored = [sem(f"x_stored{n}") for n in PAIR]
        PA, PB, PC, PD = (PE_2A, PE_2B, PE_2C, PE_2D)
        VA, VB, VC, VD = (DVE_2A, DVE_2B, DVE_2C, DVE_2D)
        AB, AC = (ACT_2B, ACT_2C)
        ROUNDS2 = TILES // 2

        block = ctx.enter_context(nc.Block())

        @block.sync
        def _(sp):
            sp.dma_start(w_rows[:, 0, :].rearrange("p (k i) -> p k i", k=NCH), d["L2_ffn_w_up"].rearrange("(k p) i -> p k i", p=CH)).then_inc(w_loaded, 16)
            sp.dma_start(w_rows[:, 1, :].rearrange("p (k i) -> p k i", k=NCH), d["L2_ffn_w_gate"].rearrange("(k p) i -> p k i", p=CH)).then_inc(w_loaded, 16)
            sp.dma_start(w_rows[:, 2, :], d["L2_ffn_w_down"]).then_inc(w_loaded, 16)
            for n in PAIR:
                sp.sem_inc(x_stored[n], 16)
            with sp.Fori(0, ROUNDS2) as r:
                for n in PAIR:
                    sp.wait_ge(x_stored[n], r * 16 + 16)
                    sp.dma_start(xt[n][:], x_mid[bass.ds((r * 2 + n) * SB, SB), :, :].rearrange("b t c -> t b c")).then_inc(x_loaded[n], 16)

        @block.gpsimd
        def _(pool):
            pool.wait_ge(w_loaded, 48)

        @block.tensor
        def _(pe):
            def spread(step, src):
                pe.wait_ge(scales_dve, 4 * step + 1)
                nc.tensor.transpose(aux[0:1, 0:128], src, ident[:]).then_inc(scales_pe, 1)
                pe.wait_ge(scales_dve, 4 * step + 2)
                nc.tensor.matmul(aux[:, 128:129], ones[0:1, :], col2[0:1, 1:2], start=True, stop=True).then_inc(scales_pe, 1)

            pe.sem_inc(pe_2[3], PD.per_round)
            pe.wait_ge(w_quantised, 7)
            for m in range(3):
                for k in range(NCH):
                    last = nc.tensor.transpose(acc[0][:, m, k * CH:(k + 1) * CH], w_rows[:, m, k * CH:(k + 1) * CH], ident[:])
            last.then_inc(w_turned, 1)
            spread(0, col2[:, 0:1])
            pe.wait_ge(x_quantised, 2)
            pe.wait_ge(w_turned, 2)

            def hidden(steps, sem_, m, name, r, n):
                for k in range(NCH):
                    last = nc.tensor.matmul(acc[n][:, k, :], wT[:, m, k * CH:(k + 1) * CH], xnT_all[:, bass.ds((r * 2 + n) * TTILE, TTILE)], start=True, stop=True)
                last.then_inc(sem_, steps.did(name, n))

            with pe.Fori(0, ROUNDS2) as r:
                for n in PAIR:
                    pe.wait_ge(dve_2[0], VA.value("gate", n, r - 1))
                    hidden(PA, pe_2[0], 0, "up", r, n)
                for n in PAIR:
                    pe.wait_ge(dve_2[0], VA.value("up", n, r))
                    hidden(PA, pe_2[0], 1, "gate", r, n)
            for step, src in ((1, 2), (2, 3)):
                spread(step, col2[:, src:src + 1])
            with pe.Fori(0, ROUNDS2) as r:
                for n in PAIR:
                    pe.wait_ge(act_2[1], AB.value("round", n, r - 1))
                    hidden(PB, pe_2[1], 1, "gate", r, n)
            spread(3, col2[:, 0:1])
            with pe.Fori(0, ROUNDS2) as r:
                for n in PAIR:
                    pe.wait_ge(act_2[2], AC.value("round", n, r - 1))
                    hidden(PC, pe_2[2], 0, "up", r, n)
            spread(4, col2[:, 0:1])
            with pe.Fori(0, ROUNDS2) as r:
                for n in PAIR:
                    pe.wait_ge(dve_2[3], VD.value("quant", n, r))
                    for b in range(SB):
                        for k in range(NCH):
                            last = nc.tensor.matmul(acc[n][:, 0, b * TOK:(b + 1) * TOK], stage[n][:, k * TTILE + b * TOK:k * TTILE + (b + 1) * TOK],
                                                    wT[:, 2, k * CH:(k + 1) * CH], start=(k == 0), stop=(k == NCH - 1))
                    last.then_inc(pe_2[3], PD.did("down", n))

        @block.scalar
        def _(act):
            act.sem_inc(act_2[1], AB.per_round)
            act.sem_inc(act_2[2], AC.per_round)
            act.wait_ge(scales_dve, 12)
            with act.Fori(0, ROUNDS2) as r:
                for n in PAIR:
                    act.wait_ge(dve_2[1], VB.value("gated", n, r - 1))
                    act.wait_ge(pe_2[1], PB.value("gate", n, r))
                    nc.scalar.activation(stage[n][:], acc[n][:].rearrange("p k t -> p (k t)"), ACT.Identity, scale=inv[:, GATE:GATE + 1], bias=round_col[:]).then_inc(act_2[1], AB.did("round", n))
                for n in PAIR:
                    act.wait_ge(dve_2[1], VB.value("gate", n, r))
                    nc.scalar.activation(other[n][:], stage[n][:], ACT.Tanh, scale=0.5).then_inc(act_2[1], AB.did("tanh", n))
            with act.Fori(0, ROUNDS2) as r:
                for n in PAIR:
                    act.wait_ge(dve_2[2], VC.value("product", n, r - 1))
                    act.wait_ge(pe_2[2], PC.value("up", n, r))
                    nc.scalar.activation(stage[n][:], acc[n][:].rearrange("p k t -> p (k t)"), ACT.Identity, scale=inv[:, UP:UP + 1], bias=round_col[:]).then_inc(act_2[2], AC.did("round", n))
            with act.Fori(0, ROUNDS2) as r:
                for n in PAIR:
                    act.wait_ge(dve_2[3], VD.value("add", n, r))
                    act.dma_start(x_mid2[bass.ds((r * 2 + n) * SB, SB), :, :].rearrange("b t c -> t b c"), xt[n][:]).then_inc(x_stored[n], 16)
            for n in PAIR:
                act.wait_ge(x_stored[n], 16 * ROUNDS2 + 16)

        @block.vector
        def _(dve):
            for steps, sem_ in ((VA, dve_2[0]), (VB, dve_2[1]), (VC, dve_2[2]), (VD, dve_2[3])):
                dve.sem_inc(sem_, steps.per_round)
            dve.wait_ge(w_loaded, 48)
            nc.vector.memset(round_col[:], ROUND).then_inc(w_quantised, 1)
            blocks = w_rows[:].rearrange("p m (b i) -> p (m b) i", i=BLOCK)
            per_block = [128, NBLK, BLOCK]
            nc.vector.tensor_reduce(w_s[:], blocks, X_AXIS, ALU.max, apply_absolute_value=True).then_inc(w_quantised, 1)
            dve.wait_ge(w_quantised, 2)
            nc.vector.tensor_scalar(w_s[:], w_s[:], 1.0 / 7.0, 1e-12, ALU.mult, ALU.max).then_inc(w_quantised, 1)
            dve.wait_ge(w_quantised, 3)
            nc.vector.reciprocal(w_inv[:], w_s[:]).then_inc(w_quantised, 1)
            dve.wait_ge(w_quantised, 4)
            nc.vector.tensor_tensor(blocks, blocks, w_inv[:].unsqueeze(2).to_broadcast(per_block), ALU.mult).then_inc(w_quantised, 1)
            dve.wait_ge(w_quantised, 5)
            nc.vector.tensor_scalar(blocks, blocks, ROUND, None, ALU.add).then_inc(w_quantised, 1)
            dve.wait_ge(w_quantised, 6)
            nc.vector.scalar_tensor_tensor(blocks, blocks, ROUND, w_s[:].unsqueeze(2).to_broadcast(per_block), ALU.subtract, ALU.mult).then_inc(w_quantised, 1)
            dve.wait_ge(w_turned, 1)
            nc.vector.tensor_copy(wT[:], acc[0][:, :, 0:FF2]).then_inc(w_turned, 1)

            def global_scale(step, which, part, out):
                nc.vector.tensor_reduce(out, part, X_AXIS, ALU.max, apply_absolute_value=True).then_inc(scales_dve, 1)
                dve.wait_ge(scales_pe, 2 * step + 1)
                nc.vector.tensor_reduce(col2[0:1, 1:2], aux[0:1, 0:128], X_AXIS, ALU.max).then_inc(scales_dve, 1)
                dve.wait_ge(scales_pe, 2 * step + 2)
                nc.vector.tensor_scalar(scale[:, which:which + 1], aux[:, 128:129], 1.0 / QMAX, 1e-12, ALU.mult, ALU.max).then_inc(scales_dve, 1)
                dve.wait_ge(scales_dve, 4 * step + 3)
                nc.vector.reciprocal(inv[:, which:which + 1], scale[:, which:which + 1]).then_inc(scales_dve, 1)
                dve.wait_ge(scales_dve, 4 * step + 4)

            global_scale(0, X, xnT_all[:], col2[:, 0:1])
            nc.vector.tensor_scalar(xnT_all[:], xnT_all[:], inv[:, X:X + 1], ROUND, ALU.mult, ALU.add).then_inc(x_quantised, 1)
            dve.wait_ge(x_quantised, 1)
            nc.vector.tensor_scalar(xnT_all[:], xnT_all[:], ROUND, scale[:, X:X + 1], ALU.subtract, ALU.mult).then_inc(x_quantised, 1)
            with dve.Fori(0, ROUNDS2) as r:
                for m, name in enumerate(("up", "gate")):
                    for n in PAIR:
                        dve.wait_ge(pe_2[0], PA.value(name, n, r))
                        dve.sem_inc(passed, 1)
                        nc.vector.tensor_reduce(tmax[:, m, bass.ds(r * 2 + n, 1)], acc[n][:].rearrange("p k t -> p (k t)"), X_AXIS, ALU.max, apply_absolute_value=True).then_inc(dve_2[0], VA.did(name, n))
            dve.wait_ge(dve_2[0], VA.value("gate", 1, ROUNDS2 - 1))
            global_scale(1, UP, tmax[:, 0, :], col2[:, 2:3])
            global_scale(2, GATE, tmax[:, 1, :], col2[:, 3:4])
            with dve.Fori(0, ROUNDS2) as r:
                def after(name, n):
                    dve.wait_ge(dve_2[1], VB.value(name, n, r))
                for n in PAIR:
                    dve.wait_ge(act_2[1], AB.value("round", n, r))
                    nc.vector.tensor_scalar(stage[n][:], stage[n][:], ROUND, scale[:, GATE:GATE + 1], ALU.subtract, ALU.mult).then_inc(dve_2[1], VB.did("gate", n))
                for n in PAIR:
                    dve.wait_ge(act_2[1], AB.value("tanh", n, r))
                    nc.vector.tensor_scalar(other[n][:], other[n][:], 32768.0, ROUND + 32768.0, ALU.mult, ALU.add).then_inc(dve_2[1], VB.did("sigmoid", n))
                for n in PAIR:
                    after("sigmoid", n)
                    nc.vector.tensor_scalar(other[n][:], other[n][:], ROUND, 65535.0, ALU.subtract, ALU.min).then_inc(dve_2[1], VB.did("clip", n))
                for n in PAIR:
                    after("clip", n)
                    nc.vector.scalar_tensor_tensor(hid[:, bass.ds(r * 2 + n, 1), :].rearrange("p o w -> p (o w)"), other[n][:], 1.0 / 65536.0, stage[n][:], ALU.mult, ALU.mult).then_inc(dve_2[1], VB.did("gated", n))
                for n in PAIR:
                    after("gated", n)
                    dve.sem_inc(passed, 1)
                    nc.vector.tensor_reduce(tmax[:, 0, bass.ds(r * 2 + n, 1)], hid[:, bass.ds(r * 2 + n, 1), :].rearrange("p o w -> p (o w)"), X_AXIS, ALU.max, apply_absolute_value=True).then_inc(dve_2[1], VB.did("max", n))
            dve.wait_ge(dve_2[1], VB.value("max", 1, ROUNDS2 - 1))
            global_scale(3, GATED, tmax[:, 0, :], col2[:, 0:1])
            nc.vector.tensor_tensor(up_gated[:], scale[:, UP:UP + 1], scale[:, GATED:GATED + 1], ALU.mult).then_inc(x_quantised, 1)
            dve.wait_ge(x_quantised, 3)
            with dve.Fori(0, ROUNDS2) as r:
                def after(name, n):
                    dve.wait_ge(dve_2[2], VC.value(name, n, r))
                for n in PAIR:
                    nc.vector.tensor_scalar(other[n][:], hid[:, bass.ds(r * 2 + n, 1), :].rearrange("p o w -> p (o w)"), inv[:, GATED:GATED + 1], ROUND, ALU.mult, ALU.add).then_inc(dve_2[2], VC.did("round", n))
                for n in PAIR:
                    dve.wait_ge(act_2[2], AC.value("round", n, r))
                    nc.vector.tensor_scalar(stage[n][:], stage[n][:], ROUND, up_gated[:], ALU.subtract, ALU.mult).then_inc(dve_2[2], VC.did("up", n))
                for n in PAIR:
                    after("up", n)
                    nc.vector.scalar_tensor_tensor(hid[:, bass.ds(r * 2 + n, 1), :].rearrange("p o w -> p (o w)"), other[n][:], ROUND, stage[n][:], ALU.subtract, ALU.mult).then_inc(dve_2[2], VC.did("product", n))
                for n in PAIR:
                    after("product", n)
                    dve.sem_inc(passed, 1)
                    nc.vector.tensor_reduce(tmax[:, 1, bass.ds(r * 2 + n, 1)], hid[:, bass.ds(r * 2 + n, 1), :].rearrange("p o w -> p (o w)"), X_AXIS, ALU.max, apply_absolute_value=True).then_inc(dve_2[2], VC.did("max", n))
            dve.wait_ge(dve_2[2], VC.value("max", 1, ROUNDS2 - 1))
            global_scale(4, OUT, tmax[:, 1, :], col2[:, 0:1])
            with dve.Fori(0, ROUNDS2) as r:
                for n in PAIR:
                    dve.wait_ge(pe_2[3], PD.value("down", n, r - 1))
                    nc.vector.tensor_scalar(stage[n][:], hid[:, bass.ds(r * 2 + n, 1), :].rearrange("p o w -> p (o w)"), inv[:, OUT:OUT + 1], ROUND, ALU.mult, ALU.add).then_inc(dve_2[3], VD.did("round", n))
                for n in PAIR:
                    dve.wait_ge(dve_2[3], VD.value("round", n, r))
                    nc.vector.tensor_scalar(stage[n][:], stage[n][:], ROUND, scale[:, OUT:OUT + 1], ALU.subtract, ALU.mult).then_inc(dve_2[3], VD.did("quant", n))
                for n in PAIR:
                    dve.wait_ge(pe_2[3], PD.value("down", n, r))
                    dve.wait_ge(x_loaded[n], r * 16 + 16)
                    nc.vector.tensor_tensor(xt[n][:].rearrange("p b c -> p (b c)"), acc[n][:, 0, :], xt[n][:].rearrange("p b c -> p (b c)"), ALU.add).then_inc(dve_2[3], VD.did("add", n))


def part_3(nc, d, shared):
    ident, ones, first, minus_half, x_mid2 = (shared[k] for k in ("ident", "ones", "first", "minus_half", "x_mid2"))
    S = range(STREAMS)
    CHUNKS = 4
    LAST = KEYS - CHUNKS * KT
    KPAD = (CHUNKS + 1) * KT
    ROWS = 32
    with ExitStack() as ctx:
        def sb(name, shape, dt=F32):
            return ctx.enter_context(nc.sbuf_tensor(name, shape, dt))

        def per_stream(name, shape, dt=F32):
            return [sb(f"{name}{s}", shape, dt) for s in S]

        def sem(name):
            return ctx.enter_context(nc.semaphore(name))

        before = sb("before", [128, 128])
        mask3_i = sb("mask3_i", [128, BATCH * KEYS], I32)
        mask3 = sb("mask3", [128, BATCH * KEYS + KPAD - KEYS])
        w_txt = sb("w_txt", [128, DIM])
        w_feat = sb("w_feat", [128, DIM])
        w_row = sb("w_row", [128, 2 * ROWS - 1])
        b_e = sb("b_e", [128, 1])
        w_gate = sb("w_gate", [128, 2])
        b_gate = sb("b_gate", [128, 2])
        w_route = sb("w_route", [128, MOE3])
        w_exp = sb("w_exp", [128, MOE3, DIM])
        b_exp = sb("b_exp", [1, MOE3 * DIM])

        x_in = per_stream("x_in3", [128, DIM])
        ctx_in = per_stream("ctx_in3", [KEYS, DIM])
        ctxT_in = per_stream("ctxT_in3", [128, KEYS])
        x = per_stream("x3", [128, DIM])
        cx = per_stream("cx3", [KEYS, DIM])
        cxT = per_stream("cxT3", [128, KEYS])
        xn = per_stream("xn3", [128, DIM])
        xnT = per_stream("xnT3", [128, TOK])
        txt = per_stream("txt3", [128, KEYS])
        feat = per_stream("feat3", [128, TOK])
        th = per_stream("th3", [128, KT, TOK])
        th_last = per_stream("th_last3", [128, KT, TOK])
        prob = per_stream("prob3", [128, KPAD])
        probT = per_stream("probT3", [KEYS, TOK])
        hT = per_stream("hT3", [128, TOK])
        col = per_stream("col3", [128, 72])
        taken = per_stream("taken3", [128, MOE3])
        carry = sb("carry3", [128, MOE3])
        ps = [ctx.enter_context(nc.psum_tensor(f"ps3{s}", [128, 2, BANK], F32)) for s in S]

        weights_in, ready3, mask_set, zeros_set, carried = (sem(n) for n in ("weights_in3", "ready3", "mask_set", "zeros_set", "carried"))
        loads_in = [sem(f"loads_in3{s}") for s in S]
        stores_out = [sem(f"stores_out3{s}") for s in S]
        inputs_ready = sem("inputs_ready3")
        passed = sem("passed3")
        pe_done, act_done, dve_done, pool_done = (sem(n) for n in ("pe_done3", "act_done3", "dve_done3", "pool_done3"))

        weight_loads = [
            (before[:], d["before"]), (mask3_i[:], d["mask_BxS2_ik0"].to_broadcast([128, BATCH * KEYS])),
            (w_txt[:], d["L3_xattn_Ws"]), (w_feat[:], d["L3_xattn_W"]), (w_row[:, ROWS - 1:ROWS], d["L3_xattn_w"]), (b_e[:], d["L3_xattn_b"]),
            (w_gate[:, 0:1], d["L3_xattn_Wcw"]), (w_gate[:, 1:2], d["L3_xattn_Wcb"]),
            (b_gate[:, 0:1], d["L3_xattn_bcw"].to_broadcast([128, 1])), (b_gate[:, 1:2], d["L3_xattn_bcb"].to_broadcast([128, 1])),
            (w_route[:], d["L3_ffn_wg"]), (w_exp[:], d["L3_ffn_W"].rearrange("e h f -> h e f")), (b_exp[:], d["L3_ffn_b"]),
        ]
        block = ctx.enter_context(nc.Block())

        @block.sync
        def _(sp):
            def load(s, b):
                sp.dma_start(x_in[s][:], x_mid2[bass.ds(b, 1), :, :].rearrange("o t c -> t (o c)")).then_inc(loads_in[s], 16)
                sp.dma_start(ctx_in[s][:], d["ctx"][bass.ds(b, 1), :, :].rearrange("o t c -> t (o c)")).then_inc(loads_in[s], 16)
                sp.dma_start(ctxT_in[s][:], d["ctxT"][bass.ds(b, 1), :, :].rearrange("o t c -> t (o c)")).then_inc(loads_in[s], 16)

            for s in S:
                load(s, s)
            sp.wait_ge(ready3, 1)
            for dst, src in weight_loads:
                sp.dma_start(dst, src).then_inc(weights_in, 16)
            with sp.Fori(0, ROUNDS - 1) as r:
                for s in S:
                    sp.wait_ge(inputs_ready, r * STREAMS + s + 1)
                    load(s, r * STREAMS + (STREAMS + s))

        @block.gpsimd
        def _(pool):
            def take_inputs(s, value):
                pool.wait_ge(loads_in[s], value)
                pool.sem_inc(passed, 1)
                nc.gpsimd.tensor_copy(x[s][:], x_in[s][:])
                nc.gpsimd.tensor_copy(cx[s][:], ctx_in[s][:])
                nc.gpsimd.tensor_copy(cxT[s][:], ctxT_in[s][:]).then_inc(inputs_ready, 1)

            def steps(r):
                for p in ("x3", "f3"):
                    for s in S:
                        pool.wait_ge(dve_done, DVE_3.value(f"{p}.eps", s, r))
                        nc.gpsimd.tensor_tensor(col[s][:, 9:10], col[s][:, 8:9], minus_half[:], ALU.pow).then_inc(pool_done, POOL_3.did(f"{p}.rstd", s))

            nc.gpsimd.memset(w_row[:], 0.0).then_inc(ready3, 1)
            nc.gpsimd.memset(mask3[:, BATCH * KEYS:], 0.0)
            for s in S:
                last = nc.gpsimd.memset(th_last[s][:], 0.0)
            last.then_inc(zeros_set, 1)
            for s in S:
                take_inputs(s, 48)
            with pool.Fori(0, ROUNDS - 1) as r:
                steps(r)
                for s in S:
                    pool.wait_ge(stores_out[s], r * 16 + 16)
                    take_inputs(s, r * 48 + 96)
            steps(ROUNDS - 1)

        @block.scalar
        def _(act):
            act.wait_ge(weights_in, 16 * len(weight_loads))
            act.wait_ge(zeros_set, 1)
            with act.Fori(0, ROUNDS) as r:
                def at(steps_, name, s):
                    return steps_.value(name, s, r)

                def xT(p):
                    for s in S:
                        act.wait_ge(pe_done, at(PE_3, f"{p}.T", s))
                        nc.scalar.copy(xnT[s][:], ps[s][:, 0, 0:TOK]).then_inc(act_done, ACT_3.did(f"{p}.xT", s))

                xT("x3")
                for s in S:
                    act.wait_ge(pe_done, at(PE_3, "x3.proj", s))
                    nc.scalar.copy(txt[s][:], ps[s][:, 0, 0:KEYS])
                    nc.scalar.activation(feat[s][:], ps[s][:, 0, 128:128 + TOK], ACT.Identity, bias=b_e[:]).then_inc(act_done, ACT_3.did("x3.proj", s))
                for c in range(CHUNKS):
                    for s in S:
                        act.wait_ge(dve_done, at(DVE_3, f"x3.sum{c}", s))
                        nc.scalar.activation(th[s][:], th[s][:], ACT.Tanh).then_inc(act_done, ACT_3.did(f"x3.tanh{c}", s))
                    if c == 0:
                        for s in S:
                            act.wait_ge(act_done, at(ACT_3, "x3.proj", s))
                            for k in range(LAST):
                                last = nc.scalar.activation(th_last[s][:, k, :], feat[s][:], ACT.Tanh, bias=txt[s][:, CHUNKS * KT + k:CHUNKS * KT + k + 1])
                            last.then_inc(act_done, ACT_3.did("x3.tanh_last", s))
                for s in S:
                    act.wait_ge(pe_done, at(PE_3, f"x3.rho{CHUNKS - 1}", s))
                    nc.scalar.copy(th[s][:, 0:4, :].rearrange("p k f -> p (k f)"), ps[s][:, 1, :]).then_inc(act_done, ACT_3.did("x3.rho", s))
                for s in S:
                    act.wait_ge(dve_done, at(DVE_3, "x3.nmax", s))
                    nc.scalar.activation(prob[s][:, 0:KEYS], prob[s][:, 0:KEYS], ACT.Exp, bias=col[s][:, 16:17], accum_out=col[s][:, 17:18]).then_inc(act_done, ACT_3.did("x3.exp", s))
                for s in S:
                    act.wait_ge(pe_done, at(PE_3, "x3.PT", s))
                    nc.scalar.copy(probT[s][:], ps[s][0:KEYS, 0, 0:TOK]).then_inc(act_done, ACT_3.did("x3.PT", s))
                for s in S:
                    act.wait_ge(pe_done, at(PE_3, "x3.h", s))
                    nc.scalar.copy(hT[s][:], ps[s][:, 0, 0:TOK]).then_inc(act_done, ACT_3.did("x3.h", s))
                for s in S:
                    act.wait_ge(dve_done, at(DVE_3, "x3.gb", s))
                    nc.scalar.activation(col[s][:, 20:22], col[s][:, 18:20], ACT.Tanh).then_inc(act_done, ACT_3.did("x3.gate", s))
                xT("f3")
                for s in S:
                    act.wait_ge(dve_done, at(DVE_3, "f3.nmax", s))
                    nc.scalar.activation(col[s][:, 24:32], ps[s][:, 1, 0:MOE3], ACT.Exp, bias=col[s][:, 16:17], accum_out=col[s][:, 17:18]).then_inc(act_done, ACT_3.did("f3.exp", s))
                for s in S:
                    act.wait_ge(dve_done, at(DVE_3, f"f3.add{MOE3 - 1}", s))
                    act.dma_start(d["out"][bass.ds(r * STREAMS + s, 1), :, :].rearrange("o t c -> t (o c)"), x[s][:]).then_inc(stores_out[s], 16)
            for s in S:
                act.wait_ge(stores_out[s], 16 * ROUNDS)

        @block.tensor
        def _(pe):
            pe.wait_ge(weights_in, 16 * len(weight_loads))
            with pe.Fori(0, ROUNDS) as r:
                def at(steps_, name, s):
                    return steps_.value(name, s, r)

                def transpose_xn(p):
                    for s in S:
                        pe.wait_ge(dve_done, at(DVE_3, f"{p}.norm", s))
                        nc.tensor.transpose(ps[s][:, 0, 0:TOK], xn[s][:], ident[:]).then_inc(pe_done, PE_3.did(f"{p}.T", s))

                transpose_xn("x3")
                for s in S:
                    pe.wait_ge(act_done, at(ACT_3, "x3.xT", s))
                    nc.tensor.matmul(ps[s][:, 0, 0:KEYS], w_txt[:], cxT[s][:], start=True, stop=True)
                    nc.tensor.matmul(ps[s][:, 0, 128:128 + TOK], w_feat[:], xnT[s][:], start=True, stop=True).then_inc(pe_done, PE_3.did("x3.proj", s))
                def rho(a, tanh, s, start, stop):
                    for b in range(4):
                        last = nc.tensor.matmul(ps[s][ROWS * b:ROWS * (b + 1), 1, :], w_row[:, ROWS - 1 - a:2 * ROWS - 1 - a],
                                                tanh[:, 4 * b:4 * b + 4, :], start=start, stop=stop, tile_position=(0, ROWS * b))
                    return last

                for c in range(CHUNKS):
                    for s in S:
                        pe.wait_ge(act_done, at(ACT_3, f"x3.tanh{c}", s))
                        rho(c, th[s], s, c == 0, c == CHUNKS - 1).then_inc(pe_done, PE_3.did(f"x3.rho{c}", s))
                    if c == 0:
                        for s in S:
                            pe.wait_ge(act_done, at(ACT_3, "x3.tanh_last", s))
                            rho(CHUNKS, th_last[s], s, False, False).then_inc(pe_done, PE_3.did("x3.rho_last", s))
                for s in S:
                    pe.wait_ge(act_done, at(ACT_3, "x3.rho", s))
                    for k in range(4):
                        last = nc.tensor.transpose(ps[s][:, 0, k * TOK:(k + 1) * TOK], th[s][:, k, :], ident[:])
                    last.then_inc(pe_done, PE_3.did("x3.rhoT", s))
                for s in S:
                    pe.wait_ge(dve_done, at(DVE_3, "x3.P", s))
                    nc.tensor.transpose(ps[s][0:KEYS, 0, 0:TOK], prob[s][:, 0:KEYS], ident[:]).then_inc(pe_done, PE_3.did("x3.PT", s))
                for s in S:
                    pe.wait_ge(act_done, at(ACT_3, "x3.PT", s))
                    nc.tensor.matmul(ps[s][:, 0, 0:TOK], cx[s][:], probT[s][:], start=True, stop=True).then_inc(pe_done, PE_3.did("x3.h", s))
                for s in S:
                    pe.wait_ge(act_done, at(ACT_3, "x3.h", s))
                    nc.tensor.matmul(ps[s][:, 1, 0:2], hT[s][:], w_gate[:], start=True, stop=True).then_inc(pe_done, PE_3.did("x3.gate", s))
                transpose_xn("f3")
                for s in S:
                    pe.wait_ge(act_done, at(ACT_3, "f3.xT", s))
                    nc.tensor.matmul(ps[s][:, 1, 0:MOE3], xnT[s][:], w_route[:], start=True, stop=True).then_inc(pe_done, PE_3.did("f3.route", s))
                for s in S:
                    pe.wait_ge(dve_done, at(DVE_3, "f3.taken", s))
                    nc.tensor.matmul(ps[s][:, 1, 16:16 + MOE3], before[:], col[s][:, 40:48], start=True, stop=False)
                    nc.tensor.matmul(ps[s][:, 1, 16:16 + MOE3], ones[:], taken[s][:], start=False, stop=True).then_inc(pe_done, PE_3.did("f3.place", s))
                for s in S:
                    pe.wait_ge(dve_done, at(DVE_3, "f3.w", s))
                    for b in range(2):
                        nc.tensor.matmul(ps[s][:, b, :], xnT[s][:], w_exp[:, b * GROUP:(b + 1) * GROUP, :], start=True, stop=False)
                        last = nc.tensor.matmul(ps[s][:, b, :], ones[0:1, :], b_exp[:, b * BANK:(b + 1) * BANK], start=False, stop=True)
                    last.then_inc(pe_done, PE_3.did("f3.y", s))

        @block.vector
        def _(dve):
            dve.wait_ge(weights_in, 16 * len(weight_loads))
            nc.vector.tensor_scalar(mask3[:, 0:BATCH * KEYS], mask3_i[:], 1e30, -1e30, ALU.mult, ALU.add).then_inc(mask_set, 1)
            nc.vector.memset(carry[:], 0.0).then_inc(carried, 1)
            dve.wait_ge(mask_set, 1)
            dve.wait_ge(zeros_set, 1)
            with dve.Fori(0, ROUNDS) as r:
                def at(steps_, name, s):
                    return steps_.value(name, s, r)

                def after(name, s):
                    dve.wait_ge(dve_done, at(DVE_3, name, s))

                def norm(p, prev):
                    for s in S:
                        if prev is None:
                            dve.wait_ge(inputs_ready, r * STREAMS + s + 1)
                        else:
                            after(prev, s)
                        nc.vector.bn_stats(col[s][:, 0:6], x[s][:]).then_inc(dve_done, DVE_3.did(f"{p}.stats", s))
                    for s in S:
                        after(f"{p}.stats", s)
                        dve.sem_inc(passed, 1)
                        nc.vector.bn_aggr(col[s][:, 6:8], col[s][:, 0:6]).then_inc(dve_done, DVE_3.did(f"{p}.aggr", s))
                    for s in S:
                        after(f"{p}.aggr", s)
                        nc.vector.tensor_scalar(col[s][:, 8:9], col[s][:, 7:8], LN_EPS, None, ALU.add).then_inc(dve_done, DVE_3.did(f"{p}.eps", s))
                    for s in S:
                        dve.wait_ge(pool_done, at(POOL_3, f"{p}.rstd", s))
                        nc.vector.tensor_scalar(xn[s][:], x[s][:], col[s][:, 6:7], col[s][:, 9:10], ALU.subtract, ALU.mult).then_inc(dve_done, DVE_3.did(f"{p}.norm", s))

                norm("x3", None)
                for c in range(CHUNKS):
                    for s in S:
                        if c == 0:
                            dve.wait_ge(act_done, at(ACT_3, "x3.proj", s))
                        else:
                            dve.wait_ge(pe_done, at(PE_3, f"x3.rho{c - 1}", s))
                        nc.vector.tensor_tensor(th[s][:], txt[s][:, c * KT:(c + 1) * KT].unsqueeze(2).to_broadcast([128, KT, TOK]),
                                                feat[s][:].unsqueeze(1).to_broadcast([128, KT, TOK]), ALU.add).then_inc(dve_done, DVE_3.did(f"x3.sum{c}", s))
                for s in S:
                    dve.wait_ge(pe_done, at(PE_3, "x3.rhoT", s))
                    nc.vector.tensor_tensor(prob[s][:].rearrange("p (a b k) -> p a b k", b=4, k=4),
                                            ps[s][:, 0, :].rearrange("p (k b a) -> p a b k", k=4, b=4)[:, 0:CHUNKS + 1, :, :],
                                            mask3[:, bass.ds((r * STREAMS + s) * KEYS, KPAD)].rearrange("p (a b k) -> p a b k", b=4, k=4), ALU.add).then_inc(dve_done, DVE_3.did("x3.mask", s))
                for s in S:
                    after("x3.mask", s)
                    nc.vector.tensor_reduce(col[s][:, 16:17], prob[s][:, 0:KEYS], X_AXIS, ALU.max, negate=True).then_inc(dve_done, DVE_3.did("x3.nmax", s))
                for s in S:
                    dve.wait_ge(act_done, at(ACT_3, "x3.exp", s))
                    nc.vector.reciprocal(col[s][:, 18:19], col[s][:, 17:18]).then_inc(dve_done, DVE_3.did("x3.rden", s))
                for s in S:
                    after("x3.rden", s)
                    nc.vector.tensor_scalar(prob[s][:, 0:KEYS], prob[s][:, 0:KEYS], col[s][:, 18:19], None, ALU.mult).then_inc(dve_done, DVE_3.did("x3.P", s))
                for s in S:
                    dve.wait_ge(pe_done, at(PE_3, "x3.gate", s))
                    nc.vector.tensor_tensor(col[s][:, 18:20], ps[s][:, 1, 0:2], b_gate[:], ALU.add).then_inc(dve_done, DVE_3.did("x3.gb", s))
                for s in S:
                    dve.wait_ge(act_done, at(ACT_3, "x3.gate", s))
                    nc.vector.tensor_scalar(xn[s][:], xn[s][:], col[s][:, 20:21], col[s][:, 21:22], ALU.mult, ALU.add).then_inc(dve_done, DVE_3.did("x3.y", s))
                for s in S:
                    after("x3.y", s)
                    nc.vector.tensor_tensor(x[s][:], x[s][:], xn[s][:], ALU.add).then_inc(dve_done, DVE_3.did("x3.x", s))
                norm("f3", "x3.x")
                for s in S:
                    dve.wait_ge(pe_done, at(PE_3, "f3.route", s))
                    nc.vector.tensor_reduce(col[s][:, 16:17], ps[s][:, 1, 0:MOE3], X_AXIS, ALU.max, negate=True).then_inc(dve_done, DVE_3.did("f3.nmax", s))
                for s in S:
                    dve.wait_ge(act_done, at(ACT_3, "f3.exp", s))
                    nc.vector.reciprocal(col[s][:, 18:19], col[s][:, 17:18]).then_inc(dve_done, DVE_3.did("f3.rden", s))
                for s in S:
                    after("f3.rden", s)
                    nc.vector.tensor_scalar(col[s][:, 24:32], col[s][:, 24:32], col[s][:, 18:19], None, ALU.mult).then_inc(dve_done, DVE_3.did("f3.probs", s))
                for s in S:
                    after("f3.probs", s)
                    nc.vector.tensor_reduce(col[s][:, 19:20], col[s][:, 24:32], X_AXIS, ALU.max).then_inc(dve_done, DVE_3.did("f3.pmax", s))
                for s in S:
                    after("f3.pmax", s)
                    nc.vector.scalar_tensor_tensor(col[s][:, 32:40], col[s][:, 24:32], col[s][:, 19:20], first[:], ALU.is_equal, ALU.mult).then_inc(dve_done, DVE_3.did("f3.eq", s))
                for s in S:
                    after("f3.eq", s)
                    nc.vector.tensor_reduce(col[s][:, 20:21], col[s][:, 32:40], X_AXIS, ALU.max).then_inc(dve_done, DVE_3.did("f3.first", s))
                for s in S:
                    after("f3.first", s)
                    nc.vector.tensor_scalar(col[s][:, 40:48], col[s][:, 32:40], col[s][:, 20:21], None, ALU.is_equal).then_inc(dve_done, DVE_3.did("f3.pick", s))
                for s in S:
                    if s == 0:
                        dve.wait_ge(carried, r + 1)
                        dve.sem_inc(passed, 1)
                        nc.vector.tensor_copy(taken[0][:], carry[:]).then_inc(dve_done, DVE_3.did("f3.taken", s))
                    else:
                        after("f3.pick", s - 1)
                        after("f3.taken", s - 1)
                        nc.vector.tensor_tensor(taken[s][:], taken[s - 1][:], col[s - 1][:, 40:48], ALU.add).then_inc(dve_done, DVE_3.did("f3.taken", s))
                for s in S:
                    dve.wait_ge(pe_done, at(PE_3, "f3.place", s))
                    nc.vector.scalar_tensor_tensor(col[s][:, 56:64], ps[s][:, 1, 16:16 + MOE3], float(CAPACITY), col[s][:, 40:48], ALU.is_lt, ALU.mult).then_inc(dve_done, DVE_3.did("f3.keep", s))
                for s in S:
                    after("f3.keep", s)
                    nc.vector.tensor_scalar(col[s][:, 64:72], col[s][:, 56:64], col[s][:, 19:20], None, ALU.mult).then_inc(dve_done, DVE_3.did("f3.w", s))
                nc.vector.tensor_tensor(carry[:], taken[-1][:], col[-1][:, 40:48], ALU.add).then_inc(carried, 1)
                for e in range(MOE3):
                    for s in S:
                        if e == 0:
                            dve.wait_ge(pe_done, at(PE_3, "f3.y", s))
                        else:
                            after(f"f3.add{e - 1}", s)
                        nc.vector.scalar_tensor_tensor(x[s][:], ps[s][:, e // GROUP, (e % GROUP) * DIM:(e % GROUP + 1) * DIM], col[s][:, 64 + e:65 + e], x[s][:], ALU.mult, ALU.add).then_inc(dve_done, DVE_3.did(f"f3.add{e}", s))


def kernel(**inputs):
    import concourse.bacc as bacc
    from concourse.bass_utils import run_bass_kernel_spmd

    a = {k: np.asarray(v) for k, v in inputs.items()}
    col = lambda v: v.reshape(-1, 1)
    row = lambda v: v.reshape(1, -1)
    attn = a["L0_ffn_attn_w"]
    q, k, v = attn[:, 0:DIM], attn[:, DIM:2 * DIM], attn[:, 2 * DIM:]
    host = {
        "x": a["x"], "ctx": a["ctx_1024"], "ctxT": a["ctx_1024"].transpose(0, 2, 1),
        "mask_Bx1x1xS2_bk0": row(np.ascontiguousarray(a["mask_Bx1x1xS2_bk0"]).reshape(-1).view(np.int32)),
        "mask_BxS2_ik0": row(a["mask_BxS2_ik0"]),
        "L0_xattn_Wq": a["L0_xattn_Wq"].T, "L0_xattn_Wk": a["L0_xattn_Wk"].T, "L0_xattn_Wv": a["L0_xattn_Wv"].T,
        "L0_xattn_Wo": a["L0_xattn_Wo"].T, "L0_xattn_rel_emb": a["L0_xattn_rel_emb"],
        "L0_ffn_ln1_w": col(a["L0_ffn_ln1_w"]), "L0_ffn_ln1_b": col(a["L0_ffn_ln1_b"]),
        "L0_ffn_ln2_w": col(a["L0_ffn_ln2_w"]), "L0_ffn_ln2_b": col(a["L0_ffn_ln2_b"]),
        "L0_ffn_conv_w": a["L0_ffn_conv_w"].reshape(DIM, 3),
        "attn_w5": np.stack([q, k, swap_halves(q), swap_halves(k), v], axis=1),
        "L0_ffn_proj_w": a["L0_ffn_proj_w"], "L0_ffn_router_w": a["L0_ffn_router_w"],
        "L0_ffn_expert_wv": a["L0_ffn_expert_wv"], "L0_ffn_expert_proj": a["L0_ffn_expert_proj"],
        "L1_xattn_Wq": a["L1_xattn_Wq"].T, "L1_xattn_Wk": a["L1_xattn_Wk"].T, "L1_xattn_Wv": a["L1_xattn_Wv"].T,
        "L1_xattn_bq": col(a["L1_xattn_bq"]), "L1_xattn_bk": col(a["L1_xattn_bk"]), "L1_xattn_bv": row(a["L1_xattn_bv"]),
        "L1_ffn_w1": a["L1_ffn_w1"].T, "L1_ffn_w2": a["L1_ffn_w2"].T,
        "L1_ffn_conv": np.concatenate([a["L1_ffn_conv_w"].reshape(-1, CH, 3), a["L1_ffn_conv_b"].reshape(-1, CH, 1)], axis=2).transpose(1, 0, 2),
        "L2_xattn_w_sim": a["L2_xattn_w_sim"].reshape(3, DIM).T, "L2_xattn_b_sim": row(a["L2_xattn_b_sim"]),
        "L2_xattn_W_qv": a["L2_xattn_W_qv"], "L2_xattn_b_qv": row(a["L2_xattn_b_qv"]),
        "L2_ffn_w_up": a["L2_ffn_w_up"], "L2_ffn_w_gate": a["L2_ffn_w_gate"], "L2_ffn_w_down": a["L2_ffn_w_down"],
        "L3_xattn_Ws": a["L3_xattn_Ws"], "L3_xattn_W": a["L3_xattn_W"], "L3_xattn_w": a["L3_xattn_w"],
        "L3_xattn_b": col(a["L3_xattn_b"]), "L3_xattn_Wcw": col(a["L3_xattn_Wcw"]), "L3_xattn_Wcb": col(a["L3_xattn_Wcb"]),
        "L3_xattn_bcw": row(a["L3_xattn_bcw"]), "L3_xattn_bcb": row(a["L3_xattn_bcb"]),
        "L3_ffn_wg": a["L3_ffn_wg"], "L3_ffn_W": a["L3_ffn_W"].transpose(0, 2, 1), "L3_ffn_b": row(a["L3_ffn_b"]),
        **shape_constants(),
    }
    nc = bacc.Bacc("TRN2", target_bir_lowering=False, num_devices=1)
    arrays, dram = {}, {}
    for name, value in host.items():
        value = np.ascontiguousarray(value)
        arrays[f"in_{name}"] = value
        dram[name] = nc.dram_tensor(f"in_{name}", value.shape, mybir.dt.from_np(value.dtype), kind="ExternalInput").ap()
    dram["out"] = nc.dram_tensor("out_x", (BATCH, TOK, DIM), F32, kind="ExternalOutput").ap()
    build(nc, dram)
    return run_bass_kernel_spmd(nc, [arrays], core_ids=[0]).results[0]["out_x"]
```

```python
from contextlib import ExitStack
from itertools import chain

import numpy as np

import concourse.bass as bass
from concourse import mybir

ALU = mybir.AluOpType
ACT = mybir.ActivationFunctionType
F32 = mybir.dt.float32
BF16 = mybir.dt.bfloat16
I32 = mybir.dt.int32
U8 = mybir.dt.uint8
X_AXIS = mybir.AxisListType.X

BATCH, TOK, DIM = 64, 128, 128
KEYS = 77
HEADS, HDIM = 16, 8
VPAD = 32
GROUP = 4
HALF = HEADS // 2
BUCKETS, MAX_DISTANCE = 32, 128
MOE0, FF0 = 4, 512
CHUNKS0 = FF0 // 128
FF1 = 512
FF2 = 384
MOE3 = 8
CAPACITY = BATCH * TOK // MOE3
CH = 128
STREAMS = 4
PAIR = 2
ROUNDS = BATCH // STREAMS
BANK = 512
LN_EPS = 1e-5
ROUND = float(1.5 * 2 ** 23)
TTILE = 512
TILES = BATCH * TOK // TTILE
KT = 16


class Steps:

    def __init__(self, text, streams=STREAMS, primed=False):
        self.order = []
        for word in text.split():
            name, _, some = word.partition(":")
            self.order += [(name, int(s)) for s in some] if some else [(name, s) for s in range(streams)]
        self.index = {step: n for n, step in enumerate(self.order)}
        assert len(self.index) == len(self.order)
        self.per_round = len(self.order)
        self.ahead = self.per_round if primed else 0
        self.next = 0

    def did(self, name, s):
        assert self.order[self.next % self.per_round] == (name, s), (name, s, self.next)
        self.next += 1
        return 1

    def value(self, name, s, rnd):
        return rnd * self.per_round + (self.index[(name, s)] + 1 + self.ahead)

    def value_before(self, name, s, rnd):
        return rnd * self.per_round + (self.index[(name, s)] + 1)


def take_turns(steps, chains):
    for _, s in steps.order:
        next(chains[s])


PE_0 = Steps("""
    x0.T:1 x0.qkv:1 x0.S0:1 x0.T:0 x0.qkv:0 x0.PT0:1 x0.S0:0 x0.PV0:1 x0.S1:1 x0.PT0:0 x0.PV0:0 x0.PT1:1 x0.S1:0
    x0.PV1:1 x0.ygT:1 x0.yT:1 x0.PT1:0 x0.o:1 x0.PV1:0 x0.ygT:0 f0b.T:1 x0.yT:0 x0.o:0 f0.qkv:1 f0b.T:0 f0.S0:1
    f0.qkv:0 f0.PT0:1 f0.S0:0 f0.PV0:1 f0.S1:1 f0.PT0:0 f0.PV0:0 f0.PT1:1 f0.S1:0 f0.PV1:1 f0.ygT:1 f0.yT:1 f0.PT1:0
    f0.o:1 f0.PV1:0 f0.ygT:0 f0.yT:0 f0.o:0
""")
ACT_0 = Steps("""
    x0.xT:1 x0.qv:1 x0.xT:0 x0.qv:0 x0.exp0:1 x0.PT0:1 x0.yg0:1 x0.exp0:0 x0.PT0:0 x0.exp1:1 x0.yg0:0 x0.PT1:1
    x0.yg1:1 x0.exp1:0 x0.yT:1 x0.PT1:0 x0.yg1:0 f0b.xT:1 x0.yT:0 f0.v:1 f0b.xT:0 f0.v:0 f0.exp0:1 f0.PT0:1 f0.yg0:1
    f0.exp0:0 f0.PT0:0 f0.exp1:1 f0.yg0:0 f0.PT1:1 f0.yg1:1 f0.exp1:0 f0.yT:1 f0.PT1:0 f0.yg1:0 f0.yT:0
""")
DVE_0 = Steps("""
    x0.stats:1 x0.aggr:1 x0.eps:1 x0.norm:1 x0.kT:1 x0.kblk:1 x0.stats:0 x0.aggr:0 x0.eps:0 x0.norm:0 x0.add0:1
    x0.max0:1 x0.sub0:1 x0.kT:0 x0.kblk:0 x0.add0:0 x0.max0:0 x0.sub0:0 x0.add1:1 x0.max1:1 x0.sub1:1 x0.add1:0
    x0.max1:0 x0.sub1:0 x0.rden:1 x0.y:1 x0.x:1 f0a.stats:1 f0a.aggr:1 f0a.eps:1 f0a.norm:1 f0b.stats:1 f0b.aggr:1
    f0b.eps:1 f0b.norm:1 x0.rden:0 x0.y:0 f0.conv2:1 f0.conv1:1 f0.conv0:1 x0.x:0 f0a.stats:0 f0a.aggr:0 f0a.eps:0
    f0a.norm:0 f0b.stats:0 f0b.aggr:0 f0.rope:1 f0b.eps:0 f0.qk:1 f0.kblk:1 f0b.norm:0 f0.conv2:0 f0.conv1:0
    f0.conv0:0 f0.max0:1 f0.sub0:1 f0.rope:0 f0.qk:0 f0.kblk:0 f0.max0:0 f0.sub0:0 f0.max1:1 f0.sub1:1 f0.max1:0
    f0.sub1:0 f0.rden:1 f0.y:1 f0.x:1 f0.rden:0 f0.y:0 f0.x:0
""")
POOL_0 = Steps("""
    x0.rstd:1 x0.qblk:1 x0.rstd:0 x0.qblk:0 f0a.rstd:1 f0b.rstd:1 f0a.rstd:0 f0b.rstd:0 f0.qblk:1 x0.bias:1
    f0.qblk:0 x0.bias:0
""")
PE_1 = Steps("""
    x0.T:23 x0.qkv:2 f0c.T:0 x0.qkv:3 f0c.T:1 moe.route:0 x0.S0:2 moe.gv0.0:0 x0.S0:3 moe.route:1 moe.gv0.1:0
    moe.gv0.2:0 x0.PT0:2 moe.gv0.3:0 moe.gv1.0:0 x0.PV0:2 moe.gv1.1:0 moe.gv1.2:0 x0.S1:2 moe.gv1.3:0 x0.PT0:3
    moe.down0.0:0 moe.down0.1:0 moe.gv2.0:0 x0.PT1:2 moe.gv2.1:0 x0.PV0:3 moe.gv2.2:0 x0.S1:3 moe.gv2.3:0
    moe.down1.0:0 x0.PV1:2 moe.down1.1:0 moe.gv3.0:0 x0.ygT:2 moe.gv3.1:0 x0.PT1:3 x0.yT:2 moe.gv3.2:0 moe.gv3.3:0
    x0.o:2 moe.down2.0:0 x0.PV1:3 moe.down2.1:0 x0.ygT:3 moe.down3.0:0 f0b.T:2 x0.yT:3 moe.down3.1:0 x0.o:3 f0.qkv:2
    f0b.T:3 f0.S0:2 x1.T:1 f0.qkv:3 x1.qkv:1 f0.PT0:2 x1.T:0 x1.S:1 f0.S0:3 x1.qkv:0 x1.PT:1 f0.PV0:2 x1.S:0 x1.y:1
    f0.S1:2 x1.PT:0 f0.PT0:3 f1.T:1 x1.y:0 f0.PV0:3 f1.up:1 f0.PT1:2 f1.T:0 f0.S1:3 f1.up:0 f0.PV1:2 f1.uT:1
    f0.ygT:2 f0.PT1:3 f1.uqT:1 f0.PV1:3 f1.down:1 f0.yT:2 f1.uT:0 f0.ygT:3 f0.o:2 f1.uqT:0 x2.T:1 f1.down:0 x2.S:1
    f0c.T:2 f0.yT:3 moe.route:2 f0.o:3 x2.T:0 x2.PT:1 x2.S:0 x2.M:1 f0c.T:3 x2.hq:1 x2.PT:0 moe.gv0.0:2 x2.M:0
    moe.route:3 moe.gv0.1:2 x2.hq:0 moe.gv0.2:2 moe.gv0.3:2 moe.gv1.0:2 x2.out:10 moe.gv1.1:2 moe.gv1.2:2
    moe.gv1.3:2 moe.down0.0:2 f2.T:1 moe.down0.1:2 moe.gv2.0:2 moe.gv2.1:2 moe.gv2.2:2 moe.gv2.3:2 moe.down1.0:2
    f2.T:0 x0.T:1 moe.down1.1:2 x0.qkv:1 moe.gv3.0:2 moe.gv3.1:2 x0.T:0 moe.gv3.2:2 x0.qkv:0 moe.gv3.3:2 x0.S0:1
    moe.down2.0:2 moe.down2.1:2 x0.S0:0 x0.PT0:1 moe.down3.0:2 moe.down3.1:2 x0.PV0:1 x0.PT0:0 x0.S1:1 x1.T:2
    x0.PV0:0 x1.qkv:2 x0.S1:0 x1.S:2 x1.T:3 x0.PT1:1 x1.qkv:3 x0.PV1:1 x0.PT1:0 x1.PT:2 x1.S:3 x0.ygT:1 x1.y:2
    x0.PV1:0 x1.PT:3 x0.yT:1 x0.ygT:0 x1.y:3 x0.o:1 x0.yT:0 f1.T:2 x0.o:0 f1.up:2 f0b.T:0 f0.qkv:0 f1.T:3 f0b.T:1
    f1.uT:2 f1.up:3 f0.qkv:1 f0.S0:0 f1.uqT:2 f1.down:2 f1.uT:3 f0.S0:1 f0.PT0:0 f1.uqT:3 x2.T:2 f0.PV0:0 f1.down:3
    x2.S:2 f0.S1:0 x2.PT:2 x2.T:3 f0.PT0:1 x2.M:2 x2.S:3 f0.PV0:1 x2.hq:2 x2.PT:3 f0.S1:1 f0.PT1:0 x2.out:2 x2.M:3
    f0.PV1:0 x2.hq:3 f2.T:2 f0.PT1:1 f0.ygT:0 x2.out:3 f0.yT:0 f0.PV1:1 f0.o:0 f0.ygT:1 f2.T:3 f0.yT:1 f0.o:1
""", primed=True)
ACT_1 = Steps("""
    x0.xT:23 x0.qv:2 f0c.xT:0 x0.qv:3 f0c.xT:1 moe.tanh0.0:0 x0.exp0:2 moe.tanh0.1:0 moe.tanh0.2:0 x0.exp0:3
    x0.PT0:2 moe.tanh0.3:0 moe.tanh1.0:0 x0.yg0:2 moe.tanh1.1:0 moe.tanh1.2:0 moe.tanh1.3:0 x0.PT0:3 x0.exp1:2
    moe.tanh2.0:0 x0.PT1:2 moe.tanh2.1:0 x0.yg0:3 moe.tanh2.2:0 moe.tanh2.3:0 x0.yg1:2 x0.exp1:3 moe.tanh3.0:0
    moe.tanh3.1:0 x0.PT1:3 x0.yT:2 moe.tanh3.2:0 moe.tanh3.3:0 x0.yg1:3 f0b.xT:2 x0.yT:3 f0.v:2 f0b.xT:3 x1.xT:1
    f0.v:3 f0.exp0:2 x1.qkv:1 f0.PT0:2 x1.xT:0 x1.exp:1 x1.qkv:0 x1.PT:1 f0.yg0:2 f0.exp0:3 x1.exp:0 x1.PT:0
    f0.PT0:3 f1.xT:1 f0.exp1:2 f0.yg0:3 f1.mid:1 f0.PT1:2 f1.xT:0 f1.tanh:1 f1.mid:0 f0.yg1:2 f0.exp1:3 f0.PT1:3
    f1.uqT:1 f1.tanh:0 f0.yg1:3 f0.yT:2 f1.uqT:0 x2.xT:1 f0c.xT:2 f0.yT:3 x2.exp:1 x2.xT:0 x2.PT:1 x2.exp:0 x2.p:1
    f0c.xT:3 x2.PT:0 x2.feat:1 moe.tanh0.0:2 x2.p:0 moe.tanh0.1:2 x2.feat:0 moe.tanh0.2:2 moe.tanh0.3:2
    moe.tanh1.0:2 moe.tanh1.1:2 moe.tanh1.2:2 moe.tanh1.3:2 f2.xT:1 moe.tanh2.0:2 moe.tanh2.1:2 moe.tanh2.2:2
    moe.tanh2.3:2 f2.xT:0 x0.xT:1 x0.qv:1 moe.tanh3.0:2 moe.tanh3.1:2 x0.xT:0 moe.tanh3.2:2 x0.qv:0 moe.tanh3.3:2
    x0.exp0:1 x0.PT0:1 x0.exp0:0 x0.yg0:1 x0.PT0:0 x1.xT:2 x0.yg0:0 x1.qkv:2 x0.exp1:1 x1.xT:3 x0.PT1:1 x0.exp1:0
    x1.exp:2 x1.qkv:3 x0.yg1:1 x0.PT1:0 x1.PT:2 x1.exp:3 x0.yg1:0 x1.PT:3 x0.yT:10 f1.xT:2 f1.mid:2 f0b.xT:0
    f1.tanh:2 f0.v:0 f1.xT:3 f0b.xT:1 f1.mid:3 f0.v:1 f1.tanh:3 f1.uqT:2 f0.exp0:0 f0.PT0:0 f1.uqT:3 x2.xT:2
    f0.yg0:0 f0.exp0:1 x2.exp:2 x2.PT:2 x2.xT:3 f0.PT0:1 x2.p:2 x2.exp:3 f0.exp1:0 f0.yg0:1 x2.PT:3 x2.feat:2
    f0.PT1:0 f0.exp1:1 x2.p:3 f0.yg1:0 f2.xT:2 x2.feat:3 f0.PT1:1 f0.yT:0 f0.yg1:1 f2.xT:3 f0.yT:1
""", primed=True)
DVE_1 = Steps("""
    x0.stats:2 x0.aggr:2 x0.eps:2 x0.stats:3 x0.aggr:3 x0.eps:3 f0c.stats:1 x0.norm:2 f0c.aggr:1 x0.norm:3 f0c.eps:1
    f0c.stats:0 f0c.aggr:0 f0c.eps:0 f0c.norm:10 x0.kT:2 x0.kblk:2 moe.max:0 moe.eq:0 moe.first:0 moe.pick:0 x0.kT:3
    x0.kblk:3 x0.add0:2 x0.max0:2 x0.sub0:2 moe.silu0.0:0 moe.act0.0:0 x0.add0:3 moe.max:1 moe.eq:1 moe.first:1
    moe.pick:1 x0.max0:3 x0.sub0:3 moe.silu0.1:0 moe.act0.1:0 moe.silu0.2:0 moe.act0.2:0 moe.silu0.3:0 moe.act0.3:0
    moe.silu1.0:0 moe.act1.0:0 moe.silu1.1:0 moe.act1.1:0 moe.silu1.2:0 moe.act1.2:0 x0.add1:2 x0.max1:2 x0.sub1:2
    moe.silu1.3:0 moe.act1.3:0 moe.add0.0:0 moe.add0.1:0 moe.silu2.0:0 moe.act2.0:0 moe.silu2.1:0 moe.act2.1:0
    moe.silu2.2:0 moe.act2.2:0 x0.add1:3 x0.max1:3 moe.silu2.3:0 x0.sub1:3 moe.act2.3:0 moe.add1.0:0 moe.add1.1:0
    moe.silu3.0:0 x0.rden:2 moe.act3.0:0 x0.y:2 moe.silu3.1:0 moe.act3.1:0 moe.silu3.2:0 moe.act3.2:0 x0.x:2
    f0a.stats:2 f0a.aggr:2 f0a.eps:2 moe.silu3.3:0 moe.act3.3:0 f0a.norm:2 f0b.stats:2 f0b.aggr:2 f0b.eps:2
    moe.add2.0:0 moe.add2.1:0 f0b.norm:2 x0.rden:3 x0.y:3 f0.conv2:2 f0.conv1:2 f0.conv0:2 moe.add3.0:0 moe.add3.1:0
    x0.x:3 f0a.stats:3 f0a.aggr:3 f0a.eps:3 moe.x:1 x1.stats:1 x1.aggr:1 x1.eps:1 f0a.norm:3 f0b.stats:3 f0.rope:2
    f0b.aggr:3 f0b.eps:3 f0.qk:2 f0.kblk:2 f0b.norm:3 x1.norm:1 moe.x:0 x1.stats:0 x1.aggr:0 x1.eps:0 f0.conv2:3
    f0.conv1:3 f0.conv0:3 f0.max0:2 f0.sub0:2 f0.rope:3 f0.qk:3 f0.kblk:3 x1.norm:0 x1.nmax:1 x1.rden:1 f0.max0:3
    f0.sub0:3 x1.nmax:0 x1.x:1 x1.bv:1 f1.stats:1 x1.rden:0 f1.aggr:1 f1.eps:1 f1.norm:1 f1.amax:1 f1.inv:1
    f1.scale:1 f1.round:1 f1.xq:1 f0.max1:2 f0.sub1:2 x1.x:0 x1.bv:0 f1.stats:0 f1.aggr:0 f1.eps:0 f1.norm:0
    f1.amax:0 f1.inv:0 f1.scale:0 f1.round:0 f1.xq:0 f1.tap0:1 f1.taps:1 f0.max1:3 f1.silu:1 f0.sub1:3 f1.tap0:0
    f1.uamax:1 f1.uclip:1 f1.urec:1 f1.uscale:1 f1.uround:1 f1.uq:1 f1.taps:0 f0.rden:2 f0.y:2 f1.silu:0 f1.x:1
    x2.stats:1 x2.aggr:1 x2.eps:1 f1.uamax:0 f1.uclip:0 f1.urec:0 f1.uscale:0 f1.uround:0 f1.uq:0 f0.x:2 x2.norm:1
    f0c.stats:2 f0c.aggr:2 f0c.eps:2 f0.rden:3 f0.y:3 f0c.norm:2 f1.x:0 x2.stats:0 x2.aggr:0 x2.eps:0 x2.nmax:1
    x2.smax:1 x2.score:1 x2.norm:0 x2.rden:1 moe.max:2 x2.P:1 moe.eq:2 moe.first:2 moe.pick:2 f0.x:3 f0c.stats:3
    f0c.aggr:3 f0c.eps:3 x2.M:1 x2.nmax:0 x2.smax:0 x2.score:0 x2.negM:1 f0c.norm:3 x2.rden:0 x2.P:0 x2.rsum:1
    x2.hc:1 x2.M:0 x2.negM:0 moe.max:3 moe.eq:3 moe.first:3 moe.pick:3 x2.ehq:1 moe.silu0.0:2 moe.act0.0:2
    moe.silu0.1:2 moe.act0.1:2 x2.rsum:0 x2.hc:0 x2.ehq:0 moe.silu0.2:2 moe.act0.2:2 moe.silu0.3:2 moe.act0.3:2
    moe.silu1.0:2 x2.add:0 moe.act1.0:2 x2.add:1 f2.x:1 f2.stats:1 f2.aggr:1 f2.eps:1 moe.silu1.1:2 moe.act1.1:2
    f2.norm:1 moe.silu1.2:2 moe.act1.2:2 f2.x:0 f2.stats:0 f2.aggr:0 f2.eps:0 moe.silu1.3:2 moe.act1.3:2
    moe.add0.0:2 moe.add0.1:2 x0.stats:1 moe.silu2.0:2 moe.act2.0:2 x0.aggr:1 x0.eps:1 moe.silu2.1:2 moe.act2.1:2
    x0.norm:1 f2.norm:0 moe.silu2.2:2 moe.act2.2:2 moe.silu2.3:2 moe.act2.3:2 moe.add1.0:2 moe.add1.1:2 x0.stats:0
    x0.aggr:0 x0.eps:0 x0.kT:1 x0.kblk:1 x0.norm:0 moe.silu3.0:2 moe.act3.0:2 moe.silu3.1:2 moe.act3.1:2
    moe.silu3.2:2 moe.act3.2:2 x0.kT:0 x0.kblk:0 moe.silu3.3:2 moe.act3.3:2 x0.add0:1 x0.max0:1 x0.sub0:1
    moe.add2.0:2 moe.add2.1:2 x0.add0:0 x0.max0:0 x0.sub0:0 moe.add3.0:2 moe.add3.1:2 moe.x:2 x1.stats:2 x1.aggr:2
    x1.eps:2 moe.x:3 x1.stats:3 x1.aggr:3 x1.norm:2 x1.eps:3 x0.add1:1 x0.max1:1 x0.sub1:1 x1.norm:3 x0.add1:0
    x0.max1:0 x0.sub1:0 x1.nmax:2 x1.rden:2 x1.nmax:3 x0.rden:1 x1.rden:3 x0.y:1 x1.x:2 x1.bv:2 f1.stats:2 f1.aggr:2
    f1.eps:2 f1.norm:2 f1.amax:2 f1.inv:2 f1.scale:2 x0.rden:0 x0.y:0 f1.round:2 f1.xq:2 x1.x:3 x1.bv:3 f1.stats:3
    x0.x:1 f0a.stats:1 x0.x:0 f0a.stats:0 f0a.aggr:0 f0a.eps:0 f0a.aggr:1 f0a.eps:1 f1.aggr:3 f1.eps:3 f0a.norm:0
    f0b.stats:0 f0b.aggr:0 f0b.eps:0 f1.norm:3 f1.amax:3 f1.inv:3 f1.scale:3 f0b.norm:0 f1.round:3 f1.tap0:2
    f1.taps:2 f0.conv2:0 f0.conv1:0 f0.conv0:0 f0a.norm:1 f0b.stats:1 f0b.aggr:1 f0b.eps:1 f1.silu:2 f1.xq:3
    f0b.norm:1 f0.rope:0 f0.qk:0 f0.conv2:1 f1.uamax:2 f0.conv1:1 f0.conv0:1 f1.uclip:2 f1.urec:2 f1.uscale:2
    f1.uround:2 f0.kblk:0 f1.uq:2 f1.tap0:3 f0.rope:1 f1.taps:3 f0.qk:1 f0.kblk:1 f1.silu:3 f0.max0:0 f1.x:2
    x2.stats:2 f0.sub0:0 x2.aggr:2 x2.eps:2 f1.uamax:3 f1.uclip:3 f1.urec:3 f1.uscale:3 f1.uround:3 f1.uq:3
    f0.max0:1 x2.norm:2 f0.sub0:1 f1.x:3 x2.nmax:2 x2.smax:2 x2.score:2 x2.stats:3 x2.aggr:3 x2.eps:3 x2.rden:2
    x2.P:2 x2.norm:3 f0.max1:0 x2.M:2 f0.sub1:0 x2.negM:2 x2.nmax:3 x2.smax:3 x2.score:3 x2.rden:3 x2.P:3 x2.rsum:2
    x2.hc:2 x2.M:3 x2.ehq:2 f0.max1:1 f0.sub1:1 x2.add:2 x2.negM:3 f2.x:2 f2.stats:2 f2.aggr:2 f2.eps:2 f2.norm:2
    x2.rsum:3 x2.hc:3 x2.ehq:3 f0.rden:0 f0.y:0 x2.add:3 f2.x:3 f2.stats:3 f2.aggr:3 f2.eps:3 f0.x:0 f2.norm:3
    f0.rden:1 f0.y:1 f0.x:1
""", primed=True)
POOL_1 = Steps("""
    x0.rstd:23 f0c.rstd:10 x0.qblk:23 f0a.rstd:2 f0b.rstd:2 f0a.rstd:3 x1.rstd:1 f0b.rstd:3 f0.qblk:2 x0.bias:2
    x1.rstd:0 f0.qblk:3 x0.bias:3 f1.rstd:10 x2.rstd:1 f0c.rstd:2 x2.rstd:0 f0c.rstd:3 f2.rstd:1 in:1 f2.rstd:0
    x0.rstd:1 in:0 x0.rstd:0 x0.qblk:10 x1.rstd:23 f1.rstd:2 f0a.rstd:0 f1.rstd:3 f0a.rstd:1 f0b.rstd:01 f0.qblk:0
    x0.bias:0 f0.qblk:1 x0.bias:1 x2.rstd:23 f2.rstd:2 in:2 f2.rstd:3 in:3
""", primed=True)
PE_3 = Steps("""
    x3.T x3.proj x3.rho0 x3.rho_last x3.rho1 x3.rho2 x3.rho3 x3.rhoT x3.PT x3.h x3.gate f3.T f3.route f3.place f3.y
""")
ACT_3 = Steps("""
    x3.xT x3.proj x3.tanh0 x3.tanh_last x3.tanh1 x3.tanh2 x3.tanh3 x3.rho x3.exp x3.PT x3.h x3.gate f3.xT f3.exp
""")
DVE_3 = Steps("""
    x3.stats x3.aggr x3.eps x3.norm x3.sum0 x3.sum1 x3.sum2 x3.sum3 x3.mask x3.nmax x3.rden x3.P x3.gb x3.y x3.x
    f3.stats f3.aggr f3.eps f3.norm f3.nmax f3.rden f3.probs f3.pmax f3.eq f3.first f3.pick f3.taken f3.keep f3.w
    f3.add0 f3.add1 f3.add2 f3.add3 f3.add4 f3.add5 f3.add6 f3.add7
""")
POOL_3 = Steps("""
    x3.rstd f3.rstd
""")
PE_2A = Steps("""
    up gate
""", 2)
DVE_2A = Steps("""
    up gate
""", 2, primed=True)
PE_2B = Steps("""
    gate
""", 2)
ACT_2B = Steps("""
    round tanh
""", 2, primed=True)
DVE_2B = Steps("""
    gate sigmoid clip gated max
""", 2, primed=True)
PE_2C = Steps("""
    up
""", 2)
ACT_2C = Steps("""
    round
""", 2, primed=True)
DVE_2C = Steps("""
    round up product max
""", 2, primed=True)
PE_2D = Steps("""
    down
""", 2, primed=True)
DVE_2D = Steps("""
    round quant add
""", 2, primed=True)



def shape_constants():
    c = {}
    p = np.arange(128)
    c["ident"] = np.eye(128, dtype=np.float32)
    c["causal"] = np.where(p[None, :] > p[:, None], np.float32(-1e30), np.float32(0)).astype(np.float32)
    c["before"] = (p[:, None] < p[None, :]).astype(np.float32)
    c["ingroup"] = ((p[:, None] // HDIM) % GROUP == np.arange(GROUP)[None, :]).astype(np.float32)
    c["ofgroup"] = (p[:, None] // (HDIM * GROUP) == np.arange(GROUP)[None, :]).astype(np.float32)
    c["first"] = np.tile(np.arange(MOE3, 0, -1, dtype=np.float32), (128, 1))
    n = np.clip(np.arange(-(KEYS - 1), TOK), 0, None)
    exact = BUCKETS // 2
    large = exact + (np.log(np.maximum(n, exact).astype(np.float32) / np.float32(exact) + np.float32(1e-9))
                     / np.float32(np.log(MAX_DISTANCE / exact)) * np.float32(BUCKETS - exact)).astype(np.int32)
    bucket = np.where(n < exact, n, np.minimum(large, BUCKETS - 1))
    c["bucket"] = (np.arange(BUCKETS)[:, None] == bucket[None, :]).astype(np.float32)
    inv = (np.float32(1.0) / np.float32(10000.0) ** (np.arange(0, HDIM, 2, dtype=np.float32) / np.float32(HDIM))).astype(np.float32)
    ang = np.outer(np.arange(TOK, dtype=np.float32), inv).astype(np.float32)
    i = p % HDIM
    cos = np.cos(ang)[:, i % (HDIM // 2)].T
    sin = np.sin(ang)[:, i % (HDIM // 2)].T * np.where(i < HDIM // 2, -1.0, 1.0)[:, None]
    r = 1.0 / np.sqrt(HDIM)
    c["rope"] = np.stack([cos * r, cos, sin * r, sin], axis=1).astype(np.float32)
    return c


def swap_halves(w):
    k = w.shape[0]
    return np.ascontiguousarray(w.reshape(k, HEADS, 2, HDIM // 2)[:, :, ::-1, :]).reshape(k, DIM)


def build(nc, d):
    x_mid = nc.dram_tensor("x_mid", (BATCH, TOK, DIM), F32, kind="Internal").ap()
    x_mid2 = nc.dram_tensor("x_mid2", (BATCH, TOK, DIM), F32, kind="Internal").ap()
    with ExitStack() as ctx:
        shared = dict(x_mid=x_mid, x_mid2=x_mid2)
        for name, shape in (("xnT_all", [128, BATCH * TOK]), ("ident", [128, 128]), ("ones", [128, 128]),
                            ("first", [128, MOE3]), ("minus_half", [128, 1])):
            shared[name] = ctx.enter_context(nc.sbuf_tensor(name, shape, F32))
        part_1(nc, d, shared)
        part_2(nc, d, shared)
        part_3(nc, d, shared)


def part_1(nc, d, shared):
    xnT_all, ident, ones, first, minus_half, x_mid = (shared[k] for k in ("xnT_all", "ident", "ones", "first", "minus_half", "x_mid"))
    S = range(STREAMS)
    A, B = (0, 1), (2, 3)
    LISTS = (PE_0, ACT_0, DVE_0, POOL_0), (PE_1, ACT_1, DVE_1, POOL_1)
    with ExitStack() as ctx:
        def sb(name, shape, dt=F32):
            return ctx.enter_context(nc.sbuf_tensor(name, shape, dt))

        def per_stream(name, shape, dt=F32):
            return [sb(f"{name}{s}", shape, dt) for s in S]

        def sem(name):
            return ctx.enter_context(nc.semaphore(name))

        ident_bf = sb("ident_bf", [128, 128], BF16)
        causal_bf = sb("causal_bf", [128, 128], BF16)
        ingroup = sb("ingroup", [128, GROUP])
        ofgroup = sb("ofgroup", [128, GROUP])
        rope = sb("rope", [128, 4, TOK])
        mask_words = sb("mask_words", [128, (BATCH + 2 * STREAMS) * KEYS // 4], I32)
        mask = mask_words[:].bitcast(U8)
        bias0 = sb("bias0", [128, HEADS, KEYS])
        w_xa0 = sb("w_xa0", [128, 4, DIM])
        ln_col = sb("ln_col", [128, 4])
        conv0_col = sb("conv0_col", [128, 3])
        w_at0 = sb("w_at0", [128, 5, DIM])
        w_pr0 = sb("w_pr0", [128, DIM])
        w_ro0 = sb("w_ro0", [128, MOE0])
        w_gv0 = sb("w_gv0", [128, MOE0, 2 * FF0])
        w_dn0 = sb("w_dn0", [128, MOE0, FF0 // CH, DIM])
        w_xa1 = sb("w_xa1", [128, 3, DIM])
        b_xa1 = sb("b_xa1", [128, 2])
        bv1 = sb("bv1", [128, DIM])
        w_up1 = sb("w_up1", [128, FF1])
        conv1_col = sb("conv1_col", [128, FF1 // CH, 4])
        w_dn1 = sb("w_dn1", [128, FF1 // CH, DIM])
        w_dn1_q = sb("w_dn1_q", [128, FF1 // CH, DIM], BF16)
        sim_col = sb("sim_col", [128, 3])
        b_sim = sb("b_sim", [128, 1])
        w_qv2 = sb("w_qv2", [128, 4, DIM])
        b_qv2 = sb("b_qv2", [128, DIM])
        prep = sb("prep", [128, 16])

        x_in = per_stream("x_in", [128, DIM])
        ctx_in = per_stream("ctx_in", [KEYS, DIM])
        ctxT_in = per_stream("ctxT_in", [128, KEYS])
        x = per_stream("x", [128, DIM])
        cx = per_stream("cx", [KEYS, DIM])
        cxT = per_stream("cxT", [128, KEYS])
        xn = per_stream("xn", [128, DIM])
        xnT_4 = sb("xnT_4", [128, STREAMS, TOK])
        xnT = [xnT_4[:, s, :] for s in S]
        h0 = per_stream("h0", [128, DIM])
        attended = per_stream("attended", [128, KEYS])
        thr = per_stream("thr", [128, KEYS])
        bias_m = per_stream("bias_m", [128, HEADS, KEYS])
        qT = per_stream("qT", [128, TOK])
        kT = per_stream("kT", [128, TOK])
        kblk = per_stream("kblk", [128, GROUP, TOK])
        qblk = per_stream("qblk", [128, GROUP, TOK])
        vaug = per_stream("vaug", [128, HEADS, VPAD])
        yg = per_stream("yg", [128, GROUP, TOK])
        prob = per_stream("prob", [128, 2 * BANK])
        probT = per_stream("probT", [128, 2 * BANK])
        y = per_stream("y", [128, DIM])
        yT = per_stream("yT", [128, TOK])
        col = per_stream("col", [128, 48])
        ps = [ctx.enter_context(nc.psum_tensor(f"ps{s}", [128, 2, BANK], F32)) for s in S]

        weights_in, consts_done, setup_pe, setup_act, setup_dve = (sem(n) for n in (
            "weights_in", "consts_done", "setup_pe", "setup_act", "setup_dve"))
        loads_in = [sem(f"loads_in{s}") for s in S]
        stores_out = [sem(f"stores_out{s}") for s in S]
        inputs_ready, mask_made, mask_ready, bias_kept, bias_ready = ([sem(f"{n}{s}") for s in S] for n in (
            "inputs_ready", "mask_made", "mask_ready", "bias_kept", "bias_ready"))
        mask_tail = sem("mask_tail")
        passed = sem("passed")
        pe_done, act_done, dve_done, pool_done = (sem(n) for n in ("pe_done", "act_done", "dve_done", "pool_done"))

        weight_loads = [
            (ident[:], d["ident"]), (first[:], d["first"]), (ingroup[:], d["ingroup"]), (ofgroup[:], d["ofgroup"]), (rope[:], d["rope"]),
            (prob[0][:, 0:128], d["causal"]), (prob[0][0:BUCKETS, 128:128 + TOK + KEYS - 1], d["bucket"]),
            (prob[0][0:BUCKETS, 384:384 + HEADS], d["L0_xattn_rel_emb"]),
            (mask_words[:, 0:BATCH * KEYS // 4], d["mask_Bx1x1xS2_bk0"].to_broadcast([128, BATCH * KEYS // 4])),
            (w_xa0[:, 0, :], d["L0_xattn_Wq"]), (w_xa0[:, 1, :], d["L0_xattn_Wk"]),
            (w_xa0[:, 2, :], d["L0_xattn_Wv"]), (w_xa0[:, 3, :], d["L0_xattn_Wo"]),
            (ln_col[:, 0:1], d["L0_ffn_ln1_w"]), (ln_col[:, 1:2], d["L0_ffn_ln1_b"]),
            (ln_col[:, 2:3], d["L0_ffn_ln2_w"]), (ln_col[:, 3:4], d["L0_ffn_ln2_b"]),
            (conv0_col[:], d["L0_ffn_conv_w"]), (w_at0[:], d["attn_w5"]), (w_pr0[:], d["L0_ffn_proj_w"]),
            (w_ro0[:], d["L0_ffn_router_w"]), (w_gv0[:], d["L0_ffn_expert_wv"].rearrange("e c n -> c e n")),
            (w_dn0[:], d["L0_ffn_expert_proj"].rearrange("e (k c) n -> c e k n", c=CH)),
            (w_xa1[:, 0, :], d["L1_xattn_Wq"]), (w_xa1[:, 1, :], d["L1_xattn_Wk"]), (w_xa1[:, 2, :], d["L1_xattn_Wv"]),
            (b_xa1[:, 0:1], d["L1_xattn_bq"]), (b_xa1[:, 1:2], d["L1_xattn_bk"]),
            (bv1[:], d["L1_xattn_bv"].to_broadcast([128, DIM])),
            (w_up1[:], d["L1_ffn_w1"]), (w_dn1[:], d["L1_ffn_w2"].rearrange("(k c) n -> c k n", c=CH)),
            (conv1_col[:], d["L1_ffn_conv"]), (sim_col[:], d["L2_xattn_w_sim"]), (b_sim[:], d["L2_xattn_b_sim"].to_broadcast([128, 1])),
            (w_qv2[:], d["L2_xattn_W_qv"].rearrange("(k c) n -> c k n", c=DIM)),
            (b_qv2[:], d["L2_xattn_b_qv"].to_broadcast([128, DIM])),
        ]

        def unit_bank(pair, u):
            return ps[pair[u % 3 // 2]][:, u % 3 % 2, :]

        def hidden(pair, e, c):
            return prob[pair[e % 2]][:, c * PAIR * TOK:(c + 1) * PAIR * TOK]

        SETUP_BIAS, SETUP_SUMS, SETUP_DVE = 1, 4, 13

        block = ctx.enter_context(nc.Block())

        @block.sync
        def _(sp):
            def load(s, b):
                sp.dma_start(x_in[s][:], d["x"][bass.ds(b, 1), :, :].rearrange("o t c -> t (o c)")).then_inc(loads_in[s], 16)
                sp.dma_start(ctx_in[s][:], d["ctx"][bass.ds(b, 1), :, :].rearrange("o t c -> t (o c)")).then_inc(loads_in[s], 16)
                sp.dma_start(ctxT_in[s][:], d["ctxT"][bass.ds(b, 1), :, :].rearrange("o t c -> t (o c)")).then_inc(loads_in[s], 16)

            for dst, src in weight_loads:
                sp.dma_start(dst, src).then_inc(weights_in, 16)
            for s in S:
                load(s, s)
            with sp.Fori(0, ROUNDS - 1) as r:
                for s in S:
                    sp.wait_ge(inputs_ready[s], r + 1)
                    load(s, r * STREAMS + (STREAMS + s))
            for s in S:
                sp.wait_ge(inputs_ready[s], ROUNDS)
                load(s, s)

        @block.gpsimd
        def _(pool):
            def take_inputs(s, value):
                pool.wait_ge(loads_in[s], value)
                pool.sem_inc(passed, 1)
                nc.gpsimd.tensor_copy(x[s][:], x_in[s][:])
                nc.gpsimd.tensor_copy(cx[s][:], ctx_in[s][:])
                nc.gpsimd.tensor_copy(cxT[s][:], ctxT_in[s][:]).then_inc(inputs_ready[s], 1)

            def mask_bias(s, rnd):
                pool.wait_ge(mask_ready[s], rnd + 1)
                nc.gpsimd.tensor_tensor(bias_m[s][:], bias0[:], attended[s][:].unsqueeze(1).to_broadcast([128, HEADS, KEYS]), ALU.mult).then_inc(bias_kept[s], 1)
                pool.wait_ge(bias_kept[s], rnd + 1)
                nc.gpsimd.tensor_tensor(bias_m[s][:], bias_m[s][:], thr[s][:].unsqueeze(1).to_broadcast([128, HEADS, KEYS]), ALU.add).then_inc(bias_ready[s], 1)

            def program(k, it):
                PE_L, ACT_L, DVE_L, POOL_L = LISTS[k]

                def at(steps_, name, s):
                    return steps_.value(name, s, it)

                def qblocks(s, p, ready):
                    ready(s)
                    nc.gpsimd.tensor_tensor(qblk[s][:], qT[s][:].unsqueeze(1).to_broadcast([128, GROUP, TOK]),
                                            ofgroup[:].unsqueeze(2).to_broadcast([128, GROUP, TOK]), ALU.mult).then_inc(pool_done, POOL_L.did(f"{p}.qblk", s))
                    yield

                def rstd(s, p):
                    pool.wait_ge(dve_done, at(DVE_L, f"{p}.eps", s))
                    nc.gpsimd.tensor_tensor(col[s][:, 9:10], col[s][:, 8:9], minus_half[:], ALU.pow).then_inc(pool_done, POOL_L.did(f"{p}.rstd", s))
                    yield

                def first_half(s, rnd):
                    yield from rstd(s, "x0")
                    yield from qblocks(s, "x0", lambda s: pool.wait_ge(act_done, at(ACT_L, "x0.qv", s)))
                    yield from rstd(s, "f0a")
                    yield from rstd(s, "f0b")
                    yield from qblocks(s, "f0", lambda s: pool.wait_ge(dve_done, at(DVE_L, "f0.qk", s)))
                    pool.wait_ge(dve_done, at(DVE_L, "x0.add1", s))
                    mask_bias(s, rnd + 1)
                    pool.wait_ge(bias_ready[s], rnd + 2)
                    pool.sem_inc(pool_done, POOL_L.did("x0.bias", s))
                    yield

                def second_half(s, rnd):
                    for p in ("f0c", "x1", "f1", "x2", "f2"):
                        yield from rstd(s, p)
                    pool.wait_ge(act_done, at(ACT_L, "f2.xT", s))
                    pool.wait_ge(stores_out[s], rnd * 16 + 16)
                    take_inputs(s, rnd * 48 + 96)
                    pool.wait_ge(inputs_ready[s], rnd + 2)
                    pool.sem_inc(pool_done, POOL_L.did("in", s))
                    yield

                return first_half, second_half

            nc.gpsimd.memset(minus_half[:], -0.5).then_inc(consts_done, 1)
            nc.gpsimd.memset(ones[:], 1.0).then_inc(consts_done, 1)
            for s in S:
                nc.gpsimd.memset(vaug[s][:], 1.0).then_inc(consts_done, 1)
            pool.wait_ge(consts_done, 2 + STREAMS)
            pool.wait_ge(setup_act, 3)
            for s in S:
                take_inputs(s, 48)
            for s in S:
                mask_bias(s, 0)
            take_turns(POOL_0, [program(0, 0)[0](s, 0) for s in A])
            pool.wait_ge(pool_done, POOL_0.per_round)
            pool.sem_inc(pool_done, POOL_1.per_round - POOL_0.per_round)
            with pool.Fori(0, ROUNDS) as r:
                first_half, second_half = program(1, r)
                take_turns(POOL_1, [chain(second_half(s, r), first_half(s, r + 1)) for s in A] + [chain(first_half(s, r), second_half(s, r)) for s in B])

        @block.scalar
        def _(act):
            act.wait_ge(setup_pe, SETUP_BIAS)
            act.wait_ge(consts_done, 2 + STREAMS)
            for n in range(3):
                k0, k1 = n * 32, min(KEYS, n * 32 + 32)
                bank = ps[n // 2][:, n % 2, 0:(k1 - k0) * HEADS]
                nc.scalar.copy(bias0[:, :, k0:k1], bank.rearrange("p (k h) -> p h k", h=HEADS)).then_inc(setup_act, 1)
            def program(k, it):
                PE_L, ACT_L, DVE_L, POOL_L = LISTS[k]

                def at(steps_, name, s):
                    return steps_.value(name, s, it)

                def xT(s, p, w=None):
                    act.wait_ge(pe_done, at(PE_L, f"{p}.T", s))
                    if w is None:
                        nc.scalar.copy(xnT[s][:], ps[s][:, 0, 0:TOK]).then_inc(act_done, ACT_L.did(f"{p}.xT", s))
                        yield
                    else:
                        nc.scalar.activation(xnT[s][:], ps[s][:, 0, 0:TOK], ACT.Identity, scale=ln_col[:, w:w + 1], bias=ln_col[:, w + 1:w + 2]).then_inc(act_done, ACT_L.did(f"{p}.xT", s))
                        yield

                def heads(s, p, nk):
                    for hf in range(2):
                        act.wait_ge(dve_done, at(DVE_L, f"{p}.sub{hf}", s))
                        nc.scalar.activation(prob[s][:, 0:HALF * nk], prob[s][:, 0:HALF * nk], ACT.Exp).then_inc(act_done, ACT_L.did(f"{p}.exp{hf}", s))
                        yield
                        act.wait_ge(pe_done, at(PE_L, f"{p}.PT{hf}", s))
                        nc.scalar.copy(probT[s][0:nk, :], ps[s][0:nk, :, :].rearrange("p b n -> p (b n)")).then_inc(act_done, ACT_L.did(f"{p}.PT{hf}", s))
                        yield
                        act.wait_ge(pe_done, at(PE_L, f"{p}.PV{hf}", s))
                        nc.scalar.copy(yg[s][:, 2 * hf:2 * hf + 2, :], ps[s][:, 0, 0:2 * TOK].rearrange("p (g t) -> p g t", g=2)).then_inc(act_done, ACT_L.did(f"{p}.yg{hf}", s))
                        yield
                    act.wait_ge(pe_done, at(PE_L, f"{p}.yT", s))
                    nc.scalar.copy(yT[s][:], ps[s][:, 1, 0:TOK]).then_inc(act_done, ACT_L.did(f"{p}.yT", s))
                    yield

                def first_half(s, rnd):
                    yield from xT(s, "x0")
                    act.wait_ge(pe_done, at(PE_L, "x0.qkv", s))
                    nc.scalar.activation(qT[s][:], ps[s][:, 0, 0:TOK], ACT.Copy, scale=float(HDIM) ** -0.5)
                    nc.scalar.copy(vaug[s][0:KEYS, :, 0:HDIM], ps[s][0:KEYS, 0, 256:256 + DIM].rearrange("p (h e) -> p h e", h=HEADS)).then_inc(act_done, ACT_L.did("x0.qv", s))
                    yield
                    yield from heads(s, "x0", KEYS)
                    yield from xT(s, "f0b", 0)
                    act.wait_ge(pe_done, at(PE_L, "f0.qkv", s))
                    nc.scalar.copy(vaug[s][:, :, 0:HDIM], ps[s][:, 1, 0:DIM].rearrange("p (h e) -> p h e", h=HEADS)).then_inc(act_done, ACT_L.did("f0.v", s))
                    yield
                    yield from heads(s, "f0", TOK)

                def second_half(s, rnd):
                    yield from xT(s, "f0c", 2)
                    if s % PAIR == 0:
                        pair = (s, s + 1)
                        for e in range(MOE0):
                            for c in range(CHUNKS0):
                                if e >= 2:
                                    act.wait_ge(pe_done, at(PE_L, f"moe.down{e - 2}.1", pair[0]))
                                act.wait_ge(pe_done, at(PE_L, f"moe.gv{e}.{c}", pair[0]))
                                nc.scalar.activation(hidden(pair, e, c), unit_bank(pair, e * CHUNKS0 + c)[:, 0:PAIR * TOK], ACT.Tanh, scale=0.5).then_inc(act_done, ACT_L.did(f"moe.tanh{e}.{c}", pair[0]))
                                yield
                    yield from xT(s, "x1")
                    act.wait_ge(pe_done, at(PE_L, "x1.qkv", s))
                    nc.scalar.activation(qT[s][:], ps[s][:, 0, 0:TOK], ACT.Identity, bias=b_xa1[:, 0:1])
                    nc.scalar.activation(kT[s][:, 0:KEYS], ps[s][:, 0, 128:128 + KEYS], ACT.Identity, bias=b_xa1[:, 1:2])
                    nc.scalar.copy(y[s][0:KEYS, :], ps[s][0:KEYS, 0, 256:256 + DIM]).then_inc(act_done, ACT_L.did("x1.qkv", s))
                    yield
                    act.wait_ge(dve_done, at(DVE_L, "x1.nmax", s))
                    nc.scalar.activation(prob[s][:, 0:KEYS], ps[s][:, 1, 0:KEYS], ACT.Exp, bias=col[s][:, 16:17], accum_out=col[s][:, 17:18]).then_inc(act_done, ACT_L.did("x1.exp", s))
                    yield
                    act.wait_ge(pe_done, at(PE_L, "x1.PT", s))
                    nc.scalar.copy(probT[s][0:KEYS, 0:TOK], ps[s][0:KEYS, 0, 0:TOK]).then_inc(act_done, ACT_L.did("x1.PT", s))
                    yield
                    yield from xT(s, "f1")
                    act.wait_ge(pe_done, at(PE_L, "f1.up", s))
                    for c in range(FF1 // CH):
                        last = nc.scalar.activation(prob[s][:, c * TOK:(c + 1) * TOK], ps[s][:, 0, c * TOK:(c + 1) * TOK], ACT.Identity, scale=conv1_col[:, c, 1:2], bias=conv1_col[:, c, 3:4])
                    last.then_inc(act_done, ACT_L.did("f1.mid", s))
                    yield
                    act.wait_ge(dve_done, at(DVE_L, "f1.taps", s))
                    nc.scalar.activation(prob[s][:, BANK:2 * BANK], prob[s][:, 0:BANK], ACT.Tanh, scale=0.5).then_inc(act_done, ACT_L.did("f1.tanh", s))
                    yield
                    act.wait_ge(pe_done, at(PE_L, "f1.uqT", s))
                    nc.scalar.copy(probT[s][:, 256:512].bitcast(BF16), ps[s][:, 1, 0:256].bitcast(BF16)).then_inc(act_done, ACT_L.did("f1.uqT", s))
                    yield
                    act.wait_ge(pe_done, at(PE_L, "x2.T", s))
                    nc.scalar.activation(qT[s][:], ps[s][:, 0, 0:TOK], ACT.Identity, scale=sim_col[:, 2:3], bias=sim_col[:, 1:2])
                    nc.scalar.copy(xnT[s][:], ps[s][:, 0, 0:TOK]).then_inc(act_done, ACT_L.did("x2.xT", s))
                    yield
                    act.wait_ge(dve_done, at(DVE_L, "x2.score", s))
                    nc.scalar.activation(prob[s][:, 0:KEYS], ps[s][:, 1, 0:KEYS], ACT.Exp, bias=col[s][:, 16:17], accum_out=col[s][:, 17:18]).then_inc(act_done, ACT_L.did("x2.exp", s))
                    yield
                    act.wait_ge(pe_done, at(PE_L, "x2.PT", s))
                    nc.scalar.copy(probT[s][0:KEYS, 0:TOK], ps[s][0:KEYS, 0, 0:TOK]).then_inc(act_done, ACT_L.did("x2.PT", s))
                    yield
                    act.wait_ge(dve_done, at(DVE_L, "x2.negM", s))
                    nc.scalar.activation(col[s][:, 22:23], col[s][:, 19:20], ACT.Exp, bias=col[s][:, 21:22]).then_inc(act_done, ACT_L.did("x2.p", s))
                    yield
                    act.wait_ge(pe_done, at(PE_L, "x2.hq", s))
                    nc.scalar.copy(kT[s][:], ps[s][:, 0, 0:TOK])
                    act.wait_ge(dve_done, at(DVE_L, "x2.hc", s))
                    nc.scalar.activation(yT[s][:], xnT[s][:], ACT.Copy, scale=col[s][:, 24:25]).then_inc(act_done, ACT_L.did("x2.feat", s))
                    yield
                    act.wait_ge(dve_done, at(DVE_L, "f2.x", s))
                    act.dma_start(x_mid[bass.ds(rnd * STREAMS + s, 1), :, :].rearrange("o t c -> t (o c)"), x[s][:]).then_inc(stores_out[s], 16)
                    act.wait_ge(pe_done, at(PE_L, "f2.T", s))
                    act.sem_inc(passed, 1)
                    nc.scalar.copy(xnT_all[:, bass.ds((rnd * STREAMS + s) * TOK, TOK)], ps[s][:, 0, 0:TOK]).then_inc(act_done, ACT_L.did("f2.xT", s))
                    yield

                return first_half, second_half

            take_turns(ACT_0, [program(0, 0)[0](s, 0) for s in A])
            act.wait_ge(act_done, ACT_0.per_round)
            act.sem_inc(act_done, ACT_1.per_round - ACT_0.per_round)
            with act.Fori(0, ROUNDS) as r:
                first_half, second_half = program(1, r)
                take_turns(ACT_1, [chain(second_half(s, r), first_half(s, r + 1)) for s in A] + [chain(first_half(s, r), second_half(s, r)) for s in B])

            for s in S:
                act.wait_ge(stores_out[s], 16 * ROUNDS)

        @block.tensor
        def _(pe):
            pe.wait_ge(weights_in, 16 * len(weight_loads))
            pe.wait_ge(consts_done, 2 + STREAMS)
            for k in range(KEYS):
                n, j = k // 32, k % 32
                last = nc.tensor.matmul(ps[n // 2][:, n % 2, j * HEADS:(j + 1) * HEADS], prob[0][0:BUCKETS, 128 + KEYS - 1 - k:128 + KEYS - 1 - k + TOK],
                                        prob[0][0:BUCKETS, 384:384 + HEADS], start=True, stop=True)
            last.then_inc(setup_pe, 1)
            pe.wait_ge(setup_dve, SETUP_SUMS)
            nc.tensor.matmul(ps[3][:, 0, 0:2], ones[:], prep[:, 0:2], start=True, stop=True).then_inc(setup_pe, 1)
            pe.wait_ge(setup_dve, SETUP_DVE)
            pe.wait_ge(setup_act, 3)
            def program(k, it):
                PE_L, ACT_L, DVE_L, POOL_L = LISTS[k]

                def at(steps_, name, s):
                    return steps_.value(name, s, it)

                def transpose_xn(s, p):
                    pe.wait_ge(dve_done, at(DVE_L, f"{p}.norm", s))
                    nc.tensor.transpose(ps[s][:, 0, 0:TOK], xn[s][:], ident[:]).then_inc(pe_done, PE_L.did(f"{p}.T", s))
                    yield

                def heads(s, p, nk, w_out):
                    for hf in range(2):
                        if hf == 0:
                            pe.wait_ge(dve_done, at(DVE_L, f"{p}.kblk", s))
                            pe.wait_ge(pool_done, at(POOL_L, f"{p}.qblk", s))
                            pe.wait_ge(act_done, at(ACT_L, "x0.qv" if p == "x0" else "f0.v", s))
                        else:
                            pe.wait_ge(act_done, at(ACT_L, f"{p}.yg0", s))
                        for b in range(2):
                            last = nc.tensor.matmul(ps[s][:, b, 0:GROUP * nk], qblk[s][:, 2 * hf + b, :], kblk[s][:, :, 0:nk], start=True, stop=(p == "x0"))
                        if p == "f0":
                            for b in range(2):
                                last = nc.tensor.matmul(ps[s][:, b, :], ident_bf[:], causal_bf[:].unsqueeze(1).to_broadcast([128, GROUP, TOK]), start=False, stop=True)
                        last.then_inc(pe_done, PE_L.did(f"{p}.S{hf}", s))
                        yield
                        pe.wait_ge(act_done, at(ACT_L, f"{p}.exp{hf}", s))
                        for h in range(HALF):
                            last = nc.tensor.transpose(ps[s][0:nk, h // GROUP, (h % GROUP) * TOK:(h % GROUP + 1) * TOK], prob[s][:, h * nk:(h + 1) * nk], ident[:])
                        last.then_inc(pe_done, PE_L.did(f"{p}.PT{hf}", s))
                        yield
                        pe.wait_ge(act_done, at(ACT_L, f"{p}.PT{hf}", s))
                        for h in range(HALF):
                            g, j = h // GROUP, h % GROUP
                            last = nc.tensor.matmul(ps[s][VPAD * j:VPAD * (j + 1), 0, g * TOK:(g + 1) * TOK], vaug[s][0:nk, HALF * hf + h, :], probT[s][0:nk, h * TOK:(h + 1) * TOK],
                                                    start=True, stop=True, tile_position=(0, VPAD * j))
                        last.then_inc(pe_done, PE_L.did(f"{p}.PV{hf}", s))
                        yield
                    pe.wait_ge(act_done, at(ACT_L, f"{p}.yg1", s))
                    for g in range(GROUP):
                        last = nc.tensor.transpose(ps[s][:, 1, g * TOK:(g + 1) * TOK], yg[s][:, g, :], ident[:])
                    last.then_inc(pe_done, PE_L.did(f"{p}.ygT", s))
                    yield
                    pe.wait_ge(dve_done, at(DVE_L, f"{p}.y", s))
                    nc.tensor.transpose(ps[s][:, 1, 0:TOK], y[s][:], ident[:]).then_inc(pe_done, PE_L.did(f"{p}.yT", s))
                    yield
                    pe.wait_ge(act_done, at(ACT_L, f"{p}.yT", s))
                    nc.tensor.matmul(ps[s][:, 0, 0:DIM], yT[s][:], w_out, start=True, stop=True).then_inc(pe_done, PE_L.did(f"{p}.o", s))
                    yield

                def gate_and_value(pair, e):
                    for c in range(CHUNKS0):
                        u = e * CHUNKS0 + c
                        if u == 0:
                            pe.wait_ge(act_done, at(ACT_L, "f0c.xT", pair[1]))
                        if u < 3:
                            pe.wait_ge(dve_done, at(DVE_L, "moe.pick", pair[u // 2]))
                        else:
                            pe.wait_ge(dve_done, at(DVE_L, f"moe.act{(u - 3) // CHUNKS0}.{(u - 3) % CHUNKS0}", pair[0]))
                        for v in range(2):
                            last = nc.tensor.matmul(unit_bank(pair, u)[:, v * PAIR * TOK:(v + 1) * PAIR * TOK], w_gv0[:, e, v * FF0 + c * CH:v * FF0 + (c + 1) * CH],
                                                    xnT_4[:, pair[0]:pair[0] + PAIR, :].rearrange("p s t -> p (s t)"), start=True, stop=True)
                        last.then_inc(pe_done, PE_L.did(f"moe.gv{e}.{c}", pair[0]))
                        yield

                def down(pair, e):
                    for n, s in enumerate(pair):
                        if n == 0:
                            pe.wait_ge(dve_done, at(DVE_L, f"moe.act{e}.{CHUNKS0 - 1}", pair[0]))
                            pe.wait_ge(dve_done, at(DVE_L, *(("moe.pick", pair[1]) if e == 0 else (f"moe.add{e - 1}.1", pair[0]))))
                        for c in range(CHUNKS0):
                            last = nc.tensor.matmul(ps[pair[1]][:, 1, n * DIM:(n + 1) * DIM], hidden(pair, e, c)[:, n * TOK:(n + 1) * TOK], w_dn0[:, e, c, :], start=(c == 0), stop=(c == CHUNKS0 - 1))
                        last.then_inc(pe_done, PE_L.did(f"moe.down{e}.{n}", pair[0]))
                        yield

                def first_half(s, rnd):
                    yield from transpose_xn(s, "x0")
                    pe.wait_ge(act_done, at(ACT_L, "x0.xT", s))
                    nc.tensor.matmul(ps[s][:, 0, 0:TOK], w_xa0[:, 0, :], xnT[s][:], start=True, stop=True)
                    nc.tensor.matmul(ps[s][:, 0, 128:128 + KEYS], w_xa0[:, 1, :], cxT[s][:], start=True, stop=True)
                    nc.tensor.matmul(ps[s][0:KEYS, 0, 256:256 + DIM], cxT[s][:], w_xa0[:, 2, :], start=True, stop=True).then_inc(pe_done, PE_L.did("x0.qkv", s))
                    yield
                    yield from heads(s, "x0", KEYS, w_xa0[:, 3, :])
                    yield from transpose_xn(s, "f0b")
                    pe.wait_ge(dve_done, at(DVE_L, "f0.conv0", s))
                    for n in range(4):
                        nc.tensor.matmul(ps[s][:, 0, n * TOK:(n + 1) * TOK], w_at0[:, n, :], yT[s][:], start=True, stop=True)
                    nc.tensor.matmul(ps[s][:, 1, 0:DIM], yT[s][:], w_at0[:, 4, :], start=True, stop=True).then_inc(pe_done, PE_L.did("f0.qkv", s))
                    yield
                    yield from heads(s, "f0", TOK, w_pr0[:])

                def second_half(s, rnd):
                    yield from transpose_xn(s, "f0c")
                    pe.wait_ge(act_done, at(ACT_L, "f0c.xT", s))
                    nc.tensor.matmul(ps[s][:, 1, 0:MOE0], xnT[s][:], w_ro0[:], start=True, stop=True).then_inc(pe_done, PE_L.did("moe.route", s))
                    yield
                    if s % PAIR == 0:
                        pair = (s, s + 1)
                        yield from gate_and_value(pair, 0)
                        for e in range(MOE0):
                            if e + 1 < MOE0:
                                yield from gate_and_value(pair, e + 1)
                            yield from down(pair, e)
                    yield from transpose_xn(s, "x1")
                    pe.wait_ge(act_done, at(ACT_L, "x1.xT", s))
                    nc.tensor.matmul(ps[s][:, 0, 0:TOK], w_xa1[:, 0, :], xnT[s][:], start=True, stop=True)
                    nc.tensor.matmul(ps[s][:, 0, 128:128 + KEYS], w_xa1[:, 1, :], cxT[s][:], start=True, stop=True)
                    nc.tensor.matmul(ps[s][0:KEYS, 0, 256:256 + DIM], cxT[s][:], w_xa1[:, 2, :], start=True, stop=True).then_inc(pe_done, PE_L.did("x1.qkv", s))
                    yield
                    pe.wait_ge(act_done, at(ACT_L, "x1.qkv", s))
                    nc.tensor.matmul(ps[s][:, 1, 0:KEYS], qT[s][:], kT[s][:, 0:KEYS], start=True, stop=True).then_inc(pe_done, PE_L.did("x1.S", s))
                    yield
                    pe.wait_ge(act_done, at(ACT_L, "x1.exp", s))
                    nc.tensor.transpose(ps[s][0:KEYS, 0, 0:TOK], prob[s][:, 0:KEYS], ident[:]).then_inc(pe_done, PE_L.did("x1.PT", s))
                    yield
                    pe.wait_ge(act_done, at(ACT_L, "x1.PT", s))
                    nc.tensor.matmul(ps[s][:, 1, 0:DIM], probT[s][0:KEYS, 0:TOK], y[s][0:KEYS, :], start=True, stop=True).then_inc(pe_done, PE_L.did("x1.y", s))
                    yield
                    pe.wait_ge(dve_done, at(DVE_L, "f1.xq", s))
                    nc.tensor.transpose(ps[s][:, 0, 0:TOK], xn[s][:], ident[:]).then_inc(pe_done, PE_L.did("f1.T", s))
                    yield
                    pe.wait_ge(act_done, at(ACT_L, "f1.xT", s))
                    for c in range(FF1 // CH):
                        last = nc.tensor.matmul(ps[s][:, 0, c * TOK:(c + 1) * TOK], w_up1[:, c * CH:(c + 1) * CH], xnT[s][:], start=True, stop=True)
                    last.then_inc(pe_done, PE_L.did("f1.up", s))
                    yield
                    pe.wait_ge(dve_done, at(DVE_L, "f1.silu", s))
                    for c in range(FF1 // CH):
                        last = nc.tensor.transpose(ps[s][:, 0, c * CH:(c + 1) * CH], prob[s][:, c * TOK:(c + 1) * TOK], ident[:])
                    last.then_inc(pe_done, PE_L.did("f1.uT", s))
                    yield
                    pe.wait_ge(dve_done, at(DVE_L, "f1.uq", s))
                    for c in range(FF1 // CH):
                        last = nc.tensor.transpose(ps[s][:, 1, 0:256].bitcast(BF16)[:, c * TOK:(c + 1) * TOK], probT[s][:, 0:256].bitcast(BF16)[:, c * CH:(c + 1) * CH], ident_bf[:])
                    last.then_inc(pe_done, PE_L.did("f1.uqT", s))
                    yield
                    pe.wait_ge(act_done, at(ACT_L, "f1.uqT", s))
                    for c in range(FF1 // CH):
                        last = nc.tensor.matmul(ps[s][:, 0, 0:DIM], probT[s][:, 256:512].bitcast(BF16)[:, c * TOK:(c + 1) * TOK], w_dn1_q[:, c, :], start=(c == 0), stop=(c == FF1 // CH - 1))
                    last.then_inc(pe_done, PE_L.did("f1.down", s))
                    yield
                    yield from transpose_xn(s, "x2")
                    pe.wait_ge(act_done, at(ACT_L, "x2.xT", s))
                    nc.tensor.matmul(ps[s][:, 1, 0:KEYS], qT[s][:], cxT[s][:], start=True, stop=True)
                    nc.tensor.matmul(ps[s][:, 1, 80:81], xnT[s][:], sim_col[:, 0:1], start=True, stop=True).then_inc(pe_done, PE_L.did("x2.S", s))
                    yield
                    pe.wait_ge(dve_done, at(DVE_L, "x2.P", s))
                    nc.tensor.transpose(ps[s][0:KEYS, 0, 0:TOK], prob[s][:, 0:KEYS], ident[:])
                    nc.tensor.transpose(ps[s][0:1, 0, 128:128 + TOK], col[s][:, 19:20], ident[:]).then_inc(pe_done, PE_L.did("x2.PT", s))
                    yield
                    pe.wait_ge(dve_done, at(DVE_L, "x2.M", s))
                    nc.tensor.matmul(ps[s][:, 0, 256:257], ones[0:1, :], col[s][0:1, 20:21], start=True, stop=True).then_inc(pe_done, PE_L.did("x2.M", s))
                    yield
                    pe.wait_ge(act_done, at(ACT_L, "x2.p", s))
                    nc.tensor.matmul(ps[s][:, 1, 0:1], xn[s][:], col[s][:, 22:23], start=True, stop=True)
                    nc.tensor.matmul(ps[s][:, 1, 2:3], ones[:], col[s][:, 22:23], start=True, stop=True)
                    nc.tensor.matmul(ps[s][:, 0, 0:TOK], cx[s][:], probT[s][0:KEYS, 0:TOK], start=True, stop=True).then_inc(pe_done, PE_L.did("x2.hq", s))
                    yield
                    pe.wait_ge(act_done, at(ACT_L, "x2.feat", s))
                    pe.wait_ge(dve_done, at(DVE_L, "x2.ehq", s))
                    for n, f in enumerate((xnT, kT, qT, yT)):
                        last = nc.tensor.matmul(ps[s][:, 1, 0:DIM], f[s][:], w_qv2[:, n, :], start=(n == 0), stop=(n == 3))
                    last.then_inc(pe_done, PE_L.did("x2.out", s))
                    yield
                    yield from transpose_xn(s, "f2")

                return first_half, second_half

            take_turns(PE_0, [program(0, 0)[0](s, 0) for s in A])
            pe.wait_ge(pe_done, PE_0.per_round)
            pe.sem_inc(pe_done, PE_1.per_round - PE_0.per_round)
            with pe.Fori(0, ROUNDS) as r:
                first_half, second_half = program(1, r)
                take_turns(PE_1, [chain(second_half(s, r), first_half(s, r + 1)) for s in A] + [chain(first_half(s, r), second_half(s, r)) for s in B])

        @block.vector
        def _(dve):
            dve.wait_ge(weights_in, 16 * len(weight_loads))
            nc.vector.tensor_copy(causal_bf[:], prob[0][:, 0:128]).then_inc(setup_dve, 1)
            nc.vector.tensor_copy(ident_bf[:], ident[:]).then_inc(setup_dve, 1)
            flat = w_dn1[:].rearrange("p k n -> p (k n)")
            nc.vector.tensor_reduce(prep[:, 0:1], w_up1[:], X_AXIS, ALU.add, apply_absolute_value=True).then_inc(setup_dve, 1)
            nc.vector.tensor_reduce(prep[:, 1:2], flat, X_AXIS, ALU.add, apply_absolute_value=True).then_inc(setup_dve, 1)
            dve.wait_ge(setup_pe, 2)
            nc.vector.tensor_scalar(prep[:, 2:4], ps[3][:, 0, 0:2], 1.0 / (FF1 * DIM), 1e-5, ALU.mult, ALU.max).then_inc(setup_dve, 1)
            dve.wait_ge(setup_dve, 5)
            nc.vector.reciprocal(prep[:, 4:6], prep[:, 2:4]).then_inc(setup_dve, 1)
            dve.wait_ge(setup_dve, 6)
            for n, (w, out) in enumerate(((w_up1[:], w_up1[:]), (flat, w_dn1_q[:].rearrange("p k n -> p (k n)")))):
                nc.vector.tensor_scalar(w, w, prep[:, 4 + n:5 + n], ROUND, ALU.mult, ALU.add).then_inc(setup_dve, 1)
                dve.wait_ge(setup_dve, 7 + 3 * n)
                nc.vector.tensor_scalar(w, w, ROUND, 1.0, ALU.subtract, ALU.min).then_inc(setup_dve, 1)
                dve.wait_ge(setup_dve, 8 + 3 * n)
                if n == 0:
                    nc.vector.tensor_scalar(out, w, -1.0, prep[:, 2:3], ALU.max, ALU.mult).then_inc(setup_dve, 1)
                else:
                    nc.vector.tensor_scalar(out, w, -1.0, None, ALU.max).then_inc(setup_dve, 1)
                dve.wait_ge(setup_dve, 9 + 3 * n)
            nc.vector.tensor_scalar(prep[:, 6:7], prep[:, 3:4], 1.0 / 127.0, None, ALU.mult).then_inc(setup_dve, 1)

            def next_mask(s, b, made):
                nc.vector.tensor_copy(attended[s][:], mask[:, bass.ds(b * KEYS, KEYS)]).then_inc(mask_made[s], 1)
                dve.wait_ge(mask_made[s], made)
                nc.vector.tensor_scalar(thr[s][:], attended[s][:], 1e9, -1e9, ALU.mult, ALU.add).then_inc(mask_ready[s], 1)

            nc.vector.memset(mask_words[:, BATCH * KEYS // 4:], 0).then_inc(mask_tail, 1)
            dve.wait_ge(mask_tail, 1)
            for s in S:
                next_mask(s, s, 1)
            def program(k, it):
                PE_L, ACT_L, DVE_L, POOL_L = LISTS[k]

                def at(steps_, name, s):
                    return steps_.value(name, s, it)

                def after(name, s):
                    dve.wait_ge(dve_done, at(DVE_L, name, s))

                def norm(s, p, src, dst, prev=None, ready=None):
                    if ready is not None:
                        ready(s)
                    else:
                        after(prev, s)
                    nc.vector.bn_stats(col[s][:, 0:6], src[s][:]).then_inc(dve_done, DVE_L.did(f"{p}.stats", s))
                    yield
                    after(f"{p}.stats", s)
                    dve.sem_inc(passed, 1)
                    nc.vector.bn_aggr(col[s][:, 6:8], col[s][:, 0:6]).then_inc(dve_done, DVE_L.did(f"{p}.aggr", s))
                    yield
                    after(f"{p}.aggr", s)
                    nc.vector.tensor_scalar(col[s][:, 8:9], col[s][:, 7:8], LN_EPS, None, ALU.add).then_inc(dve_done, DVE_L.did(f"{p}.eps", s))
                    yield
                    dve.wait_ge(pool_done, at(POOL_L, f"{p}.rstd", s))
                    nc.vector.tensor_scalar(dst[s][:], src[s][:], col[s][:, 6:7], col[s][:, 9:10], ALU.subtract, ALU.mult).then_inc(dve_done, DVE_L.did(f"{p}.norm", s))
                    yield

                def heads(s, p, nk, rnd):
                    for hf in range(2):
                        if p == "x0":
                            dve.wait_ge(pe_done, at(PE_L, f"{p}.S{hf}", s))
                            dve.wait_ge(bias_ready[s], rnd + 1)
                            nc.vector.tensor_tensor(prob[s][:, 0:HALF * nk].rearrange("p (b n) -> p b n", b=2), ps[s][:, :, 0:GROUP * nk],
                                                    bias_m[s][:, HALF * hf:HALF * (hf + 1), :].rearrange("p (b h) k -> p b (h k)", b=2), ALU.add).then_inc(dve_done, DVE_L.did(f"{p}.add{hf}", s))
                            yield
                        if p == "x0":
                            if hf == 1:
                                next_mask(s, (rnd + 1) * STREAMS + s, rnd + 2)
                            after(f"{p}.add{hf}", s)
                            scores = prob[s][:, 0:HALF * nk].rearrange("p (h k) -> p h k", h=HALF)
                        else:
                            dve.wait_ge(pe_done, at(PE_L, f"{p}.S{hf}", s))
                            scores = ps[s][:].rearrange("p b (h k) -> p (b h) k", h=GROUP)
                        nc.vector.tensor_reduce(col[s][:, 16:16 + HALF], scores, X_AXIS, ALU.max).then_inc(dve_done, DVE_L.did(f"{p}.max{hf}", s))
                        yield
                        after(f"{p}.max{hf}", s)
                        out = prob[s][:, 0:HALF * nk].rearrange("p (h k) -> p h k", h=HALF)
                        scores = out if p == "x0" else ps[s][:].rearrange("p b (h k) -> p (b h) k", h=GROUP)
                        nc.vector.tensor_tensor(out, scores, col[s][:, 16:16 + HALF].unsqueeze(2).to_broadcast([128, HALF, nk]), ALU.subtract).then_inc(dve_done, DVE_L.did(f"{p}.sub{hf}", s))
                        yield
                    dve.wait_ge(pe_done, at(PE_L, f"{p}.ygT", s))
                    out = ps[s][:, 1, :].rearrange("p (h e) -> p h e", h=HEADS)
                    nc.vector.reciprocal(col[s][:, 24:24 + HEADS].unsqueeze(2), out[:, :, HDIM:HDIM + 1]).then_inc(dve_done, DVE_L.did(f"{p}.rden", s))
                    yield
                    after(f"{p}.rden", s)
                    out = ps[s][:, 1, :].rearrange("p (h e) -> p h e", h=HEADS)
                    nc.vector.tensor_tensor(y[s][:].rearrange("p (h e) -> p h e", h=HEADS), out[:, :, 0:HDIM],
                                            col[s][:, 24:24 + HEADS].unsqueeze(2).to_broadcast([128, HEADS, HDIM]), ALU.mult).then_inc(dve_done, DVE_L.did(f"{p}.y", s))
                    yield

                def add_expert(pair, e):
                    for n, s in enumerate(pair):
                        if n == 0:
                            dve.wait_ge(pe_done, at(PE_L, f"moe.down{e}.1", pair[0]))
                        if e == MOE0 - 1:
                            after(f"moe.add{e - 1}.{n}", pair[0])
                        nc.vector.scalar_tensor_tensor(h0[s][:], ps[pair[1]][:, 1, n * DIM:(n + 1) * DIM], col[s][:, 24 + e:25 + e], h0[s][:], ALU.mult, ALU.add).then_inc(dve_done, DVE_L.did(f"moe.add{e}.{n}", pair[0]))
                        yield

                def first_half(s, rnd):
                    yield from norm(s, "x0", x, xn, ready=lambda s: dve.wait_ge(inputs_ready[s], rnd + 1))
                    dve.wait_ge(act_done, at(ACT_L, "x0.qv", s))
                    nc.vector.tensor_tensor(kT[s][:, 0:KEYS], ps[s][:, 0, 128:128 + KEYS], attended[s][:], ALU.mult).then_inc(dve_done, DVE_L.did("x0.kT", s))
                    yield
                    after("x0.kT", s)
                    nc.vector.tensor_tensor(kblk[s][:, :, 0:KEYS], kT[s][:, 0:KEYS].unsqueeze(1).to_broadcast([128, GROUP, KEYS]),
                                            ingroup[:].unsqueeze(2).to_broadcast([128, GROUP, KEYS]), ALU.mult).then_inc(dve_done, DVE_L.did("x0.kblk", s))
                    yield
                    yield from heads(s, "x0", KEYS, rnd)
                    dve.wait_ge(pe_done, at(PE_L, "x0.o", s))
                    nc.vector.tensor_tensor(x[s][:], ps[s][:, 0, 0:DIM], x[s][:], ALU.add).then_inc(dve_done, DVE_L.did("x0.x", s))
                    yield
                    yield from norm(s, "f0a", x, h0, "x0.x")
                    yield from norm(s, "f0b", h0, xn, "f0a.norm")
                    for n, (name, tap) in enumerate((("f0.conv2", 2), ("f0.conv1", 1), ("f0.conv0", 0))):
                        if tap == 2:
                            dve.wait_ge(act_done, at(ACT_L, "f0b.xT", s))
                            nc.vector.tensor_scalar(yT[s][:], xnT[s][:], conv0_col[:, 2:3], None, ALU.mult).then_inc(dve_done, DVE_L.did(name, s))
                            yield
                        else:
                            after(f"f0.conv{tap + 1}", s)
                            sh = 2 - tap
                            nc.vector.scalar_tensor_tensor(yT[s][:, sh:], xnT[s][:, 0:TOK - sh], conv0_col[:, tap:tap + 1], yT[s][:, sh:], ALU.mult, ALU.add).then_inc(dve_done, DVE_L.did(name, s))
                            yield
                    dve.wait_ge(pe_done, at(PE_L, "f0.qkv", s))
                    nc.vector.tensor_tensor(prob[s][:, 0:BANK].rearrange("p (n t) -> p n t", n=4), ps[s][:, 0, :].rearrange("p (n t) -> p n t", n=4), rope[:], ALU.mult).then_inc(dve_done, DVE_L.did("f0.rope", s))
                    yield
                    after("f0.rope", s)
                    nc.vector.tensor_tensor(qT[s][:], prob[s][:, 0:128], prob[s][:, 256:384], ALU.add)
                    nc.vector.tensor_tensor(kT[s][:], prob[s][:, 128:256], prob[s][:, 384:512], ALU.add).then_inc(dve_done, DVE_L.did("f0.qk", s))
                    yield
                    after("f0.qk", s)
                    nc.vector.tensor_tensor(kblk[s][:], kT[s][:].unsqueeze(1).to_broadcast([128, GROUP, TOK]),
                                            ingroup[:].unsqueeze(2).to_broadcast([128, GROUP, TOK]), ALU.mult).then_inc(dve_done, DVE_L.did("f0.kblk", s))
                    yield
                    yield from heads(s, "f0", TOK, rnd)
                    dve.wait_ge(pe_done, at(PE_L, "f0.o", s))
                    nc.vector.tensor_tensor(h0[s][:], ps[s][:, 0, 0:DIM], h0[s][:], ALU.add).then_inc(dve_done, DVE_L.did("f0.x", s))
                    yield

                def second_half(s, rnd):
                    yield from norm(s, "f0c", h0, xn, ready=lambda s: dve.wait_ge(dve_done, (DVE_L.value_before if s in A else DVE_L.value)("f0.x", s, it)))
                    dve.wait_ge(pe_done, at(PE_L, "moe.route", s))
                    nc.vector.tensor_reduce(col[s][:, 16:17], ps[s][:, 1, 0:MOE0], X_AXIS, ALU.max).then_inc(dve_done, DVE_L.did("moe.max", s))
                    yield
                    after("moe.max", s)
                    nc.vector.scalar_tensor_tensor(col[s][:, 20:24], ps[s][:, 1, 0:MOE0], col[s][:, 16:17], first[:, 0:MOE0], ALU.is_equal, ALU.mult).then_inc(dve_done, DVE_L.did("moe.eq", s))
                    yield
                    after("moe.eq", s)
                    nc.vector.tensor_reduce(col[s][:, 17:18], col[s][:, 20:24], X_AXIS, ALU.max).then_inc(dve_done, DVE_L.did("moe.first", s))
                    yield
                    after("moe.first", s)
                    nc.vector.tensor_scalar(col[s][:, 24:28], col[s][:, 20:24], col[s][:, 17:18], None, ALU.is_equal).then_inc(dve_done, DVE_L.did("moe.pick", s))
                    yield
                    if s % PAIR == 0:
                        pair = (s, s + 1)
                        for e in range(MOE0):
                            for c in range(CHUNKS0):
                                bank = unit_bank(pair, e * CHUNKS0 + c)
                                dve.wait_ge(act_done, at(ACT_L, f"moe.tanh{e}.{c}", pair[0]))
                                nc.vector.scalar_tensor_tensor(hidden(pair, e, c), hidden(pair, e, c), 1.0, bank[:, 0:PAIR * TOK], ALU.add, ALU.mult).then_inc(dve_done, DVE_L.did(f"moe.silu{e}.{c}", pair[0]))
                                yield
                                dve.wait_ge(dve_done, at(DVE_L, f"moe.silu{e}.{c}", pair[0]))
                                nc.vector.scalar_tensor_tensor(hidden(pair, e, c), hidden(pair, e, c), 0.5, bank[:, PAIR * TOK:], ALU.mult, ALU.mult).then_inc(dve_done, DVE_L.did(f"moe.act{e}.{c}", pair[0]))
                                yield
                            if e >= 1:
                                yield from add_expert(pair, e - 1)
                        yield from add_expert(pair, MOE0 - 1)
                    after(f"moe.add{MOE0 - 1}.{s % PAIR}", s - s % PAIR)
                    nc.vector.tensor_tensor(x[s][:], x[s][:], h0[s][:], ALU.add).then_inc(dve_done, DVE_L.did("moe.x", s))
                    yield
                    yield from norm(s, "x1", x, xn, "moe.x")
                    dve.wait_ge(pe_done, at(PE_L, "x1.S", s))
                    nc.vector.tensor_reduce(col[s][:, 16:17], ps[s][:, 1, 0:KEYS], X_AXIS, ALU.max, negate=True).then_inc(dve_done, DVE_L.did("x1.nmax", s))
                    yield
                    dve.wait_ge(act_done, at(ACT_L, "x1.exp", s))
                    nc.vector.reciprocal(col[s][:, 18:19], col[s][:, 17:18]).then_inc(dve_done, DVE_L.did("x1.rden", s))
                    yield
                    dve.wait_ge(pe_done, at(PE_L, "x1.y", s))
                    after("x1.rden", s)
                    nc.vector.scalar_tensor_tensor(x[s][:], ps[s][:, 1, 0:DIM], col[s][:, 18:19], x[s][:], ALU.mult, ALU.add).then_inc(dve_done, DVE_L.did("x1.x", s))
                    yield
                    after("x1.x", s)
                    nc.vector.tensor_tensor(x[s][:], x[s][:], bv1[:], ALU.add).then_inc(dve_done, DVE_L.did("x1.bv", s))
                    yield
                    yield from norm(s, "f1", x, xn, "x1.bv")
                    after("f1.norm", s)
                    nc.vector.tensor_reduce(col[s][:, 16:17], xn[s][:], X_AXIS, ALU.max, apply_absolute_value=True).then_inc(dve_done, DVE_L.did("f1.amax", s))
                    yield
                    after("f1.amax", s)
                    nc.vector.tensor_scalar(col[s][:, 17:18], col[s][:, 16:17], 1e-5, 1.0 / 127.0, ALU.max, ALU.mult).then_inc(dve_done, DVE_L.did("f1.inv", s))
                    yield
                    after("f1.inv", s)
                    nc.vector.reciprocal(col[s][:, 18:19], col[s][:, 17:18]).then_inc(dve_done, DVE_L.did("f1.scale", s))
                    yield
                    after("f1.scale", s)
                    nc.vector.tensor_scalar(xn[s][:], xn[s][:], col[s][:, 18:19], ROUND, ALU.mult, ALU.add).then_inc(dve_done, DVE_L.did("f1.round", s))
                    yield
                    after("f1.round", s)
                    nc.vector.tensor_scalar(xn[s][:], xn[s][:], ROUND, col[s][:, 17:18], ALU.subtract, ALU.mult).then_inc(dve_done, DVE_L.did("f1.xq", s))
                    yield
                    dve.wait_ge(act_done, at(ACT_L, "f1.mid", s))
                    for c in range(FF1 // CH):
                        a = c * TOK
                        last = nc.vector.scalar_tensor_tensor(prob[s][:, a + 1:a + TOK], ps[s][:, 0, a:a + TOK - 1], conv1_col[:, c, 0:1], prob[s][:, a + 1:a + TOK], ALU.mult, ALU.add)
                    last.then_inc(dve_done, DVE_L.did("f1.tap0", s))
                    yield
                    after("f1.tap0", s)
                    for c in range(FF1 // CH):
                        a = c * TOK
                        last = nc.vector.scalar_tensor_tensor(prob[s][:, a:a + TOK - 1], ps[s][:, 0, a + 1:a + TOK], conv1_col[:, c, 2:3], prob[s][:, a:a + TOK - 1], ALU.mult, ALU.add)
                    last.then_inc(dve_done, DVE_L.did("f1.taps", s))
                    yield
                    dve.wait_ge(act_done, at(ACT_L, "f1.tanh", s))
                    nc.vector.scalar_tensor_tensor(prob[s][:, 0:BANK], prob[s][:, BANK:2 * BANK], 1.0, prob[s][:, 0:BANK], ALU.add, ALU.mult).then_inc(dve_done, DVE_L.did("f1.silu", s))
                    yield
                    dve.wait_ge(pe_done, at(PE_L, "f1.uT", s))
                    nc.vector.tensor_reduce(col[s][:, 16:17], ps[s][:, 0, :], X_AXIS, ALU.max, apply_absolute_value=True).then_inc(dve_done, DVE_L.did("f1.uamax", s))
                    yield
                    after("f1.uamax", s)
                    nc.vector.tensor_scalar(col[s][:, 17:18], col[s][:, 16:17], 0.5, 1e-5, ALU.mult, ALU.max).then_inc(dve_done, DVE_L.did("f1.uclip", s))
                    yield
                    after("f1.uclip", s)
                    nc.vector.reciprocal(col[s][:, 18:19], col[s][:, 17:18]).then_inc(dve_done, DVE_L.did("f1.urec", s))
                    yield
                    after("f1.urec", s)
                    nc.vector.tensor_scalar(col[s][:, 19:20], col[s][:, 18:19], 127.0 / 2, None, ALU.mult)
                    nc.vector.tensor_scalar(col[s][:, 20:21], col[s][:, 17:18], prep[:, 6:7], None, ALU.mult).then_inc(dve_done, DVE_L.did("f1.uscale", s))
                    yield
                    after("f1.uscale", s)
                    nc.vector.tensor_scalar(prob[s][:, 0:BANK], ps[s][:, 0, :], col[s][:, 19:20], ROUND, ALU.mult, ALU.add).then_inc(dve_done, DVE_L.did("f1.uround", s))
                    yield
                    after("f1.uround", s)
                    nc.vector.tensor_scalar(probT[s][:, 0:256].bitcast(BF16), prob[s][:, 0:BANK], ROUND, None, ALU.subtract).then_inc(dve_done, DVE_L.did("f1.uq", s))
                    yield
                    dve.wait_ge(pe_done, at(PE_L, "f1.down", s))
                    nc.vector.scalar_tensor_tensor(x[s][:], ps[s][:, 0, 0:DIM], col[s][:, 20:21], x[s][:], ALU.mult, ALU.add).then_inc(dve_done, DVE_L.did("f1.x", s))
                    yield
                    yield from norm(s, "x2", x, xn, "f1.x")
                    dve.wait_ge(pe_done, at(PE_L, "x2.S", s))
                    nc.vector.tensor_reduce(col[s][:, 16:17], ps[s][:, 1, 0:KEYS], X_AXIS, ALU.max, negate=True).then_inc(dve_done, DVE_L.did("x2.nmax", s))
                    yield
                    after("x2.nmax", s)
                    nc.vector.scalar_tensor_tensor(col[s][:, 18:19], col[s][:, 16:17], -1.0, ps[s][:, 1, 80:81], ALU.mult, ALU.add).then_inc(dve_done, DVE_L.did("x2.smax", s))
                    yield
                    after("x2.smax", s)
                    nc.vector.tensor_scalar(col[s][:, 19:20], col[s][:, 18:19], b_sim[:], None, ALU.add).then_inc(dve_done, DVE_L.did("x2.score", s))
                    yield
                    dve.wait_ge(act_done, at(ACT_L, "x2.exp", s))
                    nc.vector.reciprocal(col[s][:, 18:19], col[s][:, 17:18]).then_inc(dve_done, DVE_L.did("x2.rden", s))
                    yield
                    after("x2.rden", s)
                    nc.vector.tensor_scalar(prob[s][:, 0:KEYS], prob[s][:, 0:KEYS], col[s][:, 18:19], None, ALU.mult).then_inc(dve_done, DVE_L.did("x2.P", s))
                    yield
                    dve.wait_ge(act_done, at(ACT_L, "x2.PT", s))
                    nc.vector.tensor_reduce(col[s][0:1, 20:21], ps[s][0:1, 0, 128:128 + TOK], X_AXIS, ALU.max).then_inc(dve_done, DVE_L.did("x2.M", s))
                    yield
                    dve.wait_ge(pe_done, at(PE_L, "x2.M", s))
                    nc.vector.tensor_scalar(col[s][:, 21:22], ps[s][:, 0, 256:257], -1.0, None, ALU.mult).then_inc(dve_done, DVE_L.did("x2.negM", s))
                    yield
                    dve.wait_ge(pe_done, at(PE_L, "x2.hq", s))
                    nc.vector.reciprocal(col[s][:, 23:24], ps[s][:, 1, 2:3]).then_inc(dve_done, DVE_L.did("x2.rsum", s))
                    yield
                    after("x2.rsum", s)
                    nc.vector.tensor_scalar(col[s][:, 24:25], ps[s][:, 1, 0:1], col[s][:, 23:24], None, ALU.mult).then_inc(dve_done, DVE_L.did("x2.hc", s))
                    yield
                    dve.wait_ge(act_done, at(ACT_L, "x2.feat", s))
                    nc.vector.tensor_tensor(qT[s][:], ps[s][:, 0, 0:TOK], xnT[s][:], ALU.mult).then_inc(dve_done, DVE_L.did("x2.ehq", s))
                    yield
                    dve.wait_ge(pe_done, at(PE_L, "x2.out", s))
                    nc.vector.tensor_tensor(x[s][:], ps[s][:, 1, 0:DIM], x[s][:], ALU.add).then_inc(dve_done, DVE_L.did("x2.add", s))
                    yield
                    after("x2.add", s)
                    nc.vector.tensor_tensor(x[s][:], x[s][:], b_qv2[:], ALU.add).then_inc(dve_done, DVE_L.did("f2.x", s))
                    yield
                    yield from norm(s, "f2", x, xn, "f2.x")

                return first_half, second_half

            take_turns(DVE_0, [program(0, 0)[0](s, 0) for s in A])
            dve.wait_ge(dve_done, DVE_0.per_round)
            dve.sem_inc(dve_done, DVE_1.per_round - DVE_0.per_round)
            with dve.Fori(0, ROUNDS) as r:
                first_half, second_half = program(1, r)
                take_turns(DVE_1, [chain(second_half(s, r), first_half(s, r + 1)) for s in A] + [chain(first_half(s, r), second_half(s, r)) for s in B])


def part_2(nc, d, shared):
    xnT_all, ident, ones, x_mid, x_mid2 = (shared[k] for k in ("xnT_all", "ident", "ones", "x_mid", "x_mid2"))
    NCH = FF2 // CH
    WIDE = NCH * TTILE
    QMAX = 32767.0
    BLOCK = 32
    NBLK = 3 * FF2 // BLOCK
    PAIR = (0, 1)
    X, UP, GATE, GATED, OUT = range(5)
    SB = TTILE // TOK
    with ExitStack() as ctx:
        def sb(name, shape, dt=F32):
            return ctx.enter_context(nc.sbuf_tensor(name, shape, dt))

        def sem(name):
            return ctx.enter_context(nc.semaphore(name))

        w_rows = sb("w_rows", [128, 3, FF2])
        w_s = sb("w_s", [128, NBLK])
        w_inv = sb("w_inv", [128, NBLK])
        wT = sb("wT", [128, 3, FF2])
        hid = sb("hid", [128, TILES, WIDE])
        stage = [sb(f"stage{n}", [128, WIDE]) for n in PAIR]
        other = [sb(f"other{n}", [128, WIDE]) for n in PAIR]
        xt = [sb(f"xt{n}", [128, SB, DIM]) for n in PAIR]
        tmax = sb("tmax", [128, 2, TILES])
        col2 = sb("stats2", [128, 8])
        scale = sb("scale", [128, 5])
        inv = sb("inv", [128, 5])
        up_gated = sb("up_gated", [128, 1])
        round_col = sb("round_col", [128, 1])
        acc = [ctx.enter_context(nc.psum_tensor(f"acc{n}", [128, NCH, BANK], F32)) for n in PAIR]
        aux = ctx.enter_context(nc.psum_tensor("aux", [128, BANK], F32))

        w_loaded, w_quantised, w_turned, scales_dve, scales_pe, x_quantised = (sem(n) for n in (
            "w_loaded", "w_quantised", "w_turned", "scales_dve", "scales_pe", "x_quantised"))
        pe_2, act_2, dve_2 = ([sem(f"{e}_2{l}") for l in "abcd"] for e in ("pe", "act", "dve"))
        passed = sem("passed2")
        x_loaded = [sem(f"x_loaded{n}") for n in PAIR]
        x_stored = [sem(f"x_stored{n}") for n in PAIR]
        PA, PB, PC, PD = (PE_2A, PE_2B, PE_2C, PE_2D)
        VA, VB, VC, VD = (DVE_2A, DVE_2B, DVE_2C, DVE_2D)
        AB, AC = (ACT_2B, ACT_2C)
        ROUNDS2 = TILES // 2

        block = ctx.enter_context(nc.Block())

        @block.sync
        def _(sp):
            sp.dma_start(w_rows[:, 0, :].rearrange("p (k i) -> p k i", k=NCH), d["L2_ffn_w_up"].rearrange("(k p) i -> p k i", p=CH)).then_inc(w_loaded, 16)
            sp.dma_start(w_rows[:, 1, :].rearrange("p (k i) -> p k i", k=NCH), d["L2_ffn_w_gate"].rearrange("(k p) i -> p k i", p=CH)).then_inc(w_loaded, 16)
            sp.dma_start(w_rows[:, 2, :], d["L2_ffn_w_down"]).then_inc(w_loaded, 16)
            for n in PAIR:
                sp.sem_inc(x_stored[n], 16)
            with sp.Fori(0, ROUNDS2) as r:
                for n in PAIR:
                    sp.wait_ge(x_stored[n], r * 16 + 16)
                    sp.dma_start(xt[n][:], x_mid[bass.ds((r * 2 + n) * SB, SB), :, :].rearrange("b t c -> t b c")).then_inc(x_loaded[n], 16)

        @block.gpsimd
        def _(pool):
            pool.wait_ge(w_loaded, 48)

        @block.tensor
        def _(pe):
            def spread(step, src):
                pe.wait_ge(scales_dve, 4 * step + 1)
                nc.tensor.transpose(aux[0:1, 0:128], src, ident[:]).then_inc(scales_pe, 1)
                pe.wait_ge(scales_dve, 4 * step + 2)
                nc.tensor.matmul(aux[:, 128:129], ones[0:1, :], col2[0:1, 1:2], start=True, stop=True).then_inc(scales_pe, 1)

            pe.sem_inc(pe_2[3], PD.per_round)
            pe.wait_ge(w_quantised, 7)
            for m in range(3):
                for k in range(NCH):
                    last = nc.tensor.transpose(acc[0][:, m, k * CH:(k + 1) * CH], w_rows[:, m, k * CH:(k + 1) * CH], ident[:])
            last.then_inc(w_turned, 1)
            spread(0, col2[:, 0:1])
            pe.wait_ge(x_quantised, 2)
            pe.wait_ge(w_turned, 2)

            def hidden(steps, sem_, m, name, r, n):
                for k in range(NCH):
                    last = nc.tensor.matmul(acc[n][:, k, :], wT[:, m, k * CH:(k + 1) * CH], xnT_all[:, bass.ds((r * 2 + n) * TTILE, TTILE)], start=True, stop=True)
                last.then_inc(sem_, steps.did(name, n))

            with pe.Fori(0, ROUNDS2) as r:
                for n in PAIR:
                    pe.wait_ge(dve_2[0], VA.value("gate", n, r - 1))
                    hidden(PA, pe_2[0], 0, "up", r, n)
                for n in PAIR:
                    pe.wait_ge(dve_2[0], VA.value("up", n, r))
                    hidden(PA, pe_2[0], 1, "gate", r, n)
            for step, src in ((1, 2), (2, 3)):
                spread(step, col2[:, src:src + 1])
            with pe.Fori(0, ROUNDS2) as r:
                for n in PAIR:
                    pe.wait_ge(act_2[1], AB.value("round", n, r - 1))
                    hidden(PB, pe_2[1], 1, "gate", r, n)
            spread(3, col2[:, 0:1])
            with pe.Fori(0, ROUNDS2) as r:
                for n in PAIR:
                    pe.wait_ge(act_2[2], AC.value("round", n, r - 1))
                    hidden(PC, pe_2[2], 0, "up", r, n)
            spread(4, col2[:, 0:1])
            with pe.Fori(0, ROUNDS2) as r:
                for n in PAIR:
                    pe.wait_ge(dve_2[3], VD.value("quant", n, r))
                    for b in range(SB):
                        for k in range(NCH):
                            last = nc.tensor.matmul(acc[n][:, 0, b * TOK:(b + 1) * TOK], stage[n][:, k * TTILE + b * TOK:k * TTILE + (b + 1) * TOK],
                                                    wT[:, 2, k * CH:(k + 1) * CH], start=(k == 0), stop=(k == NCH - 1))
                    last.then_inc(pe_2[3], PD.did("down", n))

        @block.scalar
        def _(act):
            act.sem_inc(act_2[1], AB.per_round)
            act.sem_inc(act_2[2], AC.per_round)
            act.wait_ge(scales_dve, 12)
            with act.Fori(0, ROUNDS2) as r:
                for n in PAIR:
                    act.wait_ge(dve_2[1], VB.value("gated", n, r - 1))
                    act.wait_ge(pe_2[1], PB.value("gate", n, r))
                    nc.scalar.activation(stage[n][:], acc[n][:].rearrange("p k t -> p (k t)"), ACT.Identity, scale=inv[:, GATE:GATE + 1], bias=round_col[:]).then_inc(act_2[1], AB.did("round", n))
                for n in PAIR:
                    act.wait_ge(dve_2[1], VB.value("gate", n, r))
                    nc.scalar.activation(other[n][:], stage[n][:], ACT.Tanh, scale=0.5).then_inc(act_2[1], AB.did("tanh", n))
            with act.Fori(0, ROUNDS2) as r:
                for n in PAIR:
                    act.wait_ge(dve_2[2], VC.value("product", n, r - 1))
                    act.wait_ge(pe_2[2], PC.value("up", n, r))
                    nc.scalar.activation(stage[n][:], acc[n][:].rearrange("p k t -> p (k t)"), ACT.Identity, scale=inv[:, UP:UP + 1], bias=round_col[:]).then_inc(act_2[2], AC.did("round", n))
            with act.Fori(0, ROUNDS2) as r:
                for n in PAIR:
                    act.wait_ge(dve_2[3], VD.value("add", n, r))
                    act.dma_start(x_mid2[bass.ds((r * 2 + n) * SB, SB), :, :].rearrange("b t c -> t b c"), xt[n][:]).then_inc(x_stored[n], 16)
            for n in PAIR:
                act.wait_ge(x_stored[n], 16 * ROUNDS2 + 16)

        @block.vector
        def _(dve):
            for steps, sem_ in ((VA, dve_2[0]), (VB, dve_2[1]), (VC, dve_2[2]), (VD, dve_2[3])):
                dve.sem_inc(sem_, steps.per_round)
            dve.wait_ge(w_loaded, 48)
            nc.vector.memset(round_col[:], ROUND).then_inc(w_quantised, 1)
            blocks = w_rows[:].rearrange("p m (b i) -> p (m b) i", i=BLOCK)
            per_block = [128, NBLK, BLOCK]
            nc.vector.tensor_reduce(w_s[:], blocks, X_AXIS, ALU.max, apply_absolute_value=True).then_inc(w_quantised, 1)
            dve.wait_ge(w_quantised, 2)
            nc.vector.tensor_scalar(w_s[:], w_s[:], 1.0 / 7.0, 1e-12, ALU.mult, ALU.max).then_inc(w_quantised, 1)
            dve.wait_ge(w_quantised, 3)
            nc.vector.reciprocal(w_inv[:], w_s[:]).then_inc(w_quantised, 1)
            dve.wait_ge(w_quantised, 4)
            nc.vector.tensor_tensor(blocks, blocks, w_inv[:].unsqueeze(2).to_broadcast(per_block), ALU.mult).then_inc(w_quantised, 1)
            dve.wait_ge(w_quantised, 5)
            nc.vector.tensor_scalar(blocks, blocks, ROUND, None, ALU.add).then_inc(w_quantised, 1)
            dve.wait_ge(w_quantised, 6)
            nc.vector.scalar_tensor_tensor(blocks, blocks, ROUND, w_s[:].unsqueeze(2).to_broadcast(per_block), ALU.subtract, ALU.mult).then_inc(w_quantised, 1)
            dve.wait_ge(w_turned, 1)
            nc.vector.tensor_copy(wT[:], acc[0][:, :, 0:FF2]).then_inc(w_turned, 1)

            def global_scale(step, which, part, out):
                nc.vector.tensor_reduce(out, part, X_AXIS, ALU.max, apply_absolute_value=True).then_inc(scales_dve, 1)
                dve.wait_ge(scales_pe, 2 * step + 1)
                nc.vector.tensor_reduce(col2[0:1, 1:2], aux[0:1, 0:128], X_AXIS, ALU.max).then_inc(scales_dve, 1)
                dve.wait_ge(scales_pe, 2 * step + 2)
                nc.vector.tensor_scalar(scale[:, which:which + 1], aux[:, 128:129], 1.0 / QMAX, 1e-12, ALU.mult, ALU.max).then_inc(scales_dve, 1)
                dve.wait_ge(scales_dve, 4 * step + 3)
                nc.vector.reciprocal(inv[:, which:which + 1], scale[:, which:which + 1]).then_inc(scales_dve, 1)
                dve.wait_ge(scales_dve, 4 * step + 4)

            global_scale(0, X, xnT_all[:], col2[:, 0:1])
            nc.vector.tensor_scalar(xnT_all[:], xnT_all[:], inv[:, X:X + 1], ROUND, ALU.mult, ALU.add).then_inc(x_quantised, 1)
            dve.wait_ge(x_quantised, 1)
            nc.vector.tensor_scalar(xnT_all[:], xnT_all[:], ROUND, scale[:, X:X + 1], ALU.subtract, ALU.mult).then_inc(x_quantised, 1)
            with dve.Fori(0, ROUNDS2) as r:
                for m, name in enumerate(("up", "gate")):
                    for n in PAIR:
                        dve.wait_ge(pe_2[0], PA.value(name, n, r))
                        dve.sem_inc(passed, 1)
                        nc.vector.tensor_reduce(tmax[:, m, bass.ds(r * 2 + n, 1)], acc[n][:].rearrange("p k t -> p (k t)"), X_AXIS, ALU.max, apply_absolute_value=True).then_inc(dve_2[0], VA.did(name, n))
            dve.wait_ge(dve_2[0], VA.value("gate", 1, ROUNDS2 - 1))
            global_scale(1, UP, tmax[:, 0, :], col2[:, 2:3])
            global_scale(2, GATE, tmax[:, 1, :], col2[:, 3:4])
            with dve.Fori(0, ROUNDS2) as r:
                def after(name, n):
                    dve.wait_ge(dve_2[1], VB.value(name, n, r))
                for n in PAIR:
                    dve.wait_ge(act_2[1], AB.value("round", n, r))
                    nc.vector.tensor_scalar(stage[n][:], stage[n][:], ROUND, scale[:, GATE:GATE + 1], ALU.subtract, ALU.mult).then_inc(dve_2[1], VB.did("gate", n))
                for n in PAIR:
                    dve.wait_ge(act_2[1], AB.value("tanh", n, r))
                    nc.vector.tensor_scalar(other[n][:], other[n][:], 32768.0, ROUND + 32768.0, ALU.mult, ALU.add).then_inc(dve_2[1], VB.did("sigmoid", n))
                for n in PAIR:
                    after("sigmoid", n)
                    nc.vector.tensor_scalar(other[n][:], other[n][:], ROUND, 65535.0, ALU.subtract, ALU.min).then_inc(dve_2[1], VB.did("clip", n))
                for n in PAIR:
                    after("clip", n)
                    nc.vector.scalar_tensor_tensor(hid[:, bass.ds(r * 2 + n, 1), :].rearrange("p o w -> p (o w)"), other[n][:], 1.0 / 65536.0, stage[n][:], ALU.mult, ALU.mult).then_inc(dve_2[1], VB.did("gated", n))
                for n in PAIR:
                    after("gated", n)
                    dve.sem_inc(passed, 1)
                    nc.vector.tensor_reduce(tmax[:, 0, bass.ds(r * 2 + n, 1)], hid[:, bass.ds(r * 2 + n, 1), :].rearrange("p o w -> p (o w)"), X_AXIS, ALU.max, apply_absolute_value=True).then_inc(dve_2[1], VB.did("max", n))
            dve.wait_ge(dve_2[1], VB.value("max", 1, ROUNDS2 - 1))
            global_scale(3, GATED, tmax[:, 0, :], col2[:, 0:1])
            nc.vector.tensor_tensor(up_gated[:], scale[:, UP:UP + 1], scale[:, GATED:GATED + 1], ALU.mult).then_inc(x_quantised, 1)
            dve.wait_ge(x_quantised, 3)
            with dve.Fori(0, ROUNDS2) as r:
                def after(name, n):
                    dve.wait_ge(dve_2[2], VC.value(name, n, r))
                for n in PAIR:
                    nc.vector.tensor_scalar(other[n][:], hid[:, bass.ds(r * 2 + n, 1), :].rearrange("p o w -> p (o w)"), inv[:, GATED:GATED + 1], ROUND, ALU.mult, ALU.add).then_inc(dve_2[2], VC.did("round", n))
                for n in PAIR:
                    dve.wait_ge(act_2[2], AC.value("round", n, r))
                    nc.vector.tensor_scalar(stage[n][:], stage[n][:], ROUND, up_gated[:], ALU.subtract, ALU.mult).then_inc(dve_2[2], VC.did("up", n))
                for n in PAIR:
                    after("up", n)
                    nc.vector.scalar_tensor_tensor(hid[:, bass.ds(r * 2 + n, 1), :].rearrange("p o w -> p (o w)"), other[n][:], ROUND, stage[n][:], ALU.subtract, ALU.mult).then_inc(dve_2[2], VC.did("product", n))
                for n in PAIR:
                    after("product", n)
                    dve.sem_inc(passed, 1)
                    nc.vector.tensor_reduce(tmax[:, 1, bass.ds(r * 2 + n, 1)], hid[:, bass.ds(r * 2 + n, 1), :].rearrange("p o w -> p (o w)"), X_AXIS, ALU.max, apply_absolute_value=True).then_inc(dve_2[2], VC.did("max", n))
            dve.wait_ge(dve_2[2], VC.value("max", 1, ROUNDS2 - 1))
            global_scale(4, OUT, tmax[:, 1, :], col2[:, 0:1])
            with dve.Fori(0, ROUNDS2) as r:
                for n in PAIR:
                    dve.wait_ge(pe_2[3], PD.value("down", n, r - 1))
                    nc.vector.tensor_scalar(stage[n][:], hid[:, bass.ds(r * 2 + n, 1), :].rearrange("p o w -> p (o w)"), inv[:, OUT:OUT + 1], ROUND, ALU.mult, ALU.add).then_inc(dve_2[3], VD.did("round", n))
                for n in PAIR:
                    dve.wait_ge(dve_2[3], VD.value("round", n, r))
                    nc.vector.tensor_scalar(stage[n][:], stage[n][:], ROUND, scale[:, OUT:OUT + 1], ALU.subtract, ALU.mult).then_inc(dve_2[3], VD.did("quant", n))
                for n in PAIR:
                    dve.wait_ge(pe_2[3], PD.value("down", n, r))
                    dve.wait_ge(x_loaded[n], r * 16 + 16)
                    nc.vector.tensor_tensor(xt[n][:].rearrange("p b c -> p (b c)"), acc[n][:, 0, :], xt[n][:].rearrange("p b c -> p (b c)"), ALU.add).then_inc(dve_2[3], VD.did("add", n))


def part_3(nc, d, shared):
    ident, ones, first, minus_half, x_mid2 = (shared[k] for k in ("ident", "ones", "first", "minus_half", "x_mid2"))
    S = range(STREAMS)
    CHUNKS = 4
    LAST = KEYS - CHUNKS * KT
    KPAD = (CHUNKS + 1) * KT
    ROWS = 32
    with ExitStack() as ctx:
        def sb(name, shape, dt=F32):
            return ctx.enter_context(nc.sbuf_tensor(name, shape, dt))

        def per_stream(name, shape, dt=F32):
            return [sb(f"{name}{s}", shape, dt) for s in S]

        def sem(name):
            return ctx.enter_context(nc.semaphore(name))

        before = sb("before", [128, 128])
        mask3_i = sb("mask3_i", [128, BATCH * KEYS], I32)
        mask3 = sb("mask3", [128, BATCH * KEYS + KPAD - KEYS])
        w_txt = sb("w_txt", [128, DIM])
        w_feat = sb("w_feat", [128, DIM])
        w_row = sb("w_row", [128, 2 * ROWS - 1])
        b_e = sb("b_e", [128, 1])
        w_gate = sb("w_gate", [128, 2])
        b_gate = sb("b_gate", [128, 2])
        w_route = sb("w_route", [128, MOE3])
        w_exp = sb("w_exp", [128, MOE3, DIM])
        b_exp = sb("b_exp", [1, MOE3 * DIM])

        x_in = per_stream("x_in3", [128, DIM])
        ctx_in = per_stream("ctx_in3", [KEYS, DIM])
        ctxT_in = per_stream("ctxT_in3", [128, KEYS])
        x = per_stream("x3", [128, DIM])
        cx = per_stream("cx3", [KEYS, DIM])
        cxT = per_stream("cxT3", [128, KEYS])
        xn = per_stream("xn3", [128, DIM])
        xnT = per_stream("xnT3", [128, TOK])
        txt = per_stream("txt3", [128, KEYS])
        feat = per_stream("feat3", [128, TOK])
        th = per_stream("th3", [128, KT, TOK])
        th_last = per_stream("th_last3", [128, KT, TOK])
        prob = per_stream("prob3", [128, KPAD])
        probT = per_stream("probT3", [KEYS, TOK])
        hT = per_stream("hT3", [128, TOK])
        col = per_stream("col3", [128, 72])
        taken = per_stream("taken3", [128, MOE3])
        carry = sb("carry3", [128, MOE3])
        ps = [ctx.enter_context(nc.psum_tensor(f"ps3{s}", [128, 2, BANK], F32)) for s in S]

        weights_in, ready3, mask_set, zeros_set, carried = (sem(n) for n in ("weights_in3", "ready3", "mask_set", "zeros_set", "carried"))
        loads_in = [sem(f"loads_in3{s}") for s in S]
        stores_out = [sem(f"stores_out3{s}") for s in S]
        inputs_ready = sem("inputs_ready3")
        passed = sem("passed3")
        pe_done, act_done, dve_done, pool_done = (sem(n) for n in ("pe_done3", "act_done3", "dve_done3", "pool_done3"))

        weight_loads = [
            (before[:], d["before"]), (mask3_i[:], d["mask_BxS2_ik0"].to_broadcast([128, BATCH * KEYS])),
            (w_txt[:], d["L3_xattn_Ws"]), (w_feat[:], d["L3_xattn_W"]), (w_row[:, ROWS - 1:ROWS], d["L3_xattn_w"]), (b_e[:], d["L3_xattn_b"]),
            (w_gate[:, 0:1], d["L3_xattn_Wcw"]), (w_gate[:, 1:2], d["L3_xattn_Wcb"]),
            (b_gate[:, 0:1], d["L3_xattn_bcw"].to_broadcast([128, 1])), (b_gate[:, 1:2], d["L3_xattn_bcb"].to_broadcast([128, 1])),
            (w_route[:], d["L3_ffn_wg"]), (w_exp[:], d["L3_ffn_W"].rearrange("e h f -> h e f")), (b_exp[:], d["L3_ffn_b"]),
        ]
        block = ctx.enter_context(nc.Block())

        @block.sync
        def _(sp):
            def load(s, b):
                sp.dma_start(x_in[s][:], x_mid2[bass.ds(b, 1), :, :].rearrange("o t c -> t (o c)")).then_inc(loads_in[s], 16)
                sp.dma_start(ctx_in[s][:], d["ctx"][bass.ds(b, 1), :, :].rearrange("o t c -> t (o c)")).then_inc(loads_in[s], 16)
                sp.dma_start(ctxT_in[s][:], d["ctxT"][bass.ds(b, 1), :, :].rearrange("o t c -> t (o c)")).then_inc(loads_in[s], 16)

            for s in S:
                load(s, s)
            sp.wait_ge(ready3, 1)
            for dst, src in weight_loads:
                sp.dma_start(dst, src).then_inc(weights_in, 16)
            with sp.Fori(0, ROUNDS - 1) as r:
                for s in S:
                    sp.wait_ge(inputs_ready, r * STREAMS + s + 1)
                    load(s, r * STREAMS + (STREAMS + s))

        @block.gpsimd
        def _(pool):
            def take_inputs(s, value):
                pool.wait_ge(loads_in[s], value)
                pool.sem_inc(passed, 1)
                nc.gpsimd.tensor_copy(x[s][:], x_in[s][:])
                nc.gpsimd.tensor_copy(cx[s][:], ctx_in[s][:])
                nc.gpsimd.tensor_copy(cxT[s][:], ctxT_in[s][:]).then_inc(inputs_ready, 1)

            def steps(r):
                for p in ("x3", "f3"):
                    for s in S:
                        pool.wait_ge(dve_done, DVE_3.value(f"{p}.eps", s, r))
                        nc.gpsimd.tensor_tensor(col[s][:, 9:10], col[s][:, 8:9], minus_half[:], ALU.pow).then_inc(pool_done, POOL_3.did(f"{p}.rstd", s))

            nc.gpsimd.memset(w_row[:], 0.0).then_inc(ready3, 1)
            nc.gpsimd.memset(mask3[:, BATCH * KEYS:], 0.0)
            for s in S:
                last = nc.gpsimd.memset(th_last[s][:], 0.0)
            last.then_inc(zeros_set, 1)
            for s in S:
                take_inputs(s, 48)
            with pool.Fori(0, ROUNDS - 1) as r:
                steps(r)
                for s in S:
                    pool.wait_ge(stores_out[s], r * 16 + 16)
                    take_inputs(s, r * 48 + 96)
            steps(ROUNDS - 1)

        @block.scalar
        def _(act):
            act.wait_ge(weights_in, 16 * len(weight_loads))
            act.wait_ge(zeros_set, 1)
            with act.Fori(0, ROUNDS) as r:
                def at(steps_, name, s):
                    return steps_.value(name, s, r)

                def xT(p):
                    for s in S:
                        act.wait_ge(pe_done, at(PE_3, f"{p}.T", s))
                        nc.scalar.copy(xnT[s][:], ps[s][:, 0, 0:TOK]).then_inc(act_done, ACT_3.did(f"{p}.xT", s))

                xT("x3")
                for s in S:
                    act.wait_ge(pe_done, at(PE_3, "x3.proj", s))
                    nc.scalar.copy(txt[s][:], ps[s][:, 0, 0:KEYS])
                    nc.scalar.activation(feat[s][:], ps[s][:, 0, 128:128 + TOK], ACT.Identity, bias=b_e[:]).then_inc(act_done, ACT_3.did("x3.proj", s))
                for c in range(CHUNKS):
                    for s in S:
                        act.wait_ge(dve_done, at(DVE_3, f"x3.sum{c}", s))
                        nc.scalar.activation(th[s][:], th[s][:], ACT.Tanh).then_inc(act_done, ACT_3.did(f"x3.tanh{c}", s))
                    if c == 0:
                        for s in S:
                            act.wait_ge(act_done, at(ACT_3, "x3.proj", s))
                            for k in range(LAST):
                                last = nc.scalar.activation(th_last[s][:, k, :], feat[s][:], ACT.Tanh, bias=txt[s][:, CHUNKS * KT + k:CHUNKS * KT + k + 1])
                            last.then_inc(act_done, ACT_3.did("x3.tanh_last", s))
                for s in S:
                    act.wait_ge(pe_done, at(PE_3, f"x3.rho{CHUNKS - 1}", s))
                    nc.scalar.copy(th[s][:, 0:4, :].rearrange("p k f -> p (k f)"), ps[s][:, 1, :]).then_inc(act_done, ACT_3.did("x3.rho", s))
                for s in S:
                    act.wait_ge(dve_done, at(DVE_3, "x3.nmax", s))
                    nc.scalar.activation(prob[s][:, 0:KEYS], prob[s][:, 0:KEYS], ACT.Exp, bias=col[s][:, 16:17], accum_out=col[s][:, 17:18]).then_inc(act_done, ACT_3.did("x3.exp", s))
                for s in S:
                    act.wait_ge(pe_done, at(PE_3, "x3.PT", s))
                    nc.scalar.copy(probT[s][:], ps[s][0:KEYS, 0, 0:TOK]).then_inc(act_done, ACT_3.did("x3.PT", s))
                for s in S:
                    act.wait_ge(pe_done, at(PE_3, "x3.h", s))
                    nc.scalar.copy(hT[s][:], ps[s][:, 0, 0:TOK]).then_inc(act_done, ACT_3.did("x3.h", s))
                for s in S:
                    act.wait_ge(dve_done, at(DVE_3, "x3.gb", s))
                    nc.scalar.activation(col[s][:, 20:22], col[s][:, 18:20], ACT.Tanh).then_inc(act_done, ACT_3.did("x3.gate", s))
                xT("f3")
                for s in S:
                    act.wait_ge(dve_done, at(DVE_3, "f3.nmax", s))
                    nc.scalar.activation(col[s][:, 24:32], ps[s][:, 1, 0:MOE3], ACT.Exp, bias=col[s][:, 16:17], accum_out=col[s][:, 17:18]).then_inc(act_done, ACT_3.did("f3.exp", s))
                for s in S:
                    act.wait_ge(dve_done, at(DVE_3, f"f3.add{MOE3 - 1}", s))
                    act.dma_start(d["out"][bass.ds(r * STREAMS + s, 1), :, :].rearrange("o t c -> t (o c)"), x[s][:]).then_inc(stores_out[s], 16)
            for s in S:
                act.wait_ge(stores_out[s], 16 * ROUNDS)

        @block.tensor
        def _(pe):
            pe.wait_ge(weights_in, 16 * len(weight_loads))
            with pe.Fori(0, ROUNDS) as r:
                def at(steps_, name, s):
                    return steps_.value(name, s, r)

                def transpose_xn(p):
                    for s in S:
                        pe.wait_ge(dve_done, at(DVE_3, f"{p}.norm", s))
                        nc.tensor.transpose(ps[s][:, 0, 0:TOK], xn[s][:], ident[:]).then_inc(pe_done, PE_3.did(f"{p}.T", s))

                transpose_xn("x3")
                for s in S:
                    pe.wait_ge(act_done, at(ACT_3, "x3.xT", s))
                    nc.tensor.matmul(ps[s][:, 0, 0:KEYS], w_txt[:], cxT[s][:], start=True, stop=True)
                    nc.tensor.matmul(ps[s][:, 0, 128:128 + TOK], w_feat[:], xnT[s][:], start=True, stop=True).then_inc(pe_done, PE_3.did("x3.proj", s))
                def rho(a, tanh, s, start, stop):
                    for b in range(4):
                        last = nc.tensor.matmul(ps[s][ROWS * b:ROWS * (b + 1), 1, :], w_row[:, ROWS - 1 - a:2 * ROWS - 1 - a],
                                                tanh[:, 4 * b:4 * b + 4, :], start=start, stop=stop, tile_position=(0, ROWS * b))
                    return last

                for c in range(CHUNKS):
                    for s in S:
                        pe.wait_ge(act_done, at(ACT_3, f"x3.tanh{c}", s))
                        rho(c, th[s], s, c == 0, c == CHUNKS - 1).then_inc(pe_done, PE_3.did(f"x3.rho{c}", s))
                    if c == 0:
                        for s in S:
                            pe.wait_ge(act_done, at(ACT_3, "x3.tanh_last", s))
                            rho(CHUNKS, th_last[s], s, False, False).then_inc(pe_done, PE_3.did("x3.rho_last", s))
                for s in S:
                    pe.wait_ge(act_done, at(ACT_3, "x3.rho", s))
                    for k in range(4):
                        last = nc.tensor.transpose(ps[s][:, 0, k * TOK:(k + 1) * TOK], th[s][:, k, :], ident[:])
                    last.then_inc(pe_done, PE_3.did("x3.rhoT", s))
                for s in S:
                    pe.wait_ge(dve_done, at(DVE_3, "x3.P", s))
                    nc.tensor.transpose(ps[s][0:KEYS, 0, 0:TOK], prob[s][:, 0:KEYS], ident[:]).then_inc(pe_done, PE_3.did("x3.PT", s))
                for s in S:
                    pe.wait_ge(act_done, at(ACT_3, "x3.PT", s))
                    nc.tensor.matmul(ps[s][:, 0, 0:TOK], cx[s][:], probT[s][:], start=True, stop=True).then_inc(pe_done, PE_3.did("x3.h", s))
                for s in S:
                    pe.wait_ge(act_done, at(ACT_3, "x3.h", s))
                    nc.tensor.matmul(ps[s][:, 1, 0:2], hT[s][:], w_gate[:], start=True, stop=True).then_inc(pe_done, PE_3.did("x3.gate", s))
                transpose_xn("f3")
                for s in S:
                    pe.wait_ge(act_done, at(ACT_3, "f3.xT", s))
                    nc.tensor.matmul(ps[s][:, 1, 0:MOE3], xnT[s][:], w_route[:], start=True, stop=True).then_inc(pe_done, PE_3.did("f3.route", s))
                for s in S:
                    pe.wait_ge(dve_done, at(DVE_3, "f3.taken", s))
                    nc.tensor.matmul(ps[s][:, 1, 16:16 + MOE3], before[:], col[s][:, 40:48], start=True, stop=False)
                    nc.tensor.matmul(ps[s][:, 1, 16:16 + MOE3], ones[:], taken[s][:], start=False, stop=True).then_inc(pe_done, PE_3.did("f3.place", s))
                for s in S:
                    pe.wait_ge(dve_done, at(DVE_3, "f3.w", s))
                    for b in range(2):
                        nc.tensor.matmul(ps[s][:, b, :], xnT[s][:], w_exp[:, b * GROUP:(b + 1) * GROUP, :], start=True, stop=False)
                        last = nc.tensor.matmul(ps[s][:, b, :], ones[0:1, :], b_exp[:, b * BANK:(b + 1) * BANK], start=False, stop=True)
                    last.then_inc(pe_done, PE_3.did("f3.y", s))

        @block.vector
        def _(dve):
            dve.wait_ge(weights_in, 16 * len(weight_loads))
            nc.vector.tensor_scalar(mask3[:, 0:BATCH * KEYS], mask3_i[:], 1e30, -1e30, ALU.mult, ALU.add).then_inc(mask_set, 1)
            nc.vector.memset(carry[:], 0.0).then_inc(carried, 1)
            dve.wait_ge(mask_set, 1)
            dve.wait_ge(zeros_set, 1)
            with dve.Fori(0, ROUNDS) as r:
                def at(steps_, name, s):
                    return steps_.value(name, s, r)

                def after(name, s):
                    dve.wait_ge(dve_done, at(DVE_3, name, s))

                def norm(p, prev):
                    for s in S:
                        if prev is None:
                            dve.wait_ge(inputs_ready, r * STREAMS + s + 1)
                        else:
                            after(prev, s)
                        nc.vector.bn_stats(col[s][:, 0:6], x[s][:]).then_inc(dve_done, DVE_3.did(f"{p}.stats", s))
                    for s in S:
                        after(f"{p}.stats", s)
                        dve.sem_inc(passed, 1)
                        nc.vector.bn_aggr(col[s][:, 6:8], col[s][:, 0:6]).then_inc(dve_done, DVE_3.did(f"{p}.aggr", s))
                    for s in S:
                        after(f"{p}.aggr", s)
                        nc.vector.tensor_scalar(col[s][:, 8:9], col[s][:, 7:8], LN_EPS, None, ALU.add).then_inc(dve_done, DVE_3.did(f"{p}.eps", s))
                    for s in S:
                        dve.wait_ge(pool_done, at(POOL_3, f"{p}.rstd", s))
                        nc.vector.tensor_scalar(xn[s][:], x[s][:], col[s][:, 6:7], col[s][:, 9:10], ALU.subtract, ALU.mult).then_inc(dve_done, DVE_3.did(f"{p}.norm", s))

                norm("x3", None)
                for c in range(CHUNKS):
                    for s in S:
                        if c == 0:
                            dve.wait_ge(act_done, at(ACT_3, "x3.proj", s))
                        else:
                            dve.wait_ge(pe_done, at(PE_3, f"x3.rho{c - 1}", s))
                        nc.vector.tensor_tensor(th[s][:], txt[s][:, c * KT:(c + 1) * KT].unsqueeze(2).to_broadcast([128, KT, TOK]),
                                                feat[s][:].unsqueeze(1).to_broadcast([128, KT, TOK]), ALU.add).then_inc(dve_done, DVE_3.did(f"x3.sum{c}", s))
                for s in S:
                    dve.wait_ge(pe_done, at(PE_3, "x3.rhoT", s))
                    nc.vector.tensor_tensor(prob[s][:].rearrange("p (a b k) -> p a b k", b=4, k=4),
                                            ps[s][:, 0, :].rearrange("p (k b a) -> p a b k", k=4, b=4)[:, 0:CHUNKS + 1, :, :],
                                            mask3[:, bass.ds((r * STREAMS + s) * KEYS, KPAD)].rearrange("p (a b k) -> p a b k", b=4, k=4), ALU.add).then_inc(dve_done, DVE_3.did("x3.mask", s))
                for s in S:
                    after("x3.mask", s)
                    nc.vector.tensor_reduce(col[s][:, 16:17], prob[s][:, 0:KEYS], X_AXIS, ALU.max, negate=True).then_inc(dve_done, DVE_3.did("x3.nmax", s))
                for s in S:
                    dve.wait_ge(act_done, at(ACT_3, "x3.exp", s))
                    nc.vector.reciprocal(col[s][:, 18:19], col[s][:, 17:18]).then_inc(dve_done, DVE_3.did("x3.rden", s))
                for s in S:
                    after("x3.rden", s)
                    nc.vector.tensor_scalar(prob[s][:, 0:KEYS], prob[s][:, 0:KEYS], col[s][:, 18:19], None, ALU.mult).then_inc(dve_done, DVE_3.did("x3.P", s))
                for s in S:
                    dve.wait_ge(pe_done, at(PE_3, "x3.gate", s))
                    nc.vector.tensor_tensor(col[s][:, 18:20], ps[s][:, 1, 0:2], b_gate[:], ALU.add).then_inc(dve_done, DVE_3.did("x3.gb", s))
                for s in S:
                    dve.wait_ge(act_done, at(ACT_3, "x3.gate", s))
                    nc.vector.tensor_scalar(xn[s][:], xn[s][:], col[s][:, 20:21], col[s][:, 21:22], ALU.mult, ALU.add).then_inc(dve_done, DVE_3.did("x3.y", s))
                for s in S:
                    after("x3.y", s)
                    nc.vector.tensor_tensor(x[s][:], x[s][:], xn[s][:], ALU.add).then_inc(dve_done, DVE_3.did("x3.x", s))
                norm("f3", "x3.x")
                for s in S:
                    dve.wait_ge(pe_done, at(PE_3, "f3.route", s))
                    nc.vector.tensor_reduce(col[s][:, 16:17], ps[s][:, 1, 0:MOE3], X_AXIS, ALU.max, negate=True).then_inc(dve_done, DVE_3.did("f3.nmax", s))
                for s in S:
                    dve.wait_ge(act_done, at(ACT_3, "f3.exp", s))
                    nc.vector.reciprocal(col[s][:, 18:19], col[s][:, 17:18]).then_inc(dve_done, DVE_3.did("f3.rden", s))
                for s in S:
                    after("f3.rden", s)
                    nc.vector.tensor_scalar(col[s][:, 24:32], col[s][:, 24:32], col[s][:, 18:19], None, ALU.mult).then_inc(dve_done, DVE_3.did("f3.probs", s))
                for s in S:
                    after("f3.probs", s)
                    nc.vector.tensor_reduce(col[s][:, 19:20], col[s][:, 24:32], X_AXIS, ALU.max).then_inc(dve_done, DVE_3.did("f3.pmax", s))
                for s in S:
                    after("f3.pmax", s)
                    nc.vector.scalar_tensor_tensor(col[s][:, 32:40], col[s][:, 24:32], col[s][:, 19:20], first[:], ALU.is_equal, ALU.mult).then_inc(dve_done, DVE_3.did("f3.eq", s))
                for s in S:
                    after("f3.eq", s)
                    nc.vector.tensor_reduce(col[s][:, 20:21], col[s][:, 32:40], X_AXIS, ALU.max).then_inc(dve_done, DVE_3.did("f3.first", s))
                for s in S:
                    after("f3.first", s)
                    nc.vector.tensor_scalar(col[s][:, 40:48], col[s][:, 32:40], col[s][:, 20:21], None, ALU.is_equal).then_inc(dve_done, DVE_3.did("f3.pick", s))
                for s in S:
                    if s == 0:
                        dve.wait_ge(carried, r + 1)
                        dve.sem_inc(passed, 1)
                        nc.vector.tensor_copy(taken[0][:], carry[:]).then_inc(dve_done, DVE_3.did("f3.taken", s))
                    else:
                        after("f3.pick", s - 1)
                        after("f3.taken", s - 1)
                        nc.vector.tensor_tensor(taken[s][:], taken[s - 1][:], col[s - 1][:, 40:48], ALU.add).then_inc(dve_done, DVE_3.did("f3.taken", s))
                for s in S:
                    dve.wait_ge(pe_done, at(PE_3, "f3.place", s))
                    nc.vector.scalar_tensor_tensor(col[s][:, 56:64], ps[s][:, 1, 16:16 + MOE3], float(CAPACITY), col[s][:, 40:48], ALU.is_lt, ALU.mult).then_inc(dve_done, DVE_3.did("f3.keep", s))
                for s in S:
                    after("f3.keep", s)
                    nc.vector.tensor_scalar(col[s][:, 64:72], col[s][:, 56:64], col[s][:, 19:20], None, ALU.mult).then_inc(dve_done, DVE_3.did("f3.w", s))
                nc.vector.tensor_tensor(carry[:], taken[-1][:], col[-1][:, 40:48], ALU.add).then_inc(carried, 1)
                for e in range(MOE3):
                    for s in S:
                        if e == 0:
                            dve.wait_ge(pe_done, at(PE_3, "f3.y", s))
                        else:
                            after(f"f3.add{e - 1}", s)
                        nc.vector.scalar_tensor_tensor(x[s][:], ps[s][:, e // GROUP, (e % GROUP) * DIM:(e % GROUP + 1) * DIM], col[s][:, 64 + e:65 + e], x[s][:], ALU.mult, ALU.add).then_inc(dve_done, DVE_3.did(f"f3.add{e}", s))


def kernel(**inputs):
    import concourse.bacc as bacc
    from concourse.bass_utils import run_bass_kernel_spmd

    a = {k: np.asarray(v) for k, v in inputs.items()}
    col = lambda v: v.reshape(-1, 1)
    row = lambda v: v.reshape(1, -1)
    attn = a["L0_ffn_attn_w"]
    q, k, v = attn[:, 0:DIM], attn[:, DIM:2 * DIM], attn[:, 2 * DIM:]
    host = {
        "x": a["x"], "ctx": a["ctx_1024"], "ctxT": a["ctx_1024"].transpose(0, 2, 1),
        "mask_Bx1x1xS2_bk0": row(np.ascontiguousarray(a["mask_Bx1x1xS2_bk0"]).reshape(-1).view(np.int32)),
        "mask_BxS2_ik0": row(a["mask_BxS2_ik0"]),
        "L0_xattn_Wq": a["L0_xattn_Wq"].T, "L0_xattn_Wk": a["L0_xattn_Wk"].T, "L0_xattn_Wv": a["L0_xattn_Wv"].T,
        "L0_xattn_Wo": a["L0_xattn_Wo"].T, "L0_xattn_rel_emb": a["L0_xattn_rel_emb"],
        "L0_ffn_ln1_w": col(a["L0_ffn_ln1_w"]), "L0_ffn_ln1_b": col(a["L0_ffn_ln1_b"]),
        "L0_ffn_ln2_w": col(a["L0_ffn_ln2_w"]), "L0_ffn_ln2_b": col(a["L0_ffn_ln2_b"]),
        "L0_ffn_conv_w": a["L0_ffn_conv_w"].reshape(DIM, 3),
        "attn_w5": np.stack([q, k, swap_halves(q), swap_halves(k), v], axis=1),
        "L0_ffn_proj_w": a["L0_ffn_proj_w"], "L0_ffn_router_w": a["L0_ffn_router_w"],
        "L0_ffn_expert_wv": a["L0_ffn_expert_wv"], "L0_ffn_expert_proj": a["L0_ffn_expert_proj"],
        "L1_xattn_Wq": a["L1_xattn_Wq"].T, "L1_xattn_Wk": a["L1_xattn_Wk"].T, "L1_xattn_Wv": a["L1_xattn_Wv"].T,
        "L1_xattn_bq": col(a["L1_xattn_bq"]), "L1_xattn_bk": col(a["L1_xattn_bk"]), "L1_xattn_bv": row(a["L1_xattn_bv"]),
        "L1_ffn_w1": a["L1_ffn_w1"].T, "L1_ffn_w2": a["L1_ffn_w2"].T,
        "L1_ffn_conv": np.concatenate([a["L1_ffn_conv_w"].reshape(-1, CH, 3), a["L1_ffn_conv_b"].reshape(-1, CH, 1)], axis=2).transpose(1, 0, 2),
        "L2_xattn_w_sim": a["L2_xattn_w_sim"].reshape(3, DIM).T, "L2_xattn_b_sim": row(a["L2_xattn_b_sim"]),
        "L2_xattn_W_qv": a["L2_xattn_W_qv"], "L2_xattn_b_qv": row(a["L2_xattn_b_qv"]),
        "L2_ffn_w_up": a["L2_ffn_w_up"], "L2_ffn_w_gate": a["L2_ffn_w_gate"], "L2_ffn_w_down": a["L2_ffn_w_down"],
        "L3_xattn_Ws": a["L3_xattn_Ws"], "L3_xattn_W": a["L3_xattn_W"], "L3_xattn_w": a["L3_xattn_w"],
        "L3_xattn_b": col(a["L3_xattn_b"]), "L3_xattn_Wcw": col(a["L3_xattn_Wcw"]), "L3_xattn_Wcb": col(a["L3_xattn_Wcb"]),
        "L3_xattn_bcw": row(a["L3_xattn_bcw"]), "L3_xattn_bcb": row(a["L3_xattn_bcb"]),
        "L3_ffn_wg": a["L3_ffn_wg"], "L3_ffn_W": a["L3_ffn_W"].transpose(0, 2, 1), "L3_ffn_b": row(a["L3_ffn_b"]),
        **shape_constants(),
    }
    nc = bacc.Bacc("TRN2", target_bir_lowering=False, num_devices=1)
    arrays, dram = {}, {}
    for name, value in host.items():
        value = np.ascontiguousarray(value)
        arrays[f"in_{name}"] = value
        dram[name] = nc.dram_tensor(f"in_{name}", value.shape, mybir.dt.from_np(value.dtype), kind="ExternalInput").ap()
    dram["out"] = nc.dram_tensor("out_x", (BATCH, TOK, DIM), F32, kind="ExternalOutput").ap()
    build(nc, dram)
    return run_bass_kernel_spmd(nc, [arrays], core_ids=[0]).results[0]["out_x"]
```

```python
from contextlib import ExitStack
from itertools import chain

import numpy as np

import concourse.bass as bass
from concourse import mybir

ALU = mybir.AluOpType
ACT = mybir.ActivationFunctionType
F32 = mybir.dt.float32
BF16 = mybir.dt.bfloat16
I32 = mybir.dt.int32
U8 = mybir.dt.uint8
X_AXIS = mybir.AxisListType.X

BATCH, TOK, DIM = 64, 128, 128
KEYS = 77
HEADS, HDIM = 16, 8
VPAD = 32
GROUP = 4
HALF = HEADS // 2
BUCKETS, MAX_DISTANCE = 32, 128
MOE0, FF0 = 4, 512
CHUNKS0 = FF0 // 128
FF1 = 512
FF2 = 384
MOE3 = 8
CAPACITY = BATCH * TOK // MOE3
CH = 128
STREAMS = 4
PAIR = 2
ROUNDS = BATCH // STREAMS
BANK = 512
LN_EPS = 1e-5
ROUND = float(1.5 * 2 ** 23)
TTILE = 512
TILES = BATCH * TOK // TTILE
KT = 16


class Steps:

    def __init__(self, text, streams=STREAMS, primed=False):
        self.order = []
        for word in text.split():
            name, _, some = word.partition(":")
            self.order += [(name, int(s)) for s in some] if some else [(name, s) for s in range(streams)]
        self.index = {step: n for n, step in enumerate(self.order)}
        assert len(self.index) == len(self.order)
        self.per_round = len(self.order)
        self.ahead = self.per_round if primed else 0
        self.next = 0

    def did(self, name, s):
        assert self.order[self.next % self.per_round] == (name, s), (name, s, self.next)
        self.next += 1
        return 1

    def value(self, name, s, rnd):
        return rnd * self.per_round + (self.index[(name, s)] + 1 + self.ahead)

    def value_before(self, name, s, rnd):
        return rnd * self.per_round + (self.index[(name, s)] + 1)


def take_turns(steps, chains):
    for _, s in steps.order:
        next(chains[s])


PE_0 = Steps("""
    x0.T:0 x0.qkv:0 x0.T:1 x0.qkv:1 x0.S0:01 x0.PT0:01 x0.PV0:01 x0.S1:01 x0.PT1:01 x0.PV1:01 x0.ygT:01 x0.yT:01
    x0.o:01 f0b.T:01 f0.qkv:01 f0.S0:0 f0.PT0:0 f0.S0:1 f0.PV0:0 f0.S1:0 f0.PT0:1 f0.PV0:1 f0.PT1:0 f0.S1:1 f0.PV1:0
    f0.ygT:0 f0.yT:0 f0.PT1:1 f0.o:0 f0.PV1:1 f0.ygT:1 f0.yT:1 f0.o:1
""")
ACT_0 = Steps("""
    x0.xT:0 x0.qv:0 x0.xT:1 x0.qv:1 x0.exp0:01 x0.PT0:01 x0.yg0:01 x0.exp1:01 x0.PT1:01 x0.yg1:01 x0.yT:01 f0b.xT:01
    f0.v:01 f0.exp0:0 f0.PT0:0 f0.yg0:0 f0.exp0:1 f0.PT0:1 f0.exp1:0 f0.yg0:1 f0.PT1:0 f0.yg1:0 f0.exp1:1 f0.yT:0
    f0.PT1:1 f0.yg1:1 f0.yT:1
""")
DVE_0 = Steps("""
    x0.stats:0 x0.aggr:0 x0.eps:0 x0.stats:1 x0.norm:0 x0.aggr:1 x0.eps:1 x0.norm:1 x0.kT:01 x0.add0:0 x0.nmax0:0
    x0.add0:1 x0.nmax0:1 x0.add1:0 x0.nmax1:0 x0.add1:1 x0.nmax1:1 x0.rden:0 x0.y:0 x0.rden:1 x0.y:1 x0.x:0
    f0a.stats:0 x0.x:1 f0a.aggr:0 f0a.stats:1 f0a.eps:0 f0a.aggr:1 f0a.eps:1 f0a.norm:0 f0b.stats:0 f0a.norm:1
    f0b.aggr:0 f0b.stats:1 f0b.eps:0 f0b.aggr:1 f0b.eps:1 f0b.norm:01 f0.conv2:0 f0.conv1:0 f0.conv2:1 f0.conv0:0
    f0.conv1:1 f0.conv0:1 f0.rope:0 f0.qk:0 f0.rope:1 f0.qk:1 f0.nmax0:01 f0.nmax1:01 f0.rden:0 f0.y:0 f0.x:0
    f0.rden:1 f0.y:1 f0.x:1
""")
POOL_0 = Steps("""
    x0.rstd:01 x0.qblk:0 x0.kblk:0 x0.qblk:1 x0.kblk:1 f0a.rstd:01 f0b.rstd:01 f0.qblk:0 f0.kblk:0 f0.qblk:1
    x0.bias:0 f0.kblk:1 x0.bias:1
""")
PE_1 = Steps("""
    f0c.T:01 x0.T:2 moe.route:01 x0.qkv:2 moe.gv0.0:0 moe.gv0.1:0 x0.S0:2 moe.gv0.2:0 moe.gv0.3:0 moe.gv1.0:0
    moe.gv1.1:0 moe.gv1.2:0 x0.PT0:2 moe.gv1.3:0 moe.down0.0:0 x0.PV0:2 moe.down0.1:0 x0.T:3 moe.gv2.0:0 x0.qkv:3
    moe.gv2.1:0 x0.S1:2 moe.gv2.2:0 x0.S0:3 moe.gv2.3:0 moe.down1.0:0 moe.down1.1:0 moe.gv3.0:0 x0.PT1:2 moe.gv3.1:0
    x0.PT0:3 moe.gv3.2:0 x0.PV1:2 x0.PV0:3 moe.gv3.3:0 x0.S1:3 moe.down2.0:0 x0.ygT:2 moe.down2.1:0 x0.yT:2
    moe.down3.0:0 moe.down3.1:0 x0.PT1:3 x0.o:2 x0.PV1:3 x1.T:0 x0.ygT:3 x1.T:1 x1.qkv:01 x0.yT:3 x1.S:0 f0b.T:2
    x1.S:1 x0.o:3 x1.PT:01 x1.y:01 f0.qkv:2 f0b.T:3 f1.T:0 f1.up:0 f0.qkv:3 f0.S0:2 f1.T:1 f1.up:1 f1.uT:0 f0.S0:3
    f0.PT0:2 f1.uT:1 f0.PV0:2 f0.PT0:3 f0.S1:2 f1.uqT:0 f0.PV0:3 f1.uqT:1 f1.down:0 f0.S1:3 f1.down:1 x2.T:0
    f0.PT1:2 x2.S:0 x2.T:1 f0.PT1:3 f0.PV1:2 x2.S:1 x2.PT:0 f0.PV1:3 f0.ygT:2 x2.M:0 f0.ygT:3 x2.PT:1 f0.yT:2
    x2.hq:0 x2.M:1 f0.o:2 f0.yT:3 x2.hq:1 f0.o:3 x2.out:0 f0c.T:2 x2.out:1 moe.route:2 f0c.T:3 moe.route:3 f2.T:0
    moe.gv0.0:2 moe.gv0.1:2 f2.T:1 moe.gv0.2:2 x0.T:0 moe.gv0.3:2 x0.qkv:0 moe.gv1.0:2 moe.gv1.1:2 moe.gv1.2:2
    moe.gv1.3:2 x0.T:1 x0.S0:0 x0.qkv:1 moe.down0.0:2 moe.down0.1:2 moe.gv2.0:2 moe.gv2.1:2 x0.S0:1 x0.PT0:0
    moe.gv2.2:2 moe.gv2.3:2 x0.PV0:0 moe.down1.0:2 moe.down1.1:2 x0.S1:0 x0.PT0:1 moe.gv3.0:2 moe.gv3.1:2 x0.PV0:1
    moe.gv3.2:2 moe.gv3.3:2 x0.PT1:0 x0.S1:1 moe.down2.0:2 x0.PV1:0 moe.down2.1:2 x0.ygT:0 moe.down3.0:2 x0.yT:0
    moe.down3.1:2 x0.PT1:1 x0.o:0 x0.PV1:1 x0.ygT:1 x1.T:23 x1.qkv:23 x0.yT:1 x1.S:2 f0b.T:0 x1.S:3 x0.o:1 x1.PT:23
    x1.y:23 f0.qkv:0 f0b.T:1 f1.T:23 f1.up:2 f0.qkv:1 f0.S0:0 f1.up:3 f1.uT:2 f0.S0:1 f0.PT0:0 f1.uT:3 f0.PV0:0
    f1.uqT:2 f0.PT0:1 f1.down:2 f0.S1:0 f1.uqT:3 x2.T:2 f0.PV0:1 f1.down:3 x2.S:2 f0.S1:1 x2.T:3 f0.PT1:0 x2.S:3
    x2.PT:2 f0.PV1:0 f0.PT1:1 f0.ygT:0 x2.PT:3 x2.M:2 f0.PV1:1 x2.M:3 x2.hq:2 f0.ygT:1 x2.hq:3 f0.yT:1 x2.out:2
    f0.o:1 f0.yT:0 x2.out:3 f0.o:0 f2.T:23
""", primed=True)
ACT_1 = Steps("""
    f0c.xT:01 x0.xT:2 x0.qv:2 moe.tanh0.0:0 moe.tanh0.1:0 moe.tanh0.2:0 moe.tanh0.3:0 x0.exp0:2 moe.tanh1.0:0
    moe.tanh1.1:0 moe.tanh1.2:0 x0.PT0:2 moe.tanh1.3:0 x0.yg0:2 x0.xT:3 moe.tanh2.0:0 x0.qv:3 moe.tanh2.1:0
    moe.tanh2.2:0 x0.exp1:2 moe.tanh2.3:0 x0.exp0:3 moe.tanh3.0:0 x0.PT1:2 moe.tanh3.1:0 x0.PT0:3 moe.tanh3.2:0
    x0.yg1:2 x0.yg0:3 moe.tanh3.3:0 x0.exp1:3 x0.yT:2 x0.PT1:3 x0.yg1:3 x1.xT:01 x1.qkv:01 x0.yT:3 x1.exp:0 f0b.xT:2
    x1.exp:1 x1.PT:01 f0.v:2 f0b.xT:3 f1.xT:0 f1.mid:0 f0.v:3 f1.xT:1 f1.tanh:0 f1.mid:1 f0.exp0:2 f1.tanh:1
    f0.PT0:2 f0.exp0:3 f0.yg0:2 f0.PT0:3 f1.uqT:0 f0.yg0:3 f1.uqT:1 f0.exp1:2 x2.xT:0 f0.exp1:3 f0.PT1:2 x2.xT:1
    x2.exp:0 f0.PT1:3 f0.yg1:2 x2.PT:0 x2.exp:1 f0.yg1:3 x2.p:0 x2.PT:1 f0.yT:2 x2.p:1 x2.feat:0 f0.yT:3 x2.feat:1
    f0c.xT:23 f2.xT:0 moe.tanh0.0:2 moe.tanh0.1:2 f2.xT:1 moe.tanh0.2:2 x0.xT:0 moe.tanh0.3:2 x0.qv:0 moe.tanh1.0:2
    moe.tanh1.1:2 moe.tanh1.2:2 moe.tanh1.3:2 x0.xT:1 x0.qv:1 x0.exp0:0 moe.tanh2.0:2 moe.tanh2.1:2 x0.PT0:0
    moe.tanh2.2:2 x0.exp0:1 x0.yg0:0 moe.tanh2.3:2 x0.PT0:1 moe.tanh3.0:2 x0.exp1:0 moe.tanh3.1:2 x0.yg0:1
    moe.tanh3.2:2 moe.tanh3.3:2 x0.PT1:0 x0.yg1:0 x0.exp1:1 x0.yT:0 x0.PT1:1 x0.yg1:1 x1.xT:23 x1.qkv:23 x0.yT:1
    f0b.xT:0 x1.exp:23 x1.PT:23 f0.v:0 f0b.xT:1 f1.xT:23 f1.mid:2 f0.v:1 f1.tanh:2 f1.mid:3 f0.exp0:0 f1.tanh:3
    f0.PT0:0 f0.exp0:1 f0.yg0:0 f1.uqT:2 f0.PT0:1 f1.uqT:3 x2.xT:2 f0.yg0:1 f0.exp1:0 x2.exp:2 x2.xT:3 f0.PT1:0
    f0.exp1:1 x2.exp:3 f0.yg1:0 x2.PT:2 f0.PT1:1 x2.PT:3 x2.p:2 f0.yg1:1 x2.p:3 x2.feat:2 f0.yT:1 x2.feat:3 f0.yT:0
    f2.xT:23
""", primed=True)
DVE_1 = Steps("""
    f0c.stats:01 f0c.aggr:0 x0.stats:2 f0c.eps:0 f0c.aggr:1 x0.aggr:2 f0c.eps:1 x0.eps:2 f0c.norm:01 x0.norm:2
    moe.max:0 moe.eq:0 moe.max:1 moe.first:0 moe.eq:1 moe.pick:0 moe.first:1 moe.pick:1 x0.kT:2 moe.silu0.0:0
    moe.act0.0:0 moe.silu0.1:0 moe.act0.1:0 x0.add0:2 x0.nmax0:2 moe.silu0.2:0 moe.act0.2:0 moe.silu0.3:0
    moe.act0.3:0 moe.silu1.0:0 moe.act1.0:0 moe.silu1.1:0 x0.stats:3 moe.act1.1:0 x0.aggr:3 moe.silu1.2:0 x0.eps:3
    moe.act1.2:0 moe.silu1.3:0 x0.norm:3 moe.act1.3:0 moe.add0.0:0 moe.add0.1:0 moe.silu2.0:0 moe.act2.0:0 x0.kT:3
    moe.silu2.1:0 moe.act2.1:0 x0.add1:2 x0.nmax1:2 moe.silu2.2:0 x0.add0:3 moe.act2.2:0 x0.nmax0:3 moe.silu2.3:0
    moe.act2.3:0 moe.add1.0:0 moe.add1.1:0 moe.silu3.0:0 moe.act3.0:0 moe.silu3.1:0 moe.act3.1:0 moe.silu3.2:0
    moe.act3.2:0 moe.silu3.3:0 moe.act3.3:0 x0.add1:3 x0.nmax1:3 x0.rden:2 moe.add2.0:0 x0.y:2 moe.add2.1:0
    moe.add3.0:0 moe.add3.1:0 moe.x:01 x1.stats:0 x0.x:2 x1.aggr:0 x1.stats:1 x1.eps:0 f0a.stats:2 x1.aggr:1
    f0a.aggr:2 x1.eps:1 f0a.eps:2 x1.norm:01 f0a.norm:2 x0.rden:3 f0b.stats:2 x0.y:3 f0b.aggr:2 f0b.eps:2 f0b.norm:2
    x1.nmax:01 x1.rden:0 x0.x:3 f0.conv2:2 f0a.stats:3 f0.conv1:2 f0a.aggr:3 x1.rden:1 f0.conv0:2 x1.x:0 f0a.eps:3
    x1.x:1 x1.bv:01 f1.stats:0 f0a.norm:3 f1.aggr:0 f1.stats:1 f0b.stats:3 f1.eps:0 f0.rope:2 f0b.aggr:3 f1.norm:0
    f0b.eps:3 f0.qk:2 f1.amax:0 f1.aggr:1 f0b.norm:3 f1.eps:1 f1.inv:0 f1.scale:0 f1.round:0 f1.xq:0 f0.conv2:3
    f1.norm:1 f0.conv1:3 f1.amax:1 f0.conv0:3 f1.inv:1 f1.scale:1 f1.round:1 f1.xq:1 f1.tap0:0 f0.rope:3 f1.taps:0
    f0.qk:3 f0.nmax0:2 f1.silu:0 f1.uamax:0 f1.tap0:1 f1.uclip:0 f1.taps:1 f0.nmax0:3 f1.silu:1 f1.urec:0
    f1.uscale:0 f1.uround:0 f1.uamax:1 f1.uq:0 f1.uclip:1 f1.urec:1 f1.uscale:1 f1.uround:1 f1.uq:1 f0.nmax1:2
    f1.x:0 x2.stats:0 x2.aggr:0 x2.eps:0 x2.norm:0 f0.nmax1:3 f1.x:1 x2.stats:1 x2.nmax:0 x2.aggr:1 x2.smax:0
    x2.eps:1 x2.score:0 x2.norm:1 x2.rden:0 x2.P:0 x2.nmax:1 x2.smax:1 x2.score:1 x2.M:0 x2.rden:1 x2.P:1 f0.rden:2
    x2.negM:0 f0.y:2 f0.rden:3 f0.y:3 x2.M:1 x2.rsum:0 x2.negM:1 x2.hc:0 f0.x:2 f0c.stats:2 f0c.aggr:2 f0c.eps:2
    x2.ehq:0 f0c.norm:2 x2.rsum:1 f0.x:3 x2.hc:1 f0c.stats:3 f0c.aggr:3 f0c.eps:3 x2.ehq:1 x2.add:0 f0c.norm:3
    f2.x:0 f2.stats:0 f2.aggr:0 f2.eps:0 x2.add:1 moe.max:2 f2.x:1 f2.norm:0 moe.eq:2 f2.stats:1 moe.first:2
    f2.aggr:1 moe.pick:2 moe.max:3 f2.eps:1 moe.eq:3 moe.first:3 moe.pick:3 x0.stats:0 x0.aggr:0 f2.norm:1 x0.eps:0
    moe.silu0.0:2 moe.act0.0:2 x0.norm:0 moe.silu0.1:2 moe.act0.1:2 moe.silu0.2:2 moe.act0.2:2 x0.stats:1
    moe.silu0.3:2 x0.aggr:1 moe.act0.3:2 x0.eps:1 x0.kT:0 moe.silu1.0:2 moe.act1.0:2 x0.norm:1 moe.silu1.1:2
    moe.act1.1:2 moe.silu1.2:2 moe.act1.2:2 moe.silu1.3:2 moe.act1.3:2 x0.add0:0 x0.nmax0:0 x0.kT:1 moe.add0.0:2
    moe.add0.1:2 moe.silu2.0:2 moe.act2.0:2 x0.add0:1 moe.silu2.1:2 x0.nmax0:1 moe.act2.1:2 moe.silu2.2:2
    moe.act2.2:2 moe.silu2.3:2 moe.act2.3:2 moe.add1.0:2 x0.add1:0 moe.add1.1:2 x0.nmax1:0 moe.silu3.0:2
    moe.act3.0:2 moe.silu3.1:2 moe.act3.1:2 moe.silu3.2:2 moe.act3.2:2 moe.silu3.3:2 x0.add1:1 moe.act3.3:2
    x0.nmax1:1 moe.add2.0:2 moe.add2.1:2 x0.rden:0 x0.y:0 moe.add3.0:2 moe.add3.1:2 moe.x:32 x0.x:0 x1.stats:2
    f0a.stats:0 x1.stats:3 x1.aggr:2 f0a.aggr:0 x1.aggr:3 x1.eps:2 f0a.eps:0 x1.eps:3 x1.norm:23 x0.rden:1
    f0a.norm:0 x0.y:1 f0b.stats:0 f0b.aggr:0 f0b.eps:0 f0b.norm:0 x1.nmax:23 f0.conv2:0 x0.x:1 x1.rden:2 f0.conv1:0
    x1.rden:3 f0a.stats:1 f0.conv0:0 f0a.aggr:1 x1.x:2 f0a.eps:1 x1.x:3 x1.bv:23 f1.stats:23 f1.aggr:2 f0a.norm:1
    f1.eps:2 f1.aggr:3 f0b.stats:1 f1.eps:3 f0.rope:0 f1.norm:2 f0b.aggr:1 f1.norm:3 f0b.eps:1 f1.amax:23 f1.inv:2
    f0.qk:0 f0b.norm:1 f1.scale:2 f1.inv:3 f1.round:2 f1.scale:3 f1.xq:2 f1.round:3 f0.conv2:1 f1.xq:3 f0.conv1:1
    f0.conv0:1 f1.tap0:2 f0.rope:1 f1.taps:2 f0.qk:1 f0.nmax0:0 f1.silu:2 f1.tap0:3 f1.uamax:2 f1.taps:3 f1.uclip:2
    f1.urec:2 f1.uscale:2 f0.nmax0:1 f1.silu:3 f1.uround:2 f1.uq:2 f1.uamax:3 f1.uclip:3 f1.urec:3 f1.uscale:3
    f1.uround:3 f1.uq:3 f1.x:2 x2.stats:2 x2.aggr:2 x2.eps:2 x2.norm:2 f0.nmax1:0 f1.x:3 x2.stats:3 x2.nmax:2
    x2.aggr:3 x2.smax:2 x2.eps:3 x2.score:2 x2.norm:3 x2.rden:2 x2.P:2 f0.nmax1:1 x2.nmax:3 x2.smax:3 x2.score:3
    x2.rden:3 x2.P:3 x2.M:2 f0.rden:0 f0.y:0 x2.negM:2 x2.M:3 x2.negM:3 x2.rsum:2 x2.hc:2 f0.rden:1 f0.y:1 x2.ehq:2
    x2.rsum:3 x2.hc:3 x2.ehq:3 x2.add:2 f0.x:1 f2.x:2 f2.stats:2 f2.aggr:2 f2.eps:2 x2.add:3 f0.x:0 f2.x:3 f2.norm:2
    f2.stats:3 f2.aggr:3 f2.eps:3 f2.norm:3
""", primed=True)
POOL_1 = Steps("""
    f0c.rstd:01 x0.rstd:2 x0.qblk:2 x0.kblk:2 x0.rstd:3 x0.qblk:3 x0.kblk:3 x1.rstd:01 f0a.rstd:2 f0b.rstd:2
    f0a.rstd:3 f1.rstd:0 f0b.rstd:3 f0.qblk:2 f1.rstd:1 f0.kblk:2 x0.bias:2 f0.qblk:3 f0.kblk:3 x0.bias:3 x2.rstd:01
    f0c.rstd:23 f2.rstd:0 in:0 f2.rstd:1 x0.rstd:0 in:1 x0.qblk:0 x0.rstd:1 x0.kblk:0 x0.qblk:1 x0.kblk:1 x1.rstd:23
    f0a.rstd:0 f0b.rstd:0 f0a.rstd:1 f1.rstd:23 f0b.rstd:1 f0.qblk:0 f0.kblk:0 x0.bias:0 f0.qblk:1 f0.kblk:1
    x0.bias:1 x2.rstd:23 f2.rstd:23 in:23
""", primed=True)
PE_3S = Steps("""
    x3.T:1 x3.proj:1 x3.T:0 x3.proj:0 x3.rho0:1 x3.rho_last:1 x3.rho0:0 x3.rho1:1 x3.rho_last:0 x3.rho1:0 x3.rho2:10
    x3.rho3:1 x3.rhoT:1 x3.rho3:0 x3.PT:1 x3.rhoT:0 x3.h:1 x3.gate:1 x3.PT:0 x3.h:0 x3.gate:0
""")
ACT_3S = Steps("""
    x3.xT:1 x3.proj:1 x3.xT:0 x3.proj:0 x3.tanh0:1 x3.tanh_last:1 x3.tanh0:0 x3.tanh1:1 x3.tanh_last:0 x3.tanh1:0
    x3.tanh2:10 x3.tanh3:1 x3.rho:1 x3.tanh3:0 x3.exp:1 x3.rho:0 x3.PT:1 x3.h:1 x3.exp:0 x3.gate:1 x3.PT:0 x3.h:0
    x3.gate:0
""")
DVE_3S = Steps("""
    x3.stats:1 x3.aggr:1 x3.eps:1 x3.stats:0 x3.aggr:0 x3.norm:1 x3.eps:0 x3.norm:0 x3.sum0:10 x3.sum1:10 x3.sum2:10
    x3.sum3:10 x3.mask:1 x3.nmax:1 x3.rden:1 x3.P:1 x3.mask:0 x3.nmax:0 x3.rden:0 x3.gb:1 x3.P:0 x3.y:1 x3.x:1
    x3.gb:0 x3.y:0 x3.x:0
""")
POOL_3S = Steps("""
    x3.rstd:10
""")
PE_3 = Steps("""
    x3.T:2 f3.T:1 x3.proj:2 f3.route:1 x3.T:3 f3.T:0 x3.proj:3 f3.route:0 x3.rho0:2 f3.place:01 x3.rho_last:2
    f3.wT:01 x3.rho0:3 x3.rho1:2 f3.bias:0 f3.y:0 x3.rho_last:3 f3.bias:1 x3.rho1:3 x3.rho2:2 f3.y:1 x3.rho2:3
    x3.rho3:2 x3.rhoT:2 x3.rho3:3 x3.PT:2 x3.rhoT:3 x3.h:2 x3.gate:2 x3.T:0 x3.PT:3 x3.proj:0 x3.T:1 x3.h:3
    x3.proj:1 f3.T:2 x3.gate:3 f3.route:2 x3.rho0:0 x3.rho_last:0 f3.T:3 x3.rho0:1 f3.place:2 x3.rho1:0 f3.route:3
    x3.rho_last:1 f3.wT:2 x3.rho1:1 f3.bias:2 f3.place:3 x3.rho2:0 f3.y:2 f3.wT:3 x3.rho2:1 f3.bias:3 x3.rho3:0
    f3.y:3 x3.rhoT:0 x3.rho3:1 x3.PT:0 x3.rhoT:1 x3.h:0 x3.gate:0 x3.PT:1 x3.h:1 x3.gate:1
""", primed=True)
ACT_3 = Steps("""
    x3.xT:2 f3.xT:1 x3.proj:2 x3.xT:3 f3.exp:1 f3.xT:0 x3.proj:3 x3.tanh0:2 f3.exp:0 x3.tanh_last:2 x3.tanh0:3
    x3.tanh1:2 f3.wT:0 x3.tanh_last:3 f3.wT:1 x3.tanh1:3 x3.tanh2:23 x3.tanh3:2 x3.rho:2 x3.tanh3:3 x3.exp:2
    x3.rho:3 x3.PT:2 x3.h:2 x3.exp:3 x3.gate:2 x3.xT:0 x3.PT:3 x3.proj:0 x3.xT:1 x3.h:3 x3.proj:1 f3.xT:2 x3.tanh0:0
    x3.gate:3 x3.tanh_last:0 f3.exp:2 x3.tanh0:1 f3.xT:3 x3.tanh1:0 x3.tanh_last:1 f3.exp:3 x3.tanh1:1 f3.wT:2
    x3.tanh2:01 x3.tanh3:0 f3.wT:3 x3.rho:0 x3.tanh3:1 x3.exp:0 x3.rho:1 x3.PT:0 x3.h:0 x3.exp:1 x3.gate:0 x3.PT:1
    x3.h:1 x3.gate:1
""", primed=True)
DVE_3 = Steps("""
    x3.stats:2 f3.stats:1 x3.aggr:2 f3.aggr:1 x3.eps:2 f3.eps:1 x3.norm:2 x3.stats:3 f3.norm:1 f3.stats:0 x3.aggr:3
    f3.aggr:0 x3.eps:3 f3.eps:0 x3.norm:3 f3.norm:0 f3.nmax:1 x3.sum0:2 f3.nmax:0 x3.sum0:3 f3.rden:01 f3.probs:01
    f3.pmax:01 f3.eq:01 f3.first:01 f3.pick:01 f3.taken:01 x3.sum1:2 f3.keep:01 f3.w:01 x3.sum1:3 f3.bias:0
    x3.sum2:2 f3.add0:0 f3.add1:0 f3.add2:0 f3.add3:0 f3.bias:1 f3.add4:0 f3.add5:0 f3.add6:0 x3.sum2:3 x3.sum3:2
    f3.add0:1 f3.add7:0 f3.add1:1 f3.add2:1 f3.add3:1 x3.sum3:3 f3.add4:1 f3.add5:1 f3.add6:1 x3.stats:0 x3.mask:2
    f3.add7:1 x3.nmax:2 x3.aggr:0 x3.eps:0 x3.rden:2 x3.P:2 x3.mask:3 x3.nmax:3 x3.stats:1 x3.rden:3 x3.gb:2
    x3.aggr:1 x3.norm:0 x3.y:2 x3.eps:1 x3.P:3 x3.x:2 f3.stats:2 x3.norm:1 f3.aggr:2 f3.eps:2 f3.norm:2 x3.sum0:0
    x3.gb:3 x3.sum0:1 f3.nmax:2 x3.y:3 x3.x:3 f3.stats:3 f3.aggr:3 f3.eps:3 x3.sum1:0 f3.norm:3 f3.rden:2 f3.probs:2
    f3.pmax:2 f3.eq:2 f3.first:2 f3.pick:2 f3.taken:2 x3.sum1:1 f3.keep:2 f3.nmax:3 x3.sum2:0 f3.w:2 f3.rden:3
    f3.probs:3 f3.pmax:3 f3.eq:3 f3.first:3 f3.pick:3 f3.taken:3 x3.sum2:1 f3.bias:2 x3.sum3:0 f3.keep:3 f3.w:3
    f3.add0:2 f3.add1:2 f3.add2:2 f3.add3:2 f3.add4:2 f3.bias:3 x3.sum3:1 f3.add5:2 f3.add6:2 f3.add7:2 f3.add0:3
    f3.add1:3 x3.mask:0 f3.add2:3 x3.nmax:0 f3.add3:3 f3.add4:3 x3.rden:0 f3.add5:3 x3.P:0 f3.add6:3 f3.add7:3
    x3.mask:1 x3.nmax:1 x3.rden:1 x3.gb:0 x3.P:1 x3.y:0 x3.x:0 x3.gb:1 x3.y:1 x3.x:1
""", primed=True)
POOL_3 = Steps("""
    x3.rstd:2 f3.rstd:1 x3.rstd:3 f3.rstd:0 in:01 x3.rstd:01 f3.rstd:23 in:23
""", primed=True)
PE_2A = Steps("""
    up gate
""", 2)
DVE_2A = Steps("""
    up gate
""", 2, primed=True)
PE_2B = Steps("""
    gate
""", 2)
ACT_2B = Steps("""
    round tanh
""", 2, primed=True)
DVE_2B = Steps("""
    gate sigmoid clip gated max
""", 2, primed=True)
PE_2C = Steps("""
    up
""", 2)
ACT_2C = Steps("""
    round
""", 2, primed=True)
DVE_2C = Steps("""
    round up product max
""", 2, primed=True)
PE_2D = Steps("""
    down
""", 2, primed=True)
DVE_2D = Steps("""
    round quant add
""", 2, primed=True)



def shape_constants():
    c = {}
    p = np.arange(128)
    c["ident"] = np.eye(128, dtype=np.float32)
    c["causal"] = np.where(p[None, :] > p[:, None], np.float32(-1e30), np.float32(0)).astype(np.float32)
    c["before"] = (p[:, None] < p[None, :]).astype(np.float32)
    c["ingroup"] = ((p[:, None] // HDIM) % GROUP == np.arange(GROUP)[None, :]).astype(np.float32)
    c["ofgroup"] = (p[:, None] // (HDIM * GROUP) == np.arange(GROUP)[None, :]).astype(np.float32)
    c["first"] = np.tile(np.arange(MOE3, 0, -1, dtype=np.float32), (128, 1))
    n = np.clip(np.arange(-(KEYS - 1), TOK), 0, None)
    exact = BUCKETS // 2
    large = exact + (np.log(np.maximum(n, exact).astype(np.float32) / np.float32(exact) + np.float32(1e-9))
                     / np.float32(np.log(MAX_DISTANCE / exact)) * np.float32(BUCKETS - exact)).astype(np.int32)
    bucket = np.where(n < exact, n, np.minimum(large, BUCKETS - 1))
    c["bucket"] = (np.arange(BUCKETS)[:, None] == bucket[None, :]).astype(np.float32)
    inv = (np.float32(1.0) / np.float32(10000.0) ** (np.arange(0, HDIM, 2, dtype=np.float32) / np.float32(HDIM))).astype(np.float32)
    ang = np.outer(np.arange(TOK, dtype=np.float32), inv).astype(np.float32)
    i = p % HDIM
    cos = np.cos(ang)[:, i % (HDIM // 2)].T
    sin = np.sin(ang)[:, i % (HDIM // 2)].T * np.where(i < HDIM // 2, -1.0, 1.0)[:, None]
    r = 1.0 / np.sqrt(HDIM)
    c["rope"] = np.stack([cos * r, cos, sin * r, sin], axis=1).astype(np.float32)
    return c


def swap_halves(w):
    k = w.shape[0]
    return np.ascontiguousarray(w.reshape(k, HEADS, 2, HDIM // 2)[:, :, ::-1, :]).reshape(k, DIM)


def build(nc, d):
    x_mid = nc.dram_tensor("x_mid", (BATCH, TOK, DIM), F32, kind="Internal").ap()
    x_mid2 = nc.dram_tensor("x_mid2", (BATCH, TOK, DIM), F32, kind="Internal").ap()
    with ExitStack() as ctx:
        shared = dict(x_mid=x_mid, x_mid2=x_mid2)
        for name, shape in (("xnT_all", [128, BATCH * TOK]), ("ident", [128, 128]), ("ones", [128, 128]),
                            ("first", [128, MOE3]), ("minus_half", [128, 1])):
            shared[name] = ctx.enter_context(nc.sbuf_tensor(name, shape, F32))
        part_1(nc, d, shared)
        part_2(nc, d, shared)
        part_3(nc, d, shared)


def part_1(nc, d, shared):
    xnT_all, ident, ones, first, minus_half, x_mid = (shared[k] for k in ("xnT_all", "ident", "ones", "first", "minus_half", "x_mid"))
    S = range(STREAMS)
    A, B = (0, 1), (2, 3)
    LISTS = (PE_0, ACT_0, DVE_0, POOL_0), (PE_1, ACT_1, DVE_1, POOL_1)
    with ExitStack() as ctx:
        def sb(name, shape, dt=F32):
            return ctx.enter_context(nc.sbuf_tensor(name, shape, dt))

        def per_stream(name, shape, dt=F32):
            return [sb(f"{name}{s}", shape, dt) for s in S]

        def sem(name):
            return ctx.enter_context(nc.semaphore(name))

        ident_bf = sb("ident_bf", [128, 128], BF16)
        causal_bf = sb("causal_bf", [128, 128], BF16)
        ingroup = sb("ingroup", [128, GROUP])
        ofgroup = sb("ofgroup", [128, GROUP])
        rope = sb("rope", [128, 4, TOK])
        mask_words = sb("mask_words", [128, (BATCH + 2 * STREAMS) * KEYS // 4], I32)
        mask = mask_words[:].bitcast(U8)
        bias0 = sb("bias0", [128, HEADS, KEYS])
        w_xa0 = sb("w_xa0", [128, 4, DIM])
        ln_col = sb("ln_col", [128, 4])
        conv0_col = sb("conv0_col", [128, 3])
        w_at0 = sb("w_at0", [128, 5, DIM])
        w_pr0 = sb("w_pr0", [128, DIM])
        w_ro0 = sb("w_ro0", [128, MOE0])
        w_gv0 = sb("w_gv0", [128, MOE0, 2 * FF0])
        w_dn0 = sb("w_dn0", [128, MOE0, FF0 // CH, DIM])
        w_xa1 = sb("w_xa1", [128, 3, DIM])
        b_xa1 = sb("b_xa1", [128, 2])
        bv1 = sb("bv1", [128, DIM])
        w_up1 = sb("w_up1", [128, FF1])
        conv1_col = sb("conv1_col", [128, FF1 // CH, 4])
        w_dn1 = sb("w_dn1", [128, FF1 // CH, DIM])
        w_dn1_q = sb("w_dn1_q", [128, FF1 // CH, DIM], BF16)
        sim_col = sb("sim_col", [128, 3])
        b_sim = sb("b_sim", [128, 1])
        w_qv2 = sb("w_qv2", [128, 4, DIM])
        b_qv2 = sb("b_qv2", [128, DIM])
        prep = sb("prep", [128, 16])

        x_in = per_stream("x_in", [128, DIM])
        ctx_in = per_stream("ctx_in", [KEYS, DIM])
        ctxT_in = per_stream("ctxT_in", [128, KEYS])
        x = per_stream("x", [128, DIM])
        cx = per_stream("cx", [KEYS, DIM])
        cxT = per_stream("cxT", [128, KEYS])
        xn = per_stream("xn", [128, DIM])
        xnT_4 = sb("xnT_4", [128, STREAMS, TOK])
        xnT = [xnT_4[:, s, :] for s in S]
        h0 = per_stream("h0", [128, DIM])
        attended = per_stream("attended", [128, KEYS])
        thr = per_stream("thr", [128, KEYS])
        bias_m = per_stream("bias_m", [128, HEADS, KEYS])
        qT = per_stream("qT", [128, TOK])
        kT = per_stream("kT", [128, TOK])
        kblk = per_stream("kblk", [128, GROUP, TOK])
        qblk = per_stream("qblk", [128, GROUP, TOK])
        vaug = per_stream("vaug", [128, HEADS, VPAD])
        yg = per_stream("yg", [128, GROUP, TOK])
        prob = per_stream("prob", [128, 2 * BANK])
        probT = per_stream("probT", [128, 2 * BANK])
        y = per_stream("y", [128, DIM])
        yT = per_stream("yT", [128, TOK])
        col = per_stream("col", [128, 48])
        ps = [ctx.enter_context(nc.psum_tensor(f"ps{s}", [128, 2, BANK], F32)) for s in S]

        weights_in, consts_done, setup_pe, setup_act, setup_dve = (sem(n) for n in (
            "weights_in", "consts_done", "setup_pe", "setup_act", "setup_dve"))
        loads_in = [sem(f"loads_in{s}") for s in S]
        stores_out = [sem(f"stores_out{s}") for s in S]
        inputs_ready, mask_made, mask_ready, bias_kept, bias_ready = ([sem(f"{n}{s}") for s in S] for n in (
            "inputs_ready", "mask_made", "mask_ready", "bias_kept", "bias_ready"))
        mask_tail = sem("mask_tail")
        passed = sem("passed")
        pe_done, act_done, dve_done, pool_done = (sem(n) for n in ("pe_done", "act_done", "dve_done", "pool_done"))

        weight_loads = [
            (ident[:], d["ident"]), (first[:], d["first"]), (ingroup[:], d["ingroup"]), (ofgroup[:], d["ofgroup"]), (rope[:], d["rope"]),
            (prob[0][:, 0:128], d["causal"]), (prob[0][0:BUCKETS, 128:128 + TOK + KEYS - 1], d["bucket"]),
            (prob[0][0:BUCKETS, 384:384 + HEADS], d["L0_xattn_rel_emb"]),
            (mask_words[:, 0:BATCH * KEYS // 4], d["mask_Bx1x1xS2_bk0"].to_broadcast([128, BATCH * KEYS // 4])),
            (w_xa0[:, 0, :], d["L0_xattn_Wq"]), (w_xa0[:, 1, :], d["L0_xattn_Wk"]),
            (w_xa0[:, 2, :], d["L0_xattn_Wv"]), (w_xa0[:, 3, :], d["L0_xattn_Wo"]),
            (ln_col[:, 0:1], d["L0_ffn_ln1_w"]), (ln_col[:, 1:2], d["L0_ffn_ln1_b"]),
            (ln_col[:, 2:3], d["L0_ffn_ln2_w"]), (ln_col[:, 3:4], d["L0_ffn_ln2_b"]),
            (conv0_col[:], d["L0_ffn_conv_w"]), (w_at0[:], d["attn_w5"]), (w_pr0[:], d["L0_ffn_proj_w"]),
            (w_ro0[:], d["L0_ffn_router_w"]), (w_gv0[:], d["L0_ffn_expert_wv"].rearrange("e c n -> c e n")),
            (w_dn0[:], d["L0_ffn_expert_proj"].rearrange("e (k c) n -> c e k n", c=CH)),
            (w_xa1[:, 0, :], d["L1_xattn_Wq"]), (w_xa1[:, 1, :], d["L1_xattn_Wk"]), (w_xa1[:, 2, :], d["L1_xattn_Wv"]),
            (b_xa1[:, 0:1], d["L1_xattn_bq"]), (b_xa1[:, 1:2], d["L1_xattn_bk"]),
            (bv1[:], d["L1_xattn_bv"].to_broadcast([128, DIM])),
            (w_up1[:], d["L1_ffn_w1"]), (w_dn1[:], d["L1_ffn_w2"].rearrange("(k c) n -> c k n", c=CH)),
            (conv1_col[:], d["L1_ffn_conv"]), (sim_col[:], d["L2_xattn_w_sim"]), (b_sim[:], d["L2_xattn_b_sim"].to_broadcast([128, 1])),
            (w_qv2[:], d["L2_xattn_W_qv"].rearrange("(k c) n -> c k n", c=DIM)),
            (b_qv2[:], d["L2_xattn_b_qv"].to_broadcast([128, DIM])),
        ]

        def unit_bank(pair, u):
            return ps[pair[u % 3 // 2]][:, u % 3 % 2, :]

        def hidden(pair, e, c):
            return prob[pair[e % 2]][:, c * PAIR * TOK:(c + 1) * PAIR * TOK]

        SETUP_BIAS, SETUP_SUMS, SETUP_DVE = 1, 4, 13

        block = ctx.enter_context(nc.Block())

        @block.sync
        def _(sp):
            def load(s, b):
                sp.dma_start(x_in[s][:], d["x"][bass.ds(b, 1), :, :].rearrange("o t c -> t (o c)")).then_inc(loads_in[s], 16)
                sp.dma_start(ctx_in[s][:], d["ctx"][bass.ds(b, 1), :, :].rearrange("o t c -> t (o c)")).then_inc(loads_in[s], 16)
                sp.dma_start(ctxT_in[s][:], d["ctxT"][bass.ds(b, 1), :, :].rearrange("o t c -> t (o c)")).then_inc(loads_in[s], 16)

            for dst, src in weight_loads:
                sp.dma_start(dst, src).then_inc(weights_in, 16)
            for s in S:
                load(s, s)
            with sp.Fori(0, ROUNDS - 1) as r:
                for s in S:
                    sp.wait_ge(inputs_ready[s], r + 1)
                    load(s, r * STREAMS + (STREAMS + s))
            for s in S:
                sp.wait_ge(inputs_ready[s], ROUNDS)
                load(s, s)

        @block.gpsimd
        def _(pool):
            def take_inputs(s, value):
                pool.wait_ge(loads_in[s], value)
                pool.sem_inc(passed, 1)
                nc.gpsimd.tensor_copy(x[s][:], x_in[s][:])
                nc.gpsimd.tensor_copy(cx[s][:], ctx_in[s][:])
                nc.gpsimd.tensor_copy(cxT[s][:], ctxT_in[s][:]).then_inc(inputs_ready[s], 1)

            def mask_bias(s, rnd):
                pool.wait_ge(mask_ready[s], rnd + 1)
                nc.gpsimd.tensor_tensor(bias_m[s][:], bias0[:], attended[s][:].unsqueeze(1).to_broadcast([128, HEADS, KEYS]), ALU.mult).then_inc(bias_kept[s], 1)
                pool.wait_ge(bias_kept[s], rnd + 1)
                nc.gpsimd.tensor_tensor(bias_m[s][:], bias_m[s][:], thr[s][:].unsqueeze(1).to_broadcast([128, HEADS, KEYS]), ALU.add).then_inc(bias_ready[s], 1)

            def program(k, it):
                PE_L, ACT_L, DVE_L, POOL_L = LISTS[k]

                def at(steps_, name, s):
                    return steps_.value(name, s, it)

                def blocks(s, p, nk):
                    if p == "x0":
                        pool.wait_ge(act_done, at(ACT_L, "x0.qv", s))
                    else:
                        pool.wait_ge(dve_done, at(DVE_L, "f0.qk", s))
                    nc.gpsimd.tensor_tensor(qblk[s][:], qT[s][:].unsqueeze(1).to_broadcast([128, GROUP, TOK]),
                                            ofgroup[:].unsqueeze(2).to_broadcast([128, GROUP, TOK]), ALU.mult).then_inc(pool_done, POOL_L.did(f"{p}.qblk", s))
                    yield
                    if p == "x0":
                        pool.wait_ge(dve_done, at(DVE_L, "x0.kT", s))
                    nc.gpsimd.tensor_tensor(kblk[s][:, :, 0:nk], kT[s][:, 0:nk].unsqueeze(1).to_broadcast([128, GROUP, nk]),
                                            ingroup[:].unsqueeze(2).to_broadcast([128, GROUP, nk]), ALU.mult).then_inc(pool_done, POOL_L.did(f"{p}.kblk", s))
                    yield

                def rstd(s, p):
                    pool.wait_ge(dve_done, at(DVE_L, f"{p}.eps", s))
                    nc.gpsimd.tensor_tensor(col[s][:, 9:10], col[s][:, 8:9], minus_half[:], ALU.pow).then_inc(pool_done, POOL_L.did(f"{p}.rstd", s))
                    yield

                def first_half(s, rnd):
                    yield from rstd(s, "x0")
                    yield from blocks(s, "x0", KEYS)
                    yield from rstd(s, "f0a")
                    yield from rstd(s, "f0b")
                    yield from blocks(s, "f0", TOK)
                    pool.wait_ge(dve_done, at(DVE_L, "x0.add1", s))
                    mask_bias(s, rnd + 1)
                    pool.wait_ge(bias_ready[s], rnd + 2)
                    pool.sem_inc(pool_done, POOL_L.did("x0.bias", s))
                    yield

                def second_half(s, rnd):
                    for p in ("f0c", "x1", "f1", "x2", "f2"):
                        yield from rstd(s, p)
                    pool.wait_ge(act_done, at(ACT_L, "f2.xT", s))
                    pool.wait_ge(stores_out[s], rnd * 16 + 16)
                    take_inputs(s, rnd * 48 + 96)
                    pool.wait_ge(inputs_ready[s], rnd + 2)
                    pool.sem_inc(pool_done, POOL_L.did("in", s))
                    yield

                return first_half, second_half

            nc.gpsimd.memset(minus_half[:], -0.5).then_inc(consts_done, 1)
            nc.gpsimd.memset(ones[:], 1.0).then_inc(consts_done, 1)
            for s in S:
                nc.gpsimd.memset(vaug[s][:], 1.0).then_inc(consts_done, 1)
            pool.wait_ge(consts_done, 2 + STREAMS)
            pool.wait_ge(setup_act, 3)
            for s in S:
                take_inputs(s, 48)
            for s in S:
                mask_bias(s, 0)
            take_turns(POOL_0, [program(0, 0)[0](s, 0) for s in A])
            pool.wait_ge(pool_done, POOL_0.per_round)
            pool.sem_inc(pool_done, POOL_1.per_round - POOL_0.per_round)
            with pool.Fori(0, ROUNDS) as r:
                first_half, second_half = program(1, r)
                take_turns(POOL_1, [chain(second_half(s, r), first_half(s, r + 1)) for s in A] + [chain(first_half(s, r), second_half(s, r)) for s in B])

        @block.scalar
        def _(act):
            act.wait_ge(setup_pe, SETUP_BIAS)
            act.wait_ge(consts_done, 2 + STREAMS)
            for n in range(3):
                k0, k1 = n * 32, min(KEYS, n * 32 + 32)
                bank = ps[n // 2][:, n % 2, 0:(k1 - k0) * HEADS]
                nc.scalar.copy(bias0[:, :, k0:k1], bank.rearrange("p (k h) -> p h k", h=HEADS)).then_inc(setup_act, 1)
            def program(k, it):
                PE_L, ACT_L, DVE_L, POOL_L = LISTS[k]

                def at(steps_, name, s):
                    return steps_.value(name, s, it)

                def xT(s, p, w=None):
                    act.wait_ge(pe_done, at(PE_L, f"{p}.T", s))
                    if w is None:
                        nc.scalar.copy(xnT[s][:], ps[s][:, 0, 0:TOK]).then_inc(act_done, ACT_L.did(f"{p}.xT", s))
                        yield
                    else:
                        nc.scalar.activation(xnT[s][:], ps[s][:, 0, 0:TOK], ACT.Identity, scale=ln_col[:, w:w + 1], bias=ln_col[:, w + 1:w + 2]).then_inc(act_done, ACT_L.did(f"{p}.xT", s))
                        yield

                def heads(s, p, nk):
                    for hf in range(2):
                        act.wait_ge(dve_done, at(DVE_L, f"{p}.nmax{hf}", s))
                        for h in range(HALF):
                            out = prob[s][:, h * nk:(h + 1) * nk]
                            scores = out if p == "x0" else ps[s][:, h // GROUP, (h % GROUP) * nk:(h % GROUP + 1) * nk]
                            last = nc.scalar.activation(out, scores, ACT.Exp, bias=col[s][:, 16 + h:17 + h])
                        last.then_inc(act_done, ACT_L.did(f"{p}.exp{hf}", s))
                        yield
                        act.wait_ge(pe_done, at(PE_L, f"{p}.PT{hf}", s))
                        nc.scalar.copy(probT[s][0:nk, :], ps[s][0:nk, :, :].rearrange("p b n -> p (b n)")).then_inc(act_done, ACT_L.did(f"{p}.PT{hf}", s))
                        yield
                        act.wait_ge(pe_done, at(PE_L, f"{p}.PV{hf}", s))
                        nc.scalar.copy(yg[s][:, 2 * hf:2 * hf + 2, :], ps[s][:, 0, 0:2 * TOK].rearrange("p (g t) -> p g t", g=2)).then_inc(act_done, ACT_L.did(f"{p}.yg{hf}", s))
                        yield
                    act.wait_ge(pe_done, at(PE_L, f"{p}.yT", s))
                    nc.scalar.copy(yT[s][:], ps[s][:, 1, 0:TOK]).then_inc(act_done, ACT_L.did(f"{p}.yT", s))
                    yield

                def first_half(s, rnd):
                    yield from xT(s, "x0")
                    act.wait_ge(pe_done, at(PE_L, "x0.qkv", s))
                    nc.scalar.activation(qT[s][:], ps[s][:, 0, 0:TOK], ACT.Copy, scale=float(HDIM) ** -0.5)
                    nc.scalar.copy(vaug[s][0:KEYS, :, 0:HDIM], ps[s][0:KEYS, 0, 256:256 + DIM].rearrange("p (h e) -> p h e", h=HEADS)).then_inc(act_done, ACT_L.did("x0.qv", s))
                    yield
                    yield from heads(s, "x0", KEYS)
                    yield from xT(s, "f0b", 0)
                    act.wait_ge(pe_done, at(PE_L, "f0.qkv", s))
                    nc.scalar.copy(vaug[s][:, :, 0:HDIM], ps[s][:, 1, 0:DIM].rearrange("p (h e) -> p h e", h=HEADS)).then_inc(act_done, ACT_L.did("f0.v", s))
                    yield
                    yield from heads(s, "f0", TOK)

                def second_half(s, rnd):
                    yield from xT(s, "f0c", 2)
                    if s % PAIR == 0:
                        pair = (s, s + 1)
                        for e in range(MOE0):
                            for c in range(CHUNKS0):
                                if e >= 2:
                                    act.wait_ge(pe_done, at(PE_L, f"moe.down{e - 2}.1", pair[0]))
                                act.wait_ge(pe_done, at(PE_L, f"moe.gv{e}.{c}", pair[0]))
                                nc.scalar.activation(hidden(pair, e, c), unit_bank(pair, e * CHUNKS0 + c)[:, 0:PAIR * TOK], ACT.Tanh, scale=0.5).then_inc(act_done, ACT_L.did(f"moe.tanh{e}.{c}", pair[0]))
                                yield
                    yield from xT(s, "x1")
                    act.wait_ge(pe_done, at(PE_L, "x1.qkv", s))
                    nc.scalar.activation(qT[s][:], ps[s][:, 0, 0:TOK], ACT.Identity, bias=b_xa1[:, 0:1])
                    nc.scalar.activation(kT[s][:, 0:KEYS], ps[s][:, 0, 128:128 + KEYS], ACT.Identity, bias=b_xa1[:, 1:2])
                    nc.scalar.copy(y[s][0:KEYS, :], ps[s][0:KEYS, 0, 256:256 + DIM]).then_inc(act_done, ACT_L.did("x1.qkv", s))
                    yield
                    act.wait_ge(dve_done, at(DVE_L, "x1.nmax", s))
                    nc.scalar.activation(prob[s][:, 0:KEYS], ps[s][:, 1, 0:KEYS], ACT.Exp, bias=col[s][:, 16:17], accum_out=col[s][:, 17:18]).then_inc(act_done, ACT_L.did("x1.exp", s))
                    yield
                    act.wait_ge(pe_done, at(PE_L, "x1.PT", s))
                    nc.scalar.copy(probT[s][0:KEYS, 0:TOK], ps[s][0:KEYS, 0, 0:TOK]).then_inc(act_done, ACT_L.did("x1.PT", s))
                    yield
                    yield from xT(s, "f1")
                    act.wait_ge(pe_done, at(PE_L, "f1.up", s))
                    for c in range(FF1 // CH):
                        last = nc.scalar.activation(prob[s][:, c * TOK:(c + 1) * TOK], ps[s][:, 0, c * TOK:(c + 1) * TOK], ACT.Identity, scale=conv1_col[:, c, 1:2], bias=conv1_col[:, c, 3:4])
                    last.then_inc(act_done, ACT_L.did("f1.mid", s))
                    yield
                    act.wait_ge(dve_done, at(DVE_L, "f1.taps", s))
                    nc.scalar.activation(prob[s][:, BANK:2 * BANK], prob[s][:, 0:BANK], ACT.Tanh, scale=0.5).then_inc(act_done, ACT_L.did("f1.tanh", s))
                    yield
                    act.wait_ge(pe_done, at(PE_L, "f1.uqT", s))
                    nc.scalar.copy(probT[s][:, 256:512].bitcast(BF16), ps[s][:, 1, 0:256].bitcast(BF16)).then_inc(act_done, ACT_L.did("f1.uqT", s))
                    yield
                    act.wait_ge(pe_done, at(PE_L, "x2.T", s))
                    nc.scalar.activation(qT[s][:], ps[s][:, 0, 0:TOK], ACT.Identity, scale=sim_col[:, 2:3], bias=sim_col[:, 1:2])
                    nc.scalar.copy(xnT[s][:], ps[s][:, 0, 0:TOK]).then_inc(act_done, ACT_L.did("x2.xT", s))
                    yield
                    act.wait_ge(dve_done, at(DVE_L, "x2.score", s))
                    nc.scalar.activation(prob[s][:, 0:KEYS], ps[s][:, 1, 0:KEYS], ACT.Exp, bias=col[s][:, 16:17], accum_out=col[s][:, 17:18]).then_inc(act_done, ACT_L.did("x2.exp", s))
                    yield
                    act.wait_ge(pe_done, at(PE_L, "x2.PT", s))
                    nc.scalar.copy(probT[s][0:KEYS, 0:TOK], ps[s][0:KEYS, 0, 0:TOK]).then_inc(act_done, ACT_L.did("x2.PT", s))
                    yield
                    act.wait_ge(dve_done, at(DVE_L, "x2.negM", s))
                    nc.scalar.activation(col[s][:, 22:23], col[s][:, 19:20], ACT.Exp, bias=col[s][:, 21:22]).then_inc(act_done, ACT_L.did("x2.p", s))
                    yield
                    act.wait_ge(pe_done, at(PE_L, "x2.hq", s))
                    nc.scalar.copy(kT[s][:], ps[s][:, 0, 0:TOK])
                    act.wait_ge(dve_done, at(DVE_L, "x2.hc", s))
                    nc.scalar.activation(yT[s][:], xnT[s][:], ACT.Copy, scale=col[s][:, 24:25]).then_inc(act_done, ACT_L.did("x2.feat", s))
                    yield
                    act.wait_ge(dve_done, at(DVE_L, "f2.x", s))
                    act.dma_start(x_mid[bass.ds(rnd * STREAMS + s, 1), :, :].rearrange("o t c -> t (o c)"), x[s][:]).then_inc(stores_out[s], 16)
                    act.wait_ge(pe_done, at(PE_L, "f2.T", s))
                    act.sem_inc(passed, 1)
                    nc.scalar.copy(xnT_all[:, bass.ds((rnd * STREAMS + s) * TOK, TOK)], ps[s][:, 0, 0:TOK]).then_inc(act_done, ACT_L.did("f2.xT", s))
                    yield

                return first_half, second_half

            take_turns(ACT_0, [program(0, 0)[0](s, 0) for s in A])
            act.wait_ge(act_done, ACT_0.per_round)
            act.sem_inc(act_done, ACT_1.per_round - ACT_0.per_round)
            with act.Fori(0, ROUNDS) as r:
                first_half, second_half = program(1, r)
                take_turns(ACT_1, [chain(second_half(s, r), first_half(s, r + 1)) for s in A] + [chain(first_half(s, r), second_half(s, r)) for s in B])

            for s in S:
                act.wait_ge(stores_out[s], 16 * ROUNDS)

        @block.tensor
        def _(pe):
            pe.wait_ge(weights_in, 16 * len(weight_loads))
            pe.wait_ge(consts_done, 2 + STREAMS)
            for k in range(KEYS):
                n, j = k // 32, k % 32
                last = nc.tensor.matmul(ps[n // 2][:, n % 2, j * HEADS:(j + 1) * HEADS], prob[0][0:BUCKETS, 128 + KEYS - 1 - k:128 + KEYS - 1 - k + TOK],
                                        prob[0][0:BUCKETS, 384:384 + HEADS], start=True, stop=True)
            last.then_inc(setup_pe, 1)
            pe.wait_ge(setup_dve, SETUP_SUMS)
            nc.tensor.matmul(ps[3][:, 0, 0:2], ones[:], prep[:, 0:2], start=True, stop=True).then_inc(setup_pe, 1)
            pe.wait_ge(setup_dve, SETUP_DVE)
            pe.wait_ge(setup_act, 3)
            def program(k, it):
                PE_L, ACT_L, DVE_L, POOL_L = LISTS[k]

                def at(steps_, name, s):
                    return steps_.value(name, s, it)

                def transpose_xn(s, p):
                    pe.wait_ge(dve_done, at(DVE_L, f"{p}.norm", s))
                    nc.tensor.transpose(ps[s][:, 0, 0:TOK], xn[s][:], ident[:]).then_inc(pe_done, PE_L.did(f"{p}.T", s))
                    yield

                def heads(s, p, nk, w_out):
                    for hf in range(2):
                        if hf == 0:
                            pe.wait_ge(pool_done, at(POOL_L, f"{p}.kblk", s))
                            pe.wait_ge(act_done, at(ACT_L, "x0.qv" if p == "x0" else "f0.v", s))
                        else:
                            pe.wait_ge(act_done, at(ACT_L, f"{p}.yg0", s))
                        for b in range(2):
                            last = nc.tensor.matmul(ps[s][:, b, 0:GROUP * nk], qblk[s][:, 2 * hf + b, :], kblk[s][:, :, 0:nk], start=True, stop=(p == "x0"))
                        if p == "f0":
                            for b in range(2):
                                last = nc.tensor.matmul(ps[s][:, b, :], ident_bf[:], causal_bf[:].unsqueeze(1).to_broadcast([128, GROUP, TOK]), start=False, stop=True)
                        last.then_inc(pe_done, PE_L.did(f"{p}.S{hf}", s))
                        yield
                        pe.wait_ge(act_done, at(ACT_L, f"{p}.exp{hf}", s))
                        for h in range(HALF):
                            last = nc.tensor.transpose(ps[s][0:nk, h // GROUP, (h % GROUP) * TOK:(h % GROUP + 1) * TOK], prob[s][:, h * nk:(h + 1) * nk], ident[:])
                        last.then_inc(pe_done, PE_L.did(f"{p}.PT{hf}", s))
                        yield
                        pe.wait_ge(act_done, at(ACT_L, f"{p}.PT{hf}", s))
                        for h in range(HALF):
                            g, j = h // GROUP, h % GROUP
                            last = nc.tensor.matmul(ps[s][VPAD * j:VPAD * (j + 1), 0, g * TOK:(g + 1) * TOK], vaug[s][0:nk, HALF * hf + h, :], probT[s][0:nk, h * TOK:(h + 1) * TOK],
                                                    start=True, stop=True, tile_position=(0, VPAD * j))
                        last.then_inc(pe_done, PE_L.did(f"{p}.PV{hf}", s))
                        yield
                    pe.wait_ge(act_done, at(ACT_L, f"{p}.yg1", s))
                    for g in range(GROUP):
                        last = nc.tensor.transpose(ps[s][:, 1, g * TOK:(g + 1) * TOK], yg[s][:, g, :], ident[:])
                    last.then_inc(pe_done, PE_L.did(f"{p}.ygT", s))
                    yield
                    pe.wait_ge(dve_done, at(DVE_L, f"{p}.y", s))
                    nc.tensor.transpose(ps[s][:, 1, 0:TOK], y[s][:], ident[:]).then_inc(pe_done, PE_L.did(f"{p}.yT", s))
                    yield
                    pe.wait_ge(act_done, at(ACT_L, f"{p}.yT", s))
                    nc.tensor.matmul(ps[s][:, 0, 0:DIM], yT[s][:], w_out, start=True, stop=True).then_inc(pe_done, PE_L.did(f"{p}.o", s))
                    yield

                def gate_and_value(pair, e):
                    for c in range(CHUNKS0):
                        u = e * CHUNKS0 + c
                        if u == 0:
                            pe.wait_ge(act_done, at(ACT_L, "f0c.xT", pair[1]))
                        if u < 3:
                            pe.wait_ge(dve_done, at(DVE_L, "moe.pick", pair[u // 2]))
                        else:
                            pe.wait_ge(dve_done, at(DVE_L, f"moe.act{(u - 3) // CHUNKS0}.{(u - 3) % CHUNKS0}", pair[0]))
                        for v in range(2):
                            last = nc.tensor.matmul(unit_bank(pair, u)[:, v * PAIR * TOK:(v + 1) * PAIR * TOK], w_gv0[:, e, v * FF0 + c * CH:v * FF0 + (c + 1) * CH],
                                                    xnT_4[:, pair[0]:pair[0] + PAIR, :].rearrange("p s t -> p (s t)"), start=True, stop=True)
                        last.then_inc(pe_done, PE_L.did(f"moe.gv{e}.{c}", pair[0]))
                        yield

                def down(pair, e):
                    for n, s in enumerate(pair):
                        if n == 0:
                            pe.wait_ge(dve_done, at(DVE_L, f"moe.act{e}.{CHUNKS0 - 1}", pair[0]))
                            pe.wait_ge(dve_done, at(DVE_L, *(("moe.pick", pair[1]) if e == 0 else (f"moe.add{e - 1}.1", pair[0]))))
                        for c in range(CHUNKS0):
                            last = nc.tensor.matmul(ps[pair[1]][:, 1, n * DIM:(n + 1) * DIM], hidden(pair, e, c)[:, n * TOK:(n + 1) * TOK], w_dn0[:, e, c, :], start=(c == 0), stop=(c == CHUNKS0 - 1))
                        last.then_inc(pe_done, PE_L.did(f"moe.down{e}.{n}", pair[0]))
                        yield

                def first_half(s, rnd):
                    yield from transpose_xn(s, "x0")
                    pe.wait_ge(act_done, at(ACT_L, "x0.xT", s))
                    nc.tensor.matmul(ps[s][:, 0, 0:TOK], w_xa0[:, 0, :], xnT[s][:], start=True, stop=True)
                    nc.tensor.matmul(ps[s][:, 0, 128:128 + KEYS], w_xa0[:, 1, :], cxT[s][:], start=True, stop=True)
                    nc.tensor.matmul(ps[s][0:KEYS, 0, 256:256 + DIM], cxT[s][:], w_xa0[:, 2, :], start=True, stop=True).then_inc(pe_done, PE_L.did("x0.qkv", s))
                    yield
                    yield from heads(s, "x0", KEYS, w_xa0[:, 3, :])
                    yield from transpose_xn(s, "f0b")
                    pe.wait_ge(dve_done, at(DVE_L, "f0.conv0", s))
                    for n in range(4):
                        nc.tensor.matmul(ps[s][:, 0, n * TOK:(n + 1) * TOK], w_at0[:, n, :], yT[s][:], start=True, stop=True)
                    nc.tensor.matmul(ps[s][:, 1, 0:DIM], yT[s][:], w_at0[:, 4, :], start=True, stop=True).then_inc(pe_done, PE_L.did("f0.qkv", s))
                    yield
                    yield from heads(s, "f0", TOK, w_pr0[:])

                def second_half(s, rnd):
                    yield from transpose_xn(s, "f0c")
                    pe.wait_ge(act_done, at(ACT_L, "f0c.xT", s))
                    nc.tensor.matmul(ps[s][:, 1, 0:MOE0], xnT[s][:], w_ro0[:], start=True, stop=True).then_inc(pe_done, PE_L.did("moe.route", s))
                    yield
                    if s % PAIR == 0:
                        pair = (s, s + 1)
                        yield from gate_and_value(pair, 0)
                        for e in range(MOE0):
                            if e + 1 < MOE0:
                                yield from gate_and_value(pair, e + 1)
                            yield from down(pair, e)
                    yield from transpose_xn(s, "x1")
                    pe.wait_ge(act_done, at(ACT_L, "x1.xT", s))
                    nc.tensor.matmul(ps[s][:, 0, 0:TOK], w_xa1[:, 0, :], xnT[s][:], start=True, stop=True)
                    nc.tensor.matmul(ps[s][:, 0, 128:128 + KEYS], w_xa1[:, 1, :], cxT[s][:], start=True, stop=True)
                    nc.tensor.matmul(ps[s][0:KEYS, 0, 256:256 + DIM], cxT[s][:], w_xa1[:, 2, :], start=True, stop=True).then_inc(pe_done, PE_L.did("x1.qkv", s))
                    yield
                    pe.wait_ge(act_done, at(ACT_L, "x1.qkv", s))
                    nc.tensor.matmul(ps[s][:, 1, 0:KEYS], qT[s][:], kT[s][:, 0:KEYS], start=True, stop=True).then_inc(pe_done, PE_L.did("x1.S", s))
                    yield
                    pe.wait_ge(act_done, at(ACT_L, "x1.exp", s))
                    nc.tensor.transpose(ps[s][0:KEYS, 0, 0:TOK], prob[s][:, 0:KEYS], ident[:]).then_inc(pe_done, PE_L.did("x1.PT", s))
                    yield
                    pe.wait_ge(act_done, at(ACT_L, "x1.PT", s))
                    nc.tensor.matmul(ps[s][:, 1, 0:DIM], probT[s][0:KEYS, 0:TOK], y[s][0:KEYS, :], start=True, stop=True).then_inc(pe_done, PE_L.did("x1.y", s))
                    yield
                    pe.wait_ge(dve_done, at(DVE_L, "f1.xq", s))
                    nc.tensor.transpose(ps[s][:, 0, 0:TOK], xn[s][:], ident[:]).then_inc(pe_done, PE_L.did("f1.T", s))
                    yield
                    pe.wait_ge(act_done, at(ACT_L, "f1.xT", s))
                    for c in range(FF1 // CH):
                        last = nc.tensor.matmul(ps[s][:, 0, c * TOK:(c + 1) * TOK], w_up1[:, c * CH:(c + 1) * CH], xnT[s][:], start=True, stop=True)
                    last.then_inc(pe_done, PE_L.did("f1.up", s))
                    yield
                    pe.wait_ge(dve_done, at(DVE_L, "f1.silu", s))
                    for c in range(FF1 // CH):
                        last = nc.tensor.transpose(ps[s][:, 0, c * CH:(c + 1) * CH], prob[s][:, c * TOK:(c + 1) * TOK], ident[:])
                    last.then_inc(pe_done, PE_L.did("f1.uT", s))
                    yield
                    pe.wait_ge(dve_done, at(DVE_L, "f1.uq", s))
                    for c in range(FF1 // CH):
                        last = nc.tensor.transpose(ps[s][:, 1, 0:256].bitcast(BF16)[:, c * TOK:(c + 1) * TOK], probT[s][:, 0:256].bitcast(BF16)[:, c * CH:(c + 1) * CH], ident_bf[:])
                    last.then_inc(pe_done, PE_L.did("f1.uqT", s))
                    yield
                    pe.wait_ge(act_done, at(ACT_L, "f1.uqT", s))
                    for c in range(FF1 // CH):
                        last = nc.tensor.matmul(ps[s][:, 0, 0:DIM], probT[s][:, 256:512].bitcast(BF16)[:, c * TOK:(c + 1) * TOK], w_dn1_q[:, c, :], start=(c == 0), stop=(c == FF1 // CH - 1))
                    last.then_inc(pe_done, PE_L.did("f1.down", s))
                    yield
                    yield from transpose_xn(s, "x2")
                    pe.wait_ge(act_done, at(ACT_L, "x2.xT", s))
                    nc.tensor.matmul(ps[s][:, 1, 0:KEYS], qT[s][:], cxT[s][:], start=True, stop=True)
                    nc.tensor.matmul(ps[s][:, 1, 80:81], xnT[s][:], sim_col[:, 0:1], start=True, stop=True).then_inc(pe_done, PE_L.did("x2.S", s))
                    yield
                    pe.wait_ge(dve_done, at(DVE_L, "x2.P", s))
                    nc.tensor.transpose(ps[s][0:KEYS, 0, 0:TOK], prob[s][:, 0:KEYS], ident[:])
                    nc.tensor.transpose(ps[s][0:1, 0, 128:128 + TOK], col[s][:, 19:20], ident[:]).then_inc(pe_done, PE_L.did("x2.PT", s))
                    yield
                    pe.wait_ge(dve_done, at(DVE_L, "x2.M", s))
                    nc.tensor.matmul(ps[s][:, 0, 256:257], ones[0:1, :], col[s][0:1, 20:21], start=True, stop=True).then_inc(pe_done, PE_L.did("x2.M", s))
                    yield
                    pe.wait_ge(act_done, at(ACT_L, "x2.p", s))
                    nc.tensor.matmul(ps[s][:, 1, 0:1], xn[s][:], col[s][:, 22:23], start=True, stop=True)
                    nc.tensor.matmul(ps[s][:, 1, 2:3], ones[:], col[s][:, 22:23], start=True, stop=True)
                    nc.tensor.matmul(ps[s][:, 0, 0:TOK], cx[s][:], probT[s][0:KEYS, 0:TOK], start=True, stop=True).then_inc(pe_done, PE_L.did("x2.hq", s))
                    yield
                    pe.wait_ge(act_done, at(ACT_L, "x2.feat", s))
                    pe.wait_ge(dve_done, at(DVE_L, "x2.ehq", s))
                    for n, f in enumerate((xnT, kT, qT, yT)):
                        last = nc.tensor.matmul(ps[s][:, 1, 0:DIM], f[s][:], w_qv2[:, n, :], start=(n == 0), stop=(n == 3))
                    last.then_inc(pe_done, PE_L.did("x2.out", s))
                    yield
                    yield from transpose_xn(s, "f2")

                return first_half, second_half

            take_turns(PE_0, [program(0, 0)[0](s, 0) for s in A])
            pe.wait_ge(pe_done, PE_0.per_round)
            pe.sem_inc(pe_done, PE_1.per_round - PE_0.per_round)
            with pe.Fori(0, ROUNDS) as r:
                first_half, second_half = program(1, r)
                take_turns(PE_1, [chain(second_half(s, r), first_half(s, r + 1)) for s in A] + [chain(first_half(s, r), second_half(s, r)) for s in B])

        @block.vector
        def _(dve):
            dve.wait_ge(weights_in, 16 * len(weight_loads))
            nc.vector.tensor_copy(causal_bf[:], prob[0][:, 0:128]).then_inc(setup_dve, 1)
            nc.vector.tensor_copy(ident_bf[:], ident[:]).then_inc(setup_dve, 1)
            flat = w_dn1[:].rearrange("p k n -> p (k n)")
            nc.vector.tensor_reduce(prep[:, 0:1], w_up1[:], X_AXIS, ALU.add, apply_absolute_value=True).then_inc(setup_dve, 1)
            nc.vector.tensor_reduce(prep[:, 1:2], flat, X_AXIS, ALU.add, apply_absolute_value=True).then_inc(setup_dve, 1)
            dve.wait_ge(setup_pe, 2)
            nc.vector.tensor_scalar(prep[:, 2:4], ps[3][:, 0, 0:2], 1.0 / (FF1 * DIM), 1e-5, ALU.mult, ALU.max).then_inc(setup_dve, 1)
            dve.wait_ge(setup_dve, 5)
            nc.vector.reciprocal(prep[:, 4:6], prep[:, 2:4]).then_inc(setup_dve, 1)
            dve.wait_ge(setup_dve, 6)
            for n, (w, out) in enumerate(((w_up1[:], w_up1[:]), (flat, w_dn1_q[:].rearrange("p k n -> p (k n)")))):
                nc.vector.tensor_scalar(w, w, prep[:, 4 + n:5 + n], ROUND, ALU.mult, ALU.add).then_inc(setup_dve, 1)
                dve.wait_ge(setup_dve, 7 + 3 * n)
                nc.vector.tensor_scalar(w, w, ROUND, 1.0, ALU.subtract, ALU.min).then_inc(setup_dve, 1)
                dve.wait_ge(setup_dve, 8 + 3 * n)
                if n == 0:
                    nc.vector.tensor_scalar(out, w, -1.0, prep[:, 2:3], ALU.max, ALU.mult).then_inc(setup_dve, 1)
                else:
                    nc.vector.tensor_scalar(out, w, -1.0, None, ALU.max).then_inc(setup_dve, 1)
                dve.wait_ge(setup_dve, 9 + 3 * n)
            nc.vector.tensor_scalar(prep[:, 6:7], prep[:, 3:4], 1.0 / 127.0, None, ALU.mult).then_inc(setup_dve, 1)

            def next_mask(s, b, made):
                nc.vector.tensor_copy(attended[s][:], mask[:, bass.ds(b * KEYS, KEYS)]).then_inc(mask_made[s], 1)
                dve.wait_ge(mask_made[s], made)
                nc.vector.tensor_scalar(thr[s][:], attended[s][:], 1e9, -1e9, ALU.mult, ALU.add).then_inc(mask_ready[s], 1)

            nc.vector.memset(mask_words[:, BATCH * KEYS // 4:], 0).then_inc(mask_tail, 1)
            dve.wait_ge(mask_tail, 1)
            for s in S:
                next_mask(s, s, 1)
            def program(k, it):
                PE_L, ACT_L, DVE_L, POOL_L = LISTS[k]

                def at(steps_, name, s):
                    return steps_.value(name, s, it)

                def after(name, s):
                    dve.wait_ge(dve_done, at(DVE_L, name, s))

                def norm(s, p, src, dst, prev=None, ready=None):
                    if ready is not None:
                        ready(s)
                    else:
                        after(prev, s)
                    nc.vector.bn_stats(col[s][:, 0:6], src[s][:]).then_inc(dve_done, DVE_L.did(f"{p}.stats", s))
                    yield
                    after(f"{p}.stats", s)
                    dve.sem_inc(passed, 1)
                    nc.vector.bn_aggr(col[s][:, 6:8], col[s][:, 0:6]).then_inc(dve_done, DVE_L.did(f"{p}.aggr", s))
                    yield
                    after(f"{p}.aggr", s)
                    nc.vector.tensor_scalar(col[s][:, 8:9], col[s][:, 7:8], LN_EPS, None, ALU.add).then_inc(dve_done, DVE_L.did(f"{p}.eps", s))
                    yield
                    dve.wait_ge(pool_done, at(POOL_L, f"{p}.rstd", s))
                    nc.vector.tensor_scalar(dst[s][:], src[s][:], col[s][:, 6:7], col[s][:, 9:10], ALU.subtract, ALU.mult).then_inc(dve_done, DVE_L.did(f"{p}.norm", s))
                    yield

                def heads(s, p, nk, rnd):
                    for hf in range(2):
                        if p == "x0":
                            dve.wait_ge(pe_done, at(PE_L, f"{p}.S{hf}", s))
                            dve.wait_ge(bias_ready[s], rnd + 1)
                            nc.vector.tensor_tensor(prob[s][:, 0:HALF * nk].rearrange("p (b n) -> p b n", b=2), ps[s][:, :, 0:GROUP * nk],
                                                    bias_m[s][:, HALF * hf:HALF * (hf + 1), :].rearrange("p (b h) k -> p b (h k)", b=2), ALU.add).then_inc(dve_done, DVE_L.did(f"{p}.add{hf}", s))
                            yield
                        if p == "x0":
                            if hf == 1:
                                next_mask(s, (rnd + 1) * STREAMS + s, rnd + 2)
                            after(f"{p}.add{hf}", s)
                            scores = prob[s][:, 0:HALF * nk].rearrange("p (h k) -> p h k", h=HALF)
                        else:
                            dve.wait_ge(pe_done, at(PE_L, f"{p}.S{hf}", s))
                            scores = ps[s][:].rearrange("p b (h k) -> p (b h) k", h=GROUP)
                        nc.vector.tensor_reduce(col[s][:, 16:16 + HALF], scores, X_AXIS, ALU.max, negate=True).then_inc(dve_done, DVE_L.did(f"{p}.nmax{hf}", s))
                        yield
                    dve.wait_ge(pe_done, at(PE_L, f"{p}.ygT", s))
                    out = ps[s][:, 1, :].rearrange("p (h e) -> p h e", h=HEADS)
                    nc.vector.reciprocal(col[s][:, 24:24 + HEADS].unsqueeze(2), out[:, :, HDIM:HDIM + 1]).then_inc(dve_done, DVE_L.did(f"{p}.rden", s))
                    yield
                    after(f"{p}.rden", s)
                    out = ps[s][:, 1, :].rearrange("p (h e) -> p h e", h=HEADS)
                    nc.vector.tensor_tensor(y[s][:].rearrange("p (h e) -> p h e", h=HEADS), out[:, :, 0:HDIM],
                                            col[s][:, 24:24 + HEADS].unsqueeze(2).to_broadcast([128, HEADS, HDIM]), ALU.mult).then_inc(dve_done, DVE_L.did(f"{p}.y", s))
                    yield

                def add_expert(pair, e):
                    for n, s in enumerate(pair):
                        if n == 0:
                            dve.wait_ge(pe_done, at(PE_L, f"moe.down{e}.1", pair[0]))
                        if e == MOE0 - 1:
                            after(f"moe.add{e - 1}.{n}", pair[0])
                        nc.vector.scalar_tensor_tensor(h0[s][:], ps[pair[1]][:, 1, n * DIM:(n + 1) * DIM], col[s][:, 24 + e:25 + e], h0[s][:], ALU.mult, ALU.add).then_inc(dve_done, DVE_L.did(f"moe.add{e}.{n}", pair[0]))
                        yield

                def first_half(s, rnd):
                    yield from norm(s, "x0", x, xn, ready=lambda s: dve.wait_ge(inputs_ready[s], rnd + 1))
                    dve.wait_ge(act_done, at(ACT_L, "x0.qv", s))
                    nc.vector.tensor_tensor(kT[s][:, 0:KEYS], ps[s][:, 0, 128:128 + KEYS], attended[s][:], ALU.mult).then_inc(dve_done, DVE_L.did("x0.kT", s))
                    yield
                    yield from heads(s, "x0", KEYS, rnd)
                    dve.wait_ge(pe_done, at(PE_L, "x0.o", s))
                    nc.vector.tensor_tensor(x[s][:], ps[s][:, 0, 0:DIM], x[s][:], ALU.add).then_inc(dve_done, DVE_L.did("x0.x", s))
                    yield
                    yield from norm(s, "f0a", x, h0, "x0.x")
                    yield from norm(s, "f0b", h0, xn, "f0a.norm")
                    for n, (name, tap) in enumerate((("f0.conv2", 2), ("f0.conv1", 1), ("f0.conv0", 0))):
                        if tap == 2:
                            dve.wait_ge(act_done, at(ACT_L, "f0b.xT", s))
                            nc.vector.tensor_scalar(yT[s][:], xnT[s][:], conv0_col[:, 2:3], None, ALU.mult).then_inc(dve_done, DVE_L.did(name, s))
                            yield
                        else:
                            after(f"f0.conv{tap + 1}", s)
                            sh = 2 - tap
                            nc.vector.scalar_tensor_tensor(yT[s][:, sh:], xnT[s][:, 0:TOK - sh], conv0_col[:, tap:tap + 1], yT[s][:, sh:], ALU.mult, ALU.add).then_inc(dve_done, DVE_L.did(name, s))
                            yield
                    dve.wait_ge(pe_done, at(PE_L, "f0.qkv", s))
                    nc.vector.tensor_tensor(prob[s][:, 0:BANK].rearrange("p (n t) -> p n t", n=4), ps[s][:, 0, :].rearrange("p (n t) -> p n t", n=4), rope[:], ALU.mult).then_inc(dve_done, DVE_L.did("f0.rope", s))
                    yield
                    after("f0.rope", s)
                    nc.vector.tensor_tensor(qT[s][:], prob[s][:, 0:128], prob[s][:, 256:384], ALU.add)
                    nc.vector.tensor_tensor(kT[s][:], prob[s][:, 128:256], prob[s][:, 384:512], ALU.add).then_inc(dve_done, DVE_L.did("f0.qk", s))
                    yield
                    yield from heads(s, "f0", TOK, rnd)
                    dve.wait_ge(pe_done, at(PE_L, "f0.o", s))
                    nc.vector.tensor_tensor(h0[s][:], ps[s][:, 0, 0:DIM], h0[s][:], ALU.add).then_inc(dve_done, DVE_L.did("f0.x", s))
                    yield

                def second_half(s, rnd):
                    yield from norm(s, "f0c", h0, xn, ready=lambda s: dve.wait_ge(dve_done, (DVE_L.value_before if s in A else DVE_L.value)("f0.x", s, it)))
                    dve.wait_ge(pe_done, at(PE_L, "moe.route", s))
                    nc.vector.tensor_reduce(col[s][:, 16:17], ps[s][:, 1, 0:MOE0], X_AXIS, ALU.max).then_inc(dve_done, DVE_L.did("moe.max", s))
                    yield
                    after("moe.max", s)
                    nc.vector.scalar_tensor_tensor(col[s][:, 20:24], ps[s][:, 1, 0:MOE0], col[s][:, 16:17], first[:, 0:MOE0], ALU.is_equal, ALU.mult).then_inc(dve_done, DVE_L.did("moe.eq", s))
                    yield
                    after("moe.eq", s)
                    nc.vector.tensor_reduce(col[s][:, 17:18], col[s][:, 20:24], X_AXIS, ALU.max).then_inc(dve_done, DVE_L.did("moe.first", s))
                    yield
                    after("moe.first", s)
                    nc.vector.tensor_scalar(col[s][:, 24:28], col[s][:, 20:24], col[s][:, 17:18], None, ALU.is_equal).then_inc(dve_done, DVE_L.did("moe.pick", s))
                    yield
                    if s % PAIR == 0:
                        pair = (s, s + 1)
                        for e in range(MOE0):
                            for c in range(CHUNKS0):
                                bank = unit_bank(pair, e * CHUNKS0 + c)
                                dve.wait_ge(act_done, at(ACT_L, f"moe.tanh{e}.{c}", pair[0]))
                                nc.vector.scalar_tensor_tensor(hidden(pair, e, c), hidden(pair, e, c), 1.0, bank[:, 0:PAIR * TOK], ALU.add, ALU.mult).then_inc(dve_done, DVE_L.did(f"moe.silu{e}.{c}", pair[0]))
                                yield
                                dve.wait_ge(dve_done, at(DVE_L, f"moe.silu{e}.{c}", pair[0]))
                                nc.vector.scalar_tensor_tensor(hidden(pair, e, c), hidden(pair, e, c), 0.5, bank[:, PAIR * TOK:], ALU.mult, ALU.mult).then_inc(dve_done, DVE_L.did(f"moe.act{e}.{c}", pair[0]))
                                yield
                            if e >= 1:
                                yield from add_expert(pair, e - 1)
                        yield from add_expert(pair, MOE0 - 1)
                    after(f"moe.add{MOE0 - 1}.{s % PAIR}", s - s % PAIR)
                    nc.vector.tensor_tensor(x[s][:], x[s][:], h0[s][:], ALU.add).then_inc(dve_done, DVE_L.did("moe.x", s))
                    yield
                    yield from norm(s, "x1", x, xn, "moe.x")
                    dve.wait_ge(pe_done, at(PE_L, "x1.S", s))
                    nc.vector.tensor_reduce(col[s][:, 16:17], ps[s][:, 1, 0:KEYS], X_AXIS, ALU.max, negate=True).then_inc(dve_done, DVE_L.did("x1.nmax", s))
                    yield
                    dve.wait_ge(act_done, at(ACT_L, "x1.exp", s))
                    nc.vector.reciprocal(col[s][:, 18:19], col[s][:, 17:18]).then_inc(dve_done, DVE_L.did("x1.rden", s))
                    yield
                    dve.wait_ge(pe_done, at(PE_L, "x1.y", s))
                    after("x1.rden", s)
                    nc.vector.scalar_tensor_tensor(x[s][:], ps[s][:, 1, 0:DIM], col[s][:, 18:19], x[s][:], ALU.mult, ALU.add).then_inc(dve_done, DVE_L.did("x1.x", s))
                    yield
                    after("x1.x", s)
                    nc.vector.tensor_tensor(x[s][:], x[s][:], bv1[:], ALU.add).then_inc(dve_done, DVE_L.did("x1.bv", s))
                    yield
                    yield from norm(s, "f1", x, xn, "x1.bv")
                    after("f1.norm", s)
                    nc.vector.tensor_reduce(col[s][:, 16:17], xn[s][:], X_AXIS, ALU.max, apply_absolute_value=True).then_inc(dve_done, DVE_L.did("f1.amax", s))
                    yield
                    after("f1.amax", s)
                    nc.vector.tensor_scalar(col[s][:, 17:18], col[s][:, 16:17], 1e-5, 1.0 / 127.0, ALU.max, ALU.mult).then_inc(dve_done, DVE_L.did("f1.inv", s))
                    yield
                    after("f1.inv", s)
                    nc.vector.reciprocal(col[s][:, 18:19], col[s][:, 17:18]).then_inc(dve_done, DVE_L.did("f1.scale", s))
                    yield
                    after("f1.scale", s)
                    nc.vector.tensor_scalar(xn[s][:], xn[s][:], col[s][:, 18:19], ROUND, ALU.mult, ALU.add).then_inc(dve_done, DVE_L.did("f1.round", s))
                    yield
                    after("f1.round", s)
                    nc.vector.tensor_scalar(xn[s][:], xn[s][:], ROUND, col[s][:, 17:18], ALU.subtract, ALU.mult).then_inc(dve_done, DVE_L.did("f1.xq", s))
                    yield
                    dve.wait_ge(act_done, at(ACT_L, "f1.mid", s))
                    for c in range(FF1 // CH):
                        a = c * TOK
                        last = nc.vector.scalar_tensor_tensor(prob[s][:, a + 1:a + TOK], ps[s][:, 0, a:a + TOK - 1], conv1_col[:, c, 0:1], prob[s][:, a + 1:a + TOK], ALU.mult, ALU.add)
                    last.then_inc(dve_done, DVE_L.did("f1.tap0", s))
                    yield
                    after("f1.tap0", s)
                    for c in range(FF1 // CH):
                        a = c * TOK
                        last = nc.vector.scalar_tensor_tensor(prob[s][:, a:a + TOK - 1], ps[s][:, 0, a + 1:a + TOK], conv1_col[:, c, 2:3], prob[s][:, a:a + TOK - 1], ALU.mult, ALU.add)
                    last.then_inc(dve_done, DVE_L.did("f1.taps", s))
                    yield
                    dve.wait_ge(act_done, at(ACT_L, "f1.tanh", s))
                    nc.vector.scalar_tensor_tensor(prob[s][:, 0:BANK], prob[s][:, BANK:2 * BANK], 1.0, prob[s][:, 0:BANK], ALU.add, ALU.mult).then_inc(dve_done, DVE_L.did("f1.silu", s))
                    yield
                    dve.wait_ge(pe_done, at(PE_L, "f1.uT", s))
                    nc.vector.tensor_reduce(col[s][:, 16:17], ps[s][:, 0, :], X_AXIS, ALU.max, apply_absolute_value=True).then_inc(dve_done, DVE_L.did("f1.uamax", s))
                    yield
                    after("f1.uamax", s)
                    nc.vector.tensor_scalar(col[s][:, 17:18], col[s][:, 16:17], 0.5, 1e-5, ALU.mult, ALU.max).then_inc(dve_done, DVE_L.did("f1.uclip", s))
                    yield
                    after("f1.uclip", s)
                    nc.vector.reciprocal(col[s][:, 18:19], col[s][:, 17:18]).then_inc(dve_done, DVE_L.did("f1.urec", s))
                    yield
                    after("f1.urec", s)
                    nc.vector.tensor_scalar(col[s][:, 19:20], col[s][:, 18:19], 127.0 / 2, None, ALU.mult)
                    nc.vector.tensor_scalar(col[s][:, 20:21], col[s][:, 17:18], prep[:, 6:7], None, ALU.mult).then_inc(dve_done, DVE_L.did("f1.uscale", s))
                    yield
                    after("f1.uscale", s)
                    nc.vector.tensor_scalar(prob[s][:, 0:BANK], ps[s][:, 0, :], col[s][:, 19:20], ROUND, ALU.mult, ALU.add).then_inc(dve_done, DVE_L.did("f1.uround", s))
                    yield
                    after("f1.uround", s)
                    nc.vector.tensor_scalar(probT[s][:, 0:256].bitcast(BF16), prob[s][:, 0:BANK], ROUND, None, ALU.subtract).then_inc(dve_done, DVE_L.did("f1.uq", s))
                    yield
                    dve.wait_ge(pe_done, at(PE_L, "f1.down", s))
                    nc.vector.scalar_tensor_tensor(x[s][:], ps[s][:, 0, 0:DIM], col[s][:, 20:21], x[s][:], ALU.mult, ALU.add).then_inc(dve_done, DVE_L.did("f1.x", s))
                    yield
                    yield from norm(s, "x2", x, xn, "f1.x")
                    dve.wait_ge(pe_done, at(PE_L, "x2.S", s))
                    nc.vector.tensor_reduce(col[s][:, 16:17], ps[s][:, 1, 0:KEYS], X_AXIS, ALU.max, negate=True).then_inc(dve_done, DVE_L.did("x2.nmax", s))
                    yield
                    after("x2.nmax", s)
                    nc.vector.scalar_tensor_tensor(col[s][:, 18:19], col[s][:, 16:17], -1.0, ps[s][:, 1, 80:81], ALU.mult, ALU.add).then_inc(dve_done, DVE_L.did("x2.smax", s))
                    yield
                    after("x2.smax", s)
                    nc.vector.tensor_scalar(col[s][:, 19:20], col[s][:, 18:19], b_sim[:], None, ALU.add).then_inc(dve_done, DVE_L.did("x2.score", s))
                    yield
                    dve.wait_ge(act_done, at(ACT_L, "x2.exp", s))
                    nc.vector.reciprocal(col[s][:, 18:19], col[s][:, 17:18]).then_inc(dve_done, DVE_L.did("x2.rden", s))
                    yield
                    after("x2.rden", s)
                    nc.vector.tensor_scalar(prob[s][:, 0:KEYS], prob[s][:, 0:KEYS], col[s][:, 18:19], None, ALU.mult).then_inc(dve_done, DVE_L.did("x2.P", s))
                    yield
                    dve.wait_ge(act_done, at(ACT_L, "x2.PT", s))
                    nc.vector.tensor_reduce(col[s][0:1, 20:21], ps[s][0:1, 0, 128:128 + TOK], X_AXIS, ALU.max).then_inc(dve_done, DVE_L.did("x2.M", s))
                    yield
                    dve.wait_ge(pe_done, at(PE_L, "x2.M", s))
                    nc.vector.tensor_scalar(col[s][:, 21:22], ps[s][:, 0, 256:257], -1.0, None, ALU.mult).then_inc(dve_done, DVE_L.did("x2.negM", s))
                    yield
                    dve.wait_ge(pe_done, at(PE_L, "x2.hq", s))
                    nc.vector.reciprocal(col[s][:, 23:24], ps[s][:, 1, 2:3]).then_inc(dve_done, DVE_L.did("x2.rsum", s))
                    yield
                    after("x2.rsum", s)
                    nc.vector.tensor_scalar(col[s][:, 24:25], ps[s][:, 1, 0:1], col[s][:, 23:24], None, ALU.mult).then_inc(dve_done, DVE_L.did("x2.hc", s))
                    yield
                    dve.wait_ge(act_done, at(ACT_L, "x2.feat", s))
                    nc.vector.tensor_tensor(qT[s][:], ps[s][:, 0, 0:TOK], xnT[s][:], ALU.mult).then_inc(dve_done, DVE_L.did("x2.ehq", s))
                    yield
                    dve.wait_ge(pe_done, at(PE_L, "x2.out", s))
                    nc.vector.tensor_tensor(x[s][:], ps[s][:, 1, 0:DIM], x[s][:], ALU.add).then_inc(dve_done, DVE_L.did("x2.add", s))
                    yield
                    after("x2.add", s)
                    nc.vector.tensor_tensor(x[s][:], x[s][:], b_qv2[:], ALU.add).then_inc(dve_done, DVE_L.did("f2.x", s))
                    yield
                    yield from norm(s, "f2", x, xn, "f2.x")

                return first_half, second_half

            take_turns(DVE_0, [program(0, 0)[0](s, 0) for s in A])
            dve.wait_ge(dve_done, DVE_0.per_round)
            dve.sem_inc(dve_done, DVE_1.per_round - DVE_0.per_round)
            with dve.Fori(0, ROUNDS) as r:
                first_half, second_half = program(1, r)
                take_turns(DVE_1, [chain(second_half(s, r), first_half(s, r + 1)) for s in A] + [chain(first_half(s, r), second_half(s, r)) for s in B])


def part_2(nc, d, shared):
    xnT_all, ident, ones, x_mid, x_mid2 = (shared[k] for k in ("xnT_all", "ident", "ones", "x_mid", "x_mid2"))
    NCH = FF2 // CH
    WIDE = NCH * TTILE
    QMAX = 32767.0
    BLOCK = 32
    NBLK = 3 * FF2 // BLOCK
    PAIR = (0, 1)
    X, UP, GATE, GATED, OUT = range(5)
    SB = TTILE // TOK
    with ExitStack() as ctx:
        def sb(name, shape, dt=F32):
            return ctx.enter_context(nc.sbuf_tensor(name, shape, dt))

        def sem(name):
            return ctx.enter_context(nc.semaphore(name))

        w_rows = sb("w_rows", [128, 3, FF2])
        w_s = sb("w_s", [128, NBLK])
        w_inv = sb("w_inv", [128, NBLK])
        wT = sb("wT", [128, 3, FF2])
        hid = sb("hid", [128, TILES, WIDE])
        stage = [sb(f"stage{n}", [128, WIDE]) for n in PAIR]
        other = [sb(f"other{n}", [128, WIDE]) for n in PAIR]
        xt = [sb(f"xt{n}", [128, SB, DIM]) for n in PAIR]
        tmax = sb("tmax", [128, 2, TILES])
        col2 = sb("stats2", [128, 8])
        scale = sb("scale", [128, 5])
        inv = sb("inv", [128, 5])
        up_gated = sb("up_gated", [128, 1])
        round_col = sb("round_col", [128, 1])
        acc = [ctx.enter_context(nc.psum_tensor(f"acc{n}", [128, NCH, BANK], F32)) for n in PAIR]
        aux = ctx.enter_context(nc.psum_tensor("aux", [128, BANK], F32))

        w_loaded, w_quantised, w_turned, scales_dve, scales_pe, x_quantised = (sem(n) for n in (
            "w_loaded", "w_quantised", "w_turned", "scales_dve", "scales_pe", "x_quantised"))
        pe_2, act_2, dve_2 = ([sem(f"{e}_2{l}") for l in "abcd"] for e in ("pe", "act", "dve"))
        passed = sem("passed2")
        x_loaded = [sem(f"x_loaded{n}") for n in PAIR]
        x_stored = [sem(f"x_stored{n}") for n in PAIR]
        PA, PB, PC, PD = (PE_2A, PE_2B, PE_2C, PE_2D)
        VA, VB, VC, VD = (DVE_2A, DVE_2B, DVE_2C, DVE_2D)
        AB, AC = (ACT_2B, ACT_2C)
        ROUNDS2 = TILES // 2

        block = ctx.enter_context(nc.Block())

        @block.sync
        def _(sp):
            sp.dma_start(w_rows[:, 0, :].rearrange("p (k i) -> p k i", k=NCH), d["L2_ffn_w_up"].rearrange("(k p) i -> p k i", p=CH)).then_inc(w_loaded, 16)
            sp.dma_start(w_rows[:, 1, :].rearrange("p (k i) -> p k i", k=NCH), d["L2_ffn_w_gate"].rearrange("(k p) i -> p k i", p=CH)).then_inc(w_loaded, 16)
            sp.dma_start(w_rows[:, 2, :], d["L2_ffn_w_down"]).then_inc(w_loaded, 16)
            for n in PAIR:
                sp.sem_inc(x_stored[n], 16)
            with sp.Fori(0, ROUNDS2) as r:
                for n in PAIR:
                    sp.wait_ge(x_stored[n], r * 16 + 16)
                    sp.dma_start(xt[n][:], x_mid[bass.ds((r * 2 + n) * SB, SB), :, :].rearrange("b t c -> t b c")).then_inc(x_loaded[n], 16)

        @block.gpsimd
        def _(pool):
            pool.wait_ge(w_loaded, 48)

        @block.tensor
        def _(pe):
            def spread(step, src):
                pe.wait_ge(scales_dve, 4 * step + 1)
                nc.tensor.transpose(aux[0:1, 0:128], src, ident[:]).then_inc(scales_pe, 1)
                pe.wait_ge(scales_dve, 4 * step + 2)
                nc.tensor.matmul(aux[:, 128:129], ones[0:1, :], col2[0:1, 1:2], start=True, stop=True).then_inc(scales_pe, 1)

            pe.sem_inc(pe_2[3], PD.per_round)
            pe.wait_ge(w_quantised, 7)
            for m in range(3):
                for k in range(NCH):
                    last = nc.tensor.transpose(acc[0][:, m, k * CH:(k + 1) * CH], w_rows[:, m, k * CH:(k + 1) * CH], ident[:])
            last.then_inc(w_turned, 1)
            spread(0, col2[:, 0:1])
            pe.wait_ge(x_quantised, 2)
            pe.wait_ge(w_turned, 2)

            def hidden(steps, sem_, m, name, r, n):
                for k in range(NCH):
                    last = nc.tensor.matmul(acc[n][:, k, :], wT[:, m, k * CH:(k + 1) * CH], xnT_all[:, bass.ds((r * 2 + n) * TTILE, TTILE)], start=True, stop=True)
                last.then_inc(sem_, steps.did(name, n))

            with pe.Fori(0, ROUNDS2) as r:
                for n in PAIR:
                    pe.wait_ge(dve_2[0], VA.value("gate", n, r - 1))
                    hidden(PA, pe_2[0], 0, "up", r, n)
                for n in PAIR:
                    pe.wait_ge(dve_2[0], VA.value("up", n, r))
                    hidden(PA, pe_2[0], 1, "gate", r, n)
            for step, src in ((1, 2), (2, 3)):
                spread(step, col2[:, src:src + 1])
            with pe.Fori(0, ROUNDS2) as r:
                for n in PAIR:
                    pe.wait_ge(act_2[1], AB.value("round", n, r - 1))
                    hidden(PB, pe_2[1], 1, "gate", r, n)
            spread(3, col2[:, 0:1])
            with pe.Fori(0, ROUNDS2) as r:
                for n in PAIR:
                    pe.wait_ge(act_2[2], AC.value("round", n, r - 1))
                    hidden(PC, pe_2[2], 0, "up", r, n)
            spread(4, col2[:, 0:1])
            with pe.Fori(0, ROUNDS2) as r:
                for n in PAIR:
                    pe.wait_ge(dve_2[3], VD.value("quant", n, r))
                    for b in range(SB):
                        for k in range(NCH):
                            last = nc.tensor.matmul(acc[n][:, 0, b * TOK:(b + 1) * TOK], stage[n][:, k * TTILE + b * TOK:k * TTILE + (b + 1) * TOK],
                                                    wT[:, 2, k * CH:(k + 1) * CH], start=(k == 0), stop=(k == NCH - 1))
                    last.then_inc(pe_2[3], PD.did("down", n))

        @block.scalar
        def _(act):
            act.sem_inc(act_2[1], AB.per_round)
            act.sem_inc(act_2[2], AC.per_round)
            act.wait_ge(scales_dve, 12)
            with act.Fori(0, ROUNDS2) as r:
                for n in PAIR:
                    act.wait_ge(dve_2[1], VB.value("gated", n, r - 1))
                    act.wait_ge(pe_2[1], PB.value("gate", n, r))
                    nc.scalar.activation(stage[n][:], acc[n][:].rearrange("p k t -> p (k t)"), ACT.Identity, scale=inv[:, GATE:GATE + 1], bias=round_col[:]).then_inc(act_2[1], AB.did("round", n))
                for n in PAIR:
                    act.wait_ge(dve_2[1], VB.value("gate", n, r))
                    nc.scalar.activation(other[n][:], stage[n][:], ACT.Tanh, scale=0.5).then_inc(act_2[1], AB.did("tanh", n))
            with act.Fori(0, ROUNDS2) as r:
                for n in PAIR:
                    act.wait_ge(dve_2[2], VC.value("product", n, r - 1))
                    act.wait_ge(pe_2[2], PC.value("up", n, r))
                    nc.scalar.activation(stage[n][:], acc[n][:].rearrange("p k t -> p (k t)"), ACT.Identity, scale=inv[:, UP:UP + 1], bias=round_col[:]).then_inc(act_2[2], AC.did("round", n))
            with act.Fori(0, ROUNDS2) as r:
                for n in PAIR:
                    act.wait_ge(dve_2[3], VD.value("add", n, r))
                    act.dma_start(x_mid2[bass.ds((r * 2 + n) * SB, SB), :, :].rearrange("b t c -> t b c"), xt[n][:]).then_inc(x_stored[n], 16)
            for n in PAIR:
                act.wait_ge(x_stored[n], 16 * ROUNDS2 + 16)

        @block.vector
        def _(dve):
            for steps, sem_ in ((VA, dve_2[0]), (VB, dve_2[1]), (VC, dve_2[2]), (VD, dve_2[3])):
                dve.sem_inc(sem_, steps.per_round)
            dve.wait_ge(w_loaded, 48)
            nc.vector.memset(round_col[:], ROUND).then_inc(w_quantised, 1)
            blocks = w_rows[:].rearrange("p m (b i) -> p (m b) i", i=BLOCK)
            per_block = [128, NBLK, BLOCK]
            nc.vector.tensor_reduce(w_s[:], blocks, X_AXIS, ALU.max, apply_absolute_value=True).then_inc(w_quantised, 1)
            dve.wait_ge(w_quantised, 2)
            nc.vector.tensor_scalar(w_s[:], w_s[:], 1.0 / 7.0, 1e-12, ALU.mult, ALU.max).then_inc(w_quantised, 1)
            dve.wait_ge(w_quantised, 3)
            nc.vector.reciprocal(w_inv[:], w_s[:]).then_inc(w_quantised, 1)
            dve.wait_ge(w_quantised, 4)
            nc.vector.tensor_tensor(blocks, blocks, w_inv[:].unsqueeze(2).to_broadcast(per_block), ALU.mult).then_inc(w_quantised, 1)
            dve.wait_ge(w_quantised, 5)
            nc.vector.tensor_scalar(blocks, blocks, ROUND, None, ALU.add).then_inc(w_quantised, 1)
            dve.wait_ge(w_quantised, 6)
            nc.vector.scalar_tensor_tensor(blocks, blocks, ROUND, w_s[:].unsqueeze(2).to_broadcast(per_block), ALU.subtract, ALU.mult).then_inc(w_quantised, 1)
            dve.wait_ge(w_turned, 1)
            nc.vector.tensor_copy(wT[:], acc[0][:, :, 0:FF2]).then_inc(w_turned, 1)

            def global_scale(step, which, part, out):
                nc.vector.tensor_reduce(out, part, X_AXIS, ALU.max, apply_absolute_value=True).then_inc(scales_dve, 1)
                dve.wait_ge(scales_pe, 2 * step + 1)
                nc.vector.tensor_reduce(col2[0:1, 1:2], aux[0:1, 0:128], X_AXIS, ALU.max).then_inc(scales_dve, 1)
                dve.wait_ge(scales_pe, 2 * step + 2)
                nc.vector.tensor_scalar(scale[:, which:which + 1], aux[:, 128:129], 1.0 / QMAX, 1e-12, ALU.mult, ALU.max).then_inc(scales_dve, 1)
                dve.wait_ge(scales_dve, 4 * step + 3)
                nc.vector.reciprocal(inv[:, which:which + 1], scale[:, which:which + 1]).then_inc(scales_dve, 1)
                dve.wait_ge(scales_dve, 4 * step + 4)

            global_scale(0, X, xnT_all[:], col2[:, 0:1])
            nc.vector.tensor_scalar(xnT_all[:], xnT_all[:], inv[:, X:X + 1], ROUND, ALU.mult, ALU.add).then_inc(x_quantised, 1)
            dve.wait_ge(x_quantised, 1)
            nc.vector.tensor_scalar(xnT_all[:], xnT_all[:], ROUND, scale[:, X:X + 1], ALU.subtract, ALU.mult).then_inc(x_quantised, 1)
            with dve.Fori(0, ROUNDS2) as r:
                for m, name in enumerate(("up", "gate")):
                    for n in PAIR:
                        dve.wait_ge(pe_2[0], PA.value(name, n, r))
                        dve.sem_inc(passed, 1)
                        nc.vector.tensor_reduce(tmax[:, m, bass.ds(r * 2 + n, 1)], acc[n][:].rearrange("p k t -> p (k t)"), X_AXIS, ALU.max, apply_absolute_value=True).then_inc(dve_2[0], VA.did(name, n))
            dve.wait_ge(dve_2[0], VA.value("gate", 1, ROUNDS2 - 1))
            global_scale(1, UP, tmax[:, 0, :], col2[:, 2:3])
            global_scale(2, GATE, tmax[:, 1, :], col2[:, 3:4])
            with dve.Fori(0, ROUNDS2) as r:
                def after(name, n):
                    dve.wait_ge(dve_2[1], VB.value(name, n, r))
                for n in PAIR:
                    dve.wait_ge(act_2[1], AB.value("round", n, r))
                    nc.vector.tensor_scalar(stage[n][:], stage[n][:], ROUND, scale[:, GATE:GATE + 1], ALU.subtract, ALU.mult).then_inc(dve_2[1], VB.did("gate", n))
                for n in PAIR:
                    dve.wait_ge(act_2[1], AB.value("tanh", n, r))
                    nc.vector.tensor_scalar(other[n][:], other[n][:], 32768.0, ROUND + 32768.0, ALU.mult, ALU.add).then_inc(dve_2[1], VB.did("sigmoid", n))
                for n in PAIR:
                    after("sigmoid", n)
                    nc.vector.tensor_scalar(other[n][:], other[n][:], ROUND, 65535.0, ALU.subtract, ALU.min).then_inc(dve_2[1], VB.did("clip", n))
                for n in PAIR:
                    after("clip", n)
                    nc.vector.scalar_tensor_tensor(hid[:, bass.ds(r * 2 + n, 1), :].rearrange("p o w -> p (o w)"), other[n][:], 1.0 / 65536.0, stage[n][:], ALU.mult, ALU.mult).then_inc(dve_2[1], VB.did("gated", n))
                for n in PAIR:
                    after("gated", n)
                    dve.sem_inc(passed, 1)
                    nc.vector.tensor_reduce(tmax[:, 0, bass.ds(r * 2 + n, 1)], hid[:, bass.ds(r * 2 + n, 1), :].rearrange("p o w -> p (o w)"), X_AXIS, ALU.max, apply_absolute_value=True).then_inc(dve_2[1], VB.did("max", n))
            dve.wait_ge(dve_2[1], VB.value("max", 1, ROUNDS2 - 1))
            global_scale(3, GATED, tmax[:, 0, :], col2[:, 0:1])
            nc.vector.tensor_tensor(up_gated[:], scale[:, UP:UP + 1], scale[:, GATED:GATED + 1], ALU.mult).then_inc(x_quantised, 1)
            dve.wait_ge(x_quantised, 3)
            with dve.Fori(0, ROUNDS2) as r:
                def after(name, n):
                    dve.wait_ge(dve_2[2], VC.value(name, n, r))
                for n in PAIR:
                    nc.vector.tensor_scalar(other[n][:], hid[:, bass.ds(r * 2 + n, 1), :].rearrange("p o w -> p (o w)"), inv[:, GATED:GATED + 1], ROUND, ALU.mult, ALU.add).then_inc(dve_2[2], VC.did("round", n))
                for n in PAIR:
                    dve.wait_ge(act_2[2], AC.value("round", n, r))
                    nc.vector.tensor_scalar(stage[n][:], stage[n][:], ROUND, up_gated[:], ALU.subtract, ALU.mult).then_inc(dve_2[2], VC.did("up", n))
                for n in PAIR:
                    after("up", n)
                    nc.vector.scalar_tensor_tensor(hid[:, bass.ds(r * 2 + n, 1), :].rearrange("p o w -> p (o w)"), other[n][:], ROUND, stage[n][:], ALU.subtract, ALU.mult).then_inc(dve_2[2], VC.did("product", n))
                for n in PAIR:
                    after("product", n)
                    dve.sem_inc(passed, 1)
                    nc.vector.tensor_reduce(tmax[:, 1, bass.ds(r * 2 + n, 1)], hid[:, bass.ds(r * 2 + n, 1), :].rearrange("p o w -> p (o w)"), X_AXIS, ALU.max, apply_absolute_value=True).then_inc(dve_2[2], VC.did("max", n))
            dve.wait_ge(dve_2[2], VC.value("max", 1, ROUNDS2 - 1))
            global_scale(4, OUT, tmax[:, 1, :], col2[:, 0:1])
            with dve.Fori(0, ROUNDS2) as r:
                for n in PAIR:
                    dve.wait_ge(pe_2[3], PD.value("down", n, r - 1))
                    nc.vector.tensor_scalar(stage[n][:], hid[:, bass.ds(r * 2 + n, 1), :].rearrange("p o w -> p (o w)"), inv[:, OUT:OUT + 1], ROUND, ALU.mult, ALU.add).then_inc(dve_2[3], VD.did("round", n))
                for n in PAIR:
                    dve.wait_ge(dve_2[3], VD.value("round", n, r))
                    nc.vector.tensor_scalar(stage[n][:], stage[n][:], ROUND, scale[:, OUT:OUT + 1], ALU.subtract, ALU.mult).then_inc(dve_2[3], VD.did("quant", n))
                for n in PAIR:
                    dve.wait_ge(pe_2[3], PD.value("down", n, r))
                    dve.wait_ge(x_loaded[n], r * 16 + 16)
                    nc.vector.tensor_tensor(xt[n][:].rearrange("p b c -> p (b c)"), acc[n][:, 0, :], xt[n][:].rearrange("p b c -> p (b c)"), ALU.add).then_inc(dve_2[3], VD.did("add", n))


def part_3(nc, d, shared):
    ident, ones, first, minus_half, x_mid2 = (shared[k] for k in ("ident", "ones", "first", "minus_half", "x_mid2"))
    S = range(STREAMS)
    A, B = (0, 1), (2, 3)
    LISTS = (PE_3S, ACT_3S, DVE_3S, POOL_3S), (PE_3, ACT_3, DVE_3, POOL_3)
    CHUNKS = 4
    LAST = KEYS - CHUNKS * KT
    KPAD = (CHUNKS + 1) * KT
    ROWS = 32
    with ExitStack() as ctx:
        def sb(name, shape, dt=F32):
            return ctx.enter_context(nc.sbuf_tensor(name, shape, dt))

        def per_stream(name, shape, dt=F32):
            return [sb(f"{name}{s}", shape, dt) for s in S]

        def sem(name):
            return ctx.enter_context(nc.semaphore(name))

        before = sb("before", [128, 128])
        mask3_i = sb("mask3_i", [128, BATCH * KEYS], I32)
        mask3 = sb("mask3", [128, (BATCH + PAIR) * KEYS + KPAD - KEYS])
        w_txt = sb("w_txt", [128, DIM])
        w_feat = sb("w_feat", [128, DIM])
        w_row = sb("w_row", [128, 2 * ROWS - 1])
        b_e = sb("b_e", [128, 1])
        w_gate = sb("w_gate", [128, 2])
        b_gate = sb("b_gate", [128, 2])
        w_route = sb("w_route", [128, MOE3])
        w_exp = sb("w_exp", [128, MOE3, DIM])
        b_exp = sb("b_exp", [MOE3, DIM])

        x_in = per_stream("x_in3", [128, DIM])
        ctx_in = per_stream("ctx_in3", [KEYS, DIM])
        ctxT_in = per_stream("ctxT_in3", [128, KEYS])
        x = per_stream("x3", [128, DIM])
        cx = per_stream("cx3", [KEYS, DIM])
        cxT = per_stream("cxT3", [128, KEYS])
        xn = per_stream("xn3", [128, DIM])
        xnT = per_stream("xnT3", [128, TOK])
        txt = per_stream("txt3", [128, KEYS])
        feat = per_stream("feat3", [128, TOK])
        th = per_stream("th3", [128, KT, TOK])
        th_last = per_stream("th_last3", [128, KT, TOK])
        prob = per_stream("prob3", [128, KPAD])
        probT = per_stream("probT3", [KEYS, TOK])
        hT = per_stream("hT3", [128, TOK])
        wT = per_stream("wT3", [MOE3, TOK])
        col = per_stream("col3", [128, 72])
        taken = per_stream("taken3", [128, MOE3])
        carry = sb("carry3", [128, MOE3])
        ps = [ctx.enter_context(nc.psum_tensor(f"ps3{s}", [128, 2, BANK], F32)) for s in S]

        weights_in, ready3, mask_set, zeros_set, carried = (sem(n) for n in ("weights_in3", "ready3", "mask_set", "zeros_set", "carried"))
        loads_in = [sem(f"loads_in3{s}") for s in S]
        stores_out = [sem(f"stores_out3{s}") for s in S]
        inputs_ready = [sem(f"inputs_ready3{s}") for s in S]
        passed = sem("passed3")
        pe_done, act_done, dve_done, pool_done = (sem(n) for n in ("pe_done3", "act_done3", "dve_done3", "pool_done3"))

        weight_loads = [
            (before[:], d["before"]), (mask3_i[:], d["mask_BxS2_ik0"].to_broadcast([128, BATCH * KEYS])),
            (w_txt[:], d["L3_xattn_Ws"]), (w_feat[:], d["L3_xattn_W"]), (w_row[:, ROWS - 1:ROWS], d["L3_xattn_w"]), (b_e[:], d["L3_xattn_b"]),
            (w_gate[:, 0:1], d["L3_xattn_Wcw"]), (w_gate[:, 1:2], d["L3_xattn_Wcb"]),
            (b_gate[:, 0:1], d["L3_xattn_bcw"].to_broadcast([128, 1])), (b_gate[:, 1:2], d["L3_xattn_bcb"].to_broadcast([128, 1])),
            (w_route[:], d["L3_ffn_wg"]), (w_exp[:], d["L3_ffn_W"].rearrange("e h f -> h e f")), (b_exp[:], d["L3_ffn_b"]),
        ]
        block = ctx.enter_context(nc.Block())

        @block.sync
        def _(sp):
            def load(s, b):
                sp.dma_start(x_in[s][:], x_mid2[bass.ds(b, 1), :, :].rearrange("o t c -> t (o c)")).then_inc(loads_in[s], 16)
                sp.dma_start(ctx_in[s][:], d["ctx"][bass.ds(b, 1), :, :].rearrange("o t c -> t (o c)")).then_inc(loads_in[s], 16)
                sp.dma_start(ctxT_in[s][:], d["ctxT"][bass.ds(b, 1), :, :].rearrange("o t c -> t (o c)")).then_inc(loads_in[s], 16)

            for s in S:
                load(s, s)
            sp.wait_ge(ready3, 1)
            for dst, src in weight_loads:
                sp.dma_start(dst, src).then_inc(weights_in, 16)
            def store(s, r):
                sp.wait_ge(dve_done, DVE_3.value(f"f3.add{MOE3 - 1}", s, r))
                sp.dma_start(d["out"][bass.ds(r * STREAMS + s, 1), :, :].rearrange("o t c -> t (o c)"), x[s][:]).then_inc(stores_out[s], 16)

            with sp.Fori(0, ROUNDS - 1) as r:
                for pair in (A, B):
                    for s in pair:
                        sp.wait_ge(inputs_ready[s], r + 1)
                        load(s, r * STREAMS + (STREAMS + s))
                    for s in pair:
                        store(s, r)
            for pair in (A, B):
                for s in pair:
                    sp.wait_ge(inputs_ready[s], ROUNDS)
                    load(s, s)
                for s in pair:
                    store(s, ROUNDS - 1)
            for s in S:
                sp.wait_ge(stores_out[s], 16 * ROUNDS)

        @block.gpsimd
        def _(pool):
            def take_inputs(s, value):
                pool.wait_ge(loads_in[s], value)
                pool.sem_inc(passed, 1)
                nc.gpsimd.tensor_copy(x[s][:], x_in[s][:])
                nc.gpsimd.tensor_copy(cx[s][:], ctx_in[s][:])
                nc.gpsimd.tensor_copy(cxT[s][:], ctxT_in[s][:]).then_inc(inputs_ready[s], 1)

            def program(k, it):
                PE_L, ACT_L, DVE_L, POOL_L = LISTS[k]

                def rstd(s, p):
                    pool.wait_ge(dve_done, DVE_L.value(f"{p}.eps", s, it))
                    nc.gpsimd.tensor_tensor(col[s][:, 9:10], col[s][:, 8:9], minus_half[:], ALU.pow).then_inc(pool_done, POOL_L.did(f"{p}.rstd", s))
                    yield

                def first_half(s, rnd):
                    yield from rstd(s, "x3")

                def second_half(s, rnd):
                    yield from rstd(s, "f3")
                    pool.wait_ge(stores_out[s], rnd * 16 + 16)
                    take_inputs(s, rnd * 48 + 96)
                    pool.wait_ge(inputs_ready[s], rnd + 2)
                    pool.sem_inc(pool_done, POOL_L.did("in", s))
                    yield

                return first_half, second_half

            nc.gpsimd.memset(w_row[:], 0.0).then_inc(ready3, 1)
            nc.gpsimd.memset(mask3[:, BATCH * KEYS:], 0.0)
            for s in S:
                last = nc.gpsimd.memset(th_last[s][:], 0.0)
            last.then_inc(zeros_set, 1)
            for s in S:
                take_inputs(s, 48)
            take_turns(POOL_3S, [program(0, 0)[0](s, 0) for s in A])
            pool.wait_ge(pool_done, POOL_3S.per_round)
            pool.sem_inc(pool_done, POOL_3.per_round - POOL_3S.per_round)
            with pool.Fori(0, ROUNDS) as r:
                first_half, second_half = program(1, r)
                take_turns(POOL_3, [chain(second_half(s, r), first_half(s, r + 1)) for s in A] + [chain(first_half(s, r), second_half(s, r)) for s in B])

        @block.scalar
        def _(act):
            act.wait_ge(weights_in, 16 * len(weight_loads))
            act.wait_ge(zeros_set, 1)
            def program(k, it):
                PE_L, ACT_L, DVE_L, POOL_L = LISTS[k]

                def at(steps_, name, s):
                    return steps_.value(name, s, it)

                def xT(s, p):
                    act.wait_ge(pe_done, at(PE_L, f"{p}.T", s))
                    nc.scalar.copy(xnT[s][:], ps[s][:, 0, 0:TOK]).then_inc(act_done, ACT_L.did(f"{p}.xT", s))
                    yield

                def first_half(s, rnd):
                    yield from xT(s, "x3")
                    act.wait_ge(pe_done, at(PE_L, "x3.proj", s))
                    nc.scalar.copy(txt[s][:], ps[s][:, 0, 0:KEYS])
                    nc.scalar.activation(feat[s][:], ps[s][:, 0, 128:128 + TOK], ACT.Identity, bias=b_e[:]).then_inc(act_done, ACT_L.did("x3.proj", s))
                    yield
                    for c in range(CHUNKS):
                        act.wait_ge(dve_done, at(DVE_L, f"x3.sum{c}", s))
                        nc.scalar.activation(th[s][:], th[s][:], ACT.Tanh).then_inc(act_done, ACT_L.did(f"x3.tanh{c}", s))
                        yield
                        if c == 0:
                            act.wait_ge(act_done, at(ACT_L, "x3.proj", s))
                            for k in range(LAST):
                                last = nc.scalar.activation(th_last[s][:, k, :], feat[s][:], ACT.Tanh, bias=txt[s][:, CHUNKS * KT + k:CHUNKS * KT + k + 1])
                            last.then_inc(act_done, ACT_L.did("x3.tanh_last", s))
                            yield
                    act.wait_ge(pe_done, at(PE_L, f"x3.rho{CHUNKS - 1}", s))
                    nc.scalar.copy(th[s][:, 0:4, :].rearrange("p k f -> p (k f)"), ps[s][:, 1, :]).then_inc(act_done, ACT_L.did("x3.rho", s))
                    yield
                    act.wait_ge(dve_done, at(DVE_L, "x3.nmax", s))
                    nc.scalar.activation(prob[s][:, 0:KEYS], prob[s][:, 0:KEYS], ACT.Exp, bias=col[s][:, 16:17], accum_out=col[s][:, 17:18]).then_inc(act_done, ACT_L.did("x3.exp", s))
                    yield
                    act.wait_ge(pe_done, at(PE_L, "x3.PT", s))
                    nc.scalar.copy(probT[s][:], ps[s][0:KEYS, 0, 0:TOK]).then_inc(act_done, ACT_L.did("x3.PT", s))
                    yield
                    act.wait_ge(pe_done, at(PE_L, "x3.h", s))
                    nc.scalar.copy(hT[s][:], ps[s][:, 0, 0:TOK]).then_inc(act_done, ACT_L.did("x3.h", s))
                    yield
                    act.wait_ge(dve_done, at(DVE_L, "x3.gb", s))
                    nc.scalar.activation(col[s][:, 20:22], col[s][:, 18:20], ACT.Tanh).then_inc(act_done, ACT_L.did("x3.gate", s))
                    yield

                def second_half(s, rnd):
                    yield from xT(s, "f3")
                    act.wait_ge(dve_done, at(DVE_L, "f3.nmax", s))
                    nc.scalar.activation(col[s][:, 24:32], ps[s][:, 1, 0:MOE3], ACT.Exp, bias=col[s][:, 16:17], accum_out=col[s][:, 17:18]).then_inc(act_done, ACT_L.did("f3.exp", s))
                    yield
                    act.wait_ge(pe_done, at(PE_L, "f3.wT", s))
                    nc.scalar.copy(wT[s][:], ps[s][0:MOE3, 0, 0:TOK]).then_inc(act_done, ACT_L.did("f3.wT", s))
                    yield

                return first_half, second_half

            take_turns(ACT_3S, [program(0, 0)[0](s, 0) for s in A])
            act.wait_ge(act_done, ACT_3S.per_round)
            act.sem_inc(act_done, ACT_3.per_round - ACT_3S.per_round)
            with act.Fori(0, ROUNDS) as r:
                first_half, second_half = program(1, r)
                take_turns(ACT_3, [chain(second_half(s, r), first_half(s, r + 1)) for s in A] + [chain(first_half(s, r), second_half(s, r)) for s in B])

        @block.tensor
        def _(pe):
            pe.wait_ge(weights_in, 16 * len(weight_loads))
            def program(k, it):
                PE_L, ACT_L, DVE_L, POOL_L = LISTS[k]

                def at(steps_, name, s):
                    return steps_.value(name, s, it)

                def transpose_xn(s, p):
                    pe.wait_ge(dve_done, at(DVE_L, f"{p}.norm", s))
                    nc.tensor.transpose(ps[s][:, 0, 0:TOK], xn[s][:], ident[:]).then_inc(pe_done, PE_L.did(f"{p}.T", s))
                    yield

                def rho(a, tanh, s, start, stop):
                    for b in range(4):
                        last = nc.tensor.matmul(ps[s][ROWS * b:ROWS * (b + 1), 1, :], w_row[:, ROWS - 1 - a:2 * ROWS - 1 - a],
                                                tanh[:, 4 * b:4 * b + 4, :], start=start, stop=stop, tile_position=(0, ROWS * b))
                    return last

                def first_half(s, rnd):
                    yield from transpose_xn(s, "x3")
                    pe.wait_ge(act_done, at(ACT_L, "x3.xT", s))
                    nc.tensor.matmul(ps[s][:, 0, 0:KEYS], w_txt[:], cxT[s][:], start=True, stop=True)
                    nc.tensor.matmul(ps[s][:, 0, 128:128 + TOK], w_feat[:], xnT[s][:], start=True, stop=True).then_inc(pe_done, PE_L.did("x3.proj", s))
                    yield
                    for c in range(CHUNKS):
                        pe.wait_ge(act_done, at(ACT_L, f"x3.tanh{c}", s))
                        rho(c, th[s], s, c == 0, c == CHUNKS - 1).then_inc(pe_done, PE_L.did(f"x3.rho{c}", s))
                        yield
                        if c == 0:
                            pe.wait_ge(act_done, at(ACT_L, "x3.tanh_last", s))
                            rho(CHUNKS, th_last[s], s, False, False).then_inc(pe_done, PE_L.did("x3.rho_last", s))
                            yield
                    pe.wait_ge(act_done, at(ACT_L, "x3.rho", s))
                    for k in range(4):
                        last = nc.tensor.transpose(ps[s][:, 0, k * TOK:(k + 1) * TOK], th[s][:, k, :], ident[:])
                    last.then_inc(pe_done, PE_L.did("x3.rhoT", s))
                    yield
                    pe.wait_ge(dve_done, at(DVE_L, "x3.P", s))
                    nc.tensor.transpose(ps[s][0:KEYS, 0, 0:TOK], prob[s][:, 0:KEYS], ident[:]).then_inc(pe_done, PE_L.did("x3.PT", s))
                    yield
                    pe.wait_ge(act_done, at(ACT_L, "x3.PT", s))
                    nc.tensor.matmul(ps[s][:, 0, 0:TOK], cx[s][:], probT[s][:], start=True, stop=True).then_inc(pe_done, PE_L.did("x3.h", s))
                    yield
                    pe.wait_ge(act_done, at(ACT_L, "x3.h", s))
                    nc.tensor.matmul(ps[s][:, 1, 0:2], hT[s][:], w_gate[:], start=True, stop=True).then_inc(pe_done, PE_L.did("x3.gate", s))
                    yield

                def second_half(s, rnd):
                    yield from transpose_xn(s, "f3")
                    pe.wait_ge(act_done, at(ACT_L, "f3.xT", s))
                    nc.tensor.matmul(ps[s][:, 1, 0:MOE3], xnT[s][:], w_route[:], start=True, stop=True).then_inc(pe_done, PE_L.did("f3.route", s))
                    yield
                    pe.wait_ge(dve_done, at(DVE_L, "f3.taken", s))
                    nc.tensor.matmul(ps[s][:, 1, 16:16 + MOE3], before[:], col[s][:, 40:48], start=True, stop=False)
                    nc.tensor.matmul(ps[s][:, 1, 16:16 + MOE3], ones[:], taken[s][:], start=False, stop=True).then_inc(pe_done, PE_L.did("f3.place", s))
                    yield
                    pe.wait_ge(dve_done, at(DVE_L, "f3.w", s))
                    nc.tensor.transpose(ps[s][0:MOE3, 0, 0:TOK], col[s][:, 64:64 + MOE3], ident[:]).then_inc(pe_done, PE_L.did("f3.wT", s))
                    yield
                    pe.wait_ge(act_done, at(ACT_L, "f3.wT", s))
                    nc.tensor.matmul(ps[s][:, 1, 0:DIM], wT[s][:], b_exp[:], start=True, stop=True).then_inc(pe_done, PE_L.did("f3.bias", s))
                    yield
                    pe.wait_ge(dve_done, at(DVE_L, "f3.bias", s))
                    for b in range(2):
                        last = nc.tensor.matmul(ps[s][:, b, :], xnT[s][:], w_exp[:, b * GROUP:(b + 1) * GROUP, :], start=True, stop=True)
                    last.then_inc(pe_done, PE_L.did("f3.y", s))
                    yield

                return first_half, second_half

            take_turns(PE_3S, [program(0, 0)[0](s, 0) for s in A])
            pe.wait_ge(pe_done, PE_3S.per_round)
            pe.sem_inc(pe_done, PE_3.per_round - PE_3S.per_round)
            with pe.Fori(0, ROUNDS) as r:
                first_half, second_half = program(1, r)
                take_turns(PE_3, [chain(second_half(s, r), first_half(s, r + 1)) for s in A] + [chain(first_half(s, r), second_half(s, r)) for s in B])

        @block.vector
        def _(dve):
            dve.wait_ge(weights_in, 16 * len(weight_loads))
            nc.vector.tensor_scalar(mask3[:, 0:BATCH * KEYS], mask3_i[:], 1e30, -1e30, ALU.mult, ALU.add).then_inc(mask_set, 1)
            nc.vector.memset(carry[:], 0.0).then_inc(carried, 1)
            dve.wait_ge(mask_set, 1)
            dve.wait_ge(zeros_set, 1)
            def program(k, it):
                PE_L, ACT_L, DVE_L, POOL_L = LISTS[k]

                def at(steps_, name, s):
                    return steps_.value(name, s, it)

                def after(name, s):
                    dve.wait_ge(dve_done, at(DVE_L, name, s))

                def norm(s, p, prev, rnd=None):
                    if prev is None:
                        dve.wait_ge(inputs_ready[s], rnd + 1)
                    else:
                        dve.wait_ge(dve_done, (DVE_L.value_before if s in A else DVE_L.value)(prev, s, it))
                    nc.vector.bn_stats(col[s][:, 0:6], x[s][:]).then_inc(dve_done, DVE_L.did(f"{p}.stats", s))
                    yield
                    after(f"{p}.stats", s)
                    dve.sem_inc(passed, 1)
                    nc.vector.bn_aggr(col[s][:, 6:8], col[s][:, 0:6]).then_inc(dve_done, DVE_L.did(f"{p}.aggr", s))
                    yield
                    after(f"{p}.aggr", s)
                    nc.vector.tensor_scalar(col[s][:, 8:9], col[s][:, 7:8], LN_EPS, None, ALU.add).then_inc(dve_done, DVE_L.did(f"{p}.eps", s))
                    yield
                    dve.wait_ge(pool_done, at(POOL_L, f"{p}.rstd", s))
                    nc.vector.tensor_scalar(xn[s][:], x[s][:], col[s][:, 6:7], col[s][:, 9:10], ALU.subtract, ALU.mult).then_inc(dve_done, DVE_L.did(f"{p}.norm", s))
                    yield

                def first_half(s, rnd):
                    yield from norm(s, "x3", None, rnd)
                    for c in range(CHUNKS):
                        if c == 0:
                            dve.wait_ge(act_done, at(ACT_L, "x3.proj", s))
                        else:
                            dve.wait_ge(pe_done, at(PE_L, f"x3.rho{c - 1}", s))
                        nc.vector.tensor_tensor(th[s][:], txt[s][:, c * KT:(c + 1) * KT].unsqueeze(2).to_broadcast([128, KT, TOK]),
                                                feat[s][:].unsqueeze(1).to_broadcast([128, KT, TOK]), ALU.add).then_inc(dve_done, DVE_L.did(f"x3.sum{c}", s))
                        yield
                    dve.wait_ge(pe_done, at(PE_L, "x3.rhoT", s))
                    nc.vector.tensor_tensor(prob[s][:].rearrange("p (a b k) -> p a b k", b=4, k=4),
                                            ps[s][:, 0, :].rearrange("p (k b a) -> p a b k", k=4, b=4)[:, 0:CHUNKS + 1, :, :],
                                            mask3[:, bass.ds((rnd * STREAMS + s) * KEYS, KPAD)].rearrange("p (a b k) -> p a b k", b=4, k=4), ALU.add).then_inc(dve_done, DVE_L.did("x3.mask", s))
                    yield
                    after("x3.mask", s)
                    nc.vector.tensor_reduce(col[s][:, 16:17], prob[s][:, 0:KEYS], X_AXIS, ALU.max, negate=True).then_inc(dve_done, DVE_L.did("x3.nmax", s))
                    yield
                    dve.wait_ge(act_done, at(ACT_L, "x3.exp", s))
                    nc.vector.reciprocal(col[s][:, 18:19], col[s][:, 17:18]).then_inc(dve_done, DVE_L.did("x3.rden", s))
                    yield
                    after("x3.rden", s)
                    nc.vector.tensor_scalar(prob[s][:, 0:KEYS], prob[s][:, 0:KEYS], col[s][:, 18:19], None, ALU.mult).then_inc(dve_done, DVE_L.did("x3.P", s))
                    yield
                    dve.wait_ge(pe_done, at(PE_L, "x3.gate", s))
                    nc.vector.tensor_tensor(col[s][:, 18:20], ps[s][:, 1, 0:2], b_gate[:], ALU.add).then_inc(dve_done, DVE_L.did("x3.gb", s))
                    yield
                    dve.wait_ge(act_done, at(ACT_L, "x3.gate", s))
                    nc.vector.tensor_scalar(xn[s][:], xn[s][:], col[s][:, 20:21], col[s][:, 21:22], ALU.mult, ALU.add).then_inc(dve_done, DVE_L.did("x3.y", s))
                    yield
                    after("x3.y", s)
                    nc.vector.tensor_tensor(x[s][:], x[s][:], xn[s][:], ALU.add).then_inc(dve_done, DVE_L.did("x3.x", s))
                    yield

                def second_half(s, rnd):
                    yield from norm(s, "f3", "x3.x")
                    dve.wait_ge(pe_done, at(PE_L, "f3.route", s))
                    nc.vector.tensor_reduce(col[s][:, 16:17], ps[s][:, 1, 0:MOE3], X_AXIS, ALU.max, negate=True).then_inc(dve_done, DVE_L.did("f3.nmax", s))
                    yield
                    dve.wait_ge(act_done, at(ACT_L, "f3.exp", s))
                    nc.vector.reciprocal(col[s][:, 18:19], col[s][:, 17:18]).then_inc(dve_done, DVE_L.did("f3.rden", s))
                    yield
                    after("f3.rden", s)
                    nc.vector.tensor_scalar(col[s][:, 24:32], col[s][:, 24:32], col[s][:, 18:19], None, ALU.mult).then_inc(dve_done, DVE_L.did("f3.probs", s))
                    yield
                    after("f3.probs", s)
                    nc.vector.tensor_reduce(col[s][:, 19:20], col[s][:, 24:32], X_AXIS, ALU.max).then_inc(dve_done, DVE_L.did("f3.pmax", s))
                    yield
                    after("f3.pmax", s)
                    nc.vector.scalar_tensor_tensor(col[s][:, 32:40], col[s][:, 24:32], col[s][:, 19:20], first[:], ALU.is_equal, ALU.mult).then_inc(dve_done, DVE_L.did("f3.eq", s))
                    yield
                    after("f3.eq", s)
                    nc.vector.tensor_reduce(col[s][:, 20:21], col[s][:, 32:40], X_AXIS, ALU.max).then_inc(dve_done, DVE_L.did("f3.first", s))
                    yield
                    after("f3.first", s)
                    nc.vector.tensor_scalar(col[s][:, 40:48], col[s][:, 32:40], col[s][:, 20:21], None, ALU.is_equal).then_inc(dve_done, DVE_L.did("f3.pick", s))
                    yield
                    if s == 0:
                        dve.wait_ge(carried, rnd + 1)
                        dve.sem_inc(passed, 1)
                        nc.vector.tensor_copy(taken[0][:], carry[:]).then_inc(dve_done, DVE_L.did("f3.taken", s))
                        yield
                    else:
                        after("f3.pick", s - 1)
                        after("f3.taken", s - 1)
                        nc.vector.tensor_tensor(taken[s][:], taken[s - 1][:], col[s - 1][:, 40:48], ALU.add).then_inc(dve_done, DVE_L.did("f3.taken", s))
                        yield
                    if s == STREAMS - 1:
                        after("f3.taken", s)
                        nc.vector.tensor_tensor(carry[:], taken[s][:], col[s][:, 40:48], ALU.add).then_inc(carried, 1)
                    dve.wait_ge(pe_done, at(PE_L, "f3.place", s))
                    nc.vector.scalar_tensor_tensor(col[s][:, 56:64], ps[s][:, 1, 16:16 + MOE3], float(CAPACITY), col[s][:, 40:48], ALU.is_lt, ALU.mult).then_inc(dve_done, DVE_L.did("f3.keep", s))
                    yield
                    after("f3.keep", s)
                    nc.vector.tensor_scalar(col[s][:, 64:72], col[s][:, 56:64], col[s][:, 19:20], None, ALU.mult).then_inc(dve_done, DVE_L.did("f3.w", s))
                    yield
                    dve.wait_ge(pe_done, at(PE_L, "f3.bias", s))
                    nc.vector.tensor_tensor(x[s][:], x[s][:], ps[s][:, 1, 0:DIM], ALU.add).then_inc(dve_done, DVE_L.did("f3.bias", s))
                    yield
                    for e in range(MOE3):
                        if e == 0:
                            dve.wait_ge(pe_done, at(PE_L, "f3.y", s))
                        else:
                            after(f"f3.add{e - 1}", s)
                        nc.vector.scalar_tensor_tensor(x[s][:], ps[s][:, e // GROUP, (e % GROUP) * DIM:(e % GROUP + 1) * DIM], col[s][:, 64 + e:65 + e], x[s][:], ALU.mult, ALU.add).then_inc(dve_done, DVE_L.did(f"f3.add{e}", s))
                        yield

                return first_half, second_half

            take_turns(DVE_3S, [program(0, 0)[0](s, 0) for s in A])
            dve.wait_ge(dve_done, DVE_3S.per_round)
            dve.sem_inc(dve_done, DVE_3.per_round - DVE_3S.per_round)
            with dve.Fori(0, ROUNDS) as r:
                first_half, second_half = program(1, r)
                take_turns(DVE_3, [chain(second_half(s, r), first_half(s, r + 1)) for s in A] + [chain(first_half(s, r), second_half(s, r)) for s in B])



def kernel(**inputs):
    import concourse.bacc as bacc
    from concourse.bass_utils import run_bass_kernel_spmd

    a = {k: np.asarray(v) for k, v in inputs.items()}
    col = lambda v: v.reshape(-1, 1)
    row = lambda v: v.reshape(1, -1)
    attn = a["L0_ffn_attn_w"]
    q, k, v = attn[:, 0:DIM], attn[:, DIM:2 * DIM], attn[:, 2 * DIM:]
    host = {
        "x": a["x"], "ctx": a["ctx_1024"], "ctxT": a["ctx_1024"].transpose(0, 2, 1),
        "mask_Bx1x1xS2_bk0": row(np.ascontiguousarray(a["mask_Bx1x1xS2_bk0"]).reshape(-1).view(np.int32)),
        "mask_BxS2_ik0": row(a["mask_BxS2_ik0"]),
        "L0_xattn_Wq": a["L0_xattn_Wq"].T, "L0_xattn_Wk": a["L0_xattn_Wk"].T, "L0_xattn_Wv": a["L0_xattn_Wv"].T,
        "L0_xattn_Wo": a["L0_xattn_Wo"].T, "L0_xattn_rel_emb": a["L0_xattn_rel_emb"],
        "L0_ffn_ln1_w": col(a["L0_ffn_ln1_w"]), "L0_ffn_ln1_b": col(a["L0_ffn_ln1_b"]),
        "L0_ffn_ln2_w": col(a["L0_ffn_ln2_w"]), "L0_ffn_ln2_b": col(a["L0_ffn_ln2_b"]),
        "L0_ffn_conv_w": a["L0_ffn_conv_w"].reshape(DIM, 3),
        "attn_w5": np.stack([q, k, swap_halves(q), swap_halves(k), v], axis=1),
        "L0_ffn_proj_w": a["L0_ffn_proj_w"], "L0_ffn_router_w": a["L0_ffn_router_w"],
        "L0_ffn_expert_wv": a["L0_ffn_expert_wv"], "L0_ffn_expert_proj": a["L0_ffn_expert_proj"],
        "L1_xattn_Wq": a["L1_xattn_Wq"].T, "L1_xattn_Wk": a["L1_xattn_Wk"].T, "L1_xattn_Wv": a["L1_xattn_Wv"].T,
        "L1_xattn_bq": col(a["L1_xattn_bq"]), "L1_xattn_bk": col(a["L1_xattn_bk"]), "L1_xattn_bv": row(a["L1_xattn_bv"]),
        "L1_ffn_w1": a["L1_ffn_w1"].T, "L1_ffn_w2": a["L1_ffn_w2"].T,
        "L1_ffn_conv": np.concatenate([a["L1_ffn_conv_w"].reshape(-1, CH, 3), a["L1_ffn_conv_b"].reshape(-1, CH, 1)], axis=2).transpose(1, 0, 2),
        "L2_xattn_w_sim": a["L2_xattn_w_sim"].reshape(3, DIM).T, "L2_xattn_b_sim": row(a["L2_xattn_b_sim"]),
        "L2_xattn_W_qv": a["L2_xattn_W_qv"], "L2_xattn_b_qv": row(a["L2_xattn_b_qv"]),
        "L2_ffn_w_up": a["L2_ffn_w_up"], "L2_ffn_w_gate": a["L2_ffn_w_gate"], "L2_ffn_w_down": a["L2_ffn_w_down"],
        "L3_xattn_Ws": a["L3_xattn_Ws"], "L3_xattn_W": a["L3_xattn_W"], "L3_xattn_w": a["L3_xattn_w"],
        "L3_xattn_b": col(a["L3_xattn_b"]), "L3_xattn_Wcw": col(a["L3_xattn_Wcw"]), "L3_xattn_Wcb": col(a["L3_xattn_Wcb"]),
        "L3_xattn_bcw": row(a["L3_xattn_bcw"]), "L3_xattn_bcb": row(a["L3_xattn_bcb"]),
        "L3_ffn_wg": a["L3_ffn_wg"], "L3_ffn_W": a["L3_ffn_W"].transpose(0, 2, 1), "L3_ffn_b": a["L3_ffn_b"],
        **shape_constants(),
    }
    nc = bacc.Bacc("TRN2", target_bir_lowering=False, num_devices=1)
    arrays, dram = {}, {}
    for name, value in host.items():
        value = np.ascontiguousarray(value)
        arrays[f"in_{name}"] = value
        dram[name] = nc.dram_tensor(f"in_{name}", value.shape, mybir.dt.from_np(value.dtype), kind="ExternalInput").ap()
    dram["out"] = nc.dram_tensor("out_x", (BATCH, TOK, DIM), F32, kind="ExternalOutput").ap()
    build(nc, dram)
    return run_bass_kernel_spmd(nc, [arrays], core_ids=[0]).results[0]["out_x"]
```
